# Optimizing a Trainium2 kernel written in Bass

```python
import numpy as np
import jax
import jax.numpy as jnp

def _softmax(x, axis=-1):
    return jax.nn.softmax(x, axis=axis)

def _gelu(x):
    return jax.nn.gelu(x, approximate=True)

def _silu(x):
    return jax.nn.silu(x)

def _sigmoid(x):
    return jax.nn.sigmoid(x)

def _layernorm(x, axis=-1, eps=1e-05):
    m = jnp.mean(x, axis=axis, keepdims=True)
    v = jnp.var(x, axis=axis, keepdims=True)
    return (x - m) / jnp.sqrt(v + eps)

def _scatter_add(tgt, idx, src, axis=0):
    return tgt.at[idx].add(src)

def _segment_sum(src, seg, n):
    return jax.ops.segment_sum(src, seg, n)
kernel_name = 'mk_adaln_d4_jaxref_r8_f67624'

def setup_inputs(seed: int=0):
    np.random.seed(seed)
    _w = jnp.asarray

    def _L0_attn_setup():
        import jax, jax.numpy as jnp
        import numpy as np
        B, T, D_MODEL = (4, 256, 256)
        NUM_HEADS, HEAD_SIZE = (16, 128)
        MODEL_SIZE = 256
        key = jax.random.key(seed)
        ks = jax.random.split(key, 9)
        s = 0.02 / np.sqrt(D_MODEL)
        so = 0.02 / np.sqrt(NUM_HEADS * HEAD_SIZE)
        return {'query': jax.random.normal(ks[0], (B, T, D_MODEL), jnp.float32), 'w_q': jax.random.normal(ks[1], (D_MODEL, NUM_HEADS * HEAD_SIZE), jnp.float32) * s, 'b_q': jnp.zeros((NUM_HEADS * HEAD_SIZE,), jnp.float32), 'w_k': jax.random.normal(ks[2], (D_MODEL, NUM_HEADS * HEAD_SIZE), jnp.float32) * s, 'b_k': jnp.zeros((NUM_HEADS * HEAD_SIZE,), jnp.float32), 'w_v': jax.random.normal(ks[3], (D_MODEL, NUM_HEADS * HEAD_SIZE), jnp.float32) * s, 'b_v': jnp.zeros((NUM_HEADS * HEAD_SIZE,), jnp.float32), 'w_o': jax.random.normal(ks[4], (NUM_HEADS * HEAD_SIZE, MODEL_SIZE), jnp.float32) * so, 'b_o': jnp.zeros((MODEL_SIZE,), jnp.float32)}
    _L0_attn_in = _L0_attn_setup()

    def _L0_ffn_setup():
        import jax, jax.numpy as jnp
        import numpy as np
        E = 32
        K = 4
        G = 4
        TG = 2
        H = 256
        F = 128
        FS = 256
        SCALE = 2.0
        B, S = (2, 128)
        N = B * S
        CAP = 2 * (N * K // E)

        def _gate(x, gate_w, gate_bias):
            logits = x @ gate_w.T
            scores = jax.nn.sigmoid(logits)
            sc = scores + gate_bias
            n = x.shape[0]
            grp = sc.reshape(n, G, E // G)
            group_scores = jax.lax.top_k(grp, 2)[0].sum(-1)
            _, gidx = jax.lax.top_k(group_scores, TG)
            gmask = jnp.zeros((n, G), sc.dtype).at[jnp.arange(n)[:, None], gidx].set(1.0)
            smask = jnp.repeat(gmask, E // G, axis=1)
            tmp = jnp.where(smask > 0, sc, 0.0)
            _, topk_idx = jax.lax.top_k(tmp, K)
            topk_w = jnp.take_along_axis(scores, topk_idx, axis=1)
            topk_w = topk_w / (topk_w.sum(-1, keepdims=True) + 1e-20)
            return (topk_idx, topk_w * SCALE)

        def _moe(x, topk_idx, topk_w, w1, w2, w3):
            n = x.shape[0]
            flat_e = topk_idx.reshape(-1)
            oh = jax.nn.one_hot(flat_e, E, dtype=jnp.int32)
            pos = (jnp.cumsum(oh, axis=0) * oh).sum(-1) - 1
            keep = pos < CAP
            slot = jnp.where(keep, pos, CAP)
            x_rep = jnp.repeat(x, K, axis=0)
            buf = jnp.zeros((E, CAP, H), x.dtype).at[flat_e, slot].set(x_rep, mode='drop')
            h = jax.nn.silu(jnp.einsum('ech,ehf->ecf', buf, w1)) * jnp.einsum('ech,ehf->ecf', buf, w3)
            ob = jnp.einsum('ecf,efh->ech', h, w2)
            y = ob[flat_e, jnp.minimum(slot, CAP - 1)]
            y = jnp.where(keep[:, None], y, 0.0)
            return (y.reshape(n, K, H) * topk_w[:, :, None]).sum(1)
        key = jax.random.key(seed)
        ks = jax.random.split(key, 9)
        w = 0.02
        return {'hidden_states': jax.random.normal(ks[0], (B, S, H), jnp.float32), 'gate_w': jax.random.normal(ks[1], (E, H), jnp.float32) * w, 'gate_bias': jax.random.normal(ks[2], (E,), jnp.float32) * w, 'w1': jax.random.normal(ks[3], (E, H, F), jnp.float32) * w, 'w2': jax.random.normal(ks[4], (E, F, H), jnp.float32) * w, 'w3': jax.random.normal(ks[5], (E, H, F), jnp.float32) * w, 'shared_gate': jax.random.normal(ks[6], (H, FS), jnp.float32) * w, 'shared_up': jax.random.normal(ks[7], (H, FS), jnp.float32) * w, 'shared_down': jax.random.normal(ks[8], (FS, H), jnp.float32) * w}
    _L0_ffn_in = _L0_ffn_setup()
    _L0_c = _w((lambda *s: np.random.randn(*s).astype(np.float32) * 0.05)(1, 256))
    _L0_wmod = _w((lambda *s: np.random.randn(*s).astype(np.float32) * 0.05)(256, 6 * 256) * 256 ** (-0.5))

    def _L1_attn_setup():
        import jax, jax.numpy as jnp
        import numpy as np
        import math
        H = 16
        KV = 8
        D = 128
        HID = 256
        LAYER_IDX = 1
        LAMBDA_INIT = 0.8 - 0.6 * math.exp(-0.3 * LAYER_IDX)
        EPS = 1e-05
        key = jax.random.key(seed)
        ks = jax.random.split(key, 8)
        B, S = (2, 256)
        op_size = H * D + 2 * KV * D
        return {'hidden_states': jax.random.normal(ks[0], (B, S, HID), jnp.float32), 'Wqkv_w': jax.random.normal(ks[1], (op_size, HID), jnp.float32) * 0.02, 'Wqkv_b': jnp.zeros((op_size,), jnp.float32), 'lambda_q1': jax.random.normal(ks[2], (D,), jnp.float32) * 0.1, 'lambda_k1': jax.random.normal(ks[3], (D,), jnp.float32) * 0.1, 'lambda_q2': jax.random.normal(ks[4], (D,), jnp.float32) * 0.1, 'lambda_k2': jax.random.normal(ks[5], (D,), jnp.float32) * 0.1, 'subln_w': jnp.ones((2 * D,), jnp.float32), 'out_w': jax.random.normal(ks[6], (HID, H * D), jnp.float32) * 0.02, 'out_b': jnp.zeros((HID,), jnp.float32)}
    _L1_attn_in = _L1_attn_setup()

    def _L1_ffn_setup():
        import jax, jax.numpy as jnp
        import numpy as np
        HIDDEN = 256
        INTER = 704
        B, S = (2, 256)

        def _ternary(key, shape):
            return jax.random.randint(key, shape, -1, 2).astype(jnp.float32)
        key = jax.random.key(seed)
        ks = jax.random.split(key, 7)
        x = jax.random.normal(ks[0], (B, S, HIDDEN), dtype=jnp.float32)
        gate_w = _ternary(ks[1], (INTER, HIDDEN))
        up_w = _ternary(ks[2], (INTER, HIDDEN))
        down_w = _ternary(ks[3], (HIDDEN, INTER))
        gate_s = jax.random.uniform(ks[4], (INTER,), minval=0.01, maxval=0.1, dtype=jnp.float32)
        up_s = jax.random.uniform(ks[5], (INTER,), minval=0.01, maxval=0.1, dtype=jnp.float32)
        down_s = jax.random.uniform(ks[6], (HIDDEN,), minval=0.01, maxval=0.1, dtype=jnp.float32)
        return {'x': x, 'gate_w': gate_w, 'up_w': up_w, 'down_w': down_w, 'gate_s': gate_s, 'up_s': up_s, 'down_s': down_s}
    _L1_ffn_in = _L1_ffn_setup()
    _L1_c = _w((lambda *s: np.random.randn(*s).astype(np.float32) * 0.05)(1, 256))
    _L1_wmod = _w((lambda *s: np.random.randn(*s).astype(np.float32) * 0.05)(256, 6 * 256) * 256 ** (-0.5))

    def _L2_attn_setup():
        import jax, jax.numpy as jnp
        import numpy as np
        IN_FEATURES = 256
        HEAD_NUM = 64
        D = IN_FEATURES // HEAD_NUM
        SCALE = float(np.sqrt(D))
        key = jax.random.key(seed)
        ks = jax.random.split(key, 9)
        F = IN_FEATURES
        x = jax.random.normal(ks[0], (4, 128, F), dtype=jnp.float32)
        w = lambda k: jax.random.normal(k, (F, F), dtype=jnp.float32) * 0.02
        b = lambda k: jax.random.normal(k, (F,), dtype=jnp.float32) * 0.01
        return {'x': x, 'Wq': w(ks[1]), 'bq': b(ks[2]), 'Wk': w(ks[3]), 'bk': b(ks[4]), 'Wv': w(ks[5]), 'bv': b(ks[6]), 'Wo': w(ks[7]), 'bo': b(ks[8])}
    _L2_attn_in = _L2_attn_setup()

    def _L2_ffn_setup():
        import jax, jax.numpy as jnp
        import numpy as np
        DIM_IN = 256
        DIM_HIDDEN = 1024
        key = jax.random.key(seed)
        k_x, k_g, k_u, k_d = jax.random.split(key, 4)
        s_in = 1.0 / np.sqrt(DIM_IN)
        s_hid = 1.0 / np.sqrt(DIM_HIDDEN)
        x = jax.random.normal(k_x, (4, 256, DIM_IN), dtype=jnp.float32)
        w_gate = jax.random.uniform(k_g, (DIM_HIDDEN, DIM_IN), jnp.float32, -s_in, s_in)
        w_up = jax.random.uniform(k_u, (DIM_HIDDEN, DIM_IN), jnp.float32, -s_in, s_in)
        w_down = jax.random.uniform(k_d, (DIM_IN, DIM_HIDDEN), jnp.float32, -s_hid, s_hid)
        return {'x': x, 'w_gate': w_gate, 'w_up': w_up, 'w_down': w_down}
    _L2_ffn_in = _L2_ffn_setup()
    _L2_c = _w((lambda *s: np.random.randn(*s).astype(np.float32) * 0.05)(1, 256))
    _L2_wmod = _w((lambda *s: np.random.randn(*s).astype(np.float32) * 0.05)(256, 6 * 256) * 256 ** (-0.5))

    def _L3_attn_setup():
        import jax, jax.numpy as jnp
        import numpy as np
        B, T, D_IN = (8, 512, 256)
        D_HIDDEN = 256
        D_OUT = 256
        N_BLOCKS = 8
        R_MIN, R_MAX = (0.9, 0.999)
        INIT_IMAG = 0.1

        def _lecun(key, shape, fan_in):
            return (jax.random.normal(key, shape, dtype=jnp.float32) * np.sqrt(1.0 / fan_in)).astype(jnp.float32)

        def _block_diag_linear(x, W, b):
            h, i, j = W.shape
            xb = x.reshape(x.shape[0], x.shape[1], h, i)
            y = jnp.einsum('bthi,hij->bthj', xb, W) + b
            return y.reshape(y.shape[0], y.shape[1], h * j)

        def _linear_scan(a, x):

            def combine(l, r):
                al, bl = l
                ar, br = r
                return (al * ar, ar * bl + br)
            _, h = jax.lax.associative_scan(combine, (a, x), axis=1)
            return h

        def _reference_tuple_inner(x, W_in, b_in, W_gx, b_gx, W_ga, b_ga, a_real, a_imag, W_out, b_out):
            xh = x @ W_in + b_in
            gate_x = jax.nn.sigmoid(_block_diag_linear(xh, W_gx, b_gx))
            gate_a = jax.nn.sigmoid(_block_diag_linear(xh, W_ga, b_ga))
            log_a_re = -8.0 * gate_a * jax.nn.softplus(a_real)
            log_a_im = a_imag * gate_a
            a = jnp.exp(jax.lax.complex(log_a_re, log_a_im))
            a_sq = jnp.exp(jax.lax.complex(2.0 * log_a_re, 2.0 * log_a_im))
            xr, xi = jnp.split(xh, 2, axis=-1)
            xc = jax.lax.complex(xr, xi) * gate_x
            xc = jnp.sqrt(1.0 - a_sq) * xc
            h = _linear_scan(a, xc)
            h_m = jnp.concatenate([h.real, h.imag], axis=-1)
            out = h_m @ W_out + b_out
            h_last = h_m[:, -1]
            return (out, h_last)
        key = jax.random.key(seed)
        ks = jax.random.split(key, 12)
        dh2 = D_HIDDEN // 2
        bin_, bout = (dh2 // N_BLOCKS, None)
        blk_in = D_HIDDEN // N_BLOCKS
        blk_out = dh2 // N_BLOCKS
        u1 = jax.random.uniform(ks[8], (dh2,))
        a_r = 0.5 * jnp.log(u1 * (R_MAX ** 2 - R_MIN ** 2) + R_MIN ** 2 + 1e-08)
        a_real = jnp.log(jnp.exp(-a_r) - 1.0)
        u2 = jax.random.uniform(ks[9], (dh2,))
        a_imag = jnp.pi * INIT_IMAG * u2
        return {'x': jax.random.normal(ks[0], (B, T, D_IN), dtype=jnp.float32), 'W_in': _lecun(ks[1], (D_IN, D_HIDDEN), D_IN), 'b_in': jnp.zeros((D_HIDDEN,), jnp.float32), 'W_gx': _lecun(ks[2], (N_BLOCKS, blk_in, blk_out), blk_in), 'b_gx': _lecun(ks[3], (N_BLOCKS, blk_out), blk_in), 'W_ga': _lecun(ks[4], (N_BLOCKS, blk_in, blk_out), blk_in), 'b_ga': _lecun(ks[5], (N_BLOCKS, blk_out), blk_in), 'a_real': a_real, 'a_imag': a_imag, 'W_out': _lecun(ks[6], (D_HIDDEN, D_OUT), D_HIDDEN), 'b_out': jnp.zeros((D_OUT,), jnp.float32)}
    _L3_attn_in = _L3_attn_setup()

    def _L3_ffn_setup():
        import jax, jax.numpy as jnp
        import numpy as np
        B_, S, D = (4, 512, 256)
        OUT = 256
        E, R = (8, 16)
        ALPHA = 32.0
        SCALING = ALPHA / R
        key = jax.random.key(seed)
        ks = jax.random.split(key, 6)
        x = jax.random.normal(ks[0], (B_, S, D), dtype=jnp.float32)
        W_base = jax.random.normal(ks[1], (OUT, D), dtype=jnp.float32) * D ** (-0.5)
        b_base = jax.random.normal(ks[2], (OUT,), dtype=jnp.float32) * 0.01
        router_W = jax.random.normal(ks[3], (E, D), dtype=jnp.float32) * D ** (-0.5)
        A = jax.random.normal(ks[4], (E, R, D), dtype=jnp.float32) * D ** (-0.5)
        Bw = jax.random.normal(ks[5], (E, OUT, R), dtype=jnp.float32) * 0.02
        return {'x': x, 'W_base': W_base, 'b_base': b_base, 'router_W': router_W, 'A': A, 'Bw': Bw}
    _L3_ffn_in = _L3_ffn_setup()
    _L3_c = _w((lambda *s: np.random.randn(*s).astype(np.float32) * 0.05)(1, 256))
    _L3_wmod = _w((lambda *s: np.random.randn(*s).astype(np.float32) * 0.05)(256, 6 * 256) * 256 ** (-0.5))
    _d = {'L0_attn_query': _L0_attn_in['query'], 'L0_attn_w_q': _L0_attn_in['w_q'], 'L0_attn_b_q': _L0_attn_in['b_q'], 'L0_attn_w_k': _L0_attn_in['w_k'], 'L0_attn_b_k': _L0_attn_in['b_k'], 'L0_attn_w_v': _L0_attn_in['w_v'], 'L0_attn_b_v': _L0_attn_in['b_v'], 'L0_attn_w_o': _L0_attn_in['w_o'], 'L0_attn_b_o': _L0_attn_in['b_o'], 'L0_ffn_gate_w': _L0_ffn_in['gate_w'], 'L0_ffn_gate_bias': _L0_ffn_in['gate_bias'], 'L0_ffn_w1': _L0_ffn_in['w1'], 'L0_ffn_w2': _L0_ffn_in['w2'], 'L0_ffn_w3': _L0_ffn_in['w3'], 'L0_ffn_shared_gate': _L0_ffn_in['shared_gate'], 'L0_ffn_shared_up': _L0_ffn_in['shared_up'], 'L0_ffn_shared_down': _L0_ffn_in['shared_down'], 'L0_c': _L0_c, 'L0_wmod': _L0_wmod, 'L1_attn_Wqkv_w': _L1_attn_in['Wqkv_w'], 'L1_attn_Wqkv_b': _L1_attn_in['Wqkv_b'], 'L1_attn_lambda_q1': _L1_attn_in['lambda_q1'], 'L1_attn_lambda_k1': _L1_attn_in['lambda_k1'], 'L1_attn_lambda_q2': _L1_attn_in['lambda_q2'], 'L1_attn_lambda_k2': _L1_attn_in['lambda_k2'], 'L1_attn_subln_w': _L1_attn_in['subln_w'], 'L1_attn_out_w': _L1_attn_in['out_w'], 'L1_attn_out_b': _L1_attn_in['out_b'], 'L1_ffn_gate_w': _L1_ffn_in['gate_w'], 'L1_ffn_up_w': _L1_ffn_in['up_w'], 'L1_ffn_down_w': _L1_ffn_in['down_w'], 'L1_ffn_gate_s': _L1_ffn_in['gate_s'], 'L1_ffn_up_s': _L1_ffn_in['up_s'], 'L1_ffn_down_s': _L1_ffn_in['down_s'], 'L1_c': _L1_c, 'L1_wmod': _L1_wmod, 'L2_attn_Wq': _L2_attn_in['Wq'], 'L2_attn_bq': _L2_attn_in['bq'], 'L2_attn_Wk': _L2_attn_in['Wk'], 'L2_attn_bk': _L2_attn_in['bk'], 'L2_attn_Wv': _L2_attn_in['Wv'], 'L2_attn_bv': _L2_attn_in['bv'], 'L2_attn_Wo': _L2_attn_in['Wo'], 'L2_attn_bo': _L2_attn_in['bo'], 'L2_ffn_w_gate': _L2_ffn_in['w_gate'], 'L2_ffn_w_up': _L2_ffn_in['w_up'], 'L2_ffn_w_down': _L2_ffn_in['w_down'], 'L2_c': _L2_c, 'L2_wmod': _L2_wmod, 'L3_attn_W_in': _L3_attn_in['W_in'], 'L3_attn_b_in': _L3_attn_in['b_in'], 'L3_attn_W_gx': _L3_attn_in['W_gx'], 'L3_attn_b_gx': _L3_attn_in['b_gx'], 'L3_attn_W_ga': _L3_attn_in['W_ga'], 'L3_attn_b_ga': _L3_attn_in['b_ga'], 'L3_attn_a_real': _L3_attn_in['a_real'], 'L3_attn_a_imag': _L3_attn_in['a_imag'], 'L3_attn_W_out': _L3_attn_in['W_out'], 'L3_attn_b_out': _L3_attn_in['b_out'], 'L3_ffn_W_base': _L3_ffn_in['W_base'], 'L3_ffn_b_base': _L3_ffn_in['b_base'], 'L3_ffn_router_W': _L3_ffn_in['router_W'], 'L3_ffn_A': _L3_ffn_in['A'], 'L3_ffn_Bw': _L3_ffn_in['Bw'], 'L3_c': _L3_c, 'L3_wmod': _L3_wmod}
    _x0 = _d['L0_attn_query']
    _d['L0_attn_query'] = jax.random.normal(jax.random.fold_in(jax.random.key(seed), 1), (1, 1024, 256), dtype=_x0.dtype)
    del _x0
    return _d

def reference(L0_attn_query, L0_attn_w_q, L0_attn_b_q, L0_attn_w_k, L0_attn_b_k, L0_attn_w_v, L0_attn_b_v, L0_attn_w_o, L0_attn_b_o, L0_ffn_gate_w, L0_ffn_gate_bias, L0_ffn_w1, L0_ffn_w2, L0_ffn_w3, L0_ffn_shared_gate, L0_ffn_shared_up, L0_ffn_shared_down, L0_c, L0_wmod, L1_attn_Wqkv_w, L1_attn_Wqkv_b, L1_attn_lambda_q1, L1_attn_lambda_k1, L1_attn_lambda_q2, L1_attn_lambda_k2, L1_attn_subln_w, L1_attn_out_w, L1_attn_out_b, L1_ffn_gate_w, L1_ffn_up_w, L1_ffn_down_w, L1_ffn_gate_s, L1_ffn_up_s, L1_ffn_down_s, L1_c, L1_wmod, L2_attn_Wq, L2_attn_bq, L2_attn_Wk, L2_attn_bk, L2_attn_Wv, L2_attn_bv, L2_attn_Wo, L2_attn_bo, L2_ffn_w_gate, L2_ffn_w_up, L2_ffn_w_down, L2_c, L2_wmod, L3_attn_W_in, L3_attn_b_in, L3_attn_W_gx, L3_attn_b_gx, L3_attn_W_ga, L3_attn_b_ga, L3_attn_a_real, L3_attn_a_imag, L3_attn_W_out, L3_attn_b_out, L3_ffn_W_base, L3_ffn_b_base, L3_ffn_router_W, L3_ffn_A, L3_ffn_Bw, L3_c, L3_wmod):

    def _L0_attn_ref(query, w_q, b_q, w_k, b_k, w_v, b_v, w_o, b_o):
        import jax, jax.numpy as jnp
        import numpy as np
        B, T, D_MODEL = (4, 256, 256)
        NUM_HEADS, HEAD_SIZE = (16, 128)
        MODEL_SIZE = 256
        B_, T_, _ = query.shape
        q = (query @ w_q + b_q).reshape(B_, T_, NUM_HEADS, HEAD_SIZE)
        k = (query @ w_k + b_k).reshape(B_, T_, NUM_HEADS, HEAD_SIZE)
        v = (query @ w_v + b_v).reshape(B_, T_, NUM_HEADS, HEAD_SIZE)
        logits = jnp.einsum('bthd,bThd->bhtT', q, k) * jax.lax.rsqrt(jnp.float32(HEAD_SIZE))
        i = jnp.arange(T_, dtype=jnp.int32)[:, None]
        j = jnp.arange(T_, dtype=jnp.int32)
        mask = (i >= j).astype(logits.dtype)
        logits = logits - 10000000000.0 * (1.0 - mask)
        weights = jax.nn.softmax(logits, axis=-1)
        attn = jnp.einsum('bhtT,bThd->bthd', weights, v).reshape(B_, T_, NUM_HEADS * HEAD_SIZE)
        out = attn @ w_o + b_o
        return out

    def _L0_ffn_ref(hidden_states, gate_w, gate_bias, w1, w2, w3, shared_gate, shared_up, shared_down):
        import jax, jax.numpy as jnp
        import numpy as np
        E = 32
        K = 4
        G = 4
        TG = 2
        H = 256
        F = 128
        FS = 256
        SCALE = 2.0
        B, S = (2, 128)
        N = B * S
        CAP = 2 * (N * K // E)

        def _gate(x, gate_w, gate_bias):
            logits = x @ gate_w.T
            scores = jax.nn.sigmoid(logits)
            sc = scores + gate_bias
            n = x.shape[0]
            grp = sc.reshape(n, G, E // G)
            group_scores = jax.lax.top_k(grp, 2)[0].sum(-1)
            _, gidx = jax.lax.top_k(group_scores, TG)
            gmask = jnp.zeros((n, G), sc.dtype).at[jnp.arange(n)[:, None], gidx].set(1.0)
            smask = jnp.repeat(gmask, E // G, axis=1)
            tmp = jnp.where(smask > 0, sc, 0.0)
            _, topk_idx = jax.lax.top_k(tmp, K)
            topk_w = jnp.take_along_axis(scores, topk_idx, axis=1)
            topk_w = topk_w / (topk_w.sum(-1, keepdims=True) + 1e-20)
            return (topk_idx, topk_w * SCALE)

        def _moe(x, topk_idx, topk_w, w1, w2, w3):
            n = x.shape[0]
            flat_e = topk_idx.reshape(-1)
            oh = jax.nn.one_hot(flat_e, E, dtype=jnp.int32)
            pos = (jnp.cumsum(oh, axis=0) * oh).sum(-1) - 1
            keep = pos < CAP
            slot = jnp.where(keep, pos, CAP)
            x_rep = jnp.repeat(x, K, axis=0)
            buf = jnp.zeros((E, CAP, H), x.dtype).at[flat_e, slot].set(x_rep, mode='drop')
            h = jax.nn.silu(jnp.einsum('ech,ehf->ecf', buf, w1)) * jnp.einsum('ech,ehf->ecf', buf, w3)
            ob = jnp.einsum('ecf,efh->ech', h, w2)
            y = ob[flat_e, jnp.minimum(slot, CAP - 1)]
            y = jnp.where(keep[:, None], y, 0.0)
            return (y.reshape(n, K, H) * topk_w[:, :, None]).sum(1)
        b, s, h = hidden_states.shape
        x = hidden_states.reshape(-1, h)
        topk_idx, topk_w = _gate(x, gate_w, gate_bias)
        out = _moe(x, topk_idx, topk_w, w1, w2, w3)
        shared = jax.nn.silu(x @ shared_gate) * (x @ shared_up) @ shared_down
        return (out + shared).reshape(b, s, h)

    def _L1_attn_ref(hidden_states, Wqkv_w, Wqkv_b, lambda_q1, lambda_k1, lambda_q2, lambda_k2, subln_w, out_w, out_b):
        import jax, jax.numpy as jnp
        import numpy as np
        import math
        H = 16
        KV = 8
        D = 128
        HID = 256
        LAYER_IDX = 1
        LAMBDA_INIT = 0.8 - 0.6 * math.exp(-0.3 * LAYER_IDX)
        EPS = 1e-05
        B, S, _ = hidden_states.shape
        qkv = hidden_states @ Wqkv_w.T + Wqkv_b
        q, k, v = jnp.split(qkv, [H * D, H * D + KV * D], axis=-1)
        q = q.reshape(B, S, H // 2, 2, D)
        k = k.reshape(B, S, KV // 2, 2, D)
        v = v.reshape(B, S, KV // 2, 2 * D)
        rep = H // KV
        k = jnp.repeat(k, rep, axis=2)
        v = jnp.repeat(v, rep, axis=2)
        scale = D ** (-0.5)
        causal = jnp.tril(jnp.ones((S, S), bool))
        neg = jnp.finfo(jnp.float32).min

        def attn_map(qi, ki):
            s = jnp.einsum('bqhd,bkhd->bhqk', qi, ki) * scale
            s = jnp.where(causal, s, neg)
            return jax.nn.softmax(s, axis=-1)
        p1 = attn_map(q[:, :, :, 0], k[:, :, :, 0])
        p2 = attn_map(q[:, :, :, 1], k[:, :, :, 1])
        lam1 = jnp.exp(jnp.sum(lambda_q1 * lambda_k1))
        lam2 = jnp.exp(jnp.sum(lambda_q2 * lambda_k2))
        lam = lam1 - lam2 + LAMBDA_INIT
        p = p1 - lam * p2
        o = jnp.einsum('bhqk,bkhe->bqhe', p, v)
        rms = jax.lax.rsqrt(jnp.mean(o * o, axis=-1, keepdims=True) + EPS)
        o = o * rms * subln_w
        o = o * (1.0 - LAMBDA_INIT)
        o = o.reshape(B, S, H * D)
        return o @ out_w.T + out_b

    def _L1_ffn_ref(x, gate_w, up_w, down_w, gate_s, up_s, down_s):
        import jax, jax.numpy as jnp
        import numpy as np
        HIDDEN = 256
        INTER = 704
        B, S = (2, 256)

        def _ternary(key, shape):
            return jax.random.randint(key, shape, -1, 2).astype(jnp.float32)
        b, s, h = x.shape
        xf = x.reshape(b * s, h)
        g = jnp.einsum('th,ih->ti', xf, gate_w) * gate_s
        u = jnp.einsum('th,ih->ti', xf, up_w) * up_s
        hdn = jax.nn.silu(g) * u
        out = jnp.einsum('ti,hi->th', hdn, down_w) * down_s
        return out.reshape(b, s, -1)

    def _L2_attn_ref(x, Wq, bq, Wk, bk, Wv, bv, Wo, bo):
        import jax, jax.numpy as jnp
        import numpy as np
        IN_FEATURES = 256
        HEAD_NUM = 64
        D = IN_FEATURES // HEAD_NUM
        SCALE = float(np.sqrt(D))
        B, S, F = x.shape
        d = D
        h = F // d
        q = x @ Wq + bq
        k = x @ Wk + bk
        v = x @ Wv + bv

        def to_heads(t):
            return t.reshape(B, S, d, h).transpose(0, 2, 1, 3)
        q, k, v = (to_heads(q), to_heads(k), to_heads(v))
        scores = jnp.einsum('bdsh,bdth->bdst', q, k) / SCALE
        weights = jax.nn.softmax(scores, axis=-1)
        feats = jnp.einsum('bdst,bdth->bdsh', weights, v)
        feats = feats.transpose(0, 2, 1, 3).reshape(B, S, F)
        return feats @ Wo + bo

    def _L2_ffn_ref(x, w_gate, w_up, w_down):
        import jax, jax.numpy as jnp
        import numpy as np
        DIM_IN = 256
        DIM_HIDDEN = 1024
        gate = jnp.einsum('bsd,hd->bsh', x, w_gate)
        up = jnp.einsum('bsd,hd->bsh', x, w_up)
        gated = jax.nn.silu(gate) * up
        return jnp.einsum('bsh,dh->bsd', gated, w_down)

    def _L3_attn_ref(x, W_in, b_in, W_gx, b_gx, W_ga, b_ga, a_real, a_imag, W_out, b_out):
        import jax, jax.numpy as jnp
        import numpy as np
        B, T, D_IN = (8, 512, 256)
        D_HIDDEN = 256
        D_OUT = 256
        N_BLOCKS = 8
        R_MIN, R_MAX = (0.9, 0.999)
        INIT_IMAG = 0.1

        def _lecun(key, shape, fan_in):
            return (jax.random.normal(key, shape, dtype=jnp.float32) * np.sqrt(1.0 / fan_in)).astype(jnp.float32)

        def _block_diag_linear(x, W, b):
            h, i, j = W.shape
            xb = x.reshape(x.shape[0], x.shape[1], h, i)
            y = jnp.einsum('bthi,hij->bthj', xb, W) + b
            return y.reshape(y.shape[0], y.shape[1], h * j)

        def _linear_scan(a, x):

            def combine(l, r):
                al, bl = l
                ar, br = r
                return (al * ar, ar * bl + br)
            _, h = jax.lax.associative_scan(combine, (a, x), axis=1)
            return h

        def _reference_tuple_inner(x, W_in, b_in, W_gx, b_gx, W_ga, b_ga, a_real, a_imag, W_out, b_out):
            xh = x @ W_in + b_in
            gate_x = jax.nn.sigmoid(_block_diag_linear(xh, W_gx, b_gx))
            gate_a = jax.nn.sigmoid(_block_diag_linear(xh, W_ga, b_ga))
            log_a_re = -8.0 * gate_a * jax.nn.softplus(a_real)
            log_a_im = a_imag * gate_a
            a = jnp.exp(jax.lax.complex(log_a_re, log_a_im))
            a_sq = jnp.exp(jax.lax.complex(2.0 * log_a_re, 2.0 * log_a_im))
            xr, xi = jnp.split(xh, 2, axis=-1)
            xc = jax.lax.complex(xr, xi) * gate_x
            xc = jnp.sqrt(1.0 - a_sq) * xc
            h = _linear_scan(a, xc)
            h_m = jnp.concatenate([h.real, h.imag], axis=-1)
            out = h_m @ W_out + b_out
            h_last = h_m[:, -1]
            return (out, h_last)
        return _reference_tuple_inner(x, W_in, b_in, W_gx, b_gx, W_ga, b_ga, a_real, a_imag, W_out, b_out)[0]

    def _L3_ffn_ref(x, W_base, b_base, router_W, A, Bw):
        import jax, jax.numpy as jnp
        import numpy as np
        B_, S, D = (4, 512, 256)
        OUT = 256
        E, R = (8, 16)
        ALPHA = 32.0
        SCALING = ALPHA / R
        base_out = jnp.einsum('bsd,od->bso', x, W_base) + b_base
        logits = jnp.einsum('bsd,ed->bse', jax.lax.stop_gradient(x), router_W)
        routing_probs = jax.nn.softmax(logits, axis=-1)
        expert_idx = jnp.argmax(routing_probs, axis=-1)
        onehot = jax.nn.one_hot(expert_idx, E, dtype=x.dtype)
        h = jnp.einsum('bsd,erd->bser', x, A)
        h = h * onehot[..., None]
        delta = jnp.einsum('bser,eor->bso', h, Bw)
        return base_out + delta * SCALING
    x = L0_attn_query
    mod = (_silu(L0_c) @ L0_wmod).reshape(L0_c.shape[0], 6, 1, -1)
    sa, ca, ga, sb, cb, gb = (mod[:, 0], mod[:, 1], mod[:, 2], mod[:, 3], mod[:, 4], mod[:, 5])
    ga = (2 * (ga >= 0) - 1) * jnp.maximum(jnp.abs(ga), 0.25)
    gb = (2 * (gb >= 0) - 1) * jnp.maximum(jnp.abs(gb), 0.25)
    h = _layernorm(x, axis=-1) * (1 + ca) + sa
    x = x + ga * _L0_attn_ref(h, L0_attn_w_q, L0_attn_b_q, L0_attn_w_k, L0_attn_b_k, L0_attn_w_v, L0_attn_b_v, L0_attn_w_o, L0_attn_b_o)
    h = _layernorm(x, axis=-1) * (1 + cb) + sb
    x = x + gb * _L0_ffn_ref(h, L0_ffn_gate_w, L0_ffn_gate_bias, L0_ffn_w1, L0_ffn_w2, L0_ffn_w3, L0_ffn_shared_gate, L0_ffn_shared_up, L0_ffn_shared_down)
    mod = (_silu(L1_c) @ L1_wmod).reshape(L1_c.shape[0], 6, 1, -1)
    sa, ca, ga, sb, cb, gb = (mod[:, 0], mod[:, 1], mod[:, 2], mod[:, 3], mod[:, 4], mod[:, 5])
    ga = (2 * (ga >= 0) - 1) * jnp.maximum(jnp.abs(ga), 0.25)
    gb = (2 * (gb >= 0) - 1) * jnp.maximum(jnp.abs(gb), 0.25)
    h = _layernorm(x, axis=-1) * (1 + ca) + sa
    x = x + ga * _L1_attn_ref(h, L1_attn_Wqkv_w, L1_attn_Wqkv_b, L1_attn_lambda_q1, L1_attn_lambda_k1, L1_attn_lambda_q2, L1_attn_lambda_k2, L1_attn_subln_w, L1_attn_out_w, L1_attn_out_b)
    h = _layernorm(x, axis=-1) * (1 + cb) + sb
    x = x + gb * _L1_ffn_ref(h, L1_ffn_gate_w, L1_ffn_up_w, L1_ffn_down_w, L1_ffn_gate_s, L1_ffn_up_s, L1_ffn_down_s)
    mod = (_silu(L2_c) @ L2_wmod).reshape(L2_c.shape[0], 6, 1, -1)
    sa, ca, ga, sb, cb, gb = (mod[:, 0], mod[:, 1], mod[:, 2], mod[:, 3], mod[:, 4], mod[:, 5])
    ga = (2 * (ga >= 0) - 1) * jnp.maximum(jnp.abs(ga), 0.25)
    gb = (2 * (gb >= 0) - 1) * jnp.maximum(jnp.abs(gb), 0.25)
    h = _layernorm(x, axis=-1) * (1 + ca) + sa
    x = x + ga * _L2_attn_ref(h, L2_attn_Wq, L2_attn_bq, L2_attn_Wk, L2_attn_bk, L2_attn_Wv, L2_attn_bv, L2_attn_Wo, L2_attn_bo)
    h = _layernorm(x, axis=-1) * (1 + cb) + sb
    x = x + gb * _L2_ffn_ref(h, L2_ffn_w_gate, L2_ffn_w_up, L2_ffn_w_down)
    mod = (_silu(L3_c) @ L3_wmod).reshape(L3_c.shape[0], 6, 1, -1)
    sa, ca, ga, sb, cb, gb = (mod[:, 0], mod[:, 1], mod[:, 2], mod[:, 3], mod[:, 4], mod[:, 5])
    ga = (2 * (ga >= 0) - 1) * jnp.maximum(jnp.abs(ga), 0.25)
    gb = (2 * (gb >= 0) - 1) * jnp.maximum(jnp.abs(gb), 0.25)
    h = _layernorm(x, axis=-1) * (1 + ca) + sa
    x = x + ga * _L3_attn_ref(h, L3_attn_W_in, L3_attn_b_in, L3_attn_W_gx, L3_attn_b_gx, L3_attn_W_ga, L3_attn_b_ga, L3_attn_a_real, L3_attn_a_imag, L3_attn_W_out, L3_attn_b_out)
    h = _layernorm(x, axis=-1) * (1 + cb) + sb
    x = x + gb * _L3_ffn_ref(h, L3_ffn_W_base, L3_ffn_b_base, L3_ffn_router_W, L3_ffn_A, L3_ffn_Bw)
    return x

_drawn_inputs = setup_inputs


def setup_inputs(seed=0):
    import zlib

    import numpy as np

    out = dict(_drawn_inputs(seed))
    spreads = {'L0_attn_b_q': (0.0, 2.0),
     'L0_attn_b_k': (0.0, 2.0),
     'L0_attn_b_v': (0.0, 0.8),
     'L0_attn_b_o': (0.0, 0.1),
     'L1_attn_Wqkv_b': (0.0, 0.1),
     'L1_attn_subln_w': (1.0, 0.6),
     'L1_attn_out_b': (0.0, 0.298),
     'L3_attn_b_in': (0.0, 0.591),
     'L3_attn_b_out': (0.0, 1.202)}
    factors = {'L0_attn_w_q': 64.0,
     'L0_attn_w_k': 64.0,
     'L0_attn_w_v': 39.692,
     'L0_attn_w_o': 8.0,
     'L0_ffn_gate_w': 8.0,
     'L0_ffn_gate_bias': 8.0,
     'L0_ffn_w1': 8.0,
     'L0_ffn_w2': 8.0,
     'L0_ffn_w3': 8.0,
     'L0_ffn_shared_gate': 8.0,
     'L0_ffn_shared_up': 8.0,
     'L0_ffn_shared_down': 8.0,
     'L1_attn_lambda_q1': 8.0,
     'L1_attn_lambda_k1': 64.0,
     'L1_attn_lambda_q2': 64.0,
     'L1_attn_lambda_k2': 8.0,
     'L2_attn_Wq': 8.0,
     'L2_attn_bq': 8.0,
     'L2_attn_Wk': 8.0,
     'L2_attn_bk': 64.0,
     'L2_attn_Wv': 8.0,
     'L2_attn_bv': 29.871,
     'L2_attn_Wo': 8.0,
     'L2_attn_bo': 64.0,
     'L3_attn_b_gx': 19.136,
     'L3_attn_b_ga': 13.325,
     'L3_ffn_b_base': 64.0,
     'L2_ffn_w_gate': 7.815,
     'L2_ffn_w_up': 7.565,
     'L2_ffn_w_down': 7.52,
     'L3_attn_W_gx': 3.425,
     'L3_attn_W_ga': 4.862,
     'L3_attn_a_imag': 3.582,
     'L3_ffn_router_W': 5.538,
     'L3_ffn_A': 5.093,
     'L3_ffn_Bw': 5.064}
    for name, (base, spread) in spreads.items():
        noise = np.random.default_rng([zlib.crc32(name.encode()), seed]).standard_normal(out[name].shape)
        drawn = base * np.exp(spread * noise) if base else spread * noise
        out[name] = jnp.asarray(drawn.astype(out[name].dtype))
    for name, factor in factors.items():
        out[name] = (out[name] * factor).astype(out[name].dtype)
    return out
```

```python
from contextlib import ExitStack

import numpy as np

import concourse.bass as bass
from concourse import mybir

F32 = mybir.dt.float32
BF16 = mybir.dt.bfloat16
U32 = mybir.dt.uint32
I32 = mybir.dt.int32
ALU = mybir.AluOpType
ACT = mybir.ActivationFunctionType
AX_X = mybir.AxisListType.X

P = 128
TOKENS = 1024
TILES = TOKENS // P
D = 256
KT = D // P
BANK = 512
CHUNKS = TOKENS // BANK
LN_EPS = 1e-5
LAYERS = 4


class Core:

    def __init__(self, nc, ctx):
        self.nc = nc
        self.ctx = ctx
        self.taken = {}
        sb, ps = self.sb, self.psum
        self.ps = ps("acc", [P, 8, BANK], F32)
        self.x = sb("x", [P, TILES, D], F32)
        self.ht = sb("ht", [P, KT, TOKENS], F32)
        self.xn = sb("xn", [P, TILES, D], F32)
        self.ident = sb("ident", [P, P], F32)
        self.ident_bf = sb("ident_bf", [P, P], BF16)
        self.causal_bf = sb("causal_bf", [P, P], BF16)
        self.eps = sb("eps", [P, 1], F32)
        self.half_neg = sb("half_neg", [P, TILES], F32)
        self.modc = sb("modc", [P, 4, KT], F32)
        self.gate = sb("gate", [P, 2, D], F32)
        self.wmod = sb("wmod", [P, KT, 6 * D], F32)
        self.craw = sb("craw", [P, LAYERS, KT], F32)
        self.s_wmod = self.sem("s_wmod")
        self.s_x = self.sem("s_x")
        self.norm_sems = {key: self.sem("norm_" + key) for key in
                          ("stats", "mv", "veps", "rstd", "xn", "transposed",
                           "sc", "scb", "cols", "modc", "rows", "gate")}
        self.ffn_sems = {key: self.sem("ffn_" + key) for key in
                         ("w_loaded", "d_loaded", "upped", "silued", "hid_done", "downed", "gated", "added",
                          "row")}

    def unique(self, name):
        self.taken[name] = self.taken.get(name, 0) + 1
        return name if self.taken[name] == 1 else f"{name}_{self.taken[name]}"

    def sb(self, name, shape, dt, ctx=None):
        return (ctx or self.ctx).enter_context(self.nc.sbuf_tensor(self.unique(name), shape, dt))

    def psum(self, name, shape, dt):
        return self.ctx.enter_context(self.nc.psum_tensor(name, shape, dt))

    def sem(self, name, ctx=None):
        return (ctx or self.ctx).enter_context(self.nc.semaphore(self.unique(name)))


def prepare(core, A):
    nc = core.nc
    with ExitStack() as ctx:
        s_const = core.sem("s_const", ctx)
        block = ctx.enter_context(nc.Block())

        @block.sync
        def _(sp):
            sp.dma_start(core.craw[:], A["cond"]).then_inc(core.s_wmod, 16)
            sp.dma_start(core.wmod[:], A["wmod0"]).then_inc(core.s_wmod, 16)
            sp.dma_start(core.x[:], A["x"]).then_inc(core.s_x, 16)

        @block.gpsimd
        def _(pool):
            pool.memset(core.ident[:], 0.0).then_inc(s_const, 1)
            pool.memset(core.ident_bf[:], 0.0).then_inc(s_const, 1)
            pool.memset(core.causal_bf[:], 0.0).then_inc(s_const, 1)
            pool.memset(core.half_neg[:], -0.5).then_inc(s_const, 1)
            pool.memset(core.eps[:], LN_EPS).then_inc(s_const, 1)
            pool.wait_ge(s_const, 5)
            for m in (core.ident, core.ident_bf):
                pool.affine_select(out=m[:], in_=m[:], compare_op=ALU.not_equal, fill=1.0, base=0,
                                   pattern=[[-1, P]], channel_multiplier=1).then_inc(s_const, 1)
            pool.affine_select(out=core.causal_bf[:], in_=core.causal_bf[:], compare_op=ALU.is_ge,
                               fill=MASKED, base=0, pattern=[[-1, P]],
                               channel_multiplier=1).then_inc(s_const, 1)


MASKED = -1.0e10


SHIFT_A, SCALE_A, GATE_A, SHIFT_B, SCALE_B, GATE_B = range(6)


def normalise(core, A, layer, which):
    nc = core.nc
    x, xn, ht, ps = core.x, core.xn, core.ht, core.ps
    n = 2 * layer + which
    modulate = which == 0
    cols = ps[:, 4, 0:4 * KT].rearrange("p (v k) -> p v k", v=4)
    rows = ps[:, 5, :]
    s = core.norm_sems
    with ExitStack() as ctx:
        stats = core.sb("stats", [P, TILES, 6], F32, ctx)
        mv = core.sb("mv", [P, TILES, 2], F32, ctx)
        rstd = core.sb("rstd", [P, TILES], F32, ctx)
        veps = core.sb("veps", [P, TILES], F32, ctx)
        sc = core.sb("sc", [P, KT], F32, ctx)
        scb = core.sb("scb", [P, KT, P], F32, ctx)
        mag = core.sb("mag", [P, 2 * D], F32, ctx)
        sgn = core.sb("sgn", [P, 2 * D], F32, ctx)
        block = ctx.enter_context(nc.Block())

        @block.vector
        def _(dve):
            if n == 0:
                dve.wait_ge(core.s_x, 16)
            for i in range(TILES):
                dve.bn_stats(stats[:, i, :], x[:, i, :]).then_inc(s["stats"], 1)
            for i in range(TILES):
                dve.wait_ge(s["stats"], TILES * n + i + 1)
                dve.bn_aggr(mv[:, i, :], stats[:, i, :]).then_inc(s["mv"], 1)
            dve.wait_ge(s["mv"], TILES * (n + 1))
            dve.tensor_scalar(veps[:], mv[:, :, 1], LN_EPS, None, ALU.add).then_inc(s["veps"], 1)
            if modulate:
                dve.wait_ge(s["sc"], layer + 1)
                for k in range(KT):
                    dve.tensor_copy(scb[:, k, :], sc[:, k:k + 1].to_broadcast([P, P])).then_inc(s["scb"], 1)
            dve.wait_ge(s["rstd"], n + 1)
            for i in range(TILES):
                dve.tensor_scalar(xn[:, i, :], x[:, i, :], mv[:, i, 0:1], rstd[:, i:i + 1],
                                  ALU.subtract, ALU.mult).then_inc(s["xn"], 1)
                if modulate and i == 3:
                    dve.wait_ge(s["cols"], layer + 1)
                    dve.tensor_scalar(core.modc[:, 0::2, :], cols[:, 1::2, :], 1.0, None,
                                      ALU.add).then_inc(s["modc"], 1)
                    dve.tensor_copy(core.modc[:, 1::2, :], cols[:, 0::2, :]).then_inc(s["modc"], 1)
            if modulate:
                dve.wait_ge(s["rows"], layer + 1)
                dve.tensor_copy(mag[:], rows).then_inc(s["gate"], 1)
                dve.tensor_scalar(sgn[:], rows, 0.0, 2.0, ALU.is_ge, ALU.mult).then_inc(s["gate"], 1)
                dve.wait_ge(s["gate"], 4 * layer + 1)
                dve.scalar_tensor_tensor(out=mag[:], in0=mag[:], scalar=-1.0, in1=mag[:], op0=ALU.mult,
                                         op1=ALU.max).then_inc(s["gate"], 1)
                dve.wait_ge(s["gate"], 4 * layer + 3)
                dve.tensor_scalar(mag[:], mag[:], 0.25, None, ALU.max).then_inc(s["gate"], 1)
                dve.wait_ge(s["gate"], 4 * layer + 4)
                dve.scalar_tensor_tensor(out=core.gate[:].rearrange("p g d -> p (g d)"), in0=sgn[:],
                                         scalar=-1.0, in1=mag[:], op0=ALU.add, op1=ALU.mult)

        @block.gpsimd
        def _(pool):
            pool.wait_ge(s["veps"], n + 1)
            pool.tensor_tensor(rstd[:], veps[:], core.half_neg[:], ALU.pow).then_inc(s["rstd"], 1)

        @block.tensor
        def _(pe):
            if modulate:
                pe.wait_ge(s["sc"], layer + 1)
                pe.wait_ge(core.s_wmod, 32 + 16 * layer)
                for v, part in enumerate((SHIFT_A, SCALE_A, SHIFT_B, SCALE_B)):
                    for m in range(KT):
                        for k in range(KT):
                            last = pe.matmul(cols[:, v, m:m + 1],
                                             core.wmod[:, k, part * D + m * P:part * D + m * P + P],
                                             sc[:, k:k + 1], start=(k == 0), stop=(k == KT - 1))
                last.then_inc(s["cols"], 1)
                pe.wait_ge(s["scb"], KT * (layer + 1))
                for g, part in enumerate((GATE_A, GATE_B)):
                    for k in range(KT):
                        last = pe.matmul(rows[:, g * D:g * D + D], scb[:, k, :],
                                         core.wmod[:, k, part * D:part * D + D],
                                         start=(k == 0), stop=(k == KT - 1))
                last.then_inc(s["rows"], 1)
            for c in range(CHUNKS):
                for i in range(4):
                    pe.wait_ge(s["xn"], TILES * n + 4 * c + i + 1)
                    for k in range(KT):
                        last = pe.transpose(ps[:, 2 * c + k, i * P:i * P + P], xn[:, 4 * c + i, k * P:k * P + P],
                                            core.ident[:])
                last.then_inc(s["transposed"], 1)

        @block.scalar
        def _(act):
            if modulate:
                act.wait_ge(core.s_wmod, 32 + 16 * layer)
                act.activation(sc[:], core.craw[:, layer, :], ACT.Silu).then_inc(s["sc"], 1)
                act.wait_ge(s["modc"], 2 * (layer + 1))
            for c in range(CHUNKS):
                act.wait_ge(s["transposed"], CHUNKS * n + c + 1)
                for k in range(KT):
                    act.activation(ht[:, k, c * BANK:c * BANK + BANK], ps[:, 2 * c + k, :], ACT.Identity,
                                   scale=core.modc[:, 2 * which, k:k + 1], bias=core.modc[:, 2 * which + 1, k:k + 1])

        if modulate and layer + 1 < LAYERS:
            @block.sync
            def _(sp):
                sp.wait_ge(s["rows"], layer + 1)
                sp.dma_start(core.wmod[:], A[f"wmod{layer + 1}"]).then_inc(core.s_wmod, 16)


def causal_blocks(i):
    return i + 1


def attention_l0(core, A):
    nc = core.nc
    HEADS, HD = 16, 128
    PAIRS = HEADS // 2
    STEPS = 2 * TILES
    SCALE = float(np.float32(HD) ** np.float32(-0.5))
    x, ht, ps = core.x, core.ht, core.ps
    BIAS_Q, BIAS_K = 3 * KT * HD, 3 * KT * HD + 1
    CREDIT = 2
    chunks = [(causal_blocks(s % TILES) + 3) // 4 for s in range(STEPS)]
    before = [sum(chunks[:s]) for s in range(STEPS + 1)]
    PER_PAIR = before[STEPS]
    TURN_CREDIT = 3

    def turned_by(p, s):
        return PER_PAIR * p + (before[s + 1] if s >= 0 else before[s + 1 + STEPS] - PER_PAIR) + TURN_CREDIT

    GROUPS = {1: (0, 1, "q0"), 2: (1, 1, "k1"), 3: (2, 1, "q1"), 4: (3, 1, "v0"), 5: (4, 1, "v1"),
              8: (5, 0, "k0"), 9: (6, 0, "q0"), 10: (7, 0, "k1"), 11: (8, 0, "q1"), 12: (9, 0, "v0"),
              13: (10, 0, "v1"), 16: (11, 1, "k0")}
    FIRST = ((0, "k0"), (0, "q0"), (0, "k1"), (0, "q1"), (0, "v0"), (0, "v1"), (1, "k0"))
    NG, NF = len(GROUPS), len(FIRST)

    with ExitStack() as ctx:
        w = [core.sb(f"w{b}", [P, 3 * KT * HD + 2], F32, ctx) for b in range(2)]
        bias_v = core.sb("bias_v", [P, HEADS], F32, ctx)
        qt = [core.sb(f"qt{b}", [P, TOKENS], F32, ctx) for b in range(2)]
        kt = [core.sb(f"kt{b}", [P, TOKENS], F32, ctx) for b in range(2)]
        v = [core.sb(f"v{b}", [P, TILES, HD], F32, ctx) for b in range(2)]
        probs = core.sb("probs", [P, 2, TOKENS], F32, ctx)
        probs_t = core.sb("probs_t", [P, 2, TILES, P], F32, ctx)
        nmax = core.sb("nmax", [P, 2], F32, ctx)
        rsum = core.sb("rsum", [P, 2], F32, ctx)
        rinv = core.sb("rinv", [P, 2], F32, ctx)
        att = core.sb("att", [P, HEADS, TOKENS], F32, ctx)
        wo = core.sb("wo", [P, HEADS, D], F32, ctx)
        bo = core.sb("bo", [P, D], F32, ctx)
        gated = core.sb("gated", [P, 2, D], F32, ctx)
        w_sem = [core.sem(f"w_loaded{b}", ctx) for b in range(2)]
        bias_loaded = core.sem("bias_loaded", ctx)
        wo_loaded = core.sem("wo_loaded", ctx)
        projected = core.sem("projected", ctx)
        kept = core.sem("kept", ctx)
        scored = core.sem("scored", ctx)
        maxed = core.sem("maxed", ctx)
        exped = core.sem("exped", ctx)
        inverted = core.sem("inverted", ctx)
        normed = core.sem("normed", ctx)
        turned = core.sem("turned", ctx)
        turned_kept = core.sem("turned_kept", ctx)
        valued = core.sem("valued", ctx)
        att_kept = core.sem("att_kept", ctx)
        outed = core.sem("outed", ctx)
        added = core.sem("added", ctx)
        bo_gated = core.sem("bo_gated", ctx)
        block = ctx.enter_context(nc.Block())

        S = [ps[:, 0:2, :].rearrange("p a b -> p (a b)"), ps[:, 2:4, :].rearrange("p a b -> p (a b)")]
        T = [ps[:, 4, :], ps[:, 5, :]]
        V = ps[:, 6, :]
        W = ps[:, 7, :]

        @block.sync
        def _(sp):
            sp.dma_start(w[0][:], A["l0_wqkv"][0]).then_inc(w_sem[0], 16)
            sp.dma_start(bias_v[:], A["l0_bv"]).then_inc(bias_loaded, 16)
            sp.dma_start(w[1][:], A["l0_wqkv"][1]).then_inc(w_sem[1], 16)
            sp.dma_start(wo[:], A["l0_wo"]).then_inc(wo_loaded, 16)
            sp.dma_start(bo[:], A["l0_bo"].to_broadcast([P, D])).then_inc(wo_loaded, 16)
            sp.wait_ge(projected, NF - 1)
            sp.dma_start(w[0][:], A["l0_wqkv"][2]).then_inc(w_sem[0], 16)
            with sp.Fori(0, PAIRS - 2) as p:
                sp.wait_ge(projected, p * NG + NF + GROUPS[5][0] + 1)
                sp.dma_start(w[1][:], A["l0_wqkv"][bass.ds(2 * p + 3, 1)].rearrange("a p n -> (a p) n")).then_inc(w_sem[1], 16)
                sp.wait_ge(projected, p * NG + NF + GROUPS[13][0] + 1)
                sp.dma_start(w[0][:], A["l0_wqkv"][bass.ds(2 * p + 4, 1)].rearrange("a p n -> (a p) n")).then_inc(w_sem[0], 16)
            sp.wait_ge(projected, (PAIRS - 2) * NG + NF + GROUPS[5][0] + 1)
            sp.dma_start(w[1][:], A["l0_wqkv"][HEADS - 1]).then_inc(w_sem[1], 16)

        @block.tensor
        def _(pe):
            def group(b, what, n):
                if not isinstance(n, int) or n > 0:
                    pe.wait_ge(kept, n)
                part, c = "qkv".index(what[0]), int(what[1])
                if part < 2:
                    for k in range(KT):
                        last = pe.matmul(W, w[b][:, (part * KT + k) * HD:(part * KT + k + 1) * HD], ht[:, k, c * BANK:c * BANK + BANK],
                                         start=(k == 0), stop=(k == KT - 1))
                else:
                    for j in range(4):
                        t = (4 * c + j) * P
                        for k in range(KT):
                            last = pe.matmul(W[:, j * P:j * P + P], ht[:, k, t:t + P], w[b][:, (part * KT + k) * HD:(part * KT + k + 1) * HD],
                                             start=(k == 0), stop=(k == KT - 1))
                last.then_inc(projected, 1)

            def scores(p, s):
                b, i = (s // TILES) % 2, s % TILES
                pe.wait_ge(exped, STEPS * p + s - 2 + 1 + CREDIT)
                n = causal_blocks(i) * P
                for c in range(0, n, BANK):
                    e = min(n, c + BANK)
                    pe.matmul(S[s % 2][:, c:e], qt[b][:, i * P:i * P + P], kt[b][:, c:e], start=True, stop=(e < n))
                pe.matmul(S[s % 2][:, n - P:n], core.ident_bf[:], core.causal_bf[:], start=False,
                          stop=True).then_inc(scored, 1)

            def transposes(p, s):
                i = s % TILES
                pe.wait_ge(normed, STEPS * p + s + 1)
                for c in range(chunks[s]):
                    pe.wait_ge(turned_kept, PER_PAIR * p + before[s] + c - 2 + 1 + CREDIT)
                    tb = T[(before[s] + c) % 2]
                    for j in range(4 * c, min(4 * c + 4, causal_blocks(i))):
                        last = pe.transpose(tb[:, (j % 4) * P:(j % 4) * P + P], probs[:, s % 2, j * P:j * P + P],
                                            core.ident[:])
                    last.then_inc(turned, 1)

            def values(p, s):
                b, i = s // TILES, s % TILES
                if i % 4 == 0:
                    pe.wait_ge(att_kept, 4 * p + s // 4 + 1)
                for j in range(causal_blocks(i)):
                    if j % 4 == 0:
                        pe.wait_ge(turned_kept, PER_PAIR * p + before[s] + j // 4 + 1 + CREDIT)
                    last = pe.matmul(V[:, (i % 4) * P:(i % 4) * P + P], v[b][:, j, :], probs_t[:, s % 2, j, :],
                                     start=(j == 0), stop=(j == causal_blocks(i) - 1))
                last.then_inc(valued, 1)

            def pair(p, is_last):
                for s in range(1, STEPS + (not is_last)):
                    if s == TILES:
                        pe.wait_ge(kept, NG * p + NF + GROUPS[3][0] + 1)
                    if s == STEPS:
                        pe.wait_ge(kept, NG * p + NF + GROUPS[11][0] + 1)
                    scores(p, s)
                    transposes(p, s - 1)
                    if s in GROUPS and not (is_last and s >= TILES):
                        j, b, what = GROUPS[s]
                        if s == TILES:
                            pe.wait_ge(w_sem[0], 16 * (p + 2))
                        if s == STEPS:
                            pe.wait_ge(w_sem[1], 16 * (p + 2))
                        group(b, what, NG * p + NF + j)
                    if s - 1 == 0:
                        pe.wait_ge(kept, NG * p + NF - 1)
                    if s - 1 == TILES:
                        pe.wait_ge(kept, NG * p + NF + GROUPS[5][0] + 1)
                    values(p, s - 1)

            pe.sem_inc(valued, CREDIT)
            pe.sem_inc(turned, TURN_CREDIT)
            for n, (b, what) in enumerate(FIRST):
                if n == 0 or b == 1:
                    pe.wait_ge(w_sem[b], 16)
                group(b, what, n)
                if n == 5:
                    pe.wait_ge(kept, 4)
                    scores(0, 0)
            with pe.Fori(0, PAIRS - 1) as p:
                pair(p, False)
            pair(PAIRS - 1, True)
            transposes(PAIRS - 1, STEPS - 1)
            values(PAIRS - 1, STEPS - 1)
            pe.wait_ge(wo_loaded, 32)
            pe.wait_ge(att_kept, 4 * PAIRS + 1)
            for i in range(TILES):
                if i >= 2:
                    pe.wait_ge(added, i - 1)
                for h in range(HEADS):
                    last = pe.matmul(S[i % 2][:, 0:D], att[:, h, i * P:i * P + P], wo[:, h, :],
                                     start=(h == 0), stop=(h == HEADS - 1))
                last.then_inc(outed, 1)

        @block.scalar
        def _(act):
            act.sem_inc(exped, CREDIT)

            def keep(b, what, n):
                act.wait_ge(projected, n + 1)
                c = int(what[1])
                if what[0] == "v":
                    act.activation(v[b][:, 4 * c:4 * c + 4, :], W.rearrange("p (t d) -> p t d", t=4),
                                   ACT.Copy).then_inc(kept, 1)
                else:
                    act.activation(kt[b][:, c * BANK:c * BANK + BANK], W, ACT.Identity,
                                   bias=w[b][:, BIAS_K:BIAS_K + 1]).then_inc(kept, 1)

            def exps(p, s):
                n = causal_blocks(s % TILES) * P
                act.wait_ge(maxed, STEPS * p + s + 1)
                act.wait_ge(turned, turned_by(p, s - 2))
                act.activation(probs[:, s % 2, 0:n], S[s % 2][:, 0:n], ACT.Exp, bias=nmax[:, s % 2:s % 2 + 1],
                               accum_out=rsum[:, s % 2:s % 2 + 1]).then_inc(exped, 1)

            def pair(p, is_last):
                for s in range(1, STEPS + (not is_last)):
                    if s < STEPS:
                        exps(p, s)
                    else:
                        exps(p + 1, 0)
                    if s in GROUPS and not (is_last and s >= TILES):
                        j, b, what = GROUPS[s]
                        if what[0] != "q":
                            keep(b, what, NG * p + NF + j)

            for n, (b, what) in enumerate(FIRST):
                if what[0] != "q":
                    keep(b, what, n)
                if n == 5:
                    exps(0, 0)
            with act.Fori(0, PAIRS - 1) as p:
                pair(p, False)
            pair(PAIRS - 1, True)

        @block.vector
        def _(dve):
            dve.sem_inc(turned_kept, CREDIT)
            dve.sem_inc(att_kept, 1)

            def keep_q(b, what, n):
                dve.wait_ge(projected, n + 1)
                c = int(what[1])
                dve.tensor_scalar(qt[b][:, c * BANK:c * BANK + BANK], W, w[b][:, BIAS_Q:BIAS_Q + 1], SCALE,
                                  ALU.add, ALU.mult).then_inc(kept, 1)

            def keep_att(p, s):
                dve.wait_ge(valued, STEPS * p + s + 1 + CREDIT)
                h, c = 2 * p + s // TILES, (s % TILES) // 4
                dve.tensor_scalar(att[:, bass.ds(h, 1), c * BANK:c * BANK + BANK].rearrange("p a t -> p (a t)"), V,
                                  bias_v[:, bass.ds(h, 1)], None, ALU.add).then_inc(att_kept, 1)

            def maxes(p, s):
                n = causal_blocks(s % TILES) * P
                dve.wait_ge(scored, STEPS * p + s + 1)
                dve.tensor_reduce(nmax[:, s % 2:s % 2 + 1], S[s % 2][:, 0:n], AX_X, ALU.max,
                                  negate=True).then_inc(maxed, 1)

            def norm(p, s):
                n = causal_blocks(s % TILES) * P
                dve.wait_ge(exped, STEPS * p + s + 1 + CREDIT)
                dve.reciprocal(rinv[:, s % 2:s % 2 + 1], rsum[:, s % 2:s % 2 + 1]).then_inc(inverted, 1)
                dve.wait_ge(inverted, STEPS * p + s + 1)
                dve.tensor_scalar(probs[:, s % 2, 0:n], probs[:, s % 2, 0:n], rinv[:, s % 2:s % 2 + 1], None,
                                  ALU.mult).then_inc(normed, 1)

            def keep_turned(p, s):
                i = s % TILES
                for c in range(chunks[s]):
                    m = min(4, causal_blocks(i) - 4 * c)
                    dve.wait_ge(turned, PER_PAIR * p + before[s] + c + 1 + TURN_CREDIT)
                    if c == 0:
                        dve.wait_ge(valued, STEPS * p + s - 2 + 1 + CREDIT)
                    dve.tensor_copy(probs_t[:, s % 2, 4 * c:4 * c + m, :],
                                    T[(before[s] + c) % 2][:, 0:m * P].rearrange("p (t d) -> p t d", t=m)
                                    ).then_inc(turned_kept, 1)

            def pair(p, is_last):
                for s in range(1, STEPS + (not is_last)):
                    q = p + 1 if s == STEPS else p
                    maxes(q, s % STEPS)
                    keep_turned(p, s - 1)
                    norm(q, s % STEPS)
                    if s in GROUPS and GROUPS[s][2][0] == "q" and not (is_last and s >= TILES):
                        keep_q(GROUPS[s][1], GROUPS[s][2], NG * p + NF + GROUPS[s][0])
                    if (s - 1) % 4 == 3:
                        keep_att(p, s - 1)

            dve.wait_ge(bias_loaded, 16)
            for n, (b, what) in enumerate(FIRST):
                if what[0] == "q":
                    keep_q(b, what, n)
            maxes(0, 0)
            norm(0, 0)
            with dve.Fori(0, PAIRS - 1) as p:
                pair(p, False)
            pair(PAIRS - 1, True)
            keep_turned(PAIRS - 1, STEPS - 1)
            keep_att(PAIRS - 1, STEPS - 1)
            add_gated(dve, core, 0, bo, wo_loaded, 32, gated, bo_gated, [S[i % 2][:, 0:D] for i in range(TILES)],
                      outed, added)


def add_gated(dve, core, which, b, b_loaded, loaded, gated, gated_done, outs, outed, added):
    x, gate = core.x, core.gate
    dve.wait_ge(b_loaded, loaded)
    dve.tensor_tensor(gated[:, 0, :], gate[:, which, :], b[:], ALU.mult).then_inc(gated_done, 1)
    dve.wait_ge(gated_done, 1)
    dve.tensor_tensor(x[:], x[:], gated[:, 0:1, :].to_broadcast([P, TILES, D]), ALU.add).then_inc(gated_done, 1)
    dve.wait_ge(gated_done, 2)
    for i in range(TILES):
        dve.wait_ge(outed, i + 1)
        dve.tensor_tensor(gated[:, i % 2, :], outs[i], gate[:, which, :], ALU.mult).then_inc(added, 1)
        dve.wait_ge(added, i + 1)
        dve.tensor_tensor(x[:, i, :], x[:, i, :], gated[:, i % 2, :], ALU.add).then_inc(gated_done, 1)


EXPERTS, TOP, GROUPS_OF, TOP_GROUPS, GROUP = 32, 4, 4, 2, 8
FFN = 128
CAP = 2 * (256 * TOP // EXPERTS)
SLOTS = EXPERTS * CAP
ROUTE_SCALE = 2.0
DROPPED = 65536.0
PAD = -3.0e38


def moe(core, A):
    nc = core.nc
    x, xn, ht, ps = core.x, core.xn, core.ht, core.ps
    with ExitStack() as moe_ctx:
        slots_in = nc.dram_tensor("slots_in", (SLOTS, D), F32, kind="Internal").ap()
        slots_out = nc.dram_tensor("slots_out", (SLOTS, D), F32, kind="Internal").ap()
        idx = core.sb("idx", [P, TILES * TOP], U32, moe_ctx)
        wk = core.sb("wk", [P, TILES * TOP], F32, moe_ctx)
        shared = core.sb("shared", [P, TILES, D], F32, moe_ctx)
        picked = core.sb("picked", [P, TILES * TOP, D], F32, moe_ctx)
        route(core, A, moe_ctx, slots_in, idx, wk, shared, picked)
        experts(core, A, slots_in, slots_out)
        combine(core, slots_out, idx, wk, shared, picked)


def route(core, A, outer, slots_in, idx, wk, shared, picked):
    nc = core.nc
    x, xn, ht, ps = core.x, core.xn, core.ht, core.ps
    with ExitStack() as ctx:
        def buf(name, shape, dt=F32):
            return core.sb(name, shape, dt, ctx)

        gw = buf("gw", [P, KT, EXPERTS])
        gbias = buf("gbias", [P, EXPERTS])
        scores = buf("scores", [P, TILES, EXPERTS])
        sc = buf("scb_", [P, TILES, EXPERTS])
        gtop = buf("gtop", [P, TILES * GROUPS_OF, 8])
        gsum = buf("gsum", [P, TILES, 8])
        gmax = buf("gmax", [P, TILES, 8])
        gidx = buf("gidx", [P, TILES, 8], U32)
        gidf = buf("gidf", [P, TILES, TOP_GROUPS])
        gm = buf("gm", [P, TOP_GROUPS, TILES, GROUPS_OF])
        emax = buf("emax", [P, TILES, 8])
        eidx = buf("eidx", [P, TILES, 8], U32)
        eidf = buf("eidf", [P, TILES, TOP])
        hot = buf("hot", [P, TILES, TOP, EXPERTS])
        prod = buf("prod", [P, TILES, TOP, EXPERTS])
        chosen = buf("chosen", [P, TILES, EXPERTS], BF16)
        chosen_f = buf("chosen_f", [P, TILES, EXPERTS])
        s4 = buf("s4", [P, TILES, TOP])
        den = buf("den", [P, TILES])
        pos4 = buf("pos4", [P, TILES, TOP])
        late = buf("late", [P, TILES, TOP])
        early = buf("early", [P, TILES, TOP])
        slot = buf("slot", [P, TILES, TOP])
        iota_e = buf("iota_e", [P, EXPERTS])
        earlier = buf("earlier", [P, P], BF16)
        ones_bf = buf("ones_bf", [P, P], BF16)
        zero = buf("zero", [P, SLOTS * D // P // 4])
        sw = buf("sw", [P, 2, KT, D])
        sd = buf("sd", [P, KT, D])
        act_s = buf("act_s", [P, 2, BANK])
        hid = buf("hid", [P, KT, TOKENS])
        gate_loaded = core.sem("gate_loaded", ctx)
        shared_loaded = core.sem("shared_loaded", ctx)
        const_done = core.sem("const_done", ctx)
        zeroed = core.sem("zeroed", ctx)
        gated = core.sem("r_gated", ctx)
        sigmoid_done = core.sem("sigmoid_done", ctx)
        step = core.sem("route_step", ctx)
        chosen_done = core.sem("chosen_done", ctx)
        placed = core.sem("placed", ctx)
        idx_done = core.sem("idx_done", ctx)
        scattered = core.sem("scattered", ctx)
        upped = core.sem("upped", ctx)
        silued = core.sem("silued", ctx)
        hid_done = core.sem("hid_done", ctx)
        downed = core.sem("downed", ctx)
        shared_done = core.sem("shared_done", ctx)
        logits = ps[:, 0, 0:TILES * EXPERTS]
        where = ps[:, 1, 0:TILES * EXPERTS].rearrange("p (t e) -> p t e", t=TILES)
        block = ctx.enter_context(nc.Block())

        @block.sync
        def _(sp):
            sp.dma_start(gw[:], A["l0_gw"]).then_inc(gate_loaded, 16)
            sp.dma_start(gbias[:], A["l0_gbias"].to_broadcast([P, EXPERTS])).then_inc(gate_loaded, 16)
            sp.dma_start(sw[:], A["l0_shared_in"]).then_inc(shared_loaded, 16)
            sp.dma_start(sd[:], A["l0_shared_down"]).then_inc(shared_loaded, 16)
            sp.wait_ge(const_done, 6)
            for q in range(4):
                sp.dma_start(slots_in.rearrange("(q p r) d -> q p (r d)", q=4, p=P)[q], zero[:]).then_inc(zeroed, 16)
            sp.wait_ge(zeroed, 64)

        @block.gpsimd
        def _(pool):
            pool.memset(zero[:], 0.0).then_inc(const_done, 1)
            pool.memset(earlier[:], 1.0).then_inc(const_done, 1)
            pool.memset(ones_bf[:], 1.0).then_inc(const_done, 1)
            pool.iota(iota_e[:], pattern=[[1, EXPERTS]], base=0, channel_multiplier=0,
                      allow_small_or_imprecise_dtypes=True).then_inc(const_done, 1)
            pool.memset(gsum[:], PAD).then_inc(const_done, 1)
            pool.wait_ge(const_done, 5)
            pool.affine_select(out=earlier[:], in_=earlier[:], compare_op=ALU.is_gt, fill=0.0, base=0,
                               pattern=[[1, P]], channel_multiplier=-1).then_inc(const_done, 1)
            pool.memset(picked[:], 0.0)
            pool.wait_ge(zeroed, 64)
            pool.wait_ge(idx_done, 1)
            for i in range(TILES):
                for k in range(TOP):
                    j = i * TOP + k
                    pool.indirect_dma_start(out=slots_in, out_offset=bass.IndirectOffsetOnAxis(ap=idx[:, j:j + 1], axis=0),
                                            in_=xn[:, i, :], in_offset=None, bounds_check=SLOTS - 1,
                                            oob_is_err=False).then_inc(scattered, 16)
            pool.wait_ge(scattered, 16 * TILES * TOP)

        @block.tensor
        def _(pe):
            pe.wait_ge(gate_loaded, 32)
            for i in range(TILES):
                for k in range(KT):
                    last = pe.matmul(logits[:, i * EXPERTS:(i + 1) * EXPERTS], ht[:, k, i * P:i * P + P], gw[:, k, :],
                                     start=(k == 0), stop=(k == KT - 1))
            last.then_inc(gated, 1)
            pe.wait_ge(shared_loaded, 32)
            def gate_up(n):
                f, c = n % KT, n // KT
                if n >= 2:
                    pe.wait_ge(hid_done, n - 1)
                for part in range(2):
                    for k in range(KT):
                        last = pe.matmul(ps[:, 2 + 2 * (n % 2) + part, :], sw[:, part, k, f * P:f * P + P],
                                         ht[:, k, c * BANK:c * BANK + BANK], start=(k == 0), stop=(k == KT - 1))
                last.then_inc(upped, 1)
            for n in range(2):
                gate_up(n)
            pe.wait_ge(chosen_done, 1)
            pe.wait_ge(const_done, 6)
            for i in range(TILES):
                for j in range(i + 1):
                    last = pe.matmul(where[:, i, :], (earlier if j == i else ones_bf)[:], chosen[:, j, :],
                                     start=(j == 0), stop=(j == i))
            last.then_inc(placed, 1)
            for n in range(2, KT * CHUNKS):
                gate_up(n)
            pe.wait_ge(hid_done, KT * CHUNKS)
            for i in range(TILES):
                if i >= 2:
                    pe.wait_ge(shared_done, i - 1)
                for f in range(KT):
                    last = pe.matmul(ps[:, 6 + i % 2, 0:D], hid[:, f, i * P:i * P + P], sd[:, f, :],
                                     start=(f == 0), stop=(f == KT - 1))
                last.then_inc(downed, 1)

        @block.scalar
        def _(act):
            act.wait_ge(gated, 1)
            act.activation(scores[:].rearrange("p t e -> p (t e)"), logits, ACT.Sigmoid).then_inc(sigmoid_done, 1)
            for n in range(KT * CHUNKS):
                act.wait_ge(upped, n + 1)
                if n >= 2:
                    act.wait_ge(hid_done, n - 1)
                act.activation(act_s[:, n % 2, :], ps[:, 2 + 2 * (n % 2), :], ACT.Silu).then_inc(silued, 1)
            for i in range(TILES):
                act.wait_ge(downed, i + 1)
                act.activation(shared[:, i, :], ps[:, 6 + i % 2, 0:D], ACT.Copy).then_inc(shared_done, 1)

        @block.vector
        def _(dve):
            done = [0]

            def after(ins):
                ins.then_inc(step, 1)
                done[0] += 1
                dve.wait_ge(step, done[0])

            def hidden(n):
                f, c = n % KT, n // KT
                dve.wait_ge(silued, n + 1)
                dve.tensor_tensor(hid[:, f, c * BANK:c * BANK + BANK], act_s[:, n % 2, :], ps[:, 3 + 2 * (n % 2), :],
                                  ALU.mult).then_inc(hid_done, 1)

            dve.wait_ge(gate_loaded, 32)
            dve.wait_ge(sigmoid_done, 1)
            after(dve.tensor_tensor(sc[:], scores[:], gbias[:].rearrange("p (a e) -> p a e", a=1).to_broadcast([P, TILES, EXPERTS]), ALU.add))
            sc_g = sc[:].rearrange("p t (g e) -> p (t g) e", g=GROUPS_OF)
            for j in range(TILES * GROUPS_OF):
                last = dve.max(gtop[:, j, :], sc_g[:, j, :])
            after(last)
            dve.wait_ge(const_done, 6)
            gt = gtop[:].rearrange("p (t g) m -> p t g m", g=GROUPS_OF)
            after(dve.tensor_tensor(gsum[:, :, 0:GROUPS_OF], gt[:, :, :, 0], gt[:, :, :, 1], ALU.add))
            for i in range(TILES):
                last = dve.max(gmax[:, i, :], gsum[:, i, :])
            after(last)
            for i in range(TILES):
                last = dve.max_index(gidx[:, i, :], gmax[:, i, :], gsum[:, i, :])
            after(last)
            after(dve.tensor_copy(gidf[:], gidx[:, :, 0:TOP_GROUPS]))
            for m in range(TOP_GROUPS):
                last = dve.tensor_tensor(gm[:, m, :, :], gidf[:, :, m:m + 1].to_broadcast([P, TILES, GROUPS_OF]),
                                         iota_e[:, 0:GROUPS_OF].rearrange("p (a g) -> p a g", a=1).to_broadcast([P, TILES, GROUPS_OF]),
                                         ALU.is_equal)
            after(last)
            after(dve.tensor_tensor(gm[:, 0, :, :], gm[:, 0, :, :], gm[:, 1, :, :], ALU.add))
            g3 = gm[:, 0, :, :].rearrange("p t g -> p (t g)").rearrange("p (n a) -> p n a", a=1)
            after(dve.tensor_tensor(sc_g, sc_g, g3.to_broadcast([P, TILES * GROUPS_OF, GROUP]), ALU.mult))
            for i in range(TILES):
                last = dve.max(emax[:, i, :], sc[:, i, :])
            after(last)
            for i in range(TILES):
                last = dve.max_index(eidx[:, i, :], emax[:, i, :], sc[:, i, :])
            after(last)
            after(dve.tensor_copy(eidf[:], eidx[:, :, 0:TOP]))
            hot3 = hot[:].rearrange("p t k e -> p (t k) e")
            prod3 = prod[:].rearrange("p t k e -> p (t k) e")
            after(dve.tensor_tensor(hot3, eidf[:].rearrange("p t k -> p (t k)").rearrange("p (n a) -> p n a", a=1).to_broadcast([P, TILES * TOP, EXPERTS]),
                                    iota_e[:].rearrange("p (a e) -> p a e", a=1).to_broadcast([P, TILES * TOP, EXPERTS]), ALU.is_equal))
            after(dve.tensor_reduce(chosen_f[:], hot[:].rearrange("p t k e -> p t e k"), AX_X, ALU.add))
            dve.tensor_copy(chosen[:], chosen_f[:]).then_inc(chosen_done, 1)
            for i in range(TILES):
                last = dve.tensor_tensor(prod[:, i, :, :], hot[:, i, :, :], scores[:, i:i + 1, :].to_broadcast([P, TOP, EXPERTS]), ALU.mult)
            after(last)
            after(dve.tensor_reduce(s4[:].rearrange("p t k -> p (t k)"), prod3, AX_X, ALU.add))
            after(dve.tensor_reduce(den[:], s4[:], AX_X, ALU.add))
            after(dve.tensor_scalar(den[:], den[:], 1e-20, None, ALU.add))
            after(dve.reciprocal(den[:], den[:]))
            after(dve.tensor_scalar(den[:], den[:], ROUTE_SCALE, None, ALU.mult))
            after(dve.tensor_tensor(s4[:], s4[:], den[:].rearrange("p (t a) -> p t a", a=1).to_broadcast([P, TILES, TOP]), ALU.mult))
            for n in range(2):
                hidden(n)
            dve.wait_ge(placed, 1)
            for i in range(TILES):
                last = dve.tensor_tensor(prod[:, i, :, :], hot[:, i, :, :], where[:, i:i + 1, :].to_broadcast([P, TOP, EXPERTS]), ALU.mult)
            after(last)
            after(dve.tensor_reduce(pos4[:].rearrange("p t k -> p (t k)"), prod3, AX_X, ALU.add))
            after(dve.scalar_tensor_tensor(out=slot[:], in0=eidf[:], scalar=float(CAP), in1=pos4[:], op0=ALU.mult, op1=ALU.add))
            after(dve.tensor_scalar(late[:], pos4[:], float(CAP), DROPPED, ALU.is_ge, ALU.mult))
            dve.tensor_tensor(idx[:], slot[:].rearrange("p t k -> p (t k)"), late[:].rearrange("p t k -> p (t k)"), ALU.add).then_inc(idx_done, 1)
            after(dve.tensor_scalar(early[:], pos4[:], float(CAP), None, ALU.is_lt))
            dve.tensor_tensor(wk[:], s4[:].rearrange("p t k -> p (t k)"), early[:].rearrange("p t k -> p (t k)"), ALU.mult)
            for n in range(2, KT * CHUNKS):
                hidden(n)


def experts(core, A, slots_in, slots_out):
    nc = core.nc
    ps = core.ps
    RING = 4
    PAIRS = EXPERTS // 2
    ROUNDS = PAIRS // RING
    with ExitStack() as ctx:
        rows = [core.sb(f"rows{r}", [P, D], F32, ctx) for r in range(RING)]
        w13 = [core.sb(f"w13_{r}", [P, 2, 2, KT, FFN], F32, ctx) for r in range(RING)]
        w2 = [core.sb(f"w2_{r}", [P, 2, D], F32, ctx) for r in range(RING)]
        bt = [core.sb(f"bt{r}", [P, KT, P], F32, ctx) for r in range(2)]
        sil = [core.sb(f"sil{r}", [P, P], F32, ctx) for r in range(2)]
        hid = [core.sb(f"ehid{r}", [P, P], F32, ctx) for r in range(2)]
        res = [core.sb(f"res{r}", [P, D], F32, ctx) for r in range(RING)]
        loaded = [core.sem(f"e_loaded{r}", ctx) for r in range(RING)]
        rows_loaded = [core.sem(f"rows_loaded{r}", ctx) for r in range(RING)]
        turned = core.sem("e_turned", ctx)
        bt_kept = core.sem("bt_kept", ctx)
        upped = core.sem("e_upped", ctx)
        silued = core.sem("e_silued", ctx)
        hid_done = core.sem("e_hid", ctx)
        downed = core.sem("e_downed", ctx)
        res_kept = core.sem("res_kept", ctx)
        stored = [core.sem(f"e_stored{r}", ctx) for r in range(RING)]
        in_rows = slots_in.rearrange("(q p) d -> q p d", p=P)
        out_rows = slots_out.rearrange("(q p) d -> q p d", p=P)
        T = [ps[:, b, 0:D].rearrange("p (k t) -> p k t", k=KT) for b in range(2)]
        U = [ps[:, 2 + b, 0:2 * P].rearrange("p (w t) -> p w t", w=2) for b in range(2)]
        O = [ps[:, 4 + b, 0:D] for b in range(2)]
        CREDIT = 2
        block = ctx.enter_context(nc.Block())

        @block.sync
        def _(sp):
            def load(q, r):
                sp.dma_start(w13[r][:].rearrange("p e w k f -> p (e w k f)"), A["l0_w13"][q]).then_inc(loaded[r], 16)
                sp.dma_start(w2[r][:].rearrange("p e d -> p (e d)"), A["l0_w2"][q]).then_inc(loaded[r], 16)
                sp.dma_start(rows[r][:], in_rows[q]).then_inc(rows_loaded[r], 16)

            for r in range(RING):
                load(r, r)
            with sp.Fori(0, ROUNDS - 1) as g:
                for r in range(RING):
                    q = bass.ds(g * RING + RING + r, 1)
                    sp.wait_ge(downed, RING * g + r + 1 + CREDIT)
                    sp.dma_start(w13[r][:].rearrange("p e w k f -> p (e w k f)"),
                                 A["l0_w13"][q].rearrange("a p n -> (a p) n")).then_inc(loaded[r], 16)
                    sp.dma_start(w2[r][:].rearrange("p e d -> p (e d)"),
                                 A["l0_w2"][q].rearrange("a p n -> (a p) n")).then_inc(loaded[r], 16)
                    sp.dma_start(rows[r][:], in_rows[q].rearrange("a p n -> (a p) n")).then_inc(rows_loaded[r], 16)

        @block.tensor
        def _(pe):
            pe.sem_inc(downed, CREDIT)
            pe.sem_inc(upped, CREDIT)

            def turn(g, r):
                q = RING * g + r
                pe.wait_ge(rows_loaded[r], 16 * (g + 1))
                pe.wait_ge(bt_kept, q - 2 + 1 + CREDIT)
                for k in range(KT):
                    last = pe.transpose(T[r % 2][:, k, :], rows[r][:, k * P:k * P + P], core.ident[:])
                last.then_inc(turned, 1)

            def up(g, r):
                q = RING * g + r
                pe.wait_ge(loaded[r], 32 * (g + 1))
                pe.wait_ge(bt_kept, q + 1 + CREDIT)
                pe.wait_ge(hid_done, q - 2 + 1 + CREDIT)
                for w in range(2):
                    for e in range(2):
                        for k in range(KT):
                            last = pe.matmul(U[r % 2][:, w, e * CAP:(e + 1) * CAP], w13[r][:, e, w, k, :],
                                             bt[r % 2][:, k, e * CAP:(e + 1) * CAP], start=(k == 0), stop=(k == KT - 1))
                last.then_inc(upped, 1)

            def down(g, r):
                q = RING * g + r
                pe.wait_ge(hid_done, q + 1 + CREDIT)
                pe.wait_ge(res_kept, q - 2 + 1 + CREDIT)
                for e in range(2):
                    last = pe.matmul(O[r % 2][e * CAP:(e + 1) * CAP, :], hid[r % 2][:, e * CAP:(e + 1) * CAP],
                                     w2[r][:, e, :], start=True, stop=True)
                last.then_inc(downed, 1)

            def round_(g, is_last):
                for r in range(RING):
                    if r + 1 < RING:
                        turn(g, r + 1)
                    elif not is_last:
                        turn(g + 1, 0)
                    up(g, r)
                    if r > 0:
                        down(g, r - 1)
                down(g, RING - 1)

            turn(0, 0)
            with pe.Fori(0, ROUNDS - 1) as g:
                round_(g, False)
            round_(ROUNDS - 1, True)

        @block.scalar
        def _(act):
            act.sem_inc(bt_kept, CREDIT)

            def keep_turned(g, r):
                q = RING * g + r
                act.wait_ge(turned, q + 1)
                act.wait_ge(upped, q - 2 + 1 + CREDIT)
                for k in range(KT):
                    last = act.activation(bt[r % 2][:, k, :], T[r % 2][:, k, :], ACT.Identity,
                                          scale=core.modc[:, 2, k:k + 1], bias=core.modc[:, 3, k:k + 1])
                last.then_inc(bt_kept, 1)

            def silu(g, r):
                q = RING * g + r
                act.wait_ge(upped, q + 1 + CREDIT)
                act.wait_ge(hid_done, q - 2 + 1 + CREDIT)
                act.activation(sil[r % 2][:], U[r % 2][:, 0, :], ACT.Silu).then_inc(silued, 1)

            def round_(g, is_last):
                for r in range(RING):
                    if r + 1 < RING:
                        keep_turned(g, r + 1)
                    elif not is_last:
                        keep_turned(g + 1, 0)
                    silu(g, r)

            keep_turned(0, 0)
            with act.Fori(0, ROUNDS - 1) as g:
                round_(g, False)
            round_(ROUNDS - 1, True)

        @block.vector
        def _(dve):
            dve.sem_inc(hid_done, CREDIT)
            dve.sem_inc(res_kept, CREDIT)

            def hidden(g, r):
                q = RING * g + r
                dve.wait_ge(silued, q + 1)
                dve.wait_ge(downed, q - 2 + 1 + CREDIT)
                dve.tensor_tensor(hid[r % 2][:], sil[r % 2][:], U[r % 2][:, 1, :], ALU.mult).then_inc(hid_done, 1)

            def keep(g, r, first):
                q = RING * g + r
                dve.wait_ge(downed, q + 1 + CREDIT)
                if not first:
                    dve.wait_ge(stored[r], 16 * g)
                dve.tensor_copy(res[r][:], O[r % 2]).then_inc(res_kept, 1)

            def round_(g, first):
                for r in range(RING):
                    hidden(g, r)
                    if r > 0:
                        keep(g, r - 1, first)
                keep(g, RING - 1, first)

            round_(0, True)
            with dve.Fori(1, ROUNDS) as g:
                round_(g, False)

        @block.gpsimd
        def _(pool):
            with pool.Fori(0, ROUNDS) as g:
                for r in range(RING):
                    q = g * RING + r
                    pool.wait_ge(res_kept, q + 1 + CREDIT)
                    pool.dma_start(out_rows[bass.ds(q, 1)].rearrange("a p n -> (a p) n"), res[r][:]).then_inc(stored[r], 16)
            for r in range(RING):
                pool.wait_ge(stored[r], 16 * ROUNDS)


def combine(core, slots_out, idx, wk, shared, picked):
    nc = core.nc
    with ExitStack() as ctx:
        gathered = [core.sem(f"gathered{i}", ctx) for i in range(TILES // 2)]
        step = core.sem("c_step", ctx)
        block = ctx.enter_context(nc.Block())

        @block.gpsimd
        def _(pool):
            for i in range(TILES):
                for k in range(TOP):
                    j = i * TOP + k
                    pool.indirect_dma_start(out=picked[:, j, :], out_offset=None, in_=slots_out,
                                            in_offset=bass.IndirectOffsetOnAxis(ap=idx[:, j:j + 1], axis=0),
                                            bounds_check=SLOTS - 1, oob_is_err=False).then_inc(gathered[i // 2], 16)

        @block.vector
        def _(dve):
            n = 0
            for i in range(TILES):
                if i % 2 == 0:
                    dve.wait_ge(gathered[i // 2], 2 * 16 * TOP)
                for k in range(TOP):
                    j = i * TOP + k
                    dve.scalar_tensor_tensor(out=shared[:, i, :], in0=picked[:, j, :], scalar=wk[:, j:j + 1],
                                             in1=shared[:, i, :], op0=ALU.mult, op1=ALU.add).then_inc(step, 1)
                    n += 1
                    dve.wait_ge(step, n)
                dve.tensor_tensor(shared[:, i, :], shared[:, i, :], core.gate[:, 1, :], ALU.mult).then_inc(step, 1)
                n += 1
                dve.wait_ge(step, n)
                dve.tensor_tensor(core.x[:, i, :], core.x[:, i, :], shared[:, i, :], ALU.add)


def attention_l1(core, A):
    nc = core.nc
    GROUPS, HD, MAPS = 4, 128, 2
    VD = 2 * HD
    STEPS = 2 * TILES
    SCALE = float(HD) ** -0.5
    LAMBDA_INIT = 0.8 - 0.6 * float(np.exp(-0.3 * 1))
    RMS_EPS = 1e-5
    x, ht, ps = core.x, core.ht, core.ps
    chunks = [(causal_blocks(s % TILES) + 3) // 4 for s in range(STEPS)]
    PLAN = {1: [(None, "v", 1, 0)], 2: [(None, "k", 1, 0)], 3: [(None, "k", 1, 1)], 4: [(None, "v", 2, 0)],
            5: [(None, "v", 3, 0)], 6: [(1, "q", 0, 0), (1, "q", 0, 1)], 7: [(1, "q", 1, 0)], 8: [(1, "q", 1, 1)],
            9: [(0, "q", 0, 0)], 10: [(0, "q", 0, 1)], 11: [(0, "q", 1, 0)], 12: [(0, "q", 1, 1)],
            16: [(None, "k", 0, 0), (None, "k", 0, 1), (None, "v", 0, 0)]}
    FIRST = [(None, "k", 0, 0), (0, "q", 0, 0), (None, "k", 0, 1), (0, "q", 0, 1), (0, "q", 1, 0), (0, "q", 1, 1),
             (None, "v", 0, 0)]
    NF = len(FIRST)
    number, NG = {}, 0
    for s in sorted(PLAN):
        for what in PLAN[s]:
            number[s, what] = NG
            NG += 1
    turn_index, NT = {}, 0
    for s in range(1, STEPS + 1):
        for c in range(chunks[s - 1]):
            turn_index["p", s - 1, c] = NT
            NT += 1
        if s >= 2:
            turn_index["o", s - 2, 0] = NT
            NT += 1
    turn_index["o", STEPS - 1, 0] = NT
    NT += 1
    assert NT % 2 == 0

    with ExitStack() as ctx:
        wq = [core.sb(f"wq{b}", [P, MAPS * KT * HD + MAPS], F32, ctx) for b in range(2)]
        KV_BIAS = (MAPS * KT * HD) + KT * VD
        wkv = core.sb("wkv", [P, KV_BIAS + MAPS + VD], F32, ctx)
        q = [[core.sb(f"q{b}{m}", [P, TOKENS], F32, ctx) for m in range(MAPS)] for b in range(2)]
        k = [core.sb(f"k{m}", [P, TOKENS], F32, ctx) for m in range(MAPS)]
        v = core.sb("v", [P, TILES, VD], F32, ctx)
        ex = core.sb("ex", [P, 2, MAPS, TOKENS], F32, ctx)
        mixed = core.sb("mixed", [P, 2, TOKENS], F32, ctx)
        mixed_t = core.sb("mixed_t", [P, 2, TILES, P], F32, ctx)
        nmax = core.sb("nmax", [P, 2, MAPS], F32, ctx)
        rsum = core.sb("rsum", [P, 2, MAPS], F32, ctx)
        rinv = core.sb("rinv", [P, 2, MAPS], F32, ctx)
        rneg = core.sb("rneg", [P, 2], F32, ctx)
        o = core.sb("o", [P, 2, VD], F32, ctx)
        osq = core.sb("osq", [P, 2, VD], F32, ctx)
        ssq = core.sb("ssq", [P, 2], F32, ctx)
        mean_sq = core.sb("mean_sq", [P, 2], F32, ctx)
        rms = core.sb("rms", [P, 2], F32, ctx)
        on = core.sb("on", [P, 2, VD], F32, ctx)
        att = core.sb("att", [P, 2 * GROUPS * KT, TOKENS], F32, ctx)
        wo = core.sb("wo", [P, 2 * GROUPS * KT, D], F32, ctx)
        bo = core.sb("bo", [P, D], F32, ctx)
        lam_rows = core.sb("lam_rows", [P, 4, HD], F32, ctx)
        lam = core.sb("lam", [P, 8], F32, ctx)
        subln = core.sb("subln", [P, KT], F32, ctx)
        gated = core.sb("gated", [P, 2, D], F32, ctx)
        q_loaded = [core.sem(f"q_loaded{b}", ctx) for b in range(2)]
        kv_loaded = core.sem("kv_loaded", ctx)
        lam_loaded = core.sem("lam_loaded", ctx)
        wo_loaded = core.sem("wo_loaded", ctx)
        lam_step = core.sem("lam_step", ctx)
        lam_exp = core.sem("lam_exp", ctx)
        wo_scaled = core.sem("wo_scaled", ctx)
        projected = core.sem("projected", ctx)
        kept = core.sem("kept", ctx)
        scored = core.sem("scored", ctx)
        maxed = core.sem("maxed", ctx)
        exped = core.sem("exped", ctx)
        mixed_done = core.sem("mixed_done", ctx)
        mix_step = core.sem("mix_step", ctx)
        turned = core.sem("turned", ctx)
        turned_kept = core.sem("turned_kept", ctx)
        valued = core.sem("valued", ctx)
        o_kept = core.sem("o_kept", ctx)
        squared = core.sem("squared", ctx)
        meaned = core.sem("meaned", ctx)
        rms_done = core.sem("rms_done", ctx)
        on_done = core.sem("on_done", ctx)
        outed = core.sem("outed", ctx)
        added = core.sem("added", ctx)
        bo_gated = core.sem("bo_gated", ctx)
        CREDIT = 2
        TURN_CREDIT = 6
        S = [ps[:, 0:2, :].rearrange("p a b -> p (a b)"), ps[:, 2:4, :].rearrange("p a b -> p (a b)")]
        T = [ps[:, 4, :], ps[:, 5, :]]
        O = ps[:, 6, 0:VD]
        W = ps[:, 7, :]
        MICRO = STEPS * MAPS
        block = ctx.enter_context(nc.Block())

        def order(g, s, what):
            return NG * g + NF + number[s, what]

        def turn_no(g, kind, t, c):
            return NT * g + turn_index[kind, t, c]

        @block.sync
        def _(sp):
            def load(dst, name, g, sem):
                if isinstance(g, int):
                    sp.dma_start(dst[:], A[name][g]).then_inc(sem, 16)
                else:
                    sp.dma_start(dst[:], A[name][bass.ds(g, 1)].rearrange("a p n -> (a p) n")).then_inc(sem, 16)

            load(wkv, "l1_wkv", 0, kv_loaded)
            load(wq[0], "l1_wq", 0, q_loaded[0])
            load(wq[1], "l1_wq", 1, q_loaded[1])
            sp.dma_start(lam_rows[:].rearrange("p a d -> p (a d)"), A["l1_lambda"].to_broadcast([P, 4 * HD])).then_inc(lam_loaded, 16)
            sp.dma_start(subln[:], A["l1_subln"]).then_inc(lam_loaded, 16)
            sp.dma_start(wo[:], A["l1_wo"]).then_inc(wo_loaded, 16)
            sp.dma_start(bo[:], A["l1_bo"].to_broadcast([P, D])).then_inc(wo_loaded, 16)
            sp.wait_ge(kept, NF - 1)
            load(wq[0], "l1_wq", 2, q_loaded[0])
            with sp.Fori(0, GROUPS - 2) as g:
                sp.wait_ge(kept, order(g, 5, PLAN[5][0]) + 1)
                load(wkv, "l1_wkv", g + 1, kv_loaded)
                sp.wait_ge(kept, order(g, 8, PLAN[8][0]) + 1)
                load(wq[1], "l1_wq", 2 * g + 3, q_loaded[1])
                sp.wait_ge(kept, order(g, 12, PLAN[12][0]) + 1)
                load(wq[0], "l1_wq", 2 * g + 4, q_loaded[0])
            g = GROUPS - 2
            sp.wait_ge(kept, order(g, 5, PLAN[5][0]) + 1)
            load(wkv, "l1_wkv", g + 1, kv_loaded)
            sp.wait_ge(kept, order(g, 8, PLAN[8][0]) + 1)
            load(wq[1], "l1_wq", 2 * g + 3, q_loaded[1])

        @block.tensor
        def _(pe):
            def group(what, n):
                b, part, c, m = what
                if not isinstance(n, int) or n > 0:
                    pe.wait_ge(kept, n)
                if part == "v":
                    for j in range(2):
                        t = (2 * c + j) * P
                        for kk in range(KT):
                            at = (MAPS * KT * HD) + kk * VD
                            last = pe.matmul(W[:, j * VD:(j + 1) * VD], ht[:, kk, t:t + P], wkv[:, at:at + VD],
                                             start=(kk == 0), stop=(kk == KT - 1))
                else:
                    w = wkv if part == "k" else wq[b]
                    for kk in range(KT):
                        at = (m * KT + kk) * HD
                        last = pe.matmul(W, w[:, at:at + HD], ht[:, kk, c * BANK:c * BANK + BANK],
                                         start=(kk == 0), stop=(kk == KT - 1))
                last.then_inc(projected, 1)

            def scores(g, s, m):
                b, i = (s // TILES) % 2, s % TILES
                pe.wait_ge(exped, MICRO * g + MAPS * (s - 1) + m + 1 + CREDIT)
                n = causal_blocks(i) * P
                for c in range(0, n, BANK):
                    e = min(n, c + BANK)
                    pe.matmul(S[m][:, c:e], q[b][m][:, i * P:i * P + P], k[m][:, c:e], start=True, stop=(e < n))
                pe.matmul(S[m][:, n - P:n], core.ident_bf[:], core.causal_bf[:], start=False,
                          stop=True).then_inc(scored, 1)

            def turn(g, t):
                pe.wait_ge(mixed_done, STEPS * g + t + 1 + CREDIT)
                for c in range(chunks[t]):
                    n = turn_no(g, "p", t, c)
                    bank = turn_index["p", t, c] % 2
                    pe.wait_ge(turned_kept, n - 2 + 1 + CREDIT)
                    for j in range(4 * c, min(4 * c + 4, causal_blocks(t % TILES))):
                        last = pe.transpose(T[bank][:, (j % 4) * P:(j % 4) * P + P], mixed[:, t % 2, j * P:j * P + P],
                                            core.ident[:])
                    last.then_inc(turned, 1)

            def turn_out(g, t):
                n = turn_no(g, "o", t, 0)
                bank = turn_index["o", t, 0] % 2
                pe.wait_ge(on_done, STEPS * g + t + 1 + CREDIT)
                pe.wait_ge(turned_kept, n - 2 + 1 + CREDIT)
                for j in range(KT):
                    last = pe.transpose(T[bank][:, j * P:j * P + P], on[:, t % 2, j * P:j * P + P], core.ident[:])
                last.then_inc(turned, 1)

            def values(g, t):
                pe.wait_ge(o_kept, STEPS * g + t + 1)
                n = causal_blocks(t % TILES)
                for j in range(n):
                    if j % 4 == 0:
                        pe.wait_ge(turned_kept, turn_no(g, "p", t, j // 4) + 1 + CREDIT)
                    last = pe.matmul(O, mixed_t[:, t % 2, j, :], v[:, j, :], start=(j == 0), stop=(j == n - 1))
                last.then_inc(valued, 1)

            def kv_group(g, is_last):
                for s in range(1, STEPS):
                    if s in (8, 12):
                        c = (s - 8) // 4
                        at = 6 if c == 0 else 8
                        pe.wait_ge(kept, order(g, at, PLAN[at][-1]) + 1)
                    if s == 4:
                        pe.wait_ge(kept, order(g, 3, PLAN[3][0]) + 1)
                    for m in range(MAPS):
                        scores(g, s, m)
                    turn(g, s - 1)
                    for what in PLAN.get(s, []):
                        if is_last and what[0] == 0:
                            continue
                        if s == 6 and what[3] == 0:
                            pe.wait_ge(q_loaded[1], 16 * (g + 1))
                        if s == 9:
                            pe.wait_ge(q_loaded[0], 16 * (g + 2))
                        group(what, order(g, s, what))
                    if s - 1 == 0:
                        pe.wait_ge(kept, NG * g + NF)
                    if s - 1 in (2, 4, 6):
                        at = {2: 1, 4: 4, 6: 5}[s - 1]
                        pe.wait_ge(kept, order(g, at, PLAN[at][0]) + 1)
                    values(g, s - 1)
                    if s >= 2:
                        turn_out(g, s - 2)
                if not is_last:
                    pe.wait_ge(kv_loaded, 16 * (g + 2))
                    group(PLAN[16][0], order(g, 16, PLAN[16][0]))
                turn(g, STEPS - 1)
                if not is_last:
                    group(PLAN[16][1], order(g, 16, PLAN[16][1]))
                values(g, STEPS - 1)
                if not is_last:
                    pe.wait_ge(kept, order(g, 16, PLAN[16][1]) + 1)
                    for m in range(MAPS):
                        scores(g, STEPS, m)
                    group(PLAN[16][2], order(g, 16, PLAN[16][2]))
                turn_out(g, STEPS - 2)
                turn_out(g, STEPS - 1)

            pe.sem_inc(valued, CREDIT)
            pe.sem_inc(turned, TURN_CREDIT)
            for n, what in enumerate(FIRST):
                if n == 0:
                    pe.wait_ge(kv_loaded, 16)
                if n == 1:
                    pe.wait_ge(q_loaded[0], 16)
                group(what, n)
                if n == 4:
                    pe.wait_ge(kept, 4)
                    for m in range(MAPS):
                        scores(0, 0, m)
            with pe.Fori(0, GROUPS - 1) as g:
                kv_group(g, False)
            kv_group(GROUPS - 1, True)
            pe.wait_ge(wo_scaled, 2 * GROUPS * KT)
            pe.wait_ge(turned_kept, NT * GROUPS + CREDIT)
            for i in range(TILES):
                if i >= 2:
                    pe.wait_ge(added, i - 1)
                for h in range(2 * GROUPS * KT):
                    last = pe.matmul(S[i % 2][:, 0:D], att[:, h, i * P:i * P + P], wo[:, h, :],
                                     start=(h == 0), stop=(h == 2 * GROUPS * KT - 1))
                last.then_inc(outed, 1)

        @block.scalar
        def _(act):
            act.sem_inc(exped, CREDIT)
            act.sem_inc(o_kept, 1)
            act.wait_ge(lam_step, 2)
            act.activation(lam[:, 2:4], lam[:, 0:2], ACT.Exp).then_inc(lam_exp, 1)

            def keep_k(what, n):
                b, part, c, m = what
                act.wait_ge(projected, n + 1)
                act.activation(k[m][:, c * BANK:c * BANK + BANK], W, ACT.Identity,
                               bias=wkv[:, KV_BIAS + m:KV_BIAS + m + 1]).then_inc(kept, 1)

            def exps(g, s, m):
                n = causal_blocks(s % TILES) * P
                act.wait_ge(maxed, MICRO * g + MAPS * s + m + 1)
                act.wait_ge(mixed_done, STEPS * g + s - 2 + 1 + CREDIT)
                act.activation(ex[:, s % 2, m, 0:n], S[m][:, 0:n], ACT.Exp, bias=nmax[:, s % 2, m:m + 1],
                               accum_out=rsum[:, s % 2, m:m + 1]).then_inc(exped, 1)

            def keep_o(g, t):
                act.wait_ge(valued, STEPS * g + t + 1 + CREDIT)
                act.wait_ge(on_done, STEPS * g + t - 2 + 1 + CREDIT)
                act.activation(o[:, t % 2, :], O, ACT.Copy).then_inc(o_kept, 1)
                act.wait_ge(o_kept, STEPS * g + t + 1 + 1)
                act.activation(osq[:, t % 2, :], o[:, t % 2, :], ACT.Square, scale=float(VD) ** -0.5,
                               accum_out=ssq[:, t % 2:t % 2 + 1]).then_inc(squared, 1)

            def kv_group(g, is_last):
                for s in range(1, STEPS):
                    for m in range(MAPS):
                        exps(g, s, m)
                    for what in PLAN.get(s, []):
                        if what[1] == "k":
                            keep_k(what, order(g, s, what))
                    keep_o(g, s - 1)
                if not is_last:
                    for what in PLAN[16][0:2]:
                        keep_k(what, order(g, 16, what))
                keep_o(g, STEPS - 1)
                if not is_last:
                    for m in range(MAPS):
                        exps(g, STEPS, m)

            for n, what in enumerate(FIRST):
                if what[1] == "k":
                    keep_k(what, n)
            for m in range(MAPS):
                exps(0, 0, m)
            with act.Fori(0, GROUPS - 1) as g:
                kv_group(g, False)
            kv_group(GROUPS - 1, True)

        @block.gpsimd
        def _(pool):
            pool.wait_ge(lam_loaded, 32)
            pool.wait_ge(wo_loaded, 32)
            for h in range(2 * GROUPS * KT):
                pool.tensor_scalar(wo[:, h, :], wo[:, h, :], subln[:, h % KT:h % KT + 1], 1.0 - LAMBDA_INIT,
                                   ALU.mult, ALU.mult).then_inc(wo_scaled, 1)

            with pool.Fori(0, GROUPS) as g:
                for t in range(STEPS):
                    pool.wait_ge(squared, STEPS * g + t + 1)
                    pool.tensor_tensor(mean_sq[:, t % 2:t % 2 + 1], ssq[:, t % 2:t % 2 + 1], core.eps[:],
                                       ALU.add).then_inc(meaned, 1)
                    pool.wait_ge(meaned, STEPS * g + t + 1)
                    pool.tensor_tensor(rms[:, t % 2:t % 2 + 1], mean_sq[:, t % 2:t % 2 + 1], core.half_neg[:, 0:1],
                                       ALU.pow).then_inc(rms_done, 1)

        @block.vector
        def _(dve):
            dve.sem_inc(turned_kept, CREDIT)
            dve.sem_inc(mixed_done, CREDIT)
            dve.sem_inc(on_done, CREDIT)
            dve.wait_ge(lam_loaded, 32)
            for j in range(2):
                dve.tensor_tensor_reduce(out=lam_rows[:, 2 * j, :], in0=lam_rows[:, 2 * j, :], in1=lam_rows[:, 2 * j + 1, :],
                                         scale=1.0, scalar=0.0, op0=ALU.mult, op1=ALU.add,
                                         accum_out=lam[:, j:j + 1]).then_inc(lam_step, 1)
            dve.wait_ge(lam_exp, 1)
            dve.tensor_tensor(lam[:, 4:5], lam[:, 3:4], lam[:, 2:3], ALU.subtract).then_inc(lam_step, 1)
            dve.wait_ge(lam_step, 3)
            dve.tensor_scalar(lam[:, 5:6], lam[:, 4:5], -LAMBDA_INIT, None, ALU.add).then_inc(lam_step, 1)
            dve.wait_ge(lam_step, 4)

            def keep(what, n):
                b, part, c, m = what
                dve.wait_ge(projected, n + 1)
                if part == "q":
                    dve.tensor_scalar(q[b][m][:, c * BANK:c * BANK + BANK], W,
                                      wq[b][:, MAPS * KT * HD + m:MAPS * KT * HD + m + 1], SCALE,
                                      ALU.add, ALU.mult).then_inc(kept, 1)
                else:
                    dve.tensor_tensor(v[:, 2 * c:2 * c + 2, :], W.rearrange("p (t d) -> p t d", t=2),
                                      wkv[:, KV_BIAS + MAPS:].rearrange("p (a d) -> p a d", a=1).to_broadcast([P, 2, VD]),
                                      ALU.add).then_inc(kept, 1)

            def maxes(g, s):
                n = causal_blocks(s % TILES) * P
                for m in range(MAPS):
                    dve.wait_ge(scored, MICRO * g + MAPS * s + m + 1)
                    dve.tensor_reduce(nmax[:, s % 2, m:m + 1], S[m][:, 0:n], AX_X, ALU.max,
                                      negate=True).then_inc(maxed, 1)

            def turned_by(g, kind, t):
                if t >= 0:
                    c = chunks[t] - 1 if kind == "p" else 0
                    return NT * g + turn_index[kind, t, c] + 1 + TURN_CREDIT
                c = chunks[t + STEPS] - 1 if kind == "p" else 0
                return NT * g + turn_index[kind, t + STEPS, c] - NT + 1 + TURN_CREDIT

            def mix(g, s):
                n = causal_blocks(s % TILES) * P
                b = s % 2
                dve.wait_ge(exped, MICRO * g + MAPS * s + 2 + CREDIT)
                dve.reciprocal(rinv[:, b, :], rsum[:, b, :]).then_inc(mix_step, 1)
                dve.wait_ge(mix_step, 3 * (STEPS * g + s) + 1)
                dve.tensor_tensor(rneg[:, b:b + 1], rinv[:, b, 1:2], lam[:, 5:6], ALU.mult).then_inc(mix_step, 1)
                dve.wait_ge(mix_step, 3 * (STEPS * g + s) + 2)
                dve.tensor_scalar(ex[:, b, 1, 0:n], ex[:, b, 1, 0:n], rneg[:, b:b + 1], None,
                                  ALU.mult).then_inc(mix_step, 1)
                dve.wait_ge(mix_step, 3 * (STEPS * g + s) + 3)
                dve.wait_ge(turned, turned_by(g, "p", s - 2))
                dve.scalar_tensor_tensor(out=mixed[:, b, 0:n], in0=ex[:, b, 0, 0:n], scalar=rinv[:, b, 0:1],
                                         in1=ex[:, b, 1, 0:n], op0=ALU.mult, op1=ALU.add).then_inc(mixed_done, 1)

            def keep_turned(g, t):
                for c in range(chunks[t]):
                    m = min(4, causal_blocks(t % TILES) - 4 * c)
                    dve.wait_ge(turned, turn_no(g, "p", t, c) + 1 + TURN_CREDIT)
                    if c == 0:
                        dve.wait_ge(valued, STEPS * g + t - 2 + 1 + CREDIT)
                    dve.tensor_copy(mixed_t[:, t % 2, 4 * c:4 * c + m, :],
                                    T[turn_index["p", t, c] % 2][:, 0:m * P].rearrange("p (t d) -> p t d", t=m)
                                    ).then_inc(turned_kept, 1)

            def norm(g, t):
                dve.wait_ge(rms_done, STEPS * g + t + 1)
                dve.wait_ge(turned, turned_by(g, "o", t - 2))
                dve.tensor_scalar(on[:, t % 2, :], o[:, t % 2, :], rms[:, t % 2:t % 2 + 1], None,
                                  ALU.mult).then_inc(on_done, 1)

            def keep_out(g, t):
                dve.wait_ge(turned, turn_no(g, "o", t, 0) + 1 + TURN_CREDIT)
                i = t % TILES
                at = 2 * KT * g + KT * (t // TILES)
                dve.tensor_copy(att[:, bass.ds(at, KT), i * P:i * P + P],
                                T[turn_index["o", t, 0] % 2][:, 0:VD].rearrange("p (e d) -> p e d", e=KT)
                                ).then_inc(turned_kept, 1)

            def kv_group(g, is_last):
                for s in range(1, STEPS):
                    maxes(g, s)
                    keep_turned(g, s - 1)
                    mix(g, s)
                    for what in PLAN.get(s, []):
                        if what[1] != "k" and not (is_last and what[0] == 0):
                            keep(what, order(g, s, what))
                    if s >= 2:
                        norm(g, s - 2)
                        keep_out(g, s - 2)
                keep_turned(g, STEPS - 1)
                norm(g, STEPS - 2)
                if not is_last:
                    maxes(g, STEPS)
                    mix(g, STEPS)
                    keep(PLAN[16][2], order(g, 16, PLAN[16][2]))
                keep_out(g, STEPS - 2)
                norm(g, STEPS - 1)
                keep_out(g, STEPS - 1)

            for n, what in enumerate(FIRST):
                if what[1] != "k":
                    keep(what, n)
            maxes(0, 0)
            mix(0, 0)
            with dve.Fori(0, GROUPS - 1) as g:
                kv_group(g, False)
            kv_group(GROUPS - 1, True)
            add_gated(dve, core, 0, bo, wo_loaded, 32, gated, bo_gated, [S[i % 2][:, 0:D] for i in range(TILES)],
                      outed, added)


def swiglu(core, A, name, hidden, scaled, run, units_before):
    nc = core.nc
    x, ht, ps = core.x, core.ht, core.ps
    sizes = [min(P, hidden - f) for f in range(0, hidden, P)]
    NF = len(sizes)
    TILES_BEFORE = TILES * run
    UNITS = [(c, f) for c in range(CHUNKS) for f in range(NF)]
    WEIGHTS_IN = 64 if run == 0 else 96
    with ExitStack() as ctx:
        wg = core.sb("wg", [P, KT, hidden], F32, ctx)
        wu = core.sb("wu", [P, KT, hidden], F32, ctx)
        wd = core.sb("wd", [P, NF, D], F32, ctx)
        scales = core.sb("scales", [P, 2, NF], F32, ctx)
        down_s = core.sb("down_s", [P, D], F32, ctx)
        gate_row = core.sb("gate_row", [P, D], F32, ctx)
        sil = core.sb("sil", [P, 2, BANK], F32, ctx)
        hid = core.sb("hid", [P, CHUNKS, NF, BANK], F32, ctx)
        gated = core.sb("gated", [P, 2, D], F32, ctx)
        s = core.ffn_sems
        block = ctx.enter_context(nc.Block())

        @block.sync
        def _(sp):
            sp.dma_start(wg[:], A[name + "_wg"]).then_inc(s["w_loaded"], 16)
            sp.dma_start(wu[:], A[name + "_wu"]).then_inc(s["w_loaded"], 16)
            if scaled:
                sp.dma_start(scales[:], A[name + "_s"]).then_inc(s["w_loaded"], 16)
                sp.dma_start(down_s[:], A[name + "_ds"].to_broadcast([P, D])).then_inc(s["w_loaded"], 16)
            sp.dma_start(wd[:], A[name + "_wd"]).then_inc(s["d_loaded"], 16)

        @block.tensor
        def _(pe):
            def up(n):
                c, f = UNITS[n]
                m = sizes[f]
                if n >= 2:
                    pe.wait_ge(s["hid_done"], units_before + n - 1)
                for part, w in enumerate((wg, wu)):
                    for k in range(KT):
                        last = pe.matmul(ps[0:m, 2 * (n % 2) + part, :], w[:, k, f * P:f * P + m],
                                         ht[:, k, c * BANK:c * BANK + BANK], start=(k == 0), stop=(k == KT - 1))
                last.then_inc(s["upped"], 1)

            def down(c):
                pe.wait_ge(s["hid_done"], units_before + NF * (c + 1))
                for j in range(4):
                    i = 4 * c + j
                    if i >= 4:
                        pe.wait_ge(s["gated"], TILES_BEFORE + i - 3)
                    for f in range(NF):
                        m = sizes[f]
                        last = pe.matmul(ps[:, 4 + j, 0:D], hid[0:m, c, f, j * P:j * P + P], wd[0:m, f, :],
                                         start=(f == 0), stop=(f == NF - 1))
                    last.then_inc(s["downed"], 1)

            pe.wait_ge(s["w_loaded"], WEIGHTS_IN)
            for n in range(len(UNITS)):
                up(n)
                if n == NF + 1:
                    pe.wait_ge(s["d_loaded"], 16 * (run + 1))
                    down(0)
            down(1)

        @block.scalar
        def _(act):
            if scaled:
                act.wait_ge(s["w_loaded"], WEIGHTS_IN)
            for n, (c, f) in enumerate(UNITS):
                m = sizes[f]
                act.wait_ge(s["upped"], units_before + n + 1)
                if n >= 2:
                    act.wait_ge(s["hid_done"], units_before + n - 1)
                act.activation(sil[0:m, n % 2, :], ps[0:m, 2 * (n % 2), :], ACT.Silu,
                               scale=scales[0:m, 0, f:f + 1] if scaled else 1.0).then_inc(s["silued"], 1)

        @block.vector
        def _(dve):
            row = core.gate[:, 1, :]
            if scaled:
                dve.wait_ge(s["w_loaded"], WEIGHTS_IN)
                dve.tensor_tensor(gate_row[:], row, down_s[:], ALU.mult).then_inc(s["row"], 1)
                dve.wait_ge(s["row"], 1)
                row = gate_row[:]

            def hidden_unit(n):
                c, f = UNITS[n]
                m = sizes[f]
                dve.wait_ge(s["silued"], units_before + n + 1)
                if scaled:
                    dve.scalar_tensor_tensor(out=hid[0:m, c, f, :], in0=ps[0:m, 2 * (n % 2) + 1, :],
                                             scalar=scales[0:m, 1, f:f + 1], in1=sil[0:m, n % 2, :],
                                             op0=ALU.mult, op1=ALU.mult).then_inc(s["hid_done"], 1)
                else:
                    dve.tensor_tensor(hid[0:m, c, f, :], ps[0:m, 2 * (n % 2) + 1, :], sil[0:m, n % 2, :],
                                      ALU.mult).then_inc(s["hid_done"], 1)

            def add(c):
                for j in range(4):
                    i = 4 * c + j
                    dve.wait_ge(s["downed"], TILES_BEFORE + i + 1)
                    dve.tensor_tensor(gated[:, i % 2, :], ps[:, 4 + j, 0:D], row, ALU.mult).then_inc(s["gated"], 1)
                    dve.wait_ge(s["gated"], TILES_BEFORE + i + 1)
                    dve.tensor_tensor(x[:, i, :], x[:, i, :], gated[:, i % 2, :], ALU.add).then_inc(s["added"], 1)

            for n in range(len(UNITS)):
                hidden_unit(n)
                if n == NF + 1:
                    add(0)
            add(1)


def ffn_l1(core, A):
    swiglu(core, A, "l1f", 704, True, 0, 0)


def ffn_l2(core, A):
    swiglu(core, A, "l2f", 1024, False, 1, 2 * len(range(0, 704, P)))


def attention_l2(core, A):
    nc = core.nc
    HEADS, HD = 4, 64
    STEPS = 2 * HEADS
    ROUNDS = TILES // 2
    SCALE = 0.5
    x, ht, ps = core.x, core.ht, core.ps
    with ExitStack() as ctx:
        w = core.sb("w", [P, 3, KT, D], F32, ctx)
        bias = core.sb("bias", [P, 3, KT], F32, ctx)
        wo = core.sb("wo", [P, KT, D], F32, ctx)
        bo = core.sb("bo", [P, D], F32, ctx)
        qt = core.sb("qt", [P, KT, TOKENS], F32, ctx)
        kt = core.sb("kt", [P, KT, TOKENS], F32, ctx)
        v = core.sb("v", [P, TILES, D], F32, ctx)
        qc = core.sb("qc", [P, 2, KT, P], F32, ctx)
        probs = core.sb("probs", [P, 2, TOKENS], F32, ctx)
        probs_t = core.sb("probs_t", [P, 2, TILES, P], F32, ctx)
        nmax = core.sb("nmax", [P, 2], F32, ctx)
        rsum = core.sb("rsum", [P, 2], F32, ctx)
        rinv = core.sb("rinv", [P, 2], F32, ctx)
        att = core.sb("att", [P, 2, KT, P], F32, ctx)
        gated = core.sb("gated", [P, 2, D], F32, ctx)
        loaded = core.sem("loaded", ctx)
        wo_loaded = core.sem("wo_loaded", ctx)
        projected = core.sem("projected", ctx)
        kept = core.sem("kept", ctx)
        q_copied = core.sem("q_copied", ctx)
        scored = core.sem("scored", ctx)
        maxed = core.sem("maxed", ctx)
        exped = core.sem("exped", ctx)
        inverted = core.sem("inverted", ctx)
        normed = core.sem("normed", ctx)
        turned = core.sem("turned", ctx)
        turned_kept = core.sem("turned_kept", ctx)
        valued = core.sem("valued", ctx)
        att_kept = core.sem("att_kept", ctx)
        outed = core.sem("outed", ctx)
        gated_done = core.sem("gated_done", ctx)
        bo_done = core.sem("bo_done", ctx)
        CREDIT = 2
        TURN_CREDIT = 4
        S = [ps[:, 0:2, :].rearrange("p a b -> p (a b)"), ps[:, 2:4, :].rearrange("p a b -> p (a b)")]
        T = [ps[:, 4, :], ps[:, 5, :]]
        V = ps[:, 6, 0:KT * P].rearrange("p (k q) -> p k q", k=KT)
        O = ps[:, 7, 0:D]
        GROUPS = [(part, m, c) for m in range(KT) for c in range(CHUNKS) for part in (0, 1)] + [(2, c, 0) for c in range(4)]
        block = ctx.enter_context(nc.Block())

        @block.sync
        def _(sp):
            sp.dma_start(w[:], A["l2_wqkv"]).then_inc(loaded, 16)
            sp.dma_start(bias[:], A["l2_bqkv"]).then_inc(loaded, 16)
            sp.dma_start(wo[:], A["l2_wo"]).then_inc(wo_loaded, 16)
            sp.dma_start(bo[:], A["l2_bo"].to_broadcast([P, D])).then_inc(wo_loaded, 16)

        @block.tensor
        def _(pe):
            pe.sem_inc(valued, CREDIT)
            pe.sem_inc(turned, TURN_CREDIT)
            pe.sem_inc(outed, 1)
            pe.wait_ge(loaded, 32)
            for n, (part, m, c) in enumerate(GROUPS):
                if n >= 4:
                    pe.wait_ge(kept, n - 3)
                W = ps[:, 4 + n % 4, :]
                if part < 2:
                    for k in range(KT):
                        last = pe.matmul(W, w[:, part, k, m * P:m * P + P], ht[:, k, c * BANK:c * BANK + BANK],
                                         start=(k == 0), stop=(k == KT - 1))
                else:
                    for j in range(2):
                        t = (2 * m + j) * P
                        for k in range(KT):
                            last = pe.matmul(W[:, j * D:j * D + D], ht[:, k, t:t + P], w[:, part, k, :],
                                             start=(k == 0), stop=(k == KT - 1))
                last.then_inc(projected, 1)
            pe.wait_ge(kept, len(GROUPS))

            def scores(g, u):
                h, slot = u % HEADS, (u // HEADS) % 2
                if h == 0:
                    pe.wait_ge(q_copied, 2 * g + u // HEADS + 1)
                pe.wait_ge(exped, STEPS * g + u - 2 + 1 + CREDIT)
                r = HD * (h % 2)
                for c in range(CHUNKS):
                    last = pe.matmul(S[u % 2][:, c * BANK:c * BANK + BANK], qc[r:r + HD, slot, h // 2, :],
                                     kt[r:r + HD, h // 2, c * BANK:c * BANK + BANK], start=True, stop=True)
                last.then_inc(scored, 1)

            def turn(g, u):
                pe.wait_ge(normed, STEPS * g + u + 1)
                for c in range(2):
                    pe.wait_ge(turned_kept, 2 * (STEPS * g + u) + c - 2 + 1 + CREDIT)
                    for j in range(4):
                        last = pe.transpose(T[c][:, j * P:j * P + P], probs[:, u % 2, (4 * c + j) * P:(4 * c + j + 1) * P],
                                            core.ident[:])
                    last.then_inc(turned, 1)

            def values(g, u):
                h = u % HEADS
                if h == 0:
                    pe.wait_ge(att_kept, 2 * g + u // HEADS + 1)
                r = HD * (h % 2)
                for j in range(TILES):
                    if j % 4 == 0:
                        pe.wait_ge(turned_kept, 2 * (STEPS * g + u) + j // 4 + 1 + CREDIT)
                    last = pe.matmul(V[r:r + HD, h // 2, :], v[:, j, h * HD:h * HD + HD], probs_t[:, u % 2, j, :],
                                     start=(j == 0), stop=(j == TILES - 1))
                last.then_inc(valued, 1)

            def out(g, t):
                pe.wait_ge(att_kept, 2 * g + t + 1 + 1)
                pe.wait_ge(gated_done, 2 * g + t + 1)
                for k in range(KT):
                    last = pe.matmul(O, att[:, t, k, :], wo[:, k, :], start=(k == 0), stop=(k == KT - 1))
                last.then_inc(outed, 1)

            def round_(g, is_last):
                for u in range(1, STEPS + 1):
                    if not (is_last and u == STEPS):
                        scores(g, u)
                    turn(g, u - 1)
                    if u == HEADS + 1:
                        out(g, 0)
                    values(g, u - 1)
                out(g, 1)

            scores(0, 0)
            pe.wait_ge(wo_loaded, 32)
            with pe.Fori(0, ROUNDS - 1) as g:
                round_(g, False)
            round_(ROUNDS - 1, True)

        @block.scalar
        def _(act):
            act.sem_inc(exped, CREDIT)
            act.wait_ge(loaded, 32)
            for n, (part, m, c) in enumerate(GROUPS):
                if part == 0:
                    continue
                act.wait_ge(projected, n + 1)
                act.wait_ge(kept, n) if n else None
                W = ps[:, 4 + n % 4, :]
                if part == 1:
                    act.activation(kt[:, m, c * BANK:c * BANK + BANK], W, ACT.Identity,
                                   bias=bias[:, 1, m:m + 1]).then_inc(kept, 1)
                else:
                    act.activation(v[:, 2 * m:2 * m + 2, :], W.rearrange("p (t d) -> p t d", t=2),
                                   ACT.Copy).then_inc(kept, 1)

            def exps(g, u):
                act.wait_ge(maxed, STEPS * g + u + 1)
                act.wait_ge(turned, 2 * (STEPS * g + u - 2) + 2 + TURN_CREDIT)
                act.activation(probs[:, u % 2, :], S[u % 2], ACT.Exp, bias=nmax[:, u % 2:u % 2 + 1],
                               accum_out=rsum[:, u % 2:u % 2 + 1]).then_inc(exped, 1)

            def keep_att(g, t):
                act.wait_ge(valued, STEPS * g + HEADS * (t + 1) + CREDIT)
                act.wait_ge(outed, 2 * g + t - 1 + 1)
                for k in range(KT):
                    last = act.activation(att[:, t, k, :], V[:, k, :], ACT.Identity, bias=bias[:, 2, k:k + 1])
                last.then_inc(att_kept, 1)

            exps(0, 0)

            def round_(g, is_last):
                for u in range(1, STEPS + 1):
                    if not (is_last and u == STEPS):
                        exps(g, u)
                    if u % HEADS == 0:
                        keep_att(g, u // HEADS - 1)

            act.sem_inc(att_kept, 1)
            with act.Fori(0, ROUNDS - 1) as g:
                round_(g, False)
            round_(ROUNDS - 1, True)

        @block.vector
        def _(dve):
            dve.sem_inc(turned_kept, CREDIT)
            dve.sem_inc(gated_done, 1)
            dve.wait_ge(loaded, 32)
            for n, (part, m, c) in enumerate(GROUPS):
                if part:
                    continue
                dve.wait_ge(projected, n + 1)
                dve.wait_ge(kept, n) if n else None
                dve.tensor_scalar(qt[:, m, c * BANK:c * BANK + BANK], ps[:, 4 + n % 4, :], bias[:, 0, m:m + 1], SCALE,
                                  ALU.add, ALU.mult).then_inc(kept, 1)
            dve.wait_ge(wo_loaded, 32)
            dve.tensor_tensor(gated[:, 0, :], core.gate[:, 0, :], bo[:], ALU.mult).then_inc(bo_done, 1)
            dve.wait_ge(bo_done, 1)
            dve.tensor_tensor(x[:], x[:], gated[:, 0:1, :].to_broadcast([P, TILES, D]), ALU.add).then_inc(bo_done, 1)
            dve.wait_ge(bo_done, 2)
            dve.wait_ge(kept, len(GROUPS))

            def copy_q(g, t):
                tile = 2 * g + t
                at = slice(tile * P, tile * P + P) if isinstance(g, int) else bass.ds(tile * P, P)
                dve.tensor_copy(qc[:, t % 2, :, :], qt[:, :, at]).then_inc(q_copied, 1)

            def maxes(g, u):
                dve.wait_ge(scored, STEPS * g + u + 1)
                dve.tensor_reduce(nmax[:, u % 2:u % 2 + 1], S[u % 2], AX_X, ALU.max, negate=True).then_inc(maxed, 1)

            def norm(g, u):
                dve.wait_ge(exped, STEPS * g + u + 1 + CREDIT)
                dve.reciprocal(rinv[:, u % 2:u % 2 + 1], rsum[:, u % 2:u % 2 + 1]).then_inc(inverted, 1)
                dve.wait_ge(inverted, STEPS * g + u + 1)
                dve.tensor_scalar(probs[:, u % 2, :], probs[:, u % 2, :], rinv[:, u % 2:u % 2 + 1], None,
                                  ALU.mult).then_inc(normed, 1)

            def keep_turned(g, u):
                for c in range(2):
                    dve.wait_ge(turned, 2 * (STEPS * g + u) + c + 1 + TURN_CREDIT)
                    if c == 0:
                        dve.wait_ge(valued, STEPS * g + u - 2 + 1 + CREDIT)
                    dve.tensor_copy(probs_t[:, u % 2, 4 * c:4 * c + 4, :],
                                    T[c].rearrange("p (t d) -> p t d", t=4)).then_inc(turned_kept, 1)

            def add(g, t):
                dve.wait_ge(outed, 2 * g + t + 1 + 1)
                dve.tensor_tensor(gated[:, t, :], O, core.gate[:, 0, :], ALU.mult).then_inc(gated_done, 1)
                dve.wait_ge(gated_done, 2 * g + t + 1 + 1)
                tile = 2 * g + t
                at = slice(tile, tile + 1) if isinstance(g, int) else bass.ds(tile, 1)
                dve.tensor_tensor(x[:, at, :], x[:, at, :], gated[:, t:t + 1, :], ALU.add).then_inc(bo_done, 1)

            def round_(g, is_last):
                for u in range(1, STEPS + 1):
                    if u == 2 and not is_last:
                        pass
                    if not (is_last and u == STEPS):
                        if u == 1:
                            copy_q(g, 1)
                        if u == HEADS + 1 and not is_last:
                            copy_q(g, 2)
                        maxes(g, u)
                    keep_turned(g, u - 1)
                    if not (is_last and u == STEPS):
                        norm(g, u)
                    if u == HEADS + 1:
                        add(g, 0)
                add(g, 1)

            copy_q(0, 0)
            maxes(0, 0)
            norm(0, 0)
            with dve.Fori(0, ROUNDS - 1) as g:
                round_(g, False)
            round_(ROUNDS - 1, True)


ROUND = 1.5 * 2.0 ** 23
TURN = 6.283185
FRAME = 64


def recurrence_l3(core, A):
    nc = core.nc
    x, ht, ps = core.x, core.ht, core.ps
    FRAMES = TOKENS // FRAME
    with ExitStack() as ctx:
        def buf(name, shape=(P, TOKENS), dt=F32):
            return core.sb("r_" + name, list(shape), dt, ctx)

        w_in = buf("w_in", (P, KT, D))
        w_g = buf("w_g", (P, 2, KT, P))
        cols = buf("cols", (P, 6))
        w_out = buf("w_out", (P, KT, D))
        b_out = buf("b_out", (P, D))
        xh = buf("xh", (P, KT, TOKENS))
        gx = buf("gx")
        ga = buf("ga")
        c = buf("c", (P, 16))
        r1 = buf("r1")
        r2 = buf("r2")
        th = buf("th")
        keep = buf("keep")
        phi = buf("phi")
        ends = buf("ends", (P, FRAMES))
        ends_k = buf("ends_k", (P, FRAMES))
        ends_f = buf("ends_f", (P, FRAMES))
        base = buf("base", (P, FRAMES + 1))
        ones = buf("ones", (P, FRAMES))
        f1 = buf("f1")
        f2 = buf("f2")
        k1 = buf("k1")
        k2 = buf("k2")
        sin1 = buf("sin1")
        cos1 = buf("cos1")
        sin2 = buf("sin2")
        cos2 = buf("cos2")
        zr = buf("zr")
        zi = buf("zi")
        m1 = buf("m1")
        m2 = buf("m2")
        sr = buf("sr")
        si = buf("si")
        h = buf("h", (P, KT, TOKENS))
        gated = buf("gated", (P, 2, D))
        loaded = core.sem("r_loaded", ctx)
        out_loaded = core.sem("r_out_loaded", ctx)
        projected = core.sem("r_projected", ctx)
        kept = core.sem("r_kept", ctx)
        gates = core.sem("r_gates", ctx)
        gated_act = core.sem("r_gated_act", ctx)
        step = core.sem("r_step", ctx)
        c_ready = core.sem("r_c_ready", ctx)
        a_exp = core.sem("r_a_exp", ctx)
        decayed = core.sem("r_decayed", ctx)
        angle = core.sem("r_angle", ctx)
        waved = core.sem("r_waved", ctx)
        squared = core.sem("r_squared", ctx)
        rooted = core.sem("r_rooted", ctx)
        half_done = core.sem("r_half", ctx)
        ready = core.sem("r_ready", ctx)
        keep_done = core.sem("r_keep", ctx)
        outed = core.sem("r_outed", ctx)
        added = core.sem("r_added", ctx)
        bo_done = core.sem("r_bo", ctx)
        block = ctx.enter_context(nc.Block())

        @block.sync
        def _(sp):
            sp.dma_start(w_in[:], A["l3_win"]).then_inc(loaded, 16)
            sp.dma_start(w_g[:], A["l3_wg"]).then_inc(loaded, 16)
            sp.dma_start(cols[:], A["l3_cols"]).then_inc(loaded, 16)
            sp.dma_start(w_out[:], A["l3_wout"]).then_inc(out_loaded, 16)
            sp.dma_start(b_out[:], A["l3_bout"].to_broadcast([P, D])).then_inc(out_loaded, 16)

        @block.gpsimd
        def _(pool):
            pool.memset(keep[:], 1.0).then_inc(keep_done, 1)
            pool.wait_ge(keep_done, 1)
            pool.memset(keep[:].rearrange("p (f n) -> p f n", n=FRAME)[:, :, 0:1], 0.0).then_inc(keep_done, 1)
            pool.memset(ones[:], 1.0).then_inc(keep_done, 1)
            pool.memset(base[:], 0.0).then_inc(keep_done, 1)

        @block.tensor
        def _(pe):
            pe.wait_ge(loaded, 48)
            for m in range(KT):
                for n in range(CHUNKS):
                    for k in range(KT):
                        last = pe.matmul(ps[:, 2 * m + n, :], w_in[:, k, m * P:m * P + P],
                                         ht[:, k, n * BANK:n * BANK + BANK], start=(k == 0), stop=(k == KT - 1))
                    last.then_inc(projected, 1)
            pe.wait_ge(kept, KT)
            for g in (1, 0):
                for n in range(CHUNKS):
                    for k in range(KT):
                        last = pe.matmul(ps[:, 4 + 2 * g + n, :], w_g[:, g, k, :], xh[:, k, n * BANK:n * BANK + BANK],
                                         start=(k == 0), stop=(k == KT - 1))
                last.then_inc(gates, 1)
            pe.wait_ge(out_loaded, 32)
            pe.wait_ge(ready, 2)
            for i in range(TILES):
                for k in range(KT):
                    last = pe.matmul(ps[:, i % 4, 0:D], h[:, k, i * P:i * P + P], w_out[:, k, :],
                                     start=(k == 0), stop=(k == KT - 1))
                last.then_inc(outed, 1)
                if 3 <= i < TILES - 1:
                    pe.wait_ge(added, i - 2)

        @block.scalar
        def _(act):
            for m in range(KT):
                act.wait_ge(projected, 2 * m + 2)
                act.activation(xh[:, m, :], ps[:, 2 * m:2 * m + 2, :].rearrange("p a b -> p (a b)"), ACT.Identity,
                               bias=cols[:, m:m + 1]).then_inc(kept, 1)
            act.wait_ge(gates, 1)
            act.activation(ga[:], ps[:, 6:8, :].rearrange("p a b -> p (a b)"), ACT.Sigmoid,
                           bias=cols[:, 3:4]).then_inc(gated_act, 1)
            act.wait_ge(gates, 2)
            act.activation(gx[:], ps[:, 4:6, :].rearrange("p a b -> p (a b)"), ACT.Sigmoid,
                           bias=cols[:, 2:3]).then_inc(gated_act, 1)
            act.wait_ge(c_ready, 1)
            act.activation(c[:, 2:3], c[:, 1:2], ACT.Exp, scale=-1.0).then_inc(a_exp, 1)
            act.wait_ge(c_ready, 2)
            act.activation(r2[:], ga[:], ACT.Exp, scale=c[:, 8:9]).then_inc(decayed, 1)
            act.activation(r1[:], ga[:], ACT.Exp, scale=c[:, 9:10]).then_inc(decayed, 1)
            for n, (dst, src) in enumerate(((cos2, f2), (sin2, f1))):
                act.wait_ge(angle, n + 1)
                act.activation(dst[:], src[:], ACT.Sin, scale=TURN).then_inc(waved, 1)
            act.wait_ge(squared, 1)
            act.activation(m2[:], m1[:], ACT.Sqrt).then_inc(rooted, 1)
            act.wait_ge(half_done, 1)
            act.activation(sr[:], k1[:], ACT.Sqrt, scale=0.5).then_inc(rooted, 1)
            for n, (dst, src) in enumerate(((cos1, f2), (sin1, f1))):
                act.wait_ge(angle, n + 3)
                act.activation(dst[:], src[:], ACT.Sin, scale=TURN).then_inc(waved, 1)

        @block.vector
        def _(dve):
            done = [0]

            def after(ins):
                ins.then_inc(step, 1)
                done[0] += 1
                dve.wait_ge(step, done[0])

            TT, TS, STT = dve.tensor_tensor, dve.tensor_scalar, dve.scalar_tensor_tensor
            dve.wait_ge(loaded, 48)
            a_re, a_im = cols[:, 4:5], cols[:, 5:6]
            after(TS(c[:, 0:1], a_re, -1.0, None, ALU.mult))
            dve.tensor_tensor(c[:, 1:2], c[:, 0:1], a_re, ALU.max).then_inc(c_ready, 1)
            after(TS(c[:, 3:4], a_re, 0.0, None, ALU.max))
            dve.wait_ge(a_exp, 1)
            after(TS(c[:, 4:5], c[:, 2:3], 2.0, None, ALU.add))
            after(dve.reciprocal(c[:, 4:5], c[:, 4:5]))
            after(TT(c[:, 5:6], c[:, 2:3], c[:, 4:5], ALU.mult))
            after(TT(c[:, 6:7], c[:, 5:6], c[:, 5:6], ALU.mult))
            after(TS(c[:, 7:8], c[:, 6:7], 1.0 / 17, 1.0 / 15, ALU.mult, ALU.add))
            for odd in (13, 11, 9, 7, 5, 3, 1):
                after(TT(c[:, 7:8], c[:, 7:8], c[:, 6:7], ALU.mult))
                after(TS(c[:, 7:8], c[:, 7:8], 1.0 / odd, None, ALU.add))
            after(TT(c[:, 7:8], c[:, 7:8], c[:, 5:6], ALU.mult))
            after(STT(out=c[:, 7:8], in0=c[:, 7:8], scalar=2.0, in1=c[:, 3:4], op0=ALU.mult, op1=ALU.add))
            after(TS(c[:, 8:9], c[:, 7:8], -16.0, None, ALU.mult))
            TS(c[:, 9:10], c[:, 7:8], -8.0, None, ALU.mult).then_inc(c_ready, 1)
            after(TS(c[:, 10:11], a_im, 1.0 / float(np.pi), None, ALU.mult))
            after(TS(c[:, 11:12], a_im, 0.5 / float(np.pi), None, ALU.mult))

            def reduce(f, k, src, quarter):
                if quarter:
                    after(TS(f[:], src, 0.25, None, ALU.add))
                    src = f[:]
                after(TS(k[:], src, ROUND, -ROUND, ALU.add, ALU.add))
                TT(f[:], src, k[:], ALU.subtract).then_inc(angle, 1)

            dve.wait_ge(gated_act, 1)
            after(TS(th[:], ga[:], c[:, 10:11], None, ALU.mult))
            reduce(f2, k2, th[:], True)
            reduce(f1, k1, th[:], False)
            after(TS(m1[:], ga[:], c[:, 11:12], None, ALU.mult))
            dve.wait_ge(keep_done, 4)
            after(dve.tensor_tensor_scan(phi[:], keep[:], m1[:], 0.0, ALU.mult, ALU.add))
            ph3 = phi[:].rearrange("p (f n) -> p f n", n=FRAME)
            after(dve.tensor_copy(ends[:], ph3[:, :, FRAME - 1]))
            after(TS(ends_k[:], ends[:], ROUND, -ROUND, ALU.add, ALU.add))
            after(TT(ends_f[:], ends[:], ends_k[:], ALU.subtract))
            after(dve.tensor_tensor_scan(base[:, 1:FRAMES + 1], ones[:], ends_f[:], 0.0, ALU.mult, ALU.add))
            after(TT(ph3, ph3, base[:, 0:FRAMES].rearrange("p (f a) -> p f a", a=1).to_broadcast([P, FRAMES, FRAME]), ALU.add))
            dve.wait_ge(gated_act, 2)
            after(TT(xh[:, 0, :], xh[:, 0, :], gx[:], ALU.mult))
            after(TT(xh[:, 1, :], xh[:, 1, :], gx[:], ALU.mult))
            dve.wait_ge(waved, 2)
            dve.wait_ge(decayed, 1)
            after(TT(zr[:], r2[:], cos2[:], ALU.mult))
            after(TS(zr[:], zr[:], -1.0, 1.0, ALU.mult, ALU.add))
            after(STT(out=zi[:], in0=r2[:], scalar=-1.0, in1=sin2[:], op0=ALU.mult, op1=ALU.mult))
            after(TT(m1[:], zr[:], zr[:], ALU.mult))
            after(TT(m2[:], zi[:], zi[:], ALU.mult))
            after(TT(m1[:], m1[:], m2[:], ALU.add))
            TS(m1[:], m1[:], 1e-30, None, ALU.max).then_inc(squared, 1)
            dve.wait_ge(rooted, 1)
            TT(k1[:], m2[:], zr[:], ALU.add).then_inc(half_done, 1)
            reduce(f2, k2, phi[:], True)
            reduce(f1, r2, phi[:], False)
            dve.wait_ge(rooted, 2)
            after(dve.reciprocal(m1[:], sr[:]))
            after(STT(out=si[:], in0=zi[:], scalar=0.5, in1=m1[:], op0=ALU.mult, op1=ALU.mult))

            def product(outr, outi, ar, ai, br, bi, conj):
                after(TT(m1[:], ar, br, ALU.mult))
                after(TT(m2[:], ai, bi, ALU.mult))
                after(TT(outr, m1[:], m2[:], ALU.add if conj else ALU.subtract))
                after(TT(m1[:], ai, br, ALU.mult))
                after(TT(m2[:], ar, bi, ALU.mult))
                return TT(outi, m1[:], m2[:], ALU.subtract if conj else ALU.add)

            after(product(zr[:], zi[:], xh[:, 0, :], xh[:, 1, :], sr[:], si[:], False))
            dve.wait_ge(waved, 4)
            after(product(k1[:], k2[:], zr[:], zi[:], cos1[:], sin1[:], True))
            dve.wait_ge(decayed, 2)
            after(dve.tensor_tensor_scan(f1[:], r1[:], k1[:], 0.0, ALU.mult, ALU.add))
            after(dve.tensor_tensor_scan(f2[:], r1[:], k2[:], 0.0, ALU.mult, ALU.add))
            product(h[:, 0, :], h[:, 1, :], f1[:], f2[:], cos1[:], sin1[:], False).then_inc(ready, 2)
            add_gated(dve, core, 0, b_out, out_loaded, 32, gated, bo_done, [ps[:, i % 4, 0:D] for i in range(TILES)],
                      outed, added)


def lora_l3(core, A):
    nc = core.nc
    x, ht, ps = core.x, core.ht, core.ps
    E, R = 8, 16
    SCALING = 32.0 / R
    with ExitStack() as ctx:
        w_base = core.sb("w_base", [P, KT, D], F32, ctx)
        w_a = core.sb("w_a", [P, KT, P + E], F32, ctx)
        w_b = core.sb("w_b", [P, D], F32, ctx)
        b_base = core.sb("b_base", [P, D], F32, ctx)
        iota = core.sb("iota", [P, E], F32, ctx)
        logit = core.sb("logit", [P, TILES, E], F32, ctx)
        best = core.sb("best", [P, TILES, 8], F32, ctx)
        which = core.sb("which", [P, TILES, 8], U32, ctx)
        which_f = core.sb("which_f", [P, TILES], F32, ctx)
        hot = core.sb("hot", [P, TILES, E], F32, ctx)
        picked = core.sb("l_picked", [P, TILES, P], F32, ctx)
        inner = core.sb("inner", [P, TILES, P], F32, ctx)
        gated = core.sb("gated", [P, 2, D], F32, ctx)
        loaded = core.sem("l_loaded", ctx)
        base_loaded = core.sem("l_base_loaded", ctx)
        iota_done = core.sem("iota_done", ctx)
        routed = core.sem("routed", ctx)
        step = core.sem("l_step", ctx)
        picked_done = core.sem("picked_done", ctx)
        turned = core.sem("l_turned", ctx)
        inner_kept = core.sem("inner_kept", ctx)
        outed = core.sem("l_outed", ctx)
        added = core.sem("l_added", ctx)
        bo_done = core.sem("l_bo", ctx)
        IN = [ps[:, i // 3, (i % 3) * (P + E):(i % 3 + 1) * (P + E)] for i in range(TILES)]
        block = ctx.enter_context(nc.Block())

        @block.sync
        def _(sp):
            sp.dma_start(w_a[:], A["l3_wa"]).then_inc(loaded, 16)
            sp.dma_start(w_base[:], A["l3_wbase"]).then_inc(base_loaded, 16)
            sp.dma_start(w_b[:], A["l3_wb"]).then_inc(base_loaded, 16)
            sp.dma_start(b_base[:], A["l3_bbase"].to_broadcast([P, D])).then_inc(base_loaded, 16)

        @block.gpsimd
        def _(pool):
            pool.iota(iota[:], pattern=[[1, E]], base=0, channel_multiplier=0,
                      allow_small_or_imprecise_dtypes=True).then_inc(iota_done, 1)

        @block.tensor
        def _(pe):
            pe.wait_ge(loaded, 16)
            for i in range(TILES):
                for k in range(KT):
                    last = pe.matmul(IN[i], ht[:, k, i * P:i * P + P], w_a[:, k, :], start=(k == 0), stop=(k == KT - 1))
                if i % 3 == 2 or i == TILES - 1:
                    last.then_inc(routed, 1)
            for i in range(TILES):
                pe.wait_ge(picked_done, i + 1)
                if i >= 2:
                    pe.wait_ge(inner_kept, i - 1)
                pe.transpose(ps[:, 3 + i % 2, 0:P], picked[:, i, :], core.ident[:]).then_inc(turned, 1)
            pe.wait_ge(base_loaded, 48)
            for i in range(TILES):
                if i >= 2:
                    pe.wait_ge(added, i - 1)
                out = ps[:, 5 + i % 2, 0:D]
                for k in range(KT):
                    pe.matmul(out, ht[:, k, i * P:i * P + P], w_base[:, k, :], start=(k == 0), stop=False)
                pe.wait_ge(inner_kept, i + 1)
                pe.matmul(out, inner[:, i, :], w_b[:], start=False, stop=True).then_inc(outed, 1)

        @block.scalar
        def _(act):
            for i in range(TILES):
                act.wait_ge(turned, i + 1)
                act.activation(inner[:, i, :], ps[:, 3 + i % 2, 0:P], ACT.Copy).then_inc(inner_kept, 1)

        @block.vector
        def _(dve):
            done = [0]

            def after(ins):
                ins.then_inc(step, 1)
                done[0] += 1
                dve.wait_ge(step, done[0])

            for i in range(TILES):
                dve.wait_ge(routed, i // 3 + 1)
                last = dve.tensor_copy(logit[:, i, :], IN[i][:, P:P + E])
            after(last)
            for i in range(TILES):
                last = dve.max(best[:, i, :], logit[:, i, :])
            after(last)
            for i in range(TILES):
                last = dve.max_index(which[:, i, :], best[:, i, :], logit[:, i, :])
            after(last)
            after(dve.tensor_copy(which_f[:], which[:, :, 0]))
            dve.wait_ge(iota_done, 1)
            after(dve.tensor_tensor(hot[:], which_f[:].rearrange("p (t a) -> p t a", a=1).to_broadcast([P, TILES, E]),
                                    iota[:].rearrange("p (a e) -> p a e", a=1).to_broadcast([P, TILES, E]), ALU.is_equal))
            after(dve.tensor_scalar(hot[:], hot[:], SCALING, None, ALU.mult))
            for i in range(TILES):
                dve.tensor_tensor(picked[:, i, :].rearrange("p (e r) -> p e r", e=E),
                                  IN[i][:, 0:P].rearrange("p (e r) -> p e r", e=E),
                                  hot[:, i, :].rearrange("p (e a) -> p e a", a=1).to_broadcast([P, E, R]),
                                  ALU.mult).then_inc(picked_done, 1)
            add_gated(dve, core, 1, b_base, base_loaded, 48, gated, bo_done, [ps[:, 5 + i % 2, 0:D] for i in range(TILES)],
                      outed, added)


def pack(inputs):
    a = {k: np.asarray(v) for k, v in inputs.items()}
    out = {}
    c = np.stack([a[f"L{i}_c"].reshape(KT, P) for i in range(LAYERS)])
    out["cond"] = c.transpose(2, 0, 1)
    for i in range(LAYERS):
        out[f"wmod{i}"] = rows_by_partition(a[f"L{i}_wmod"])
    out["x"] = a["L0_attn_query"].reshape(TILES, P, D).transpose(1, 0, 2)
    heads, hd = 16, 128
    w = np.stack([a[f"L0_attn_w_{n}"].reshape(KT, P, heads, hd) for n in "qkv"]).transpose(3, 2, 0, 1, 4)
    b = [a[f"L0_attn_b_{n}"].reshape(heads, hd, 1) for n in "qk"]
    out["l0_wqkv"] = np.concatenate([w.reshape(heads, P, -1), *b], axis=2)
    out["l0_bv"] = a["L0_attn_b_v"].reshape(heads, hd).T
    out["l0_wo"] = a["L0_attn_w_o"].reshape(heads, hd, D).transpose(1, 0, 2)
    out["l0_bo"] = a["L0_attn_b_o"].reshape(1, D)
    out["l0_gw"] = rows_by_partition(a["L0_ffn_gate_w"].T)
    out["l0_gbias"] = a["L0_ffn_gate_bias"].reshape(1, -1)
    out["l0_shared_in"] = np.stack([rows_by_partition(a["L0_ffn_shared_gate"]),
                                    rows_by_partition(a["L0_ffn_shared_up"])], axis=1)
    out["l0_shared_down"] = rows_by_partition(a["L0_ffn_shared_down"])
    w13 = np.stack([a["L0_ffn_w1"], a["L0_ffn_w3"]]).reshape(2, 16, 2, KT, P, 128).transpose(1, 4, 2, 0, 3, 5)
    out["l0_w13"] = w13.reshape(16, P, -1)
    out["l0_w2"] = a["L0_ffn_w2"].reshape(16, 2, 128, D).transpose(0, 2, 1, 3).reshape(16, P, -1)
    groups, maps, hd = 4, 2, 128
    w, b = a["L1_attn_Wqkv_w"], a["L1_attn_Wqkv_b"]
    nq, nk = 16 * hd, 8 * hd
    wq = w[:nq].reshape(8, maps, hd, KT, P).transpose(0, 4, 1, 3, 2).reshape(8, P, -1)
    bq = b[:nq].reshape(8, maps, hd).transpose(0, 2, 1)
    out["l1_wq"] = np.concatenate([wq, bq], axis=2)
    wk = w[nq:nq + nk].reshape(groups, maps, hd, KT, P).transpose(0, 4, 1, 3, 2).reshape(groups, P, -1)
    bk = b[nq:nq + nk].reshape(groups, maps, hd).transpose(0, 2, 1)
    wv = w[nq + nk:].reshape(groups, 2 * hd, KT, P).transpose(0, 3, 2, 1).reshape(groups, P, -1)
    bv = np.broadcast_to(b[nq + nk:].reshape(groups, 1, 2 * hd), (groups, P, 2 * hd))
    out["l1_wkv"] = np.concatenate([wk, wv, bk, bv], axis=2)
    out["l1_lambda"] = np.concatenate([a[f"L1_attn_lambda_{n}"] for n in ("q1", "k1", "q2", "k2")]).reshape(1, -1)
    out["l1_subln"] = a["L1_attn_subln_w"].reshape(KT, P).T
    out["l1_wo"] = rows_by_partition(a["L1_attn_out_w"].T)
    out["l1_bo"] = a["L1_attn_out_b"].reshape(1, D)
    out["l1f_wg"] = rows_by_partition(a["L1_ffn_gate_w"].T)
    out["l1f_wu"] = rows_by_partition(a["L1_ffn_up_w"].T)
    inter = a["L1_ffn_gate_w"].shape[0]
    full = -(-inter // P) * P
    out["l1f_wd"] = rows_by_partition(np.pad(a["L1_ffn_down_w"].T, ((0, full - inter), (0, 0))))
    s = np.stack([np.pad(a[f"L1_ffn_{n}_s"], (0, full - inter)) for n in ("gate", "up")])
    out["l1f_s"] = s.reshape(2, -1, P).transpose(2, 0, 1)
    out["l1f_ds"] = a["L1_ffn_down_s"].reshape(1, D)
    out["l2_wqkv"] = np.stack([rows_by_partition(a[f"L2_attn_W{n}"]) for n in "qkv"], axis=1)
    out["l2_bqkv"] = np.stack([a[f"L2_attn_b{n}"].reshape(KT, P) for n in "qkv"]).transpose(2, 0, 1)
    out["l2_wo"] = rows_by_partition(a["L2_attn_Wo"])
    out["l2_bo"] = a["L2_attn_bo"].reshape(1, D)
    out["l2f_wg"] = rows_by_partition(a["L2_ffn_w_gate"].T)
    out["l2f_wu"] = rows_by_partition(a["L2_ffn_w_up"].T)
    out["l2f_wd"] = rows_by_partition(a["L2_ffn_w_down"].T)
    out["l3_win"] = rows_by_partition(a["L3_attn_W_in"])
    wg = np.zeros((2, D, P), a["L3_attn_W_gx"].dtype)
    for g, n in enumerate(("x", "a")):
        blocks, rows, cols = a[f"L3_attn_W_g{n}"].shape
        for b in range(blocks):
            wg[g, b * rows:(b + 1) * rows, b * cols:(b + 1) * cols] = a[f"L3_attn_W_g{n}"][b]
    out["l3_wg"] = wg.reshape(2, KT, P, P).transpose(2, 0, 1, 3)
    out["l3_cols"] = np.stack([a["L3_attn_b_in"][:P], a["L3_attn_b_in"][P:], a["L3_attn_b_gx"].reshape(-1),
                               a["L3_attn_b_ga"].reshape(-1), a["L3_attn_a_real"], a["L3_attn_a_imag"]], axis=1)
    out["l3_wout"] = rows_by_partition(a["L3_attn_W_out"])
    out["l3_bout"] = a["L3_attn_b_out"].reshape(1, D)
    out["l3_wa"] = rows_by_partition(np.concatenate([a["L3_ffn_A"].reshape(P, D), a["L3_ffn_router_W"]]).T)
    out["l3_wbase"] = rows_by_partition(a["L3_ffn_W_base"].T)
    out["l3_wb"] = a["L3_ffn_Bw"].transpose(0, 2, 1).reshape(P, D)
    out["l3_bbase"] = a["L3_ffn_b_base"].reshape(1, D)
    return {k: np.ascontiguousarray(v) for k, v in out.items()}


def rows_by_partition(w):
    return w.reshape(-1, P, w.shape[1]).transpose(1, 0, 2)


def adaln_stack(nc, A, out):
    attention = (attention_l0, attention_l1, attention_l2, recurrence_l3)
    ffn = (moe, ffn_l1, ffn_l2, lora_l3)
    with ExitStack() as ctx:
        core = Core(nc, ctx)
        stored = core.sem("stored")
        prepare(core, A)
        for layer in range(LAYERS):
            normalise(core, A, layer, 0)
            attention[layer](core, A)
            normalise(core, A, layer, 1)
            ffn[layer](core, A)
        with nc.Block() as block:
            @block.sync
            def _(sp):
                sp.dma_start(out.rearrange("a (t p) d -> p (a t) d", p=P), core.x[:]).then_inc(stored, 16)
                sp.wait_ge(stored, 16)


def kernel(**inputs):
    import concourse.bacc as bacc
    from concourse.bass_utils import run_bass_kernel_spmd

    nc = bacc.Bacc("TRN2", target_bir_lowering=False, num_devices=1)
    arrays = {f"in_{name}": array for name, array in pack(inputs).items()}
    A = {name[3:]: nc.dram_tensor(name, array.shape, mybir.dt.from_np(array.dtype), kind="ExternalInput").ap()
         for name, array in arrays.items()}
    out = nc.dram_tensor("out", (1, TOKENS, D), F32, kind="ExternalOutput").ap()
    adaln_stack(nc, A, out)
    r = run_bass_kernel_spmd(nc, [arrays], core_ids=[0])
    return r.results[0]["out"]
```

```python
from contextlib import ExitStack

import numpy as np

import concourse.bass as bass
from concourse import mybir

F32 = mybir.dt.float32
BF16 = mybir.dt.bfloat16
U32 = mybir.dt.uint32
I32 = mybir.dt.int32
ALU = mybir.AluOpType
ACT = mybir.ActivationFunctionType
AX_X = mybir.AxisListType.X

P = 128
TOKENS = 1024
TILES = TOKENS // P
D = 256
KT = D // P
BANK = 512
CHUNKS = TOKENS // BANK
LN_EPS = 1e-5
LAYERS = 4


EARLY = 1796
ARENA = 6144


def carve(base, *shapes):
    at, parts = 0, []
    for shape in shapes:
        n = int(np.prod(shape))
        part = base[:, at:at + n]
        at += n
        if len(shape) == 2:
            part = part.rearrange("p (a b) -> p a b", a=shape[0])
        elif len(shape) == 3:
            part = part.rearrange("p (a b c) -> p a b c", a=shape[0], b=shape[1])
        parts.append(part)
    return parts


class Core:

    def __init__(self, nc, ctx):
        self.nc = nc
        self.ctx = ctx
        self.taken = {}
        sb, ps = self.sb, self.psum
        self.ps = ps("acc", [P, 8, BANK], F32)
        self.x = sb("x", [P, TILES, D], F32)
        self.ht = sb("ht", [P, KT, TOKENS], F32)
        self.xn = sb("xn", [P, TILES, D], F32)
        self.ident = sb("ident", [P, P], F32)
        self.ident_bf = sb("ident_bf", [P, P], BF16)
        self.causal_bf = sb("causal_bf", [P, P], BF16)
        self.eps = sb("eps", [P, 1], F32)
        self.half_neg = sb("half_neg", [P, 1], F32)
        self.modcs = [sb(f"modc{b}", [P, 4, KT], F32) for b in range(2)]
        self.gates = [sb(f"gate{b}", [P, 2, D], F32) for b in range(2)]
        self.use_layer(0)
        self.early = sb("early", [P, EARLY], F32)
        self.arena = sb("arena", [P, ARENA], F32)
        self.early_in = self.sem("early_in")
        self.arena_in = self.sem("arena_in")
        self.wmod = sb("wmod", [P, KT, 6 * D], F32)
        self.craw = sb("craw", [P, LAYERS, KT], F32)
        self.stats = sb("stats", [P, TILES, 6], F32)
        self.mv = sb("mv", [P, TILES, 2], F32)
        self.veps = sb("veps", [P, TILES], F32)
        self.rstd = sb("rstd", [P, TILES], F32)
        self.sc = sb("sc", [P, KT], F32)
        self.scb = sb("scb", [P, KT, P], F32)
        self.sgn = sb("sgn", [P, 2 * D], F32)
        self.s_wmod = self.sem("s_wmod")
        self.s_x = self.sem("s_x")
        self.norm_sems = {key: self.sem("norm_" + key) for key in
                          ("stats", "mv", "veps", "rstd", "xn", "transposed", "ht_kept",
                           "sc", "scb", "cols", "modc", "rows", "gate")}
        self.ffn_sems = {key: self.sem("ffn_" + key) for key in
                         ("upped", "silued", "hid_done", "downed", "gated", "added",
                          "row")}

    def use_layer(self, layer):
        self.modc = self.modcs[layer % 2]
        self.gate = self.gates[layer % 2]

    def load_early(self, sp, A, layer):
        src = A[f"early{layer}"]
        sp.dma_start(self.early[:, 0:src.shape[1]], src).then_inc(self.early_in, 16)

    def load_arena(self, sp, A, layer):
        src = A[f"arena{layer}"]
        sp.dma_start(self.arena[:, 0:src.shape[1]], src).then_inc(self.arena_in, 16)

    def unique(self, name):
        self.taken[name] = self.taken.get(name, 0) + 1
        return name if self.taken[name] == 1 else f"{name}_{self.taken[name]}"

    def sb(self, name, shape, dt, ctx=None):
        return (ctx or self.ctx).enter_context(self.nc.sbuf_tensor(self.unique(name), shape, dt))

    def psum(self, name, shape, dt):
        return self.ctx.enter_context(self.nc.psum_tensor(name, shape, dt))

    def sem(self, name, ctx=None):
        return (ctx or self.ctx).enter_context(self.nc.semaphore(self.unique(name)))


MASKED = -1.0e10
SHIFT_A, SCALE_A, GATE_A, SHIFT_B, SCALE_B, GATE_B = range(6)


class Norm:

    def __init__(self, core, n):
        self.core, self.n, self.s = core, n, core.norm_sems
        self.layer, self.which = divmod(n, 2)

    def count(self, i):
        return TILES * self.n + i + 1

    def stats(self, dve, i):
        core, s = self.core, self.s
        dve.bn_stats(core.stats[:, i, :], core.x[:, i, :]).then_inc(s["stats"], 1)
        dve.wait_ge(s["stats"], self.count(i))
        dve.bn_aggr(core.mv[:, i, :], core.stats[:, i, :]).then_inc(s["mv"], 1)
        dve.wait_ge(s["mv"], self.count(i))
        dve.tensor_scalar(core.veps[:, i:i + 1], core.mv[:, i, 1:2], LN_EPS, None, ALU.add).then_inc(s["veps"], 1)

    def root(self, pool, i):
        core, s = self.core, self.s
        pool.wait_ge(s["veps"], self.count(i))
        pool.tensor_tensor(core.rstd[:, i:i + 1], core.veps[:, i:i + 1], core.half_neg[:],
                           ALU.pow).then_inc(s["rstd"], 1)

    def scale(self, dve, i):
        core, s = self.core, self.s
        dve.wait_ge(s["rstd"], self.count(i))
        dve.tensor_scalar(core.xn[:, i, :], core.x[:, i, :], core.mv[:, i, 0:1], core.rstd[:, i:i + 1],
                          ALU.subtract, ALU.mult).then_inc(s["xn"], 1)

    def turn(self, pe, i, banks):
        core, s = self.core, self.s
        pe.wait_ge(s["xn"], self.count(i))
        if i >= 2:
            pe.wait_ge(s["ht_kept"], self.count(i - 2))
        for k in range(KT):
            last = pe.transpose(banks[i % 2][:, k * P:k * P + P], core.xn[:, i, k * P:k * P + P], core.ident[:])
        last.then_inc(s["transposed"], 1)

    def keep(self, act, i, banks):
        core, s = self.core, self.s
        modc = core.modcs[self.layer % 2]
        if i == 0 and self.which == 0:
            act.wait_ge(s["modc"], 2 * (self.layer + 1))
        act.wait_ge(s["transposed"], self.count(i))
        for k in range(KT):
            last = act.activation(core.ht[:, k, i * P:i * P + P], banks[i % 2][:, k * P:k * P + P], ACT.Identity,
                                  scale=modc[:, 2 * self.which, k:k + 1], bias=modc[:, 2 * self.which + 1, k:k + 1])
        last.then_inc(s["ht_kept"], 1)


class Modulation:

    def __init__(self, core, layer, cols_bank, rows_bank):
        self.core, self.layer, self.s = core, layer, core.norm_sems
        self.cols = core.ps[:, cols_bank, 0:4 * KT].rearrange("p (v k) -> p v k", v=4)
        self.rows = core.ps[:, rows_bank, :]

    def condition(self, act):
        act.wait_ge(self.core.s_wmod, 32 + 16 * self.layer)
        act.activation(self.core.sc[:], self.core.craw[:, self.layer, :], ACT.Silu).then_inc(self.s["sc"], 1)

    def products(self, pe):
        core, s, cols, rows = self.core, self.s, self.cols, self.rows
        pe.wait_ge(s["sc"], self.layer + 1)
        pe.wait_ge(core.s_wmod, 32 + 16 * self.layer)
        for v, part in enumerate((SHIFT_A, SCALE_A, SHIFT_B, SCALE_B)):
            for m in range(KT):
                for k in range(KT):
                    last = pe.matmul(cols[:, v, m:m + 1], core.wmod[:, k, part * D + m * P:part * D + m * P + P],
                                     core.sc[:, k:k + 1], start=(k == 0), stop=(k == KT - 1))
        last.then_inc(s["cols"], 1)
        pe.wait_ge(s["scb"], KT * (self.layer + 1))
        for g, part in enumerate((GATE_A, GATE_B)):
            for k in range(KT):
                last = pe.matmul(rows[:, g * D:g * D + D], core.scb[:, k, :], core.wmod[:, k, part * D:part * D + D],
                                 start=(k == 0), stop=(k == KT - 1))
        last.then_inc(s["rows"], 1)

    def spread(self, dve):
        core, s = self.core, self.s
        dve.wait_ge(s["sc"], self.layer + 1)
        for k in range(KT):
            dve.tensor_copy(core.scb[:, k, :], core.sc[:, k:k + 1].to_broadcast([P, P])).then_inc(s["scb"], 1)

    def keep_cols(self, dve):
        core, s, cols = self.core, self.s, self.cols
        modc = core.modcs[self.layer % 2]
        dve.wait_ge(s["cols"], self.layer + 1)
        dve.tensor_scalar(modc[:, 0::2, :], cols[:, 1::2, :], 1.0, None, ALU.add).then_inc(s["modc"], 1)
        dve.tensor_copy(modc[:, 1::2, :], cols[:, 0::2, :]).then_inc(s["modc"], 1)

    def keep_rows(self, dve):
        core, s, rows = self.core, self.s, self.rows
        before = 5 * self.layer
        gate = core.gates[self.layer % 2][:].rearrange("p g d -> p (g d)")
        dve.wait_ge(s["rows"], self.layer + 1)
        dve.tensor_copy(gate, rows).then_inc(s["gate"], 1)
        dve.tensor_scalar(core.sgn[:], rows, 0.0, 2.0, ALU.is_ge, ALU.mult).then_inc(s["gate"], 1)
        dve.wait_ge(s["gate"], before + 1)
        dve.scalar_tensor_tensor(out=gate, in0=gate, scalar=-1.0, in1=gate, op0=ALU.mult,
                                 op1=ALU.max).then_inc(s["gate"], 1)
        dve.wait_ge(s["gate"], before + 3)
        dve.tensor_scalar(gate, gate, 0.25, None, ALU.max).then_inc(s["gate"], 1)
        dve.wait_ge(s["gate"], before + 4)
        dve.scalar_tensor_tensor(out=gate, in0=core.sgn[:], scalar=-1.0, in1=gate, op0=ALU.add, op1=ALU.mult).then_inc(s["gate"], 1)

    def load_next(self, sp, A):
        if self.layer + 1 < LAYERS:
            sp.wait_ge(self.s["rows"], self.layer + 1)
            sp.dma_start(self.core.wmod[:], A[f"wmod{self.layer + 1}"]).then_inc(self.core.s_wmod, 16)


def start(core, A):
    nc = core.nc
    norm = Norm(core, 0)
    mod = Modulation(core, 0, 4, 5)
    banks = [core.ps[:, b, :] for b in range(2)]
    with ExitStack() as ctx:
        s_const = core.sem("s_const", ctx)
        block = ctx.enter_context(nc.Block(no_gpsimd_drain=True))

        @block.sync
        def _(sp):
            sp.dma_start(core.craw[:], A["cond"]).then_inc(core.s_wmod, 16)
            sp.dma_start(core.x[:], A["x"]).then_inc(core.s_x, 16)
            sp.dma_start(core.wmod[:], A["wmod0"]).then_inc(core.s_wmod, 16)
            core.load_early(sp, A, 0)
            mod.load_next(sp, A)

        @block.gpsimd
        def _(pool):
            pool.memset(core.half_neg[:], -0.5).then_inc(s_const, 1)
            pool.memset(core.eps[:], LN_EPS).then_inc(s_const, 1)
            pool.memset(core.ident[:], 0.0).then_inc(s_const, 1)
            pool.memset(core.ident_bf[:], 0.0).then_inc(s_const, 1)
            pool.memset(core.causal_bf[:], 0.0).then_inc(s_const, 1)
            pool.wait_ge(s_const, 5)
            for m in (core.ident, core.ident_bf):
                pool.affine_select(out=m[:], in_=m[:], compare_op=ALU.not_equal, fill=1.0, base=0,
                                   pattern=[[-1, P]], channel_multiplier=1).then_inc(s_const, 1)
            pool.affine_select(out=core.causal_bf[:], in_=core.causal_bf[:], compare_op=ALU.is_ge,
                               fill=MASKED, base=0, pattern=[[-1, P]],
                               channel_multiplier=1).then_inc(s_const, 1)
            for i in range(TILES):
                norm.root(pool, i)

        @block.vector
        def _(dve):
            dve.wait_ge(core.s_x, 16)
            for i in range(TILES):
                norm.stats(dve, i)
                if i >= 1:
                    norm.scale(dve, i - 1)
                if i == 3:
                    mod.spread(dve)
            mod.keep_cols(dve)
            norm.scale(dve, TILES - 1)
            mod.keep_rows(dve)

        @block.scalar
        def _(act):
            mod.condition(act)
            for i in range(TILES):
                norm.keep(act, i, banks)

        @block.tensor
        def _(pe):
            pe.wait_ge(s_const, 8)
            mod.products(pe)
            for i in range(TILES):
                norm.turn(pe, i, banks)


def causal_blocks(i):
    return i + 1


def attention_l0(core, A, norm):
    nc = core.nc
    HEADS, HD = 16, 128
    PAIRS = HEADS // 2
    STEPS = 2 * TILES
    SCALE = float(np.float32(HD) ** np.float32(-0.5))
    x, ht, ps = core.x, core.ht, core.ps
    BIAS_Q, BIAS_K = 3 * KT * HD, 3 * KT * HD + 1
    CREDIT = 2
    chunks = [(causal_blocks(s % TILES) + 3) // 4 for s in range(STEPS)]
    before = [sum(chunks[:s]) for s in range(STEPS + 1)]
    PER_PAIR = before[STEPS]
    TURN_CREDIT = 3

    def turned_by(p, s):
        return PER_PAIR * p + (before[s + 1] if s >= 0 else before[s + 1 + STEPS] - PER_PAIR) + TURN_CREDIT

    GROUPS = {3: (0, 1, "q0"), 4: (1, 1, "k1"), 5: (2, 1, "q1"), 6: (3, 1, "v0"), 7: (4, 1, "v1"),
              8: (5, 0, "k0"), 9: (6, 0, "q0"), 11: (7, 0, "k1"), 12: (8, 0, "q1"), 14: (9, 0, "v0"),
              15: (10, 0, "v1"), 16: (11, 1, "k0")}
    index_of = {(b, what): n for n, b, what in GROUPS.values()}
    FIRST = ((0, "k0"), (0, "q0"), (0, "k1"), (0, "q1"), (0, "v0"), (0, "v1"), (1, "k0"))
    NG, NF = len(GROUPS), len(FIRST)

    with ExitStack() as ctx:
        w = carve(core.early, *2 * [(3 * KT * HD + 2,)])
        probs, probs_t, *qt = carve(core.arena, (2, TOKENS), (2, TILES, P), (TOKENS,), (TOKENS,))
        bias_v = core.sb("bias_v", [P, HEADS], F32, ctx)
        kt = [core.sb(f"kt{b}", [P, TOKENS], F32, ctx) for b in range(2)]
        v = [core.sb(f"v{b}", [P, TILES, HD], F32, ctx) for b in range(2)]
        nmax = core.sb("nmax", [P, 2], F32, ctx)
        rsum = core.sb("rsum", [P, 2], F32, ctx)
        rinv = core.sb("rinv", [P, 2], F32, ctx)
        att = core.sb("att", [P, HEADS, TOKENS], F32, ctx)
        wo = core.sb("wo", [P, HEADS, D], F32, ctx)
        bo = core.sb("bo", [P, D], F32, ctx)
        gated = core.sb("gated", [P, 2, D], F32, ctx)
        w_sem = [core.sem(f"w_loaded{b}", ctx) for b in range(2)]
        bias_loaded = core.sem("bias_loaded", ctx)
        wo_loaded = core.sem("wo_loaded", ctx)
        projected = core.sem("projected", ctx)
        kept = core.sem("kept", ctx)
        scored = core.sem("scored", ctx)
        maxed = core.sem("maxed", ctx)
        exped = core.sem("exped", ctx)
        inverted = core.sem("inverted", ctx)
        normed = core.sem("normed", ctx)
        turned = core.sem("turned", ctx)
        turned_kept = core.sem("turned_kept", ctx)
        valued = core.sem("valued", ctx)
        att_kept = core.sem("att_kept", ctx)
        outed = core.sem("outed", ctx)
        added = core.sem("added", ctx)
        bo_gated = core.sem("bo_gated", ctx)
        block = ctx.enter_context(nc.Block(no_gpsimd_drain=True))

        S = [ps[:, 0:2, :].rearrange("p a b -> p (a b)"), ps[:, 2:4, :].rearrange("p a b -> p (a b)")]
        T = [ps[:, 4, :], ps[:, 5, :]]
        V = ps[:, 6, :]
        W = ps[:, 7, :]

        def bank(n):
            return V if isinstance(n, int) and n < NF and (NF - 1 - n) % 2 == 1 else W

        @block.sync
        def _(sp):
            sp.dma_start(bias_v[:], A["l0_bv"]).then_inc(bias_loaded, 16)
            sp.dma_start(wo[:], A["l0_wo"]).then_inc(wo_loaded, 16)
            sp.dma_start(bo[:], A["l0_bo"].to_broadcast([P, D])).then_inc(wo_loaded, 16)
            sp.wait_ge(projected, NF - 1)
            sp.dma_start(w[0][:], A["l0_wqkv"][2]).then_inc(w_sem[0], 16)
            with sp.Fori(0, PAIRS - 2) as p:
                sp.wait_ge(projected, p * NG + NF + index_of[1, "v1"] + 1)
                sp.dma_start(w[1][:], A["l0_wqkv"][bass.ds(2 * p + 3, 1)].rearrange("a p n -> (a p) n")).then_inc(w_sem[1], 16)
                sp.wait_ge(projected, p * NG + NF + index_of[0, "v1"] + 1)
                sp.dma_start(w[0][:], A["l0_wqkv"][bass.ds(2 * p + 4, 1)].rearrange("a p n -> (a p) n")).then_inc(w_sem[0], 16)
            sp.wait_ge(projected, (PAIRS - 2) * NG + NF + index_of[1, "v1"] + 1)
            sp.dma_start(w[1][:], A["l0_wqkv"][HEADS - 1]).then_inc(w_sem[1], 16)
            sp.wait_ge(att_kept, 4 * PAIRS + 1)
            core.load_arena(sp, A, 0)

        @block.tensor
        def _(pe):
            def group(b, what, n):
                if not isinstance(n, int) or n >= NF:
                    pe.wait_ge(kept, n)
                elif n >= 2:
                    pe.wait_ge(kept, n - 1)
                W = bank(n)
                part, c = "qkv".index(what[0]), int(what[1])
                if part < 2:
                    for k in range(KT):
                        last = pe.matmul(W, w[b][:, (part * KT + k) * HD:(part * KT + k + 1) * HD], ht[:, k, c * BANK:c * BANK + BANK],
                                         start=(k == 0), stop=(k == KT - 1))
                else:
                    for j in range(4):
                        t = (4 * c + j) * P
                        for k in range(KT):
                            last = pe.matmul(W[:, j * P:j * P + P], ht[:, k, t:t + P], w[b][:, (part * KT + k) * HD:(part * KT + k + 1) * HD],
                                             start=(k == 0), stop=(k == KT - 1))
                last.then_inc(projected, 1)

            def scores(p, s):
                b, i = (s // TILES) % 2, s % TILES
                pe.wait_ge(exped, STEPS * p + s - 2 + 1 + CREDIT)
                n = causal_blocks(i) * P
                for c in range(0, n, BANK):
                    e = min(n, c + BANK)
                    pe.matmul(S[s % 2][:, c:e], qt[b][:, i * P:i * P + P], kt[b][:, c:e], start=True, stop=(e < n))
                pe.matmul(S[s % 2][:, n - P:n], core.ident_bf[:], core.causal_bf[:], start=False,
                          stop=True).then_inc(scored, 1)

            def transposes(p, s):
                i = s % TILES
                pe.wait_ge(normed, STEPS * p + s + 1)
                for c in range(chunks[s]):
                    pe.wait_ge(turned_kept, PER_PAIR * p + before[s] + c - 2 + 1 + CREDIT)
                    tb = T[(before[s] + c) % 2]
                    for j in range(4 * c, min(4 * c + 4, causal_blocks(i))):
                        last = pe.transpose(tb[:, (j % 4) * P:(j % 4) * P + P], probs[:, s % 2, j * P:j * P + P],
                                            core.ident[:])
                    last.then_inc(turned, 1)

            def values(p, s):
                b, i = s // TILES, s % TILES
                if i % 4 == 0:
                    pe.wait_ge(att_kept, 4 * p + s // 4 + 1)
                for j in range(causal_blocks(i)):
                    if j % 4 == 0:
                        pe.wait_ge(turned_kept, PER_PAIR * p + before[s] + j // 4 + 1 + CREDIT)
                    last = pe.matmul(V[:, (i % 4) * P:(i % 4) * P + P], v[b][:, j, :], probs_t[:, s % 2, j, :],
                                     start=(j == 0), stop=(j == causal_blocks(i) - 1))
                last.then_inc(valued, 1)

            def pair(p, is_last):
                for s in range(1, STEPS + (not is_last)):
                    if s == TILES:
                        pe.wait_ge(kept, NG * p + NF + index_of[1, "q1"] + 1)
                    if s == STEPS:
                        pe.wait_ge(kept, NG * p + NF + index_of[0, "q1"] + 1)
                    scores(p, s)
                    transposes(p, s - 1)
                    if s in GROUPS and not (is_last and s >= TILES):
                        j, b, what = GROUPS[s]
                        if s == TILES:
                            pe.wait_ge(w_sem[0], 16 * (p + 1))
                        if s == STEPS:
                            pe.wait_ge(w_sem[1], 16 * (p + 1))
                        group(b, what, NG * p + NF + j)
                    if s - 1 == 0:
                        pe.wait_ge(kept, NG * p + NF - 1)
                    if s - 1 == TILES:
                        pe.wait_ge(kept, NG * p + NF + index_of[1, "v1"] + 1)
                    values(p, s - 1)

            pe.sem_inc(valued, CREDIT)
            pe.sem_inc(turned, TURN_CREDIT)
            pe.wait_ge(core.early_in, 16)
            for n, (b, what) in enumerate(FIRST):
                group(b, what, n)
                if n == 5:
                    pe.wait_ge(kept, 4)
                    scores(0, 0)
            with pe.Fori(0, PAIRS - 1) as p:
                pair(p, False)
            pair(PAIRS - 1, True)
            transposes(PAIRS - 1, STEPS - 1)
            values(PAIRS - 1, STEPS - 1)
            pe.wait_ge(wo_loaded, 32)
            pe.wait_ge(att_kept, 4 * PAIRS + 1)
            for i in range(TILES):
                if i >= 2:
                    pe.wait_ge(added, i - 1)
                for h in range(HEADS):
                    last = pe.matmul(S[i % 2][:, 0:D], att[:, h, i * P:i * P + P], wo[:, h, :],
                                     start=(h == 0), stop=(h == HEADS - 1))
                last.then_inc(outed, 1)
                if i >= 1:
                    norm.turn(pe, i - 1, T)
            norm.turn(pe, TILES - 1, T)

        @block.scalar
        def _(act):
            act.sem_inc(exped, CREDIT)

            def keep(b, what, n):
                act.wait_ge(projected, n + 1)
                if isinstance(n, int) and 0 < n < NF:
                    act.wait_ge(kept, n)
                W = bank(n)
                c = int(what[1])
                if what[0] == "v":
                    act.activation(v[b][:, 4 * c:4 * c + 4, :], W.rearrange("p (t d) -> p t d", t=4),
                                   ACT.Copy).then_inc(kept, 1)
                else:
                    act.activation(kt[b][:, c * BANK:c * BANK + BANK], W, ACT.Identity,
                                   bias=w[b][:, BIAS_K:BIAS_K + 1]).then_inc(kept, 1)

            def exps(p, s):
                n = causal_blocks(s % TILES) * P
                act.wait_ge(maxed, STEPS * p + s + 1)
                act.wait_ge(turned, turned_by(p, s - 2))
                act.activation(probs[:, s % 2, 0:n], S[s % 2][:, 0:n], ACT.Exp, bias=nmax[:, s % 2:s % 2 + 1],
                               accum_out=rsum[:, s % 2:s % 2 + 1]).then_inc(exped, 1)

            def pair(p, is_last):
                for s in range(1, STEPS + (not is_last)):
                    if s < STEPS:
                        exps(p, s)
                    else:
                        exps(p + 1, 0)
                    if s in GROUPS and not (is_last and s >= TILES):
                        j, b, what = GROUPS[s]
                        if what[0] != "q":
                            keep(b, what, NG * p + NF + j)

            for n, (b, what) in enumerate(FIRST):
                if what[0] != "q":
                    keep(b, what, n)
                if n == 5:
                    exps(0, 0)
            with act.Fori(0, PAIRS - 1) as p:
                pair(p, False)
            pair(PAIRS - 1, True)
            for i in range(TILES):
                norm.keep(act, i, T)

        @block.gpsimd
        def _(pool):
            for i in range(TILES):
                norm.root(pool, i)

        @block.vector
        def _(dve):
            dve.sem_inc(turned_kept, CREDIT)
            dve.sem_inc(att_kept, 1)

            def keep_q(b, what, n):
                dve.wait_ge(projected, n + 1)
                if isinstance(n, int) and 0 < n < NF:
                    dve.wait_ge(kept, n)
                W = bank(n)
                c = int(what[1])
                dve.tensor_scalar(qt[b][:, c * BANK:c * BANK + BANK], W, w[b][:, BIAS_Q:BIAS_Q + 1], SCALE,
                                  ALU.add, ALU.mult).then_inc(kept, 1)

            def keep_att(p, s):
                dve.wait_ge(valued, STEPS * p + s + 1 + CREDIT)
                h, c = 2 * p + s // TILES, (s % TILES) // 4
                dve.tensor_scalar(att[:, bass.ds(h, 1), c * BANK:c * BANK + BANK].rearrange("p a t -> p (a t)"), V,
                                  bias_v[:, bass.ds(h, 1)], None, ALU.add).then_inc(att_kept, 1)

            def maxes(p, s):
                n = causal_blocks(s % TILES) * P
                dve.wait_ge(scored, STEPS * p + s + 1)
                dve.tensor_reduce(nmax[:, s % 2:s % 2 + 1], S[s % 2][:, 0:n], AX_X, ALU.max,
                                  negate=True).then_inc(maxed, 1)

            def scale_rows(p, s):
                n = causal_blocks(s % TILES) * P
                dve.wait_ge(exped, STEPS * p + s + 1 + CREDIT)
                dve.reciprocal(rinv[:, s % 2:s % 2 + 1], rsum[:, s % 2:s % 2 + 1]).then_inc(inverted, 1)
                dve.wait_ge(inverted, STEPS * p + s + 1)
                dve.tensor_scalar(probs[:, s % 2, 0:n], probs[:, s % 2, 0:n], rinv[:, s % 2:s % 2 + 1], None,
                                  ALU.mult).then_inc(normed, 1)

            def keep_turned(p, s):
                i = s % TILES
                for c in range(chunks[s]):
                    m = min(4, causal_blocks(i) - 4 * c)
                    dve.wait_ge(turned, PER_PAIR * p + before[s] + c + 1 + TURN_CREDIT)
                    if c == 0:
                        dve.wait_ge(valued, STEPS * p + s - 2 + 1 + CREDIT)
                    dve.tensor_copy(probs_t[:, s % 2, 4 * c:4 * c + m, :],
                                    T[(before[s] + c) % 2][:, 0:m * P].rearrange("p (t d) -> p t d", t=m)
                                    ).then_inc(turned_kept, 1)

            def pair(p, is_last):
                for s in range(1, STEPS + (not is_last)):
                    q = p + 1 if s == STEPS else p
                    maxes(q, s % STEPS)
                    keep_turned(p, s - 1)
                    scale_rows(q, s % STEPS)
                    if s in GROUPS and GROUPS[s][2][0] == "q" and not (is_last and s >= TILES):
                        keep_q(GROUPS[s][1], GROUPS[s][2], NG * p + NF + GROUPS[s][0])
                    if (s - 1) % 4 == 3:
                        keep_att(p, s - 1)

            dve.wait_ge(bias_loaded, 16)
            for n, (b, what) in enumerate(FIRST):
                if what[0] == "q":
                    keep_q(b, what, n)
            maxes(0, 0)
            scale_rows(0, 0)
            with dve.Fori(0, PAIRS - 1) as p:
                pair(p, False)
            pair(PAIRS - 1, True)
            keep_turned(PAIRS - 1, STEPS - 1)
            keep_att(PAIRS - 1, STEPS - 1)
            add_gated(dve, core, 0, bo, wo_loaded, 32, gated, bo_gated, [S[i % 2][:, 0:D] for i in range(TILES)],
                      outed, added, norm)


def add_gated(dve, core, which, b, b_loaded, loaded, gated, gated_done, outs, outed, added, norm):
    x, gate = core.x, core.gate
    dve.wait_ge(b_loaded, loaded)
    dve.tensor_tensor(gated[:, 0, :], gate[:, which, :], b[:], ALU.mult).then_inc(gated_done, 1)
    dve.wait_ge(gated_done, 1)
    dve.tensor_tensor(x[:], x[:], gated[:, 0:1, :].to_broadcast([P, TILES, D]), ALU.add).then_inc(gated_done, 1)
    dve.wait_ge(gated_done, 2)
    for i in range(TILES):
        dve.wait_ge(outed, i + 1)
        dve.tensor_tensor(gated[:, i % 2, :], outs[i], gate[:, which, :], ALU.mult).then_inc(added, 1)
        dve.wait_ge(added, i + 1)
        dve.tensor_tensor(x[:, i, :], x[:, i, :], gated[:, i % 2, :], ALU.add).then_inc(gated_done, 1)
        if norm is not None:
            dve.wait_ge(gated_done, 2 + i + 1)
            norm.stats(dve, i)
            norm.scale(dve, i)


EXPERTS, TOP, GROUPS_OF, TOP_GROUPS, GROUP = 32, 4, 4, 2, 8
FFN = 128
CAP = 2 * (256 * TOP // EXPERTS)
SLOTS = EXPERTS * CAP
ROUTE_SCALE = 2.0
DROPPED = 65536.0
PAD = -3.0e38
RING = 4


def moe(core, A, norm):
    nc = core.nc
    x, xn, ht, ps = core.x, core.xn, core.ht, core.ps
    with ExitStack() as moe_ctx:
        slots_in = nc.dram_tensor("slots_in", (SLOTS, D), F32, kind="Internal").ap()
        slots_out = nc.dram_tensor("slots_out", (SLOTS, D), F32, kind="Internal").ap()
        idx = core.sb("idx", [P, TILES * TOP], U32, moe_ctx)
        wk = core.sb("wk", [P, TILES * TOP], F32, moe_ctx)
        shared = core.sb("shared", [P, TILES, D], F32, moe_ctx)
        picked = core.sb("picked", [P, TILES * TOP, D], F32, moe_ctx)
        wexp = [core.sb(f"wexp{r}", [P, 2 * 2 * KT * FFN + 2 * D], F32, moe_ctx) for r in range(RING)]
        loaded = [core.sem(f"e_loaded{r}", moe_ctx) for r in range(RING)]
        route(core, A, slots_in, idx, wk, shared, picked, wexp, loaded)
        experts(core, A, slots_in, slots_out, wexp, loaded)
        combine(core, slots_out, idx, wk, shared, picked, norm)


def route(core, A, slots_in, idx, wk, shared, picked, wexp, loaded):
    nc = core.nc
    x, xn, ht, ps = core.x, core.xn, core.ht, core.ps
    with ExitStack() as ctx:
        def buf(name, shape, dt=F32):
            return core.sb(name, shape, dt, ctx)

        gw, gbias, sw, sd = carve(core.arena, (KT, EXPERTS), (EXPERTS,), (2, KT, D), (KT, D))
        scores = buf("scores", [P, TILES, EXPERTS])
        sc = buf("scb_", [P, TILES, EXPERTS])
        gtop = buf("gtop", [P, TILES * GROUPS_OF, 8])
        gsum = buf("gsum", [P, TILES, 8])
        gmax = buf("gmax", [P, TILES, 8])
        gidx = buf("gidx", [P, TILES, 8], U32)
        gidf = buf("gidf", [P, TILES, TOP_GROUPS])
        gm = buf("gm", [P, TOP_GROUPS, TILES, GROUPS_OF])
        emax = buf("emax", [P, TILES, 8])
        eidx = buf("eidx", [P, TILES, 8], U32)
        eidf = buf("eidf", [P, TILES, TOP])
        hot = buf("hot", [P, TILES, TOP, EXPERTS])
        prod = buf("prod", [P, TILES, TOP, EXPERTS])
        chosen = buf("chosen", [P, TILES, EXPERTS], BF16)
        chosen_f = buf("chosen_f", [P, TILES, EXPERTS])
        s4 = buf("s4", [P, TILES, TOP])
        den = buf("den", [P, TILES])
        pos4 = buf("pos4", [P, TILES, TOP])
        late = buf("late", [P, TILES, TOP])
        early = buf("early", [P, TILES, TOP])
        slot = buf("slot", [P, TILES, TOP])
        iota_e = buf("iota_e", [P, EXPERTS])
        earlier = buf("earlier", [P, P], BF16)
        ones_bf = buf("ones_bf", [P, P], BF16)
        zero = buf("zero", [P, SLOTS * D // P // 4])
        act_s = buf("act_s", [P, 2, BANK])
        hid = buf("hid", [P, KT, TOKENS])
        const_done = core.sem("const_done", ctx)
        zeroed = core.sem("zeroed", ctx)
        gated = core.sem("r_gated", ctx)
        sigmoid_done = core.sem("sigmoid_done", ctx)
        step = core.sem("route_step", ctx)
        chosen_done = core.sem("chosen_done", ctx)
        placed = core.sem("placed", ctx)
        idx_done = core.sem("idx_done", ctx)
        scattered = core.sem("scattered", ctx)
        upped = core.sem("upped", ctx)
        silued = core.sem("silued", ctx)
        hid_done = core.sem("hid_done", ctx)
        downed = core.sem("downed", ctx)
        shared_done = core.sem("shared_done", ctx)
        logits = ps[:, 0, 0:TILES * EXPERTS]
        where = ps[:, 1, 0:TILES * EXPERTS].rearrange("p (t e) -> p t e", t=TILES)
        mod = Modulation(core, 1, 6, 7)
        block = ctx.enter_context(nc.Block(no_gpsimd_drain=True))

        @block.sync
        def _(sp):
            core.load_early(sp, A, 1)
            for r in range(RING):
                sp.dma_start(wexp[r][:], A["l0_wexp"][r]).then_inc(loaded[r], 16)
            sp.wait_ge(const_done, 6)
            for q in range(4):
                sp.dma_start(slots_in.rearrange("(q p r) d -> q p (r d)", q=4, p=P)[q], zero[:]).then_inc(zeroed, 16)
            mod.load_next(sp, A)
            sp.wait_ge(zeroed, 64)

        @block.gpsimd
        def _(pool):
            pool.memset(zero[:], 0.0).then_inc(const_done, 1)
            pool.memset(earlier[:], 1.0).then_inc(const_done, 1)
            pool.memset(ones_bf[:], 1.0).then_inc(const_done, 1)
            pool.iota(iota_e[:], pattern=[[1, EXPERTS]], base=0, channel_multiplier=0,
                      allow_small_or_imprecise_dtypes=True).then_inc(const_done, 1)
            pool.memset(gsum[:], PAD).then_inc(const_done, 1)
            pool.wait_ge(const_done, 5)
            pool.affine_select(out=earlier[:], in_=earlier[:], compare_op=ALU.is_gt, fill=0.0, base=0,
                               pattern=[[1, P]], channel_multiplier=-1).then_inc(const_done, 1)
            pool.wait_ge(zeroed, 64)
            pool.wait_ge(idx_done, 1)
            for i in range(TILES):
                for k in range(TOP):
                    j = i * TOP + k
                    pool.indirect_dma_start(out=slots_in, out_offset=bass.IndirectOffsetOnAxis(ap=idx[:, j:j + 1], axis=0),
                                            in_=xn[:, i, :], in_offset=None, bounds_check=SLOTS - 1,
                                            oob_is_err=False).then_inc(scattered, 16)
            pool.wait_ge(scattered, 16 * TILES * TOP)

        @block.tensor
        def _(pe):
            pe.wait_ge(core.arena_in, 16)
            for i in range(TILES):
                for k in range(KT):
                    last = pe.matmul(logits[:, i * EXPERTS:(i + 1) * EXPERTS], ht[:, k, i * P:i * P + P], gw[:, k, :],
                                     start=(k == 0), stop=(k == KT - 1))
            last.then_inc(gated, 1)
            mod.products(pe)
            def gate_up(n):
                f, c = n % KT, n // KT
                if n >= 2:
                    pe.wait_ge(hid_done, n - 1)
                for part in range(2):
                    for k in range(KT):
                        last = pe.matmul(ps[:, 2 + 2 * (n % 2) + part, :], sw[:, part, k, f * P:f * P + P],
                                         ht[:, k, c * BANK:c * BANK + BANK], start=(k == 0), stop=(k == KT - 1))
                last.then_inc(upped, 1)
            for n in range(2):
                gate_up(n)
            pe.wait_ge(chosen_done, 1)
            pe.wait_ge(const_done, 6)
            for i in range(TILES):
                for j in range(i + 1):
                    last = pe.matmul(where[:, i, :], (earlier if j == i else ones_bf)[:], chosen[:, j, :],
                                     start=(j == 0), stop=(j == i))
            last.then_inc(placed, 1)
            for n in range(2, KT * CHUNKS):
                gate_up(n)
            pe.wait_ge(hid_done, KT * CHUNKS)
            for i in range(TILES):
                if i >= 2:
                    pe.wait_ge(shared_done, i - 1)
                for f in range(KT):
                    last = pe.matmul(ps[:, 6 + i % 2, 0:D], hid[:, f, i * P:i * P + P], sd[:, f, :],
                                     start=(f == 0), stop=(f == KT - 1))
                last.then_inc(downed, 1)

        @block.scalar
        def _(act):
            act.wait_ge(gated, 1)
            act.activation(scores[:].rearrange("p t e -> p (t e)"), logits, ACT.Sigmoid).then_inc(sigmoid_done, 1)
            mod.condition(act)
            for n in range(KT * CHUNKS):
                act.wait_ge(upped, n + 1)
                if n >= 2:
                    act.wait_ge(hid_done, n - 1)
                act.activation(act_s[:, n % 2, :], ps[:, 2 + 2 * (n % 2), :], ACT.Silu).then_inc(silued, 1)
            for i in range(TILES):
                act.wait_ge(downed, i + 1)
                act.activation(shared[:, i, :], ps[:, 6 + i % 2, 0:D], ACT.Copy).then_inc(shared_done, 1)

        @block.vector
        def _(dve):
            done = [0]

            def after(ins):
                ins.then_inc(step, 1)
                done[0] += 1
                dve.wait_ge(step, done[0])

            def hidden(n):
                f, c = n % KT, n // KT
                dve.wait_ge(silued, n + 1)
                dve.tensor_tensor(hid[:, f, c * BANK:c * BANK + BANK], act_s[:, n % 2, :], ps[:, 3 + 2 * (n % 2), :],
                                  ALU.mult).then_inc(hid_done, 1)

            dve.wait_ge(core.arena_in, 16)
            dve.wait_ge(sigmoid_done, 1)
            after(dve.tensor_tensor(sc[:], scores[:], gbias[:].rearrange("p (a e) -> p a e", a=1).to_broadcast([P, TILES, EXPERTS]), ALU.add))
            mod.spread(dve)
            sc_g = sc[:].rearrange("p t (g e) -> p (t g) e", g=GROUPS_OF)
            for j in range(TILES * GROUPS_OF):
                last = dve.max(gtop[:, j, :], sc_g[:, j, :])
            after(last)
            dve.wait_ge(const_done, 6)
            gt = gtop[:].rearrange("p (t g) m -> p t g m", g=GROUPS_OF)
            after(dve.tensor_tensor(gsum[:, :, 0:GROUPS_OF], gt[:, :, :, 0], gt[:, :, :, 1], ALU.add))
            for i in range(TILES):
                last = dve.max(gmax[:, i, :], gsum[:, i, :])
            after(last)
            for i in range(TILES):
                last = dve.max_index(gidx[:, i, :], gmax[:, i, :], gsum[:, i, :])
            after(last)
            after(dve.tensor_copy(gidf[:], gidx[:, :, 0:TOP_GROUPS]))
            for m in range(TOP_GROUPS):
                last = dve.tensor_tensor(gm[:, m, :, :], gidf[:, :, m:m + 1].to_broadcast([P, TILES, GROUPS_OF]),
                                         iota_e[:, 0:GROUPS_OF].rearrange("p (a g) -> p a g", a=1).to_broadcast([P, TILES, GROUPS_OF]),
                                         ALU.is_equal)
            after(last)
            after(dve.tensor_tensor(gm[:, 0, :, :], gm[:, 0, :, :], gm[:, 1, :, :], ALU.add))
            g3 = gm[:, 0, :, :].rearrange("p t g -> p (t g)").rearrange("p (n a) -> p n a", a=1)
            after(dve.tensor_tensor(sc_g, sc_g, g3.to_broadcast([P, TILES * GROUPS_OF, GROUP]), ALU.mult))
            for i in range(TILES):
                last = dve.max(emax[:, i, :], sc[:, i, :])
            after(last)
            for i in range(TILES):
                last = dve.max_index(eidx[:, i, :], emax[:, i, :], sc[:, i, :])
            after(last)
            after(dve.tensor_copy(eidf[:], eidx[:, :, 0:TOP]))
            hot3 = hot[:].rearrange("p t k e -> p (t k) e")
            prod3 = prod[:].rearrange("p t k e -> p (t k) e")
            after(dve.tensor_tensor(hot3, eidf[:].rearrange("p t k -> p (t k)").rearrange("p (n a) -> p n a", a=1).to_broadcast([P, TILES * TOP, EXPERTS]),
                                    iota_e[:].rearrange("p (a e) -> p a e", a=1).to_broadcast([P, TILES * TOP, EXPERTS]), ALU.is_equal))
            after(dve.tensor_reduce(chosen_f[:], hot[:].rearrange("p t k e -> p t e k"), AX_X, ALU.add))
            dve.tensor_copy(chosen[:], chosen_f[:]).then_inc(chosen_done, 1)
            for i in range(TILES):
                last = dve.tensor_tensor(prod[:, i, :, :], hot[:, i, :, :], scores[:, i:i + 1, :].to_broadcast([P, TOP, EXPERTS]), ALU.mult)
            after(last)
            after(dve.tensor_reduce(s4[:].rearrange("p t k -> p (t k)"), prod3, AX_X, ALU.add))
            after(dve.tensor_reduce(den[:], s4[:], AX_X, ALU.add))
            after(dve.tensor_scalar(den[:], den[:], 1e-20, None, ALU.add))
            after(dve.reciprocal(den[:], den[:]))
            after(dve.tensor_scalar(den[:], den[:], ROUTE_SCALE, None, ALU.mult))
            after(dve.tensor_tensor(s4[:], s4[:], den[:].rearrange("p (t a) -> p t a", a=1).to_broadcast([P, TILES, TOP]), ALU.mult))
            for n in range(2):
                hidden(n)
            dve.wait_ge(placed, 1)
            for i in range(TILES):
                last = dve.tensor_tensor(prod[:, i, :, :], hot[:, i, :, :], where[:, i:i + 1, :].to_broadcast([P, TOP, EXPERTS]), ALU.mult)
            after(last)
            after(dve.tensor_reduce(pos4[:].rearrange("p t k -> p (t k)"), prod3, AX_X, ALU.add))
            after(dve.scalar_tensor_tensor(out=slot[:], in0=eidf[:], scalar=float(CAP), in1=pos4[:], op0=ALU.mult, op1=ALU.add))
            after(dve.tensor_scalar(late[:], pos4[:], float(CAP), DROPPED, ALU.is_ge, ALU.mult))
            dve.tensor_tensor(idx[:], slot[:].rearrange("p t k -> p (t k)"), late[:].rearrange("p t k -> p (t k)"), ALU.add).then_inc(idx_done, 1)
            after(dve.tensor_scalar(early[:], pos4[:], float(CAP), None, ALU.is_lt))
            dve.tensor_tensor(wk[:], s4[:].rearrange("p t k -> p (t k)"), early[:].rearrange("p t k -> p (t k)"), ALU.mult)
            mod.keep_cols(dve)
            mod.keep_rows(dve)
            for n in range(2, KT * CHUNKS):
                hidden(n)
            dve.memset(picked[:], 0.0)


def experts(core, A, slots_in, slots_out, wexp, loaded):
    nc = core.nc
    ps = core.ps
    PAIRS = EXPERTS // 2
    ROUNDS = PAIRS // RING
    with ExitStack() as ctx:
        rows = [core.sb(f"rows{r}", [P, D], F32, ctx) for r in range(RING)]
        w13, w2 = zip(*(carve(wexp[r], (4, KT, FFN), (2, D)) for r in range(RING)))
        bt = [core.sb(f"bt{r}", [P, KT, P], F32, ctx) for r in range(2)]
        sil = [core.sb(f"sil{r}", [P, P], F32, ctx) for r in range(2)]
        hid = [core.sb(f"ehid{r}", [P, P], F32, ctx) for r in range(2)]
        res = [core.sb(f"res{r}", [P, D], F32, ctx) for r in range(RING)]
        rows_loaded = [core.sem(f"rows_loaded{r}", ctx) for r in range(RING)]
        turned = core.sem("e_turned", ctx)
        bt_kept = core.sem("bt_kept", ctx)
        upped = core.sem("e_upped", ctx)
        silued = core.sem("e_silued", ctx)
        hid_done = core.sem("e_hid", ctx)
        downed = core.sem("e_downed", ctx)
        res_kept = core.sem("res_kept", ctx)
        stored = [core.sem(f"e_stored{r}", ctx) for r in range(RING)]
        in_rows = slots_in.rearrange("(q p) d -> q p d", p=P)
        out_rows = slots_out.rearrange("(q p) d -> q p d", p=P)
        T = [ps[:, b, 0:D].rearrange("p (k t) -> p k t", k=KT) for b in range(2)]
        U = [ps[:, 2 + b, 0:2 * P].rearrange("p (w t) -> p w t", w=2) for b in range(2)]
        O = [ps[:, 4 + b, 0:D] for b in range(2)]
        CREDIT = 2
        block = ctx.enter_context(nc.Block(no_gpsimd_drain=True))

        @block.sync
        def _(sp):
            with sp.Fori(0, ROUNDS - 1) as g:
                for r in range(RING):
                    q = bass.ds(g * RING + RING + r, 1)
                    sp.wait_ge(downed, RING * g + r + 1 + CREDIT)
                    sp.dma_start(wexp[r][:], A["l0_wexp"][q].rearrange("a p n -> (a p) n")).then_inc(loaded[r], 16)

        @block.tensor
        def _(pe):
            pe.sem_inc(downed, CREDIT)
            pe.sem_inc(upped, CREDIT)

            def turn(g, r):
                q = RING * g + r
                pe.wait_ge(rows_loaded[r], 16 * (g + 1))
                pe.wait_ge(bt_kept, q - 2 + 1 + CREDIT)
                for k in range(KT):
                    last = pe.transpose(T[r % 2][:, k, :], rows[r][:, k * P:k * P + P], core.ident[:])
                last.then_inc(turned, 1)

            def up(g, r):
                q = RING * g + r
                pe.wait_ge(loaded[r], 16 * (g + 1))
                pe.wait_ge(bt_kept, q + 1 + CREDIT)
                pe.wait_ge(hid_done, q - 2 + 1 + CREDIT)
                for w in range(2):
                    for e in range(2):
                        for k in range(KT):
                            last = pe.matmul(U[r % 2][:, w, e * CAP:(e + 1) * CAP], w13[r][:, 2 * e + w, k, :],
                                             bt[r % 2][:, k, e * CAP:(e + 1) * CAP], start=(k == 0), stop=(k == KT - 1))
                last.then_inc(upped, 1)

            def down(g, r):
                q = RING * g + r
                pe.wait_ge(hid_done, q + 1 + CREDIT)
                pe.wait_ge(res_kept, q - 2 + 1 + CREDIT)
                for e in range(2):
                    last = pe.matmul(O[r % 2][e * CAP:(e + 1) * CAP, :], hid[r % 2][:, e * CAP:(e + 1) * CAP],
                                     w2[r][:, e, :], start=True, stop=True)
                last.then_inc(downed, 1)

            def round_(g, is_last):
                for r in range(RING):
                    if r + 1 < RING:
                        turn(g, r + 1)
                    elif not is_last:
                        turn(g + 1, 0)
                    up(g, r)
                    if r > 0:
                        down(g, r - 1)
                down(g, RING - 1)

            turn(0, 0)
            with pe.Fori(0, ROUNDS - 1) as g:
                round_(g, False)
            round_(ROUNDS - 1, True)

        @block.scalar
        def _(act):
            act.sem_inc(bt_kept, CREDIT)

            def keep_turned(g, r):
                q = RING * g + r
                act.wait_ge(turned, q + 1)
                act.wait_ge(upped, q - 2 + 1 + CREDIT)
                for k in range(KT):
                    last = act.activation(bt[r % 2][:, k, :], T[r % 2][:, k, :], ACT.Identity,
                                          scale=core.modc[:, 2, k:k + 1], bias=core.modc[:, 3, k:k + 1])
                last.then_inc(bt_kept, 1)

            def silu(g, r):
                q = RING * g + r
                act.wait_ge(upped, q + 1 + CREDIT)
                act.wait_ge(hid_done, q - 2 + 1 + CREDIT)
                act.activation(sil[r % 2][:], U[r % 2][:, 0, :], ACT.Silu).then_inc(silued, 1)

            def round_(g, is_last):
                for r in range(RING):
                    if r + 1 < RING:
                        keep_turned(g, r + 1)
                    elif not is_last:
                        keep_turned(g + 1, 0)
                    silu(g, r)
                    if not is_last:
                        act.dma_start(rows[r][:], in_rows[bass.ds(RING * g + r + RING, 1)].rearrange("a p n -> (a p) n")
                                      ).then_inc(rows_loaded[r], 16)

            for r in range(RING):
                act.dma_start(rows[r][:], in_rows[r]).then_inc(rows_loaded[r], 16)
            keep_turned(0, 0)
            with act.Fori(0, ROUNDS - 1) as g:
                round_(g, False)
            round_(ROUNDS - 1, True)

        @block.vector
        def _(dve):
            dve.sem_inc(hid_done, CREDIT)
            dve.sem_inc(res_kept, CREDIT)

            def hidden(g, r):
                q = RING * g + r
                dve.wait_ge(silued, q + 1)
                dve.wait_ge(downed, q - 2 + 1 + CREDIT)
                dve.tensor_tensor(hid[r % 2][:], sil[r % 2][:], U[r % 2][:, 1, :], ALU.mult).then_inc(hid_done, 1)

            def keep(g, r, first):
                q = RING * g + r
                dve.wait_ge(downed, q + 1 + CREDIT)
                if not first:
                    dve.wait_ge(stored[r], 16 * g)
                dve.tensor_copy(res[r][:], O[r % 2]).then_inc(res_kept, 1)

            def round_(g, first):
                for r in range(RING):
                    hidden(g, r)
                    if r > 0:
                        keep(g, r - 1, first)
                keep(g, RING - 1, first)

            round_(0, True)
            with dve.Fori(1, ROUNDS) as g:
                round_(g, False)

        @block.gpsimd
        def _(pool):
            with pool.Fori(0, ROUNDS) as g:
                for r in range(RING):
                    q = g * RING + r
                    pool.wait_ge(res_kept, q + 1 + CREDIT)
                    pool.dma_start(out_rows[bass.ds(q, 1)].rearrange("a p n -> (a p) n"), res[r][:]).then_inc(stored[r], 16)
            for r in range(RING):
                pool.wait_ge(stored[r], 16 * ROUNDS)


def combine(core, slots_out, idx, wk, shared, picked, norm):
    nc = core.nc
    with ExitStack() as ctx:
        gathered = [core.sem(f"gathered{i}", ctx) for i in range(TILES // 2)]
        step = core.sem("c_step", ctx)
        banks = [core.ps[:, b, :] for b in range(2)]
        LAG = 4
        block = ctx.enter_context(nc.Block(no_gpsimd_drain=True))

        @block.gpsimd
        def _(pool):
            for i in range(TILES):
                if i >= LAG:
                    norm.root(pool, i - LAG)
                for k in range(TOP):
                    j = i * TOP + k
                    pool.indirect_dma_start(out=picked[:, j, :], out_offset=None, in_=slots_out,
                                            in_offset=bass.IndirectOffsetOnAxis(ap=idx[:, j:j + 1], axis=0),
                                            bounds_check=SLOTS - 1, oob_is_err=False).then_inc(gathered[i // 2], 16)
            for i in range(TILES - LAG, TILES):
                norm.root(pool, i)

        @block.tensor
        def _(pe):
            for i in range(TILES):
                norm.turn(pe, i, banks)

        @block.scalar
        def _(act):
            for i in range(TILES):
                norm.keep(act, i, banks)

        @block.vector
        def _(dve):
            n = 0
            for i in range(TILES):
                if i % 2 == 0:
                    dve.wait_ge(gathered[i // 2], 2 * 16 * TOP)
                for k in range(TOP):
                    j = i * TOP + k
                    dve.scalar_tensor_tensor(out=shared[:, i, :], in0=picked[:, j, :], scalar=wk[:, j:j + 1],
                                             in1=shared[:, i, :], op0=ALU.mult, op1=ALU.add).then_inc(step, 1)
                    n += 1
                    dve.wait_ge(step, n)
                dve.tensor_tensor(shared[:, i, :], shared[:, i, :], core.gate[:, 1, :], ALU.mult).then_inc(step, 1)
                n += 1
                dve.wait_ge(step, n)
                dve.tensor_tensor(core.x[:, i, :], core.x[:, i, :], shared[:, i, :], ALU.add).then_inc(step, 1)
                n += 1
                dve.wait_ge(step, n)
                norm.stats(dve, i)
                if i >= LAG:
                    norm.scale(dve, i - LAG)
            for i in range(TILES - LAG, TILES):
                norm.scale(dve, i)


def attention_l1(core, A, norm):
    nc = core.nc
    GROUPS, HD, MAPS = 4, 128, 2
    VD = 2 * HD
    STEPS = 2 * TILES
    SCALE = float(HD) ** -0.5
    LAMBDA_INIT = 0.8 - 0.6 * float(np.exp(-0.3 * 1))
    RMS_EPS = 1e-5
    x, ht, ps = core.x, core.ht, core.ps
    chunks = [(causal_blocks(s % TILES) + 3) // 4 for s in range(STEPS)]
    PLAN = {1: [(None, "v", 1, 0)], 2: [(None, "k", 1, 0)], 3: [(None, "k", 1, 1)], 4: [(None, "v", 2, 0)],
            5: [(None, "v", 3, 0)], 6: [(1, "q", 0, 0), (1, "q", 0, 1)], 7: [(1, "q", 1, 0)], 8: [(1, "q", 1, 1)],
            9: [(0, "q", 0, 0)], 10: [(0, "q", 0, 1)], 11: [(0, "q", 1, 0)], 12: [(0, "q", 1, 1)],
            16: [(None, "k", 0, 0), (None, "k", 0, 1), (None, "v", 0, 0)]}
    FIRST = [(None, "k", 0, 0), (0, "q", 0, 0), (None, "k", 0, 1), (0, "q", 0, 1), (0, "q", 1, 0), (0, "q", 1, 1),
             (None, "v", 0, 0)]
    NF = len(FIRST)
    number, NG = {}, 0
    for s in sorted(PLAN):
        for what in PLAN[s]:
            number[s, what] = NG
            NG += 1
    turn_index, NT = {}, 0
    for s in range(1, STEPS + 1):
        for c in range(chunks[s - 1]):
            turn_index["p", s - 1, c] = NT
            NT += 1
        if s >= 2:
            turn_index["o", s - 2, 0] = NT
            NT += 1
    turn_index["o", STEPS - 1, 0] = NT
    NT += 1
    assert NT % 2 == 0

    with ExitStack() as ctx:
        KV_BIAS = (MAPS * KT * HD) + KT * VD
        wkv, wq0 = carve(core.early, (KV_BIAS + MAPS + VD,), (MAPS * KT * HD + MAPS,))
        wq = [wq0, core.sb("wq1", [P, MAPS * KT * HD + MAPS], F32, ctx)]
        q = [[core.sb(f"q{b}{m}", [P, TOKENS], F32, ctx) for m in range(MAPS)] for b in range(2)]
        k = [core.sb(f"k{m}", [P, TOKENS], F32, ctx) for m in range(MAPS)]
        v = core.sb("v", [P, TILES, VD], F32, ctx)
        ex, mixed = carve(core.arena, (2, MAPS, TOKENS), (2, TOKENS))
        mixed_t = core.sb("mixed_t", [P, 2, TILES, P], F32, ctx)
        nmax = core.sb("nmax", [P, 2, MAPS], F32, ctx)
        rsum = core.sb("rsum", [P, 2, MAPS], F32, ctx)
        rinv = core.sb("rinv", [P, 2, MAPS], F32, ctx)
        rneg = core.sb("rneg", [P, 2], F32, ctx)
        o = core.sb("o", [P, 2, VD], F32, ctx)
        osq = core.sb("osq", [P, 2, VD], F32, ctx)
        ssq = core.sb("ssq", [P, 2], F32, ctx)
        mean_sq = core.sb("mean_sq", [P, 2], F32, ctx)
        rms = core.sb("rms", [P, 2], F32, ctx)
        on = core.sb("on", [P, 2, VD], F32, ctx)
        att = core.sb("att", [P, 2 * GROUPS * KT, TOKENS], F32, ctx)
        wo = core.sb("wo", [P, 2 * GROUPS * KT, D], F32, ctx)
        bo = core.sb("bo", [P, D], F32, ctx)
        lam_rows = osq[:].rearrange("p a b -> p (a b)").rearrange("p (a d) -> p a d", a=4)
        lam = core.sb("lam", [P, 8], F32, ctx)
        subln = core.sb("subln", [P, KT], F32, ctx)
        gated = core.sb("gated", [P, 2, D], F32, ctx)
        q_loaded = [core.sem(f"q_loaded{b}", ctx) for b in range(2)]
        kv_loaded = core.sem("kv_loaded", ctx)
        lam_loaded = core.sem("lam_loaded", ctx)
        wo_loaded = core.sem("wo_loaded", ctx)
        lam_step = core.sem("lam_step", ctx)
        lam_exp = core.sem("lam_exp", ctx)
        wo_scaled = core.sem("wo_scaled", ctx)
        projected = core.sem("projected", ctx)
        kept = core.sem("kept", ctx)
        scored = core.sem("scored", ctx)
        maxed = core.sem("maxed", ctx)
        exped = core.sem("exped", ctx)
        mixed_done = core.sem("mixed_done", ctx)
        mix_step = core.sem("mix_step", ctx)
        turned = core.sem("turned", ctx)
        turned_kept = core.sem("turned_kept", ctx)
        valued = core.sem("valued", ctx)
        o_kept = core.sem("o_kept", ctx)
        squared = core.sem("squared", ctx)
        meaned = core.sem("meaned", ctx)
        rms_done = core.sem("rms_done", ctx)
        on_done = core.sem("on_done", ctx)
        outed = core.sem("outed", ctx)
        added = core.sem("added", ctx)
        bo_gated = core.sem("bo_gated", ctx)
        CREDIT = 2
        TURN_CREDIT = 6
        S = [ps[:, 0:2, :].rearrange("p a b -> p (a b)"), ps[:, 2:4, :].rearrange("p a b -> p (a b)")]
        T = [ps[:, 4, :], ps[:, 5, :]]
        O = ps[:, 6, 0:VD]
        W = ps[:, 7, :]

        def bank(n):
            return ps[:, 6, :] if isinstance(n, int) and n < NF and (NF - 1 - n) % 2 == 1 else W
        MICRO = STEPS * MAPS
        block = ctx.enter_context(nc.Block(no_gpsimd_drain=True))

        def order(g, s, what):
            return NG * g + NF + number[s, what]

        def turn_no(g, kind, t, c):
            return NT * g + turn_index[kind, t, c]

        @block.sync
        def _(sp):
            def load(dst, name, g, sem):
                if isinstance(g, int):
                    sp.dma_start(dst[:], A[name][g]).then_inc(sem, 16)
                else:
                    sp.dma_start(dst[:], A[name][bass.ds(g, 1)].rearrange("a p n -> (a p) n")).then_inc(sem, 16)

            load(wq[1], "l1_wq", 1, q_loaded[1])
            sp.dma_start(osq[:].rearrange("p a b -> p (a b)"), A["l1_lambda"].to_broadcast([P, 4 * HD])).then_inc(lam_loaded, 16)
            sp.dma_start(subln[:], A["l1_subln"]).then_inc(lam_loaded, 16)
            sp.dma_start(wo[:], A["l1_wo"]).then_inc(wo_loaded, 16)
            sp.dma_start(bo[:], A["l1_bo"].to_broadcast([P, D])).then_inc(wo_loaded, 16)
            sp.wait_ge(kept, NF - 1)
            load(wq[0], "l1_wq", 2, q_loaded[0])
            with sp.Fori(0, GROUPS - 2) as g:
                sp.wait_ge(kept, order(g, 5, PLAN[5][0]) + 1)
                load(wkv, "l1_wkv", g + 1, kv_loaded)
                sp.wait_ge(kept, order(g, 8, PLAN[8][0]) + 1)
                load(wq[1], "l1_wq", 2 * g + 3, q_loaded[1])
                sp.wait_ge(kept, order(g, 12, PLAN[12][0]) + 1)
                load(wq[0], "l1_wq", 2 * g + 4, q_loaded[0])
            g = GROUPS - 2
            sp.wait_ge(kept, order(g, 5, PLAN[5][0]) + 1)
            load(wkv, "l1_wkv", g + 1, kv_loaded)
            sp.wait_ge(kept, order(g, 8, PLAN[8][0]) + 1)
            load(wq[1], "l1_wq", 2 * g + 3, q_loaded[1])
            sp.wait_ge(turned_kept, NT * GROUPS + CREDIT)
            core.load_arena(sp, A, 1)

        @block.tensor
        def _(pe):
            def group(what, n):
                b, part, c, m = what
                if not isinstance(n, int) or n >= NF:
                    pe.wait_ge(kept, n)
                elif n >= 2:
                    pe.wait_ge(kept, n - 1)
                W = bank(n)
                if part == "v":
                    for j in range(2):
                        t = (2 * c + j) * P
                        for kk in range(KT):
                            at = (MAPS * KT * HD) + kk * VD
                            last = pe.matmul(W[:, j * VD:(j + 1) * VD], ht[:, kk, t:t + P], wkv[:, at:at + VD],
                                             start=(kk == 0), stop=(kk == KT - 1))
                else:
                    w = wkv if part == "k" else wq[b]
                    for kk in range(KT):
                        at = (m * KT + kk) * HD
                        last = pe.matmul(W, w[:, at:at + HD], ht[:, kk, c * BANK:c * BANK + BANK],
                                         start=(kk == 0), stop=(kk == KT - 1))
                last.then_inc(projected, 1)

            def scores(g, s, m):
                b, i = (s // TILES) % 2, s % TILES
                pe.wait_ge(exped, MICRO * g + MAPS * (s - 1) + m + 1 + CREDIT)
                n = causal_blocks(i) * P
                for c in range(0, n, BANK):
                    e = min(n, c + BANK)
                    pe.matmul(S[m][:, c:e], q[b][m][:, i * P:i * P + P], k[m][:, c:e], start=True, stop=(e < n))
                pe.matmul(S[m][:, n - P:n], core.ident_bf[:], core.causal_bf[:], start=False,
                          stop=True).then_inc(scored, 1)

            def turn(g, t):
                pe.wait_ge(mixed_done, STEPS * g + t + 1 + CREDIT)
                for c in range(chunks[t]):
                    n = turn_no(g, "p", t, c)
                    bank = turn_index["p", t, c] % 2
                    pe.wait_ge(turned_kept, n - 2 + 1 + CREDIT)
                    for j in range(4 * c, min(4 * c + 4, causal_blocks(t % TILES))):
                        last = pe.transpose(T[bank][:, (j % 4) * P:(j % 4) * P + P], mixed[:, t % 2, j * P:j * P + P],
                                            core.ident[:])
                    last.then_inc(turned, 1)

            def turn_out(g, t):
                n = turn_no(g, "o", t, 0)
                bank = turn_index["o", t, 0] % 2
                pe.wait_ge(on_done, STEPS * g + t + 1 + CREDIT)
                pe.wait_ge(turned_kept, n - 2 + 1 + CREDIT)
                for j in range(KT):
                    last = pe.transpose(T[bank][:, j * P:j * P + P], on[:, t % 2, j * P:j * P + P], core.ident[:])
                last.then_inc(turned, 1)

            def values(g, t):
                pe.wait_ge(o_kept, STEPS * g + t + 1)
                n = causal_blocks(t % TILES)
                for j in range(n):
                    if j % 4 == 0:
                        pe.wait_ge(turned_kept, turn_no(g, "p", t, j // 4) + 1 + CREDIT)
                    last = pe.matmul(O, mixed_t[:, t % 2, j, :], v[:, j, :], start=(j == 0), stop=(j == n - 1))
                last.then_inc(valued, 1)

            def kv_group(g, is_last):
                for s in range(1, STEPS):
                    if s in (8, 12):
                        c = (s - 8) // 4
                        at = 6 if c == 0 else 8
                        pe.wait_ge(kept, order(g, at, PLAN[at][-1]) + 1)
                    if s == 4:
                        pe.wait_ge(kept, order(g, 3, PLAN[3][0]) + 1)
                    for m in range(MAPS):
                        scores(g, s, m)
                    turn(g, s - 1)
                    for what in PLAN.get(s, []):
                        if is_last and what[0] == 0:
                            continue
                        if s == 6 and what[3] == 0:
                            pe.wait_ge(q_loaded[1], 16 * (g + 1))
                        if s == 9:
                            pe.wait_ge(q_loaded[0], 16 * (g + 1))
                        group(what, order(g, s, what))
                    if s - 1 == 0:
                        pe.wait_ge(kept, NG * g + NF)
                    if s - 1 in (2, 4, 6):
                        at = {2: 1, 4: 4, 6: 5}[s - 1]
                        pe.wait_ge(kept, order(g, at, PLAN[at][0]) + 1)
                    values(g, s - 1)
                    if s >= 2:
                        turn_out(g, s - 2)
                if not is_last:
                    pe.wait_ge(kv_loaded, 16 * (g + 1))
                    group(PLAN[16][0], order(g, 16, PLAN[16][0]))
                turn(g, STEPS - 1)
                if not is_last:
                    group(PLAN[16][1], order(g, 16, PLAN[16][1]))
                values(g, STEPS - 1)
                if not is_last:
                    pe.wait_ge(kept, order(g, 16, PLAN[16][1]) + 1)
                    for m in range(MAPS):
                        scores(g, STEPS, m)
                    group(PLAN[16][2], order(g, 16, PLAN[16][2]))
                turn_out(g, STEPS - 2)
                turn_out(g, STEPS - 1)

            pe.sem_inc(valued, CREDIT)
            pe.sem_inc(turned, TURN_CREDIT)
            for n, what in enumerate(FIRST):
                if n == 0:
                    pe.wait_ge(core.early_in, 32)
                group(what, n)
                if n == 4:
                    pe.wait_ge(kept, 4)
                    for m in range(MAPS):
                        scores(0, 0, m)
            with pe.Fori(0, GROUPS - 1) as g:
                kv_group(g, False)
            kv_group(GROUPS - 1, True)
            pe.wait_ge(wo_scaled, 2 * GROUPS * KT)
            pe.wait_ge(turned_kept, NT * GROUPS + CREDIT)
            for i in range(TILES):
                if i >= 2:
                    pe.wait_ge(added, i - 1)
                for h in range(2 * GROUPS * KT):
                    last = pe.matmul(S[i % 2][:, 0:D], att[:, h, i * P:i * P + P], wo[:, h, :],
                                     start=(h == 0), stop=(h == 2 * GROUPS * KT - 1))
                last.then_inc(outed, 1)
                if i >= 1:
                    norm.turn(pe, i - 1, T)
            norm.turn(pe, TILES - 1, T)

        @block.scalar
        def _(act):
            act.sem_inc(exped, CREDIT)
            act.sem_inc(o_kept, 1)
            act.wait_ge(lam_step, 2)
            act.activation(lam[:, 2:4], lam[:, 0:2], ACT.Exp).then_inc(lam_exp, 1)

            def keep_k(what, n):
                b, part, c, m = what
                act.wait_ge(projected, n + 1)
                if isinstance(n, int) and 0 < n < NF:
                    act.wait_ge(kept, n)
                W = bank(n)
                act.activation(k[m][:, c * BANK:c * BANK + BANK], W, ACT.Identity,
                               bias=wkv[:, KV_BIAS + m:KV_BIAS + m + 1]).then_inc(kept, 1)

            def exps(g, s, m):
                n = causal_blocks(s % TILES) * P
                act.wait_ge(maxed, MICRO * g + MAPS * s + m + 1)
                act.wait_ge(mixed_done, STEPS * g + s - 2 + 1 + CREDIT)
                act.activation(ex[:, s % 2, m, 0:n], S[m][:, 0:n], ACT.Exp, bias=nmax[:, s % 2, m:m + 1],
                               accum_out=rsum[:, s % 2, m:m + 1]).then_inc(exped, 1)

            def keep_o(g, t):
                act.wait_ge(valued, STEPS * g + t + 1 + CREDIT)
                act.wait_ge(on_done, STEPS * g + t - 2 + 1 + CREDIT)
                act.activation(o[:, t % 2, :], O, ACT.Copy).then_inc(o_kept, 1)
                act.wait_ge(o_kept, STEPS * g + t + 1 + 1)
                act.activation(osq[:, t % 2, :], o[:, t % 2, :], ACT.Square, scale=float(VD) ** -0.5,
                               accum_out=ssq[:, t % 2:t % 2 + 1]).then_inc(squared, 1)

            def kv_group(g, is_last):
                for s in range(1, STEPS):
                    for m in range(MAPS):
                        exps(g, s, m)
                    for what in PLAN.get(s, []):
                        if what[1] == "k":
                            keep_k(what, order(g, s, what))
                    keep_o(g, s - 1)
                if not is_last:
                    for what in PLAN[16][0:2]:
                        keep_k(what, order(g, 16, what))
                keep_o(g, STEPS - 1)
                if not is_last:
                    for m in range(MAPS):
                        exps(g, STEPS, m)

            for n, what in enumerate(FIRST):
                if what[1] == "k":
                    keep_k(what, n)
            for m in range(MAPS):
                exps(0, 0, m)
            with act.Fori(0, GROUPS - 1) as g:
                kv_group(g, False)
            kv_group(GROUPS - 1, True)
            for i in range(TILES):
                norm.keep(act, i, T)

        @block.gpsimd
        def _(pool):
            pool.wait_ge(lam_loaded, 32)
            pool.wait_ge(wo_loaded, 32)
            for h in range(2 * GROUPS * KT):
                pool.tensor_scalar(wo[:, h, :], wo[:, h, :], subln[:, h % KT:h % KT + 1], 1.0 - LAMBDA_INIT,
                                   ALU.mult, ALU.mult).then_inc(wo_scaled, 1)

            with pool.Fori(0, GROUPS) as g:
                for t in range(STEPS):
                    pool.wait_ge(squared, STEPS * g + t + 1)
                    pool.tensor_tensor(mean_sq[:, t % 2:t % 2 + 1], ssq[:, t % 2:t % 2 + 1], core.eps[:],
                                       ALU.add).then_inc(meaned, 1)
                    pool.wait_ge(meaned, STEPS * g + t + 1)
                    pool.tensor_tensor(rms[:, t % 2:t % 2 + 1], mean_sq[:, t % 2:t % 2 + 1], core.half_neg[:],
                                       ALU.pow).then_inc(rms_done, 1)
            for i in range(TILES):
                norm.root(pool, i)

        @block.vector
        def _(dve):
            dve.sem_inc(turned_kept, CREDIT)
            dve.sem_inc(mixed_done, CREDIT)
            dve.sem_inc(on_done, CREDIT)
            dve.wait_ge(lam_loaded, 32)
            for j in range(2):
                dve.tensor_tensor_reduce(out=lam_rows[:, 2 * j, :], in0=lam_rows[:, 2 * j, :], in1=lam_rows[:, 2 * j + 1, :],
                                         scale=1.0, scalar=0.0, op0=ALU.mult, op1=ALU.add,
                                         accum_out=lam[:, j:j + 1]).then_inc(lam_step, 1)
            dve.wait_ge(lam_exp, 1)
            dve.tensor_tensor(lam[:, 4:5], lam[:, 3:4], lam[:, 2:3], ALU.subtract).then_inc(lam_step, 1)
            dve.wait_ge(lam_step, 3)
            dve.tensor_scalar(lam[:, 5:6], lam[:, 4:5], -LAMBDA_INIT, None, ALU.add).then_inc(lam_step, 1)
            dve.wait_ge(lam_step, 4)

            def keep(what, n):
                b, part, c, m = what
                dve.wait_ge(projected, n + 1)
                if isinstance(n, int) and 0 < n < NF:
                    dve.wait_ge(kept, n)
                W = bank(n)
                if part == "q":
                    dve.tensor_scalar(q[b][m][:, c * BANK:c * BANK + BANK], W,
                                      wq[b][:, MAPS * KT * HD + m:MAPS * KT * HD + m + 1], SCALE,
                                      ALU.add, ALU.mult).then_inc(kept, 1)
                else:
                    dve.tensor_tensor(v[:, 2 * c:2 * c + 2, :], W.rearrange("p (t d) -> p t d", t=2),
                                      wkv[:, KV_BIAS + MAPS:].rearrange("p (a d) -> p a d", a=1).to_broadcast([P, 2, VD]),
                                      ALU.add).then_inc(kept, 1)

            def maxes(g, s):
                n = causal_blocks(s % TILES) * P
                for m in range(MAPS):
                    dve.wait_ge(scored, MICRO * g + MAPS * s + m + 1)
                    dve.tensor_reduce(nmax[:, s % 2, m:m + 1], S[m][:, 0:n], AX_X, ALU.max,
                                      negate=True).then_inc(maxed, 1)

            def turned_by(g, kind, t):
                if t >= 0:
                    c = chunks[t] - 1 if kind == "p" else 0
                    return NT * g + turn_index[kind, t, c] + 1 + TURN_CREDIT
                c = chunks[t + STEPS] - 1 if kind == "p" else 0
                return NT * g + turn_index[kind, t + STEPS, c] - NT + 1 + TURN_CREDIT

            def mix(g, s):
                n = causal_blocks(s % TILES) * P
                b = s % 2
                dve.wait_ge(exped, MICRO * g + MAPS * s + 2 + CREDIT)
                dve.reciprocal(rinv[:, b, :], rsum[:, b, :]).then_inc(mix_step, 1)
                dve.wait_ge(mix_step, 3 * (STEPS * g + s) + 1)
                dve.tensor_tensor(rneg[:, b:b + 1], rinv[:, b, 1:2], lam[:, 5:6], ALU.mult).then_inc(mix_step, 1)
                dve.wait_ge(mix_step, 3 * (STEPS * g + s) + 2)
                dve.tensor_scalar(ex[:, b, 1, 0:n], ex[:, b, 1, 0:n], rneg[:, b:b + 1], None,
                                  ALU.mult).then_inc(mix_step, 1)
                dve.wait_ge(mix_step, 3 * (STEPS * g + s) + 3)
                dve.wait_ge(turned, turned_by(g, "p", s - 2))
                dve.scalar_tensor_tensor(out=mixed[:, b, 0:n], in0=ex[:, b, 0, 0:n], scalar=rinv[:, b, 0:1],
                                         in1=ex[:, b, 1, 0:n], op0=ALU.mult, op1=ALU.add).then_inc(mixed_done, 1)

            def keep_turned(g, t):
                for c in range(chunks[t]):
                    m = min(4, causal_blocks(t % TILES) - 4 * c)
                    dve.wait_ge(turned, turn_no(g, "p", t, c) + 1 + TURN_CREDIT)
                    if c == 0:
                        dve.wait_ge(valued, STEPS * g + t - 2 + 1 + CREDIT)
                    dve.tensor_copy(mixed_t[:, t % 2, 4 * c:4 * c + m, :],
                                    T[turn_index["p", t, c] % 2][:, 0:m * P].rearrange("p (t d) -> p t d", t=m)
                                    ).then_inc(turned_kept, 1)

            def scale_rows(g, t):
                dve.wait_ge(rms_done, STEPS * g + t + 1)
                dve.wait_ge(turned, turned_by(g, "o", t - 2))
                dve.tensor_scalar(on[:, t % 2, :], o[:, t % 2, :], rms[:, t % 2:t % 2 + 1], None,
                                  ALU.mult).then_inc(on_done, 1)

            def keep_out(g, t):
                dve.wait_ge(turned, turn_no(g, "o", t, 0) + 1 + TURN_CREDIT)
                i = t % TILES
                at = 2 * KT * g + KT * (t // TILES)
                dve.tensor_copy(att[:, bass.ds(at, KT), i * P:i * P + P],
                                T[turn_index["o", t, 0] % 2][:, 0:VD].rearrange("p (e d) -> p e d", e=KT)
                                ).then_inc(turned_kept, 1)

            def kv_group(g, is_last):
                for s in range(1, STEPS):
                    maxes(g, s)
                    keep_turned(g, s - 1)
                    mix(g, s)
                    for what in PLAN.get(s, []):
                        if what[1] != "k" and not (is_last and what[0] == 0):
                            keep(what, order(g, s, what))
                    if s >= 2:
                        scale_rows(g, s - 2)
                        keep_out(g, s - 2)
                keep_turned(g, STEPS - 1)
                scale_rows(g, STEPS - 2)
                if not is_last:
                    maxes(g, STEPS)
                    mix(g, STEPS)
                    keep(PLAN[16][2], order(g, 16, PLAN[16][2]))
                keep_out(g, STEPS - 2)
                scale_rows(g, STEPS - 1)
                keep_out(g, STEPS - 1)

            for n, what in enumerate(FIRST):
                if what[1] != "k":
                    keep(what, n)
            maxes(0, 0)
            mix(0, 0)
            with dve.Fori(0, GROUPS - 1) as g:
                kv_group(g, False)
            kv_group(GROUPS - 1, True)
            add_gated(dve, core, 0, bo, wo_loaded, 32, gated, bo_gated, [S[i % 2][:, 0:D] for i in range(TILES)],
                      outed, added, norm)


def swiglu(core, A, hidden, scaled, run, units_before, norm):
    nc = core.nc
    x, ht, ps = core.x, core.ht, core.ps
    sizes = [min(P, hidden - f) for f in range(0, hidden, P)]
    NF = len(sizes)
    TILES_BEFORE = TILES * run
    UNITS = [(c, f) for c in range(CHUNKS) for f in range(NF)]
    with ExitStack() as ctx:
        wg, wu, wd, *scales_of = carve(core.arena, (KT, hidden), (KT, hidden), (NF, D), *scaled * [(2, NF), (D,)])
        if scaled:
            scales, down_s = scales_of
        gate_row = core.sb("gate_row", [P, D], F32, ctx)
        sil = core.sb("sil", [P, 2, BANK], F32, ctx)
        hid = core.sb("hid", [P, CHUNKS, NF, BANK], F32, ctx)
        gated = core.sb("gated", [P, 2, D], F32, ctx)
        s = core.ffn_sems
        mod = Modulation(core, norm.layer, 6, 7)
        OUT = [ps[:, b, 0:D] for b in (4, 5)]
        turn_banks = [ps[:, b, :] for b in (6, 7)]
        block = ctx.enter_context(nc.Block(no_gpsimd_drain=True))

        @block.sync
        def _(sp):
            core.load_early(sp, A, norm.layer)
            mod.load_next(sp, A)

        @block.tensor
        def _(pe):
            def up(n):
                c, f = UNITS[n]
                m = sizes[f]
                if n >= 2:
                    pe.wait_ge(s["hid_done"], units_before + n - 1)
                for part, w in enumerate((wg, wu)):
                    for k in range(KT):
                        last = pe.matmul(ps[0:m, 2 * (n % 2) + part, :], w[:, k, f * P:f * P + m],
                                         ht[:, k, c * BANK:c * BANK + BANK], start=(k == 0), stop=(k == KT - 1))
                last.then_inc(s["upped"], 1)

            def down(c):
                pe.wait_ge(s["hid_done"], units_before + NF * (c + 1))
                for j in range(4):
                    i = 4 * c + j
                    if i >= 2:
                        pe.wait_ge(s["gated"], TILES_BEFORE + i - 1)
                    for f in range(NF):
                        m = sizes[f]
                        last = pe.matmul(OUT[i % 2], hid[0:m, c, f, j * P:j * P + P], wd[0:m, f, :],
                                         start=(f == 0), stop=(f == NF - 1))
                    last.then_inc(s["downed"], 1)
                    if c == 1:
                        for t in ((0, 1), (2, 3), (4,), (5, 6))[j]:
                            norm.turn(pe, t, turn_banks)

            mod.products(pe)
            pe.wait_ge(core.arena_in, 16 * norm.layer)
            for n in range(len(UNITS)):
                up(n)
                if n == NF + 1:
                    down(0)
            down(1)
            norm.turn(pe, TILES - 1, turn_banks)

        @block.scalar
        def _(act):
            mod.condition(act)
            if scaled:
                act.wait_ge(core.arena_in, 16 * norm.layer)
            for n, (c, f) in enumerate(UNITS):
                m = sizes[f]
                act.wait_ge(s["upped"], units_before + n + 1)
                if n >= 2:
                    act.wait_ge(s["hid_done"], units_before + n - 1)
                act.activation(sil[0:m, n % 2, :], ps[0:m, 2 * (n % 2), :], ACT.Silu,
                               scale=scales[0:m, 0, f:f + 1] if scaled else 1.0).then_inc(s["silued"], 1)
            for i in range(TILES):
                norm.keep(act, i, turn_banks)

        @block.gpsimd
        def _(pool):
            for i in range(TILES):
                norm.root(pool, i)

        @block.vector
        def _(dve):
            row = core.gate[:, 1, :]
            mod.spread(dve)
            mod.keep_cols(dve)
            mod.keep_rows(dve)
            if scaled:
                dve.wait_ge(core.arena_in, 16 * norm.layer)
                dve.tensor_tensor(gate_row[:], row, down_s[:], ALU.mult).then_inc(s["row"], 1)
                dve.wait_ge(s["row"], 1)
                row = gate_row[:]

            def hidden_unit(n):
                c, f = UNITS[n]
                m = sizes[f]
                dve.wait_ge(s["silued"], units_before + n + 1)
                if scaled:
                    dve.scalar_tensor_tensor(out=hid[0:m, c, f, :], in0=ps[0:m, 2 * (n % 2) + 1, :],
                                             scalar=scales[0:m, 1, f:f + 1], in1=sil[0:m, n % 2, :],
                                             op0=ALU.mult, op1=ALU.mult).then_inc(s["hid_done"], 1)
                else:
                    dve.tensor_tensor(hid[0:m, c, f, :], ps[0:m, 2 * (n % 2) + 1, :], sil[0:m, n % 2, :],
                                      ALU.mult).then_inc(s["hid_done"], 1)

            def add(c):
                for j in range(4):
                    i = 4 * c + j
                    dve.wait_ge(s["downed"], TILES_BEFORE + i + 1)
                    dve.tensor_tensor(gated[:, i % 2, :], OUT[i % 2], row, ALU.mult).then_inc(s["gated"], 1)
                    dve.wait_ge(s["gated"], TILES_BEFORE + i + 1)
                    dve.tensor_tensor(x[:, i, :], x[:, i, :], gated[:, i % 2, :], ALU.add).then_inc(s["added"], 1)
                    dve.wait_ge(s["added"], TILES_BEFORE + i + 1)
                    norm.stats(dve, i)
                    if c == 1:
                        norm.scale(dve, i)

            for n in range(len(UNITS)):
                hidden_unit(n)
                if n == NF + 1:
                    add(0)
            for i in range(4):
                norm.scale(dve, i)
            add(1)


def ffn_l1(core, A, norm):
    swiglu(core, A, 704, True, 0, 0, norm)


def ffn_l2(core, A, norm):
    swiglu(core, A, 1024, False, 1, 2 * len(range(0, 704, P)), norm)


def attention_l2(core, A, norm):
    nc = core.nc
    HEADS, HD = 4, 64
    STEPS = 2 * HEADS
    ROUNDS = TILES // 2
    SCALE = 0.5
    x, ht, ps = core.x, core.ht, core.ps
    with ExitStack() as ctx:
        w, bias = carve(core.early, (3, KT, D), (3, KT))
        wo = core.sb("wo", [P, KT, D], F32, ctx)
        bo = core.sb("bo", [P, D], F32, ctx)
        qt = core.sb("qt", [P, KT, TOKENS], F32, ctx)
        kt = core.sb("kt", [P, KT, TOKENS], F32, ctx)
        v = core.sb("v", [P, TILES, D], F32, ctx)
        qc = core.sb("qc", [P, 2, KT, P], F32, ctx)
        probs = core.sb("probs", [P, 2, TOKENS], F32, ctx)
        probs_t = core.sb("probs_t", [P, 2, TILES, P], F32, ctx)
        nmax = core.sb("nmax", [P, 2], F32, ctx)
        rsum = core.sb("rsum", [P, 2], F32, ctx)
        rinv = core.sb("rinv", [P, 2], F32, ctx)
        att = core.sb("att", [P, 2, KT, P], F32, ctx)
        gated = core.sb("gated", [P, 2, D], F32, ctx)
        wo_loaded = core.sem("wo_loaded", ctx)
        projected = core.sem("projected", ctx)
        kept = core.sem("kept", ctx)
        q_copied = core.sem("q_copied", ctx)
        scored = core.sem("scored", ctx)
        maxed = core.sem("maxed", ctx)
        exped = core.sem("exped", ctx)
        inverted = core.sem("inverted", ctx)
        normed = core.sem("normed", ctx)
        turned = core.sem("turned", ctx)
        turned_kept = core.sem("turned_kept", ctx)
        valued = core.sem("valued", ctx)
        att_kept = core.sem("att_kept", ctx)
        outed = core.sem("outed", ctx)
        gated_done = core.sem("gated_done", ctx)
        bo_done = core.sem("bo_done", ctx)
        CREDIT = 2
        TURN_CREDIT = 4
        S = [ps[:, 0:2, :].rearrange("p a b -> p (a b)"), ps[:, 2:4, :].rearrange("p a b -> p (a b)")]
        T = [ps[:, 4, :], ps[:, 5, :]]
        V = ps[:, 6, 0:KT * P].rearrange("p (k q) -> p k q", k=KT)
        O = ps[:, 7, 0:D]
        GROUPS = [(part, m, c) for m in range(KT) for c in range(CHUNKS) for part in (0, 1)] + [(2, c, 0) for c in range(4)]
        block = ctx.enter_context(nc.Block(no_gpsimd_drain=True))

        @block.sync
        def _(sp):
            sp.dma_start(wo[:], A["l2_wo"]).then_inc(wo_loaded, 16)
            sp.dma_start(bo[:], A["l2_bo"].to_broadcast([P, D])).then_inc(wo_loaded, 16)
            core.load_arena(sp, A, 2)

        @block.tensor
        def _(pe):
            pe.sem_inc(valued, CREDIT)
            pe.sem_inc(turned, TURN_CREDIT)
            pe.sem_inc(outed, 1)
            pe.wait_ge(core.early_in, 48)
            for n, (part, m, c) in enumerate(GROUPS):
                if n >= 4:
                    pe.wait_ge(kept, n - 3)
                W = ps[:, 4 + n % 4, :]
                if part < 2:
                    for k in range(KT):
                        last = pe.matmul(W, w[:, part, k, m * P:m * P + P], ht[:, k, c * BANK:c * BANK + BANK],
                                         start=(k == 0), stop=(k == KT - 1))
                else:
                    for j in range(2):
                        t = (2 * m + j) * P
                        for k in range(KT):
                            last = pe.matmul(W[:, j * D:j * D + D], ht[:, k, t:t + P], w[:, part, k, :],
                                             start=(k == 0), stop=(k == KT - 1))
                last.then_inc(projected, 1)
            pe.wait_ge(kept, len(GROUPS))

            def scores(g, u):
                h, slot = u % HEADS, (u // HEADS) % 2
                if h == 0:
                    pe.wait_ge(q_copied, 2 * g + u // HEADS + 1)
                pe.wait_ge(exped, STEPS * g + u - 2 + 1 + CREDIT)
                r = HD * (h % 2)
                for c in range(CHUNKS):
                    last = pe.matmul(S[u % 2][:, c * BANK:c * BANK + BANK], qc[r:r + HD, slot, h // 2, :],
                                     kt[r:r + HD, h // 2, c * BANK:c * BANK + BANK], start=True, stop=True)
                last.then_inc(scored, 1)

            def turn(g, u):
                pe.wait_ge(normed, STEPS * g + u + 1)
                for c in range(2):
                    pe.wait_ge(turned_kept, 2 * (STEPS * g + u) + c - 2 + 1 + CREDIT)
                    for j in range(4):
                        last = pe.transpose(T[c][:, j * P:j * P + P], probs[:, u % 2, (4 * c + j) * P:(4 * c + j + 1) * P],
                                            core.ident[:])
                    last.then_inc(turned, 1)

            def values(g, u):
                h = u % HEADS
                if h == 0:
                    pe.wait_ge(att_kept, 2 * g + u // HEADS + 1)
                r = HD * (h % 2)
                for j in range(TILES):
                    if j % 4 == 0:
                        pe.wait_ge(turned_kept, 2 * (STEPS * g + u) + j // 4 + 1 + CREDIT)
                    last = pe.matmul(V[r:r + HD, h // 2, :], v[:, j, h * HD:h * HD + HD], probs_t[:, u % 2, j, :],
                                     start=(j == 0), stop=(j == TILES - 1))
                last.then_inc(valued, 1)

            def out(g, t):
                pe.wait_ge(att_kept, 2 * g + t + 1 + 1)
                pe.wait_ge(gated_done, 2 * g + t + 1)
                for k in range(KT):
                    last = pe.matmul(O, att[:, t, k, :], wo[:, k, :], start=(k == 0), stop=(k == KT - 1))
                last.then_inc(outed, 1)

            def round_(g, is_last):
                for u in range(1, STEPS + 1):
                    if not (is_last and u == STEPS):
                        scores(g, u)
                    turn(g, u - 1)
                    if u == HEADS + 1:
                        out(g, 0)
                    values(g, u - 1)
                out(g, 1)

            scores(0, 0)
            pe.wait_ge(wo_loaded, 32)
            with pe.Fori(0, ROUNDS - 1) as g:
                round_(g, False)
            round_(ROUNDS - 1, True)
            for i in range(TILES):
                norm.turn(pe, i, T)

        @block.scalar
        def _(act):
            act.sem_inc(exped, CREDIT)
            act.wait_ge(core.early_in, 48)
            for n, (part, m, c) in enumerate(GROUPS):
                if part == 0:
                    continue
                act.wait_ge(projected, n + 1)
                act.wait_ge(kept, n)
                W = ps[:, 4 + n % 4, :]
                if part == 1:
                    act.activation(kt[:, m, c * BANK:c * BANK + BANK], W, ACT.Identity,
                                   bias=bias[:, 1, m:m + 1]).then_inc(kept, 1)
                else:
                    act.activation(v[:, 2 * m:2 * m + 2, :], W.rearrange("p (t d) -> p t d", t=2),
                                   ACT.Copy).then_inc(kept, 1)

            def exps(g, u):
                act.wait_ge(maxed, STEPS * g + u + 1)
                act.wait_ge(turned, 2 * (STEPS * g + u - 2) + 2 + TURN_CREDIT)
                act.activation(probs[:, u % 2, :], S[u % 2], ACT.Exp, bias=nmax[:, u % 2:u % 2 + 1],
                               accum_out=rsum[:, u % 2:u % 2 + 1]).then_inc(exped, 1)

            def keep_att(g, t):
                act.wait_ge(valued, STEPS * g + HEADS * (t + 1) + CREDIT)
                act.wait_ge(outed, 2 * g + t - 1 + 1)
                for k in range(KT):
                    last = act.activation(att[:, t, k, :], V[:, k, :], ACT.Identity, bias=bias[:, 2, k:k + 1])
                last.then_inc(att_kept, 1)

            exps(0, 0)

            def round_(g, is_last):
                for u in range(1, STEPS + 1):
                    if not (is_last and u == STEPS):
                        exps(g, u)
                    if u % HEADS == 0:
                        keep_att(g, u // HEADS - 1)

            act.sem_inc(att_kept, 1)
            with act.Fori(0, ROUNDS - 1) as g:
                round_(g, False)
            round_(ROUNDS - 1, True)
            for i in range(TILES):
                norm.keep(act, i, T)

        @block.gpsimd
        def _(pool):
            for i in range(TILES):
                norm.root(pool, i)

        @block.vector
        def _(dve):
            dve.sem_inc(turned_kept, CREDIT)
            dve.sem_inc(gated_done, 1)
            dve.wait_ge(core.early_in, 48)
            for n, (part, m, c) in enumerate(GROUPS):
                if part:
                    continue
                dve.wait_ge(projected, n + 1)
                if n > 0:
                    dve.wait_ge(kept, n)
                dve.tensor_scalar(qt[:, m, c * BANK:c * BANK + BANK], ps[:, 4 + n % 4, :], bias[:, 0, m:m + 1], SCALE,
                                  ALU.add, ALU.mult).then_inc(kept, 1)
            dve.wait_ge(wo_loaded, 32)
            dve.tensor_tensor(gated[:, 0, :], core.gate[:, 0, :], bo[:], ALU.mult).then_inc(bo_done, 1)
            dve.wait_ge(bo_done, 1)
            dve.tensor_tensor(x[:], x[:], gated[:, 0:1, :].to_broadcast([P, TILES, D]), ALU.add).then_inc(bo_done, 1)
            dve.wait_ge(bo_done, 2)
            dve.wait_ge(kept, len(GROUPS))

            def copy_q(g, t):
                tile = 2 * g + t
                at = slice(tile * P, tile * P + P) if isinstance(g, int) else bass.ds(tile * P, P)
                dve.tensor_copy(qc[:, t % 2, :, :], qt[:, :, at]).then_inc(q_copied, 1)

            def maxes(g, u):
                dve.wait_ge(scored, STEPS * g + u + 1)
                dve.tensor_reduce(nmax[:, u % 2:u % 2 + 1], S[u % 2], AX_X, ALU.max, negate=True).then_inc(maxed, 1)

            def scale_rows(g, u):
                dve.wait_ge(exped, STEPS * g + u + 1 + CREDIT)
                dve.reciprocal(rinv[:, u % 2:u % 2 + 1], rsum[:, u % 2:u % 2 + 1]).then_inc(inverted, 1)
                dve.wait_ge(inverted, STEPS * g + u + 1)
                dve.tensor_scalar(probs[:, u % 2, :], probs[:, u % 2, :], rinv[:, u % 2:u % 2 + 1], None,
                                  ALU.mult).then_inc(normed, 1)

            def keep_turned(g, u):
                for c in range(2):
                    dve.wait_ge(turned, 2 * (STEPS * g + u) + c + 1 + TURN_CREDIT)
                    if c == 0:
                        dve.wait_ge(valued, STEPS * g + u - 2 + 1 + CREDIT)
                    dve.tensor_copy(probs_t[:, u % 2, 4 * c:4 * c + 4, :],
                                    T[c].rearrange("p (t d) -> p t d", t=4)).then_inc(turned_kept, 1)

            def add(g, t):
                dve.wait_ge(outed, 2 * g + t + 1 + 1)
                dve.tensor_tensor(gated[:, t, :], O, core.gate[:, 0, :], ALU.mult).then_inc(gated_done, 1)
                dve.wait_ge(gated_done, 2 * g + t + 1 + 1)
                tile = 2 * g + t
                at = slice(tile, tile + 1) if isinstance(g, int) else bass.ds(tile, 1)
                dve.tensor_tensor(x[:, at, :], x[:, at, :], gated[:, t:t + 1, :], ALU.add).then_inc(bo_done, 1)

            def round_(g, is_last):
                for u in range(1, STEPS + 1):
                    if not (is_last and u == STEPS):
                        if u == 1:
                            copy_q(g, 1)
                        if u == HEADS + 1 and not is_last:
                            copy_q(g, 2)
                        maxes(g, u)
                    keep_turned(g, u - 1)
                    if not (is_last and u == STEPS):
                        scale_rows(g, u)
                    if is_last and u <= TILES - 2:
                        norm.stats(dve, u - 1)
                        norm.scale(dve, u - 1)
                    if u == HEADS + 1:
                        add(g, 0)
                    if is_last and u == TILES:
                        dve.wait_ge(bo_done, 2 + TILES - 1)
                        norm.stats(dve, TILES - 2)
                        norm.scale(dve, TILES - 2)
                add(g, 1)
                if is_last:
                    dve.wait_ge(bo_done, 2 + TILES)
                    norm.stats(dve, TILES - 1)
                    norm.scale(dve, TILES - 1)

            copy_q(0, 0)
            maxes(0, 0)
            scale_rows(0, 0)
            with dve.Fori(0, ROUNDS - 1) as g:
                round_(g, False)
            round_(ROUNDS - 1, True)


ROUND = 1.5 * 2.0 ** 23
TURN = 6.283185
FRAME = 64


def recurrence_l3(core, A, norm):
    nc = core.nc
    x, ht, ps = core.x, core.ht, core.ps
    FRAMES = TOKENS // FRAME
    with ExitStack() as ctx:
        def buf(name, shape=(P, TOKENS), dt=F32):
            return core.sb("r_" + name, list(shape), dt, ctx)

        w_in, w_g, cols = carve(core.early, (KT, D), (2, KT, P), (6,))
        w_out = buf("w_out", (P, KT, D))
        b_out = buf("b_out", (P, D))
        xh = buf("xh", (P, KT, TOKENS))
        gx = buf("gx")
        ga = buf("ga")
        c = buf("c", (P, 16))
        r1 = buf("r1")
        r2 = buf("r2")
        th = buf("th")
        keep = buf("keep")
        phi = buf("phi")
        ends = buf("ends", (P, FRAMES))
        ends_k = buf("ends_k", (P, FRAMES))
        ends_f = buf("ends_f", (P, FRAMES))
        base = buf("base", (P, FRAMES + 1))
        ones = buf("ones", (P, FRAMES))
        f1 = buf("f1")
        f2 = buf("f2")
        k1 = buf("k1")
        k2 = buf("k2")
        sin1 = buf("sin1")
        cos1 = buf("cos1")
        sin2 = buf("sin2")
        cos2 = buf("cos2")
        zr = buf("zr")
        zi = buf("zi")
        m1 = buf("m1")
        m2 = buf("m2")
        sr = buf("sr")
        si = buf("si")
        h = buf("h", (P, KT, TOKENS))
        gated = buf("gated", (P, 2, D))
        out_loaded = core.sem("r_out_loaded", ctx)
        projected = core.sem("r_projected", ctx)
        kept = core.sem("r_kept", ctx)
        gates = core.sem("r_gates", ctx)
        gated_act = core.sem("r_gated_act", ctx)
        step = core.sem("r_step", ctx)
        c_ready = core.sem("r_c_ready", ctx)
        a_exp = core.sem("r_a_exp", ctx)
        decayed = core.sem("r_decayed", ctx)
        angle = core.sem("r_angle", ctx)
        waved = core.sem("r_waved", ctx)
        squared = core.sem("r_squared", ctx)
        rooted = core.sem("r_rooted", ctx)
        half_done = core.sem("r_half", ctx)
        ready = core.sem("r_ready", ctx)
        keep_done = core.sem("r_keep", ctx)
        outed = core.sem("r_outed", ctx)
        added = core.sem("r_added", ctx)
        bo_done = core.sem("r_bo", ctx)
        turn_banks = [ps[:, b, :] for b in (4, 5)]
        block = ctx.enter_context(nc.Block(no_gpsimd_drain=True))

        @block.sync
        def _(sp):
            sp.dma_start(w_out[:], A["l3_wout"]).then_inc(out_loaded, 16)
            sp.dma_start(b_out[:], A["l3_bout"].to_broadcast([P, D])).then_inc(out_loaded, 16)
            core.load_arena(sp, A, 3)

        @block.gpsimd
        def _(pool):
            pool.memset(keep[:], 1.0).then_inc(keep_done, 1)
            pool.wait_ge(keep_done, 1)
            pool.memset(keep[:].rearrange("p (f n) -> p f n", n=FRAME)[:, :, 0:1], 0.0).then_inc(keep_done, 1)
            pool.memset(ones[:], 1.0).then_inc(keep_done, 1)
            pool.memset(base[:], 0.0).then_inc(keep_done, 1)
            for i in range(TILES):
                norm.root(pool, i)

        @block.tensor
        def _(pe):
            pe.wait_ge(core.early_in, 64)
            for m in range(KT):
                for n in range(CHUNKS):
                    for k in range(KT):
                        last = pe.matmul(ps[:, 2 * m + n, :], w_in[:, k, m * P:m * P + P],
                                         ht[:, k, n * BANK:n * BANK + BANK], start=(k == 0), stop=(k == KT - 1))
                    last.then_inc(projected, 1)
            pe.wait_ge(kept, KT)
            for g in (1, 0):
                for n in range(CHUNKS):
                    for k in range(KT):
                        last = pe.matmul(ps[:, 4 + 2 * g + n, :], w_g[:, g, k, :], xh[:, k, n * BANK:n * BANK + BANK],
                                         start=(k == 0), stop=(k == KT - 1))
                last.then_inc(gates, 1)
            pe.wait_ge(out_loaded, 32)
            pe.wait_ge(ready, 2)
            for i in range(TILES):
                for k in range(KT):
                    last = pe.matmul(ps[:, i % 4, 0:D], h[:, k, i * P:i * P + P], w_out[:, k, :],
                                     start=(k == 0), stop=(k == KT - 1))
                last.then_inc(outed, 1)
                if 3 <= i < TILES - 1:
                    pe.wait_ge(added, i - 2)
                if i >= 1:
                    norm.turn(pe, i - 1, turn_banks)
            norm.turn(pe, TILES - 1, turn_banks)

        @block.scalar
        def _(act):
            for m in range(KT):
                act.wait_ge(projected, 2 * m + 2)
                act.activation(xh[:, m, :], ps[:, 2 * m:2 * m + 2, :].rearrange("p a b -> p (a b)"), ACT.Identity,
                               bias=cols[:, m:m + 1]).then_inc(kept, 1)
            act.wait_ge(gates, 1)
            act.activation(ga[:], ps[:, 6:8, :].rearrange("p a b -> p (a b)"), ACT.Sigmoid,
                           bias=cols[:, 3:4]).then_inc(gated_act, 1)
            act.wait_ge(gates, 2)
            act.activation(gx[:], ps[:, 4:6, :].rearrange("p a b -> p (a b)"), ACT.Sigmoid,
                           bias=cols[:, 2:3]).then_inc(gated_act, 1)
            act.wait_ge(c_ready, 1)
            act.activation(c[:, 2:3], c[:, 1:2], ACT.Exp, scale=-1.0).then_inc(a_exp, 1)
            act.wait_ge(c_ready, 2)
            act.activation(r2[:], ga[:], ACT.Exp, scale=c[:, 8:9]).then_inc(decayed, 1)
            act.activation(r1[:], ga[:], ACT.Exp, scale=c[:, 9:10]).then_inc(decayed, 1)
            for n, (dst, src) in enumerate(((cos2, f2), (sin2, f1))):
                act.wait_ge(angle, n + 1)
                act.activation(dst[:], src[:], ACT.Sin, scale=TURN).then_inc(waved, 1)
            act.wait_ge(squared, 1)
            act.activation(m2[:], m1[:], ACT.Sqrt).then_inc(rooted, 1)
            act.wait_ge(half_done, 1)
            act.activation(sr[:], k1[:], ACT.Sqrt, scale=0.5).then_inc(rooted, 1)
            for n, (dst, src) in enumerate(((cos1, f2), (sin1, f1))):
                act.wait_ge(angle, n + 3)
                act.activation(dst[:], src[:], ACT.Sin, scale=TURN).then_inc(waved, 1)
            for i in range(TILES):
                norm.keep(act, i, turn_banks)

        @block.vector
        def _(dve):
            done = [0]

            def after(ins):
                ins.then_inc(step, 1)
                done[0] += 1
                dve.wait_ge(step, done[0])

            TT, TS, STT = dve.tensor_tensor, dve.tensor_scalar, dve.scalar_tensor_tensor
            dve.wait_ge(core.early_in, 64)
            a_re, a_im = cols[:, 4:5], cols[:, 5:6]
            after(TS(c[:, 0:1], a_re, -1.0, None, ALU.mult))
            dve.tensor_tensor(c[:, 1:2], c[:, 0:1], a_re, ALU.max).then_inc(c_ready, 1)
            after(TS(c[:, 3:4], a_re, 0.0, None, ALU.max))
            dve.wait_ge(a_exp, 1)
            after(TS(c[:, 4:5], c[:, 2:3], 2.0, None, ALU.add))
            after(dve.reciprocal(c[:, 4:5], c[:, 4:5]))
            after(TT(c[:, 5:6], c[:, 2:3], c[:, 4:5], ALU.mult))
            after(TT(c[:, 6:7], c[:, 5:6], c[:, 5:6], ALU.mult))
            after(TS(c[:, 7:8], c[:, 6:7], 1.0 / 17, 1.0 / 15, ALU.mult, ALU.add))
            for odd in (13, 11, 9, 7, 5, 3, 1):
                after(TT(c[:, 7:8], c[:, 7:8], c[:, 6:7], ALU.mult))
                after(TS(c[:, 7:8], c[:, 7:8], 1.0 / odd, None, ALU.add))
            after(TT(c[:, 7:8], c[:, 7:8], c[:, 5:6], ALU.mult))
            after(STT(out=c[:, 7:8], in0=c[:, 7:8], scalar=2.0, in1=c[:, 3:4], op0=ALU.mult, op1=ALU.add))
            after(TS(c[:, 8:9], c[:, 7:8], -16.0, None, ALU.mult))
            TS(c[:, 9:10], c[:, 7:8], -8.0, None, ALU.mult).then_inc(c_ready, 1)
            after(TS(c[:, 10:11], a_im, 1.0 / float(np.pi), None, ALU.mult))
            after(TS(c[:, 11:12], a_im, 0.5 / float(np.pi), None, ALU.mult))

            def reduce(f, k, src, quarter):
                if quarter:
                    after(TS(f[:], src, 0.25, None, ALU.add))
                    src = f[:]
                after(TS(k[:], src, ROUND, -ROUND, ALU.add, ALU.add))
                TT(f[:], src, k[:], ALU.subtract).then_inc(angle, 1)

            dve.wait_ge(gated_act, 1)
            after(TS(th[:], ga[:], c[:, 10:11], None, ALU.mult))
            reduce(f2, k2, th[:], True)
            reduce(f1, k1, th[:], False)
            after(TS(m1[:], ga[:], c[:, 11:12], None, ALU.mult))
            dve.wait_ge(keep_done, 4)
            after(dve.tensor_tensor_scan(phi[:], keep[:], m1[:], 0.0, ALU.mult, ALU.add))
            ph3 = phi[:].rearrange("p (f n) -> p f n", n=FRAME)
            after(dve.tensor_copy(ends[:], ph3[:, :, FRAME - 1]))
            after(TS(ends_k[:], ends[:], ROUND, -ROUND, ALU.add, ALU.add))
            after(TT(ends_f[:], ends[:], ends_k[:], ALU.subtract))
            after(dve.tensor_tensor_scan(base[:, 1:FRAMES + 1], ones[:], ends_f[:], 0.0, ALU.mult, ALU.add))
            after(TT(ph3, ph3, base[:, 0:FRAMES].rearrange("p (f a) -> p f a", a=1).to_broadcast([P, FRAMES, FRAME]), ALU.add))
            dve.wait_ge(gated_act, 2)
            after(TT(xh[:, 0, :], xh[:, 0, :], gx[:], ALU.mult))
            after(TT(xh[:, 1, :], xh[:, 1, :], gx[:], ALU.mult))
            dve.wait_ge(waved, 2)
            dve.wait_ge(decayed, 1)
            after(TT(zr[:], r2[:], cos2[:], ALU.mult))
            after(TS(zr[:], zr[:], -1.0, 1.0, ALU.mult, ALU.add))
            after(STT(out=zi[:], in0=r2[:], scalar=-1.0, in1=sin2[:], op0=ALU.mult, op1=ALU.mult))
            after(TT(m1[:], zr[:], zr[:], ALU.mult))
            after(TT(m2[:], zi[:], zi[:], ALU.mult))
            after(TT(m1[:], m1[:], m2[:], ALU.add))
            TS(m1[:], m1[:], 1e-30, None, ALU.max).then_inc(squared, 1)
            dve.wait_ge(rooted, 1)
            TT(k1[:], m2[:], zr[:], ALU.add).then_inc(half_done, 1)
            reduce(f2, k2, phi[:], True)
            reduce(f1, r2, phi[:], False)
            dve.wait_ge(rooted, 2)
            after(dve.reciprocal(m1[:], sr[:]))
            after(STT(out=si[:], in0=zi[:], scalar=0.5, in1=m1[:], op0=ALU.mult, op1=ALU.mult))

            def product(outr, outi, ar, ai, br, bi, conj):
                after(TT(m1[:], ar, br, ALU.mult))
                after(TT(m2[:], ai, bi, ALU.mult))
                after(TT(outr, m1[:], m2[:], ALU.add if conj else ALU.subtract))
                after(TT(m1[:], ai, br, ALU.mult))
                after(TT(m2[:], ar, bi, ALU.mult))
                return TT(outi, m1[:], m2[:], ALU.subtract if conj else ALU.add)

            after(product(zr[:], zi[:], xh[:, 0, :], xh[:, 1, :], sr[:], si[:], False))
            dve.wait_ge(waved, 4)
            after(product(k1[:], k2[:], zr[:], zi[:], cos1[:], sin1[:], True))
            dve.wait_ge(decayed, 2)
            after(dve.tensor_tensor_scan(f1[:], r1[:], k1[:], 0.0, ALU.mult, ALU.add))
            after(dve.tensor_tensor_scan(f2[:], r1[:], k2[:], 0.0, ALU.mult, ALU.add))
            product(h[:, 0, :], h[:, 1, :], f1[:], f2[:], cos1[:], sin1[:], False).then_inc(ready, 2)
            add_gated(dve, core, 0, b_out, out_loaded, 32, gated, bo_done, [ps[:, i % 4, 0:D] for i in range(TILES)],
                      outed, added, norm)


def lora_l3(core, A):
    nc = core.nc
    x, ht, ps = core.x, core.ht, core.ps
    E, R = 8, 16
    SCALING = 32.0 / R
    with ExitStack() as ctx:
        w_a, w_base, w_b, b_base = carve(core.arena, (KT, P + E), (KT, D), (D,), (D,))
        iota = core.sb("iota", [P, E], F32, ctx)
        logit = core.sb("logit", [P, TILES, E], F32, ctx)
        best = core.sb("best", [P, TILES, 8], F32, ctx)
        which = core.sb("which", [P, TILES, 8], U32, ctx)
        which_f = core.sb("which_f", [P, TILES], F32, ctx)
        hot = core.sb("hot", [P, TILES, E], F32, ctx)
        picked = core.sb("l_picked", [P, TILES, P], F32, ctx)
        inner = core.sb("inner", [P, TILES, P], F32, ctx)
        gated = core.sb("gated", [P, 2, D], F32, ctx)
        iota_done = core.sem("iota_done", ctx)
        routed = core.sem("routed", ctx)
        step = core.sem("l_step", ctx)
        picked_done = core.sem("picked_done", ctx)
        turned = core.sem("l_turned", ctx)
        inner_kept = core.sem("inner_kept", ctx)
        outed = core.sem("l_outed", ctx)
        added = core.sem("l_added", ctx)
        bo_done = core.sem("l_bo", ctx)
        IN = [ps[:, i // 3, (i % 3) * (P + E):(i % 3 + 1) * (P + E)] for i in range(TILES)]
        block = ctx.enter_context(nc.Block(no_gpsimd_drain=True))

        @block.gpsimd
        def _(pool):
            pool.iota(iota[:], pattern=[[1, E]], base=0, channel_multiplier=0,
                      allow_small_or_imprecise_dtypes=True).then_inc(iota_done, 1)

        @block.tensor
        def _(pe):
            pe.wait_ge(core.arena_in, 64)
            for i in range(TILES):
                for k in range(KT):
                    last = pe.matmul(IN[i], ht[:, k, i * P:i * P + P], w_a[:, k, :], start=(k == 0), stop=(k == KT - 1))
                if i % 3 == 2 or i == TILES - 1:
                    last.then_inc(routed, 1)
            for i in range(TILES):
                pe.wait_ge(picked_done, i + 1)
                if i >= 2:
                    pe.wait_ge(inner_kept, i - 1)
                pe.transpose(ps[:, 3 + i % 2, 0:P], picked[:, i, :], core.ident[:]).then_inc(turned, 1)
            for i in range(TILES):
                if i >= 2:
                    pe.wait_ge(added, i - 1)
                out = ps[:, 5 + i % 2, 0:D]
                for k in range(KT):
                    pe.matmul(out, ht[:, k, i * P:i * P + P], w_base[:, k, :], start=(k == 0), stop=False)
                pe.wait_ge(inner_kept, i + 1)
                pe.matmul(out, inner[:, i, :], w_b[:], start=False, stop=True).then_inc(outed, 1)

        @block.scalar
        def _(act):
            for i in range(TILES):
                act.wait_ge(turned, i + 1)
                act.activation(inner[:, i, :], ps[:, 3 + i % 2, 0:P], ACT.Copy).then_inc(inner_kept, 1)

        @block.vector
        def _(dve):
            done = [0]

            def after(ins):
                ins.then_inc(step, 1)
                done[0] += 1
                dve.wait_ge(step, done[0])

            for i in range(TILES):
                dve.wait_ge(routed, i // 3 + 1)
                last = dve.tensor_copy(logit[:, i, :], IN[i][:, P:P + E])
            after(last)
            for i in range(TILES):
                last = dve.max(best[:, i, :], logit[:, i, :])
            after(last)
            for i in range(TILES):
                last = dve.max_index(which[:, i, :], best[:, i, :], logit[:, i, :])
            after(last)
            after(dve.tensor_copy(which_f[:], which[:, :, 0]))
            dve.wait_ge(iota_done, 1)
            after(dve.tensor_tensor(hot[:], which_f[:].rearrange("p (t a) -> p t a", a=1).to_broadcast([P, TILES, E]),
                                    iota[:].rearrange("p (a e) -> p a e", a=1).to_broadcast([P, TILES, E]), ALU.is_equal))
            after(dve.tensor_scalar(hot[:], hot[:], SCALING, None, ALU.mult))
            for i in range(TILES):
                dve.tensor_tensor(picked[:, i, :].rearrange("p (e r) -> p e r", e=E),
                                  IN[i][:, 0:P].rearrange("p (e r) -> p e r", e=E),
                                  hot[:, i, :].rearrange("p (e a) -> p e a", a=1).to_broadcast([P, E, R]),
                                  ALU.mult).then_inc(picked_done, 1)
            add_gated(dve, core, 1, b_base, core.arena_in, 64, gated, bo_done, [ps[:, 5 + i % 2, 0:D] for i in range(TILES)],
                      outed, added, None)


def pack(inputs):
    a = {k: np.asarray(v) for k, v in inputs.items()}
    out = {}
    c = np.stack([a[f"L{i}_c"].reshape(KT, P) for i in range(LAYERS)])
    out["cond"] = c.transpose(2, 0, 1)
    for i in range(LAYERS):
        out[f"wmod{i}"] = rows_by_partition(a[f"L{i}_wmod"])
    out["x"] = a["L0_attn_query"].reshape(TILES, P, D).transpose(1, 0, 2)
    heads, hd = 16, 128
    w = np.stack([a[f"L0_attn_w_{n}"].reshape(KT, P, heads, hd) for n in "qkv"]).transpose(3, 2, 0, 1, 4)
    b = [a[f"L0_attn_b_{n}"].reshape(heads, hd, 1) for n in "qk"]
    out["l0_wqkv"] = np.concatenate([w.reshape(heads, P, -1), *b], axis=2)
    out["l0_bv"] = a["L0_attn_b_v"].reshape(heads, hd).T
    out["l0_wo"] = a["L0_attn_w_o"].reshape(heads, hd, D).transpose(1, 0, 2)
    out["l0_bo"] = a["L0_attn_b_o"].reshape(1, D)
    out["early0"] = beside(out["l0_wqkv"][0], out["l0_wqkv"][1])
    out["arena0"] = beside(rows_by_partition(a["L0_ffn_gate_w"].T), on_all(a["L0_ffn_gate_bias"]),
                           *(rows_by_partition(a[f"L0_ffn_shared_{n}"]) for n in ("gate", "up", "down")))
    w13 = np.stack([a["L0_ffn_w1"], a["L0_ffn_w3"]]).reshape(2, 16, 2, KT, P, 128).transpose(1, 4, 2, 0, 3, 5)
    w2 = a["L0_ffn_w2"].reshape(16, 2, 128, D).transpose(0, 2, 1, 3)
    out["l0_wexp"] = np.concatenate([w13.reshape(16, P, -1), w2.reshape(16, P, -1)], axis=2)
    groups, maps, hd = 4, 2, 128
    w, b = a["L1_attn_Wqkv_w"], a["L1_attn_Wqkv_b"]
    nq, nk = 16 * hd, 8 * hd
    wq = w[:nq].reshape(8, maps, hd, KT, P).transpose(0, 4, 1, 3, 2).reshape(8, P, -1)
    bq = b[:nq].reshape(8, maps, hd).transpose(0, 2, 1)
    out["l1_wq"] = np.concatenate([wq, bq], axis=2)
    wk = w[nq:nq + nk].reshape(groups, maps, hd, KT, P).transpose(0, 4, 1, 3, 2).reshape(groups, P, -1)
    bk = b[nq:nq + nk].reshape(groups, maps, hd).transpose(0, 2, 1)
    wv = w[nq + nk:].reshape(groups, 2 * hd, KT, P).transpose(0, 3, 2, 1).reshape(groups, P, -1)
    bv = np.broadcast_to(b[nq + nk:].reshape(groups, 1, 2 * hd), (groups, P, 2 * hd))
    out["l1_wkv"] = np.concatenate([wk, wv, bk, bv], axis=2)
    out["early1"] = beside(out["l1_wkv"][0], out["l1_wq"][0])
    out["l1_lambda"] = np.concatenate([a[f"L1_attn_lambda_{n}"] for n in ("q1", "k1", "q2", "k2")]).reshape(1, -1)
    out["l1_subln"] = a["L1_attn_subln_w"].reshape(KT, P).T
    out["l1_wo"] = rows_by_partition(a["L1_attn_out_w"].T)
    out["l1_bo"] = a["L1_attn_out_b"].reshape(1, D)
    inter = a["L1_ffn_gate_w"].shape[0]
    full = -(-inter // P) * P
    wd = np.pad(a["L1_ffn_down_w"].T, ((0, full - inter), (0, 0)))
    s = np.stack([np.pad(a[f"L1_ffn_{n}_s"], (0, full - inter)) for n in ("gate", "up")])
    out["arena1"] = beside(rows_by_partition(a["L1_ffn_gate_w"].T), rows_by_partition(a["L1_ffn_up_w"].T),
                           rows_by_partition(wd), s.reshape(2, -1, P).transpose(2, 0, 1), on_all(a["L1_ffn_down_s"]))
    out["early2"] = beside(*(rows_by_partition(a[f"L2_attn_W{n}"]) for n in "qkv"),
                           np.stack([a[f"L2_attn_b{n}"].reshape(KT, P) for n in "qkv"]).transpose(2, 0, 1))
    out["l2_wo"] = rows_by_partition(a["L2_attn_Wo"])
    out["l2_bo"] = a["L2_attn_bo"].reshape(1, D)
    out["arena2"] = beside(*(rows_by_partition(a[f"L2_ffn_w_{n}"].T) for n in ("gate", "up", "down")))
    wg = np.zeros((2, D, P), a["L3_attn_W_gx"].dtype)
    for g, n in enumerate(("x", "a")):
        blocks, rows, cols = a[f"L3_attn_W_g{n}"].shape
        for b in range(blocks):
            wg[g, b * rows:(b + 1) * rows, b * cols:(b + 1) * cols] = a[f"L3_attn_W_g{n}"][b]
    cols = np.stack([a["L3_attn_b_in"][:P], a["L3_attn_b_in"][P:], a["L3_attn_b_gx"].reshape(-1),
                     a["L3_attn_b_ga"].reshape(-1), a["L3_attn_a_real"], a["L3_attn_a_imag"]], axis=1)
    out["early3"] = beside(rows_by_partition(a["L3_attn_W_in"]), wg.reshape(2, KT, P, P).transpose(2, 0, 1, 3), cols)
    out["l3_wout"] = rows_by_partition(a["L3_attn_W_out"])
    out["l3_bout"] = a["L3_attn_b_out"].reshape(1, D)
    inner = np.concatenate([a["L3_ffn_A"].reshape(P, D), a["L3_ffn_router_W"]])
    out["arena3"] = beside(rows_by_partition(inner.T), rows_by_partition(a["L3_ffn_W_base"].T),
                           a["L3_ffn_Bw"].transpose(0, 2, 1).reshape(P, D), on_all(a["L3_ffn_b_base"]))
    return {k: np.ascontiguousarray(v) for k, v in out.items()}


def beside(*parts):
    return np.concatenate([p.reshape(P, -1) for p in parts], axis=1)


def on_all(row):
    return np.broadcast_to(row.reshape(1, -1), (P, row.size))


def rows_by_partition(w):
    return w.reshape(-1, P, w.shape[1]).transpose(1, 0, 2)


def adaln_stack(nc, A, out):
    attention = (attention_l0, attention_l1, attention_l2, recurrence_l3)
    ffn = (moe, ffn_l1, ffn_l2)
    with ExitStack() as ctx:
        core = Core(nc, ctx)
        start(core, A)
        for layer in range(LAYERS):
            core.use_layer(layer)
            attention[layer](core, A, Norm(core, 2 * layer + 1))
            if layer + 1 < LAYERS:
                ffn[layer](core, A, Norm(core, 2 * layer + 2))
            else:
                lora_l3(core, A)
        with nc.Block(no_gpsimd_drain=True) as block:
            @block.sync
            def _(sp):
                sp.dma_start(out.rearrange("a (t p) d -> p (a t) d", p=P), core.x[:]).then_inc(core.s_x, 16)
                sp.wait_ge(core.s_x, 32)


def kernel(**inputs):
    import concourse.bacc as bacc
    from concourse.bass_utils import run_bass_kernel_spmd

    nc = bacc.Bacc("TRN2", target_bir_lowering=False, num_devices=1)
    arrays = {f"in_{name}": array for name, array in pack(inputs).items()}
    A = {name[3:]: nc.dram_tensor(name, array.shape, mybir.dt.from_np(array.dtype), kind="ExternalInput").ap()
         for name, array in arrays.items()}
    out = nc.dram_tensor("out", (1, TOKENS, D), F32, kind="ExternalOutput").ap()
    adaln_stack(nc, A, out)
    r = run_bass_kernel_spmd(nc, [arrays], core_ids=[0])
    return r.results[0]["out"]
```

```python
from contextlib import ExitStack

import numpy as np

import concourse.bass as bass
from concourse import mybir

F32 = mybir.dt.float32
BF16 = mybir.dt.bfloat16
F32R = mybir.dt.float32r
U32 = mybir.dt.uint32
I32 = mybir.dt.int32
ALU = mybir.AluOpType
ACT = mybir.ActivationFunctionType
AX_X = mybir.AxisListType.X

P = 128
TOKENS = 1024
TILES = TOKENS // P
D = 256
KT = D // P
BANK = 512
CHUNKS = TOKENS // BANK
LN_EPS = 1e-5
LAYERS = 4


EARLY = 1796
ARENA = 6144


def carve(base, *shapes):
    at, parts = 0, []
    for shape in shapes:
        n = int(np.prod(shape))
        part = base[:, at:at + n]
        at += n
        if len(shape) == 2:
            part = part.rearrange("p (a b) -> p a b", a=shape[0])
        elif len(shape) == 3:
            part = part.rearrange("p (a b c) -> p a b c", a=shape[0], b=shape[1])
        parts.append(part)
    return parts


class Core:

    def __init__(self, nc, ctx):
        self.nc = nc
        self.ctx = ctx
        self.taken = {}
        sb, ps = self.sb, self.psum
        self.ps = ps("acc", [P, 8, BANK], F32)
        self.x = sb("x", [P, TILES, D], F32)
        self.ht = sb("ht", [P, KT, TOKENS], F32)
        self.xn = sb("xn", [P, TILES, D], F32)
        self.ident = sb("ident", [P, P], F32)
        self.ident_bf = sb("ident_bf", [P, P], BF16)
        self.causal_bf = sb("causal_bf", [P, P], BF16)
        self.eps = sb("eps", [P, 1], F32)
        self.half_neg = sb("half_neg", [P, 1], F32)
        self.modcs = [sb(f"modc{b}", [P, 4, KT], F32) for b in range(2)]
        self.gates = [sb(f"gate{b}", [P, 2, D], F32) for b in range(2)]
        self.use_layer(0)
        self.early = sb("early", [P, EARLY], F32)
        self.arena = sb("arena", [P, ARENA], F32)
        self.early_in = self.sem("early_in")
        self.arena_in = self.sem("arena_in")
        self.wmod = sb("wmod", [P, KT, 6 * D], F32)
        self.craw = sb("craw", [P, LAYERS, KT], F32)
        self.stats = sb("stats", [P, TILES, 6], F32)
        self.mv = sb("mv", [P, TILES, 2], F32)
        self.veps = sb("veps", [P, TILES], F32)
        self.rstd = sb("rstd", [P, TILES], F32)
        self.sc = sb("sc", [P, KT], F32)
        self.scb = sb("scb", [P, KT, P], F32)
        self.sgn = sb("sgn", [P, 2 * D], F32)
        self.s_wmod = self.sem("s_wmod")
        self.s_x = self.sem("s_x")
        self.norm_sems = {key: self.sem("norm_" + key) for key in
                          ("stats", "mv", "veps", "rstd", "xn", "transposed", "ht_kept",
                           "sc", "scb", "cols", "modc", "rows", "gate")}
        self.ffn_sems = {key: self.sem("ffn_" + key) for key in
                         ("upped", "silued", "hid_done", "downed", "gated", "added",
                          "rounded", "rest_done")}

    def use_layer(self, layer):
        self.modc = self.modcs[layer % 2]
        self.gate = self.gates[layer % 2]

    def load_early(self, sp, A, layer):
        src = A[f"early{layer}"]
        sp.dma_start(self.early[:, 0:src.shape[1]], src).then_inc(self.early_in, 16)

    def load_arena(self, sp, A, layer):
        src = A[f"arena{layer}"]
        sp.dma_start(self.arena[:, 0:src.shape[1]], src).then_inc(self.arena_in, 16)

    def unique(self, name):
        self.taken[name] = self.taken.get(name, 0) + 1
        return name if self.taken[name] == 1 else f"{name}_{self.taken[name]}"

    def sb(self, name, shape, dt, ctx=None):
        return (ctx or self.ctx).enter_context(self.nc.sbuf_tensor(self.unique(name), shape, dt))

    def psum(self, name, shape, dt):
        return self.ctx.enter_context(self.nc.psum_tensor(name, shape, dt))

    def sem(self, name, ctx=None):
        return (ctx or self.ctx).enter_context(self.nc.semaphore(self.unique(name)))


MASKED = -1.0e10
SHIFT_A, SCALE_A, GATE_A, SHIFT_B, SCALE_B, GATE_B = range(6)


class Norm:

    def __init__(self, core, n):
        self.core, self.n, self.s = core, n, core.norm_sems
        self.layer, self.which = divmod(n, 2)

    def count(self, i):
        return TILES * self.n + i + 1

    def stats(self, dve, i):
        core, s = self.core, self.s
        dve.bn_stats(core.stats[:, i, :], core.x[:, i, :]).then_inc(s["stats"], 1)
        dve.wait_ge(s["stats"], self.count(i))
        dve.bn_aggr(core.mv[:, i, :], core.stats[:, i, :]).then_inc(s["mv"], 1)
        dve.wait_ge(s["mv"], self.count(i))
        dve.tensor_scalar(core.veps[:, i:i + 1], core.mv[:, i, 1:2], LN_EPS, None, ALU.add).then_inc(s["veps"], 1)

    def root(self, pool, i):
        core, s = self.core, self.s
        pool.wait_ge(s["veps"], self.count(i))
        pool.tensor_tensor(core.rstd[:, i:i + 1], core.veps[:, i:i + 1], core.half_neg[:],
                           ALU.pow).then_inc(s["rstd"], 1)

    def scale(self, dve, i):
        core, s = self.core, self.s
        dve.wait_ge(s["rstd"], self.count(i))
        dve.tensor_scalar(core.xn[:, i, :], core.x[:, i, :], core.mv[:, i, 0:1], core.rstd[:, i:i + 1],
                          ALU.subtract, ALU.mult).then_inc(s["xn"], 1)

    def turn(self, pe, i, banks):
        core, s = self.core, self.s
        pe.wait_ge(s["xn"], self.count(i))
        if i >= 2:
            pe.wait_ge(s["ht_kept"], self.count(i - 2))
        for k in range(KT):
            last = pe.transpose(banks[i % 2][:, k * P:k * P + P], core.xn[:, i, k * P:k * P + P], core.ident[:])
        last.then_inc(s["transposed"], 1)

    def keep(self, act, i, banks):
        core, s = self.core, self.s
        modc = core.modcs[self.layer % 2]
        if i == 0 and self.which == 0:
            act.wait_ge(s["modc"], 2 * (self.layer + 1))
        act.wait_ge(s["transposed"], self.count(i))
        for k in range(KT):
            last = act.activation(core.ht[:, k, i * P:i * P + P], banks[i % 2][:, k * P:k * P + P], ACT.Identity,
                                  scale=modc[:, 2 * self.which, k:k + 1], bias=modc[:, 2 * self.which + 1, k:k + 1])
        last.then_inc(s["ht_kept"], 1)


class Modulation:

    def __init__(self, core, layer, cols_bank, rows_bank):
        self.core, self.layer, self.s = core, layer, core.norm_sems
        self.cols = core.ps[:, cols_bank, 0:4 * KT].rearrange("p (v k) -> p v k", v=4)
        self.rows = core.ps[:, rows_bank, :]

    def condition(self, act):
        act.wait_ge(self.core.s_x, 32)
        act.activation(self.core.sc[:], self.core.craw[:, self.layer, :], ACT.Silu).then_inc(self.s["sc"], 1)

    def products(self, pe):
        core, s, cols, rows = self.core, self.s, self.cols, self.rows
        pe.wait_ge(s["sc"], self.layer + 1)
        pe.wait_ge(core.s_wmod, 16 * (self.layer + 1))
        for v, part in enumerate((SHIFT_A, SCALE_A, SHIFT_B, SCALE_B)):
            for m in range(KT):
                for k in range(KT):
                    last = pe.matmul(cols[:, v, m:m + 1], core.wmod[:, k, part * D + m * P:part * D + m * P + P],
                                     core.sc[:, k:k + 1], start=(k == 0), stop=(k == KT - 1))
        last.then_inc(s["cols"], 1)
        pe.wait_ge(s["scb"], KT * (self.layer + 1))
        for g, part in enumerate((GATE_A, GATE_B)):
            for k in range(KT):
                last = pe.matmul(rows[:, g * D:g * D + D], core.scb[:, k, :], core.wmod[:, k, part * D:part * D + D],
                                 start=(k == 0), stop=(k == KT - 1))
        last.then_inc(s["rows"], 1)

    def spread(self, dve):
        core, s = self.core, self.s
        dve.wait_ge(s["sc"], self.layer + 1)
        for k in range(KT):
            dve.tensor_copy(core.scb[:, k, :], core.sc[:, k:k + 1].to_broadcast([P, P])).then_inc(s["scb"], 1)

    def keep_cols(self, dve):
        core, s, cols = self.core, self.s, self.cols
        modc = core.modcs[self.layer % 2]
        dve.wait_ge(s["cols"], self.layer + 1)
        dve.tensor_scalar(modc[:, 0::2, :], cols[:, 1::2, :], 1.0, None, ALU.add).then_inc(s["modc"], 1)
        dve.tensor_copy(modc[:, 1::2, :], cols[:, 0::2, :]).then_inc(s["modc"], 1)

    def keep_rows(self, dve):
        core, s, rows = self.core, self.s, self.rows
        before = 5 * self.layer
        gate = core.gates[self.layer % 2][:].rearrange("p g d -> p (g d)")
        dve.wait_ge(s["rows"], self.layer + 1)
        dve.tensor_copy(gate, rows).then_inc(s["gate"], 1)
        dve.tensor_scalar(core.sgn[:], rows, 0.0, 2.0, ALU.is_ge, ALU.mult).then_inc(s["gate"], 1)
        dve.wait_ge(s["gate"], before + 1)
        dve.scalar_tensor_tensor(out=gate, in0=gate, scalar=-1.0, in1=gate, op0=ALU.mult,
                                 op1=ALU.max).then_inc(s["gate"], 1)
        dve.wait_ge(s["gate"], before + 3)
        dve.tensor_scalar(gate, gate, 0.25, None, ALU.max).then_inc(s["gate"], 1)
        dve.wait_ge(s["gate"], before + 4)
        dve.scalar_tensor_tensor(out=gate, in0=core.sgn[:], scalar=-1.0, in1=gate, op0=ALU.add, op1=ALU.mult).then_inc(s["gate"], 1)

    def load_next(self, sp, A):
        if self.layer + 1 < LAYERS:
            sp.wait_ge(self.s["rows"], self.layer + 1)
            sp.dma_start(self.core.wmod[:], A[f"wmod{self.layer + 1}"]).then_inc(self.core.s_wmod, 16)


def start(core, A):
    nc = core.nc
    norm = Norm(core, 0)
    mod = Modulation(core, 0, 4, 5)
    banks = [core.ps[:, b, :] for b in range(2)]
    with ExitStack() as ctx:
        s_const = core.sem("s_const", ctx)
        block = ctx.enter_context(nc.Block(no_gpsimd_drain=True))

        @block.sync
        def _(sp):
            sp.dma_start(core.craw[:], A["cond"]).then_inc(core.s_x, 16)
            sp.dma_start(core.x[:], A["x"]).then_inc(core.s_x, 16)
            sp.dma_start(core.wmod[:], A["wmod0"]).then_inc(core.s_wmod, 16)
            core.load_early(sp, A, 0)
            mod.load_next(sp, A)

        @block.gpsimd
        def _(pool):
            pool.memset(core.half_neg[:], -0.5).then_inc(s_const, 1)
            pool.memset(core.eps[:], LN_EPS).then_inc(s_const, 1)
            pool.memset(core.ident[:], 0.0).then_inc(s_const, 1)
            pool.memset(core.ident_bf[:], 0.0).then_inc(s_const, 1)
            pool.memset(core.causal_bf[:], 0.0).then_inc(s_const, 1)
            pool.wait_ge(s_const, 5)
            for m in (core.ident, core.ident_bf):
                pool.affine_select(out=m[:], in_=m[:], compare_op=ALU.not_equal, fill=1.0, base=0,
                                   pattern=[[-1, P]], channel_multiplier=1).then_inc(s_const, 1)
            pool.affine_select(out=core.causal_bf[:], in_=core.causal_bf[:], compare_op=ALU.is_ge,
                               fill=MASKED, base=0, pattern=[[-1, P]],
                               channel_multiplier=1).then_inc(s_const, 1)
            for i in range(TILES):
                norm.root(pool, i)

        @block.vector
        def _(dve):
            dve.wait_ge(core.s_x, 32)
            for i in range(TILES):
                norm.stats(dve, i)
                if i >= 1:
                    norm.scale(dve, i - 1)
                if i == 1:
                    mod.spread(dve)
            norm.scale(dve, TILES - 1)
            mod.keep_cols(dve)
            mod.keep_rows(dve)

        @block.scalar
        def _(act):
            mod.condition(act)
            for i in range(TILES):
                norm.keep(act, i, banks)

        @block.tensor
        def _(pe):
            pe.wait_ge(s_const, 8)
            mod.products(pe)
            for i in range(TILES):
                norm.turn(pe, i, banks)


def causal_blocks(i):
    return i + 1


def attention_l0(core, A, norm):
    nc = core.nc
    HEADS, HD = 16, 128
    PAIRS = HEADS // 2
    STEPS = 2 * TILES
    SCALE = float(np.float32(HD) ** np.float32(-0.5))
    x, ht, ps = core.x, core.ht, core.ps
    BIAS_Q, BIAS_K = 3 * KT * HD, 3 * KT * HD + 1
    CREDIT = 2
    chunks = [(causal_blocks(s % TILES) + 3) // 4 for s in range(STEPS + 1)]
    before = [sum(chunks[:s]) for s in range(STEPS + 2)]
    PER_PAIR = before[STEPS]

    def turned_by(p, s):
        return PER_PAIR * p + before[s + 1]

    GROUPS = {2: (0, 1, "q0"), 3: (1, 1, "k1"), 4: (2, 1, "q1"), 5: (3, 1, "v0"), 7: (4, 1, "v1"),
              8: (5, 0, "k0"), 9: (6, 0, "q0"), 10: (7, 0, "k1"), 11: (8, 0, "q1"), 12: (9, 0, "v0"),
              15: (10, 0, "v1"), 16: (11, 1, "k0")}
    index_of = {(b, what): n for n, b, what in GROUPS.values()}
    FIRST = ((0, "k0"), (0, "q0"), (0, "k1"), (0, "q1"), (0, "v0"), (0, "v1"), (1, "k0"))
    NG, NF = len(GROUPS), len(FIRST)

    with ExitStack() as ctx:
        w = carve(core.early, *2 * [(3 * KT * HD + 2,)])
        probs, probs_t, *qt = carve(core.arena, (2, TOKENS), (2, TILES, P), (TOKENS,), (TOKENS,))
        w_parts = [[core.sb(f"w_part{b}{m}", [P, 2, KT, HD], F32R, ctx) for m in range(2)] for b in range(2)]
        ht_parts = [core.sb(f"ht_part{m}", [P, KT, TOKENS], F32R, ctx) for m in range(2)]
        bias_v = core.sb("bias_v", [P, HEADS], F32, ctx)
        kt = [core.sb(f"kt{b}", [P, TOKENS], F32, ctx) for b in range(2)]
        v = [core.sb(f"v{b}", [P, TILES, HD], F32, ctx) for b in range(2)]
        nmax = core.sb("nmax", [P, 2], F32, ctx)
        rsum = core.sb("rsum", [P, 2], F32, ctx)
        rinv = core.sb("rinv", [P, 2], F32, ctx)
        att = core.sb("att", [P, HEADS, TOKENS], F32, ctx)
        wo = core.sb("wo", [P, HEADS, D], F32, ctx)
        bo = core.sb("bo", [P, D], F32, ctx)
        gated = core.sb("gated", [P, 2, D], F32, ctx)
        w_sem = [core.sem(f"w_loaded{b}", ctx) for b in range(2)]
        bias_loaded = core.sem("bias_loaded", ctx)
        rounded = core.sem("rounded", ctx)
        rest_done = core.sem("rest_done", ctx)
        wo_loaded = core.sem("wo_loaded", ctx)
        projected = core.sem("projected", ctx)
        kept = core.sem("kept", ctx)
        scored = core.sem("scored", ctx)
        maxed = core.sem("maxed", ctx)
        exped = core.sem("exped", ctx)
        inverted = core.sem("inverted", ctx)
        normed = core.sem("normed", ctx)
        turned = core.sem("turned", ctx)
        turned_kept = core.sem("turned_kept", ctx)
        valued = core.sem("valued", ctx)
        att_kept = core.sem("att_kept", ctx)
        outed = core.sem("outed", ctx)
        added = core.sem("added", ctx)
        bo_gated = core.sem("bo_gated", ctx)
        block = ctx.enter_context(nc.Block(no_gpsimd_drain=True))

        S = [ps[:, 0:2, :].rearrange("p a b -> p (a b)"), ps[:, 2:4, :].rearrange("p a b -> p (a b)")]
        T = [ps[:, 4, :], ps[:, 5, :]]
        V = ps[:, 6, :]
        W = ps[:, 7, :]

        def bank(n):
            return V if isinstance(n, int) and n < NF and (NF - 1 - n) % 2 == 1 else W

        @block.sync
        def _(sp):
            sp.dma_start(bias_v[:], A["l0_bv"]).then_inc(bias_loaded, 16)
            sp.dma_start(wo[:], A["l0_wo"]).then_inc(wo_loaded, 16)
            sp.dma_start(bo[:], A["l0_bo"].to_broadcast([P, D])).then_inc(wo_loaded, 16)
            sp.wait_ge(projected, NF - 1)
            sp.dma_start(w[0][:], A["l0_wqkv"][2]).then_inc(w_sem[0], 16)
            with sp.Fori(0, PAIRS - 2) as p:
                sp.wait_ge(projected, p * NG + NF + index_of[1, "v1"] + 1)
                sp.dma_start(w[1][:], A["l0_wqkv"][bass.ds(2 * p + 3, 1)].rearrange("a p n -> (a p) n")).then_inc(w_sem[1], 16)
                sp.wait_ge(projected, p * NG + NF + index_of[0, "v1"] + 1)
                sp.dma_start(w[0][:], A["l0_wqkv"][bass.ds(2 * p + 4, 1)].rearrange("a p n -> (a p) n")).then_inc(w_sem[0], 16)
            sp.wait_ge(projected, (PAIRS - 2) * NG + NF + index_of[1, "v1"] + 1)
            sp.dma_start(w[1][:], A["l0_wqkv"][HEADS - 1]).then_inc(w_sem[1], 16)
            sp.wait_ge(att_kept, 4 * PAIRS + 1)
            core.load_arena(sp, A, 0)

        @block.tensor
        def _(pe):
            def group(b, what, n):
                if not isinstance(n, int) or n >= NF:
                    pe.wait_ge(kept, n)
                elif n >= 2:
                    pe.wait_ge(kept, n - 1)
                W = bank(n)
                part, c = "qkv".index(what[0]), int(what[1])
                if part < 2 and (not isinstance(n, int) or n >= NF):
                    passes = [(hi_w, hi_h, k) for hi_w, hi_h in ((0, 0), (0, 1), (1, 0)) for k in range(KT)]
                    for at, (mw, mh, k) in enumerate(passes):
                        last = pe.matmul(W, w_parts[b][mw][:, part, k, :], ht_parts[mh][:, k, c * BANK:c * BANK + BANK],
                                         start=(at == 0), stop=(at == len(passes) - 1))
                elif part < 2:
                    for k in range(KT):
                        last = pe.matmul(W, w[b][:, (part * KT + k) * HD:(part * KT + k + 1) * HD], ht[:, k, c * BANK:c * BANK + BANK],
                                         start=(k == 0), stop=(k == KT - 1))
                else:
                    for j in range(4):
                        t = (4 * c + j) * P
                        for k in range(KT):
                            last = pe.matmul(W[:, j * P:j * P + P], ht[:, k, t:t + P], w[b][:, (part * KT + k) * HD:(part * KT + k + 1) * HD],
                                             start=(k == 0), stop=(k == KT - 1))
                last.then_inc(projected, 1)

            def scores(p, s):
                b, i = (s // TILES) % 2, s % TILES
                pe.wait_ge(exped, STEPS * p + s - 2 + 1 + CREDIT)
                n = causal_blocks(i) * P
                for c in range(0, n, BANK):
                    e = min(n, c + BANK)
                    pe.matmul(S[s % 2][:, c:e], qt[b][:, i * P:i * P + P], kt[b][:, c:e], start=True, stop=(e < n))
                pe.matmul(S[s % 2][:, n - P:n], core.ident_bf[:], core.causal_bf[:], start=False,
                          stop=True).then_inc(scored, 1)

            def transposes(p, s):
                i = s % TILES
                pe.wait_ge(normed, STEPS * p + s + 1)
                for c in range(chunks[s]):
                    pe.wait_ge(turned_kept, PER_PAIR * p + before[s] + c - 2 + 1 + CREDIT)
                    tb = T[(before[s] + c) % 2]
                    for j in range(4 * c, min(4 * c + 4, causal_blocks(i))):
                        last = pe.transpose(tb[:, (j % 4) * P:(j % 4) * P + P], probs[:, s % 2, j * P:j * P + P],
                                            core.ident[:])
                    last.then_inc(turned, 1)

            def values(p, s):
                b, i = s // TILES, s % TILES
                if i % 4 == 0:
                    pe.wait_ge(att_kept, 4 * p + s // 4 + 1)
                for j in range(causal_blocks(i)):
                    if j % 4 == 0:
                        pe.wait_ge(turned_kept, PER_PAIR * p + before[s] + j // 4 + 1 + CREDIT)
                    last = pe.matmul(V[:, (i % 4) * P:(i % 4) * P + P], v[b][:, j, :], probs_t[:, s % 2, j, :],
                                     start=(j == 0), stop=(j == causal_blocks(i) - 1))
                last.then_inc(valued, 1)

            def pair(p, is_last):
                for s in range(2, STEPS + 2):
                    if s == TILES:
                        pe.wait_ge(kept, NG * p + NF + index_of[1, "q1"] + 1)
                    if s == STEPS and not is_last:
                        pe.wait_ge(kept, NG * p + NF + index_of[0, "q1"] + 1)
                    if s < STEPS or not is_last:
                        scores(p, s)
                    if s - 1 < STEPS or not is_last:
                        transposes(p, s - 1)
                    if s in GROUPS and not (is_last and s >= TILES):
                        j, b, what = GROUPS[s]
                        if s == 2:
                            pe.wait_ge(rest_done, 2 * p + 2)
                        if s == TILES:
                            pe.wait_ge(rest_done, 2 * p + 3)
                        if s == STEPS:
                            pe.wait_ge(rest_done, 2 * p + 4)
                        group(b, what, NG * p + NF + j)
                    if s - 2 == 0:
                        pe.wait_ge(kept, NG * p + NF - 1)
                    if s - 2 == TILES:
                        pe.wait_ge(kept, NG * p + NF + index_of[1, "v1"] + 1)
                    values(p, s - 2)

            pe.sem_inc(valued, CREDIT)
            pe.wait_ge(core.early_in, 16)
            for n, (b, what) in enumerate(FIRST):
                group(b, what, n)
                if n == 5:
                    pe.wait_ge(kept, 4)
                    scores(0, 0)
                    scores(0, 1)
            transposes(0, 0)
            with pe.Fori(0, PAIRS - 1) as p:
                pair(p, False)
            pair(PAIRS - 1, True)
            pe.wait_ge(wo_loaded, 32)
            pe.wait_ge(att_kept, 4 * PAIRS + 1)
            for i in range(TILES):
                if i >= 2:
                    pe.wait_ge(added, i - 1)
                for h in range(HEADS):
                    last = pe.matmul(S[i % 2][:, 0:D], att[:, h, i * P:i * P + P], wo[:, h, :],
                                     start=(h == 0), stop=(h == HEADS - 1))
                last.then_inc(outed, 1)
                if i >= 1:
                    norm.turn(pe, i - 1, T)
            norm.turn(pe, TILES - 1, T)

        @block.scalar
        def _(act):
            act.sem_inc(exped, CREDIT)

            def keep(b, what, n):
                act.wait_ge(projected, n + 1)
                if isinstance(n, int) and 0 < n < NF:
                    act.wait_ge(kept, n)
                W = bank(n)
                c = int(what[1])
                if what[0] == "v":
                    act.activation(v[b][:, 4 * c:4 * c + 4, :], W.rearrange("p (t d) -> p t d", t=4),
                                   ACT.Copy).then_inc(kept, 1)
                else:
                    act.activation(kt[b][:, c * BANK:c * BANK + BANK], W, ACT.Identity,
                                   bias=w[b][:, BIAS_K:BIAS_K + 1]).then_inc(kept, 1)

            def exps(p, s):
                n = causal_blocks(s % TILES) * P
                act.wait_ge(maxed, STEPS * p + s + 1)
                if s >= 2:
                    act.wait_ge(turned, turned_by(p, s - 2))
                act.activation(probs[:, s % 2, 0:n], S[s % 2][:, 0:n], ACT.Exp, bias=nmax[:, s % 2:s % 2 + 1],
                               accum_out=rsum[:, s % 2:s % 2 + 1]).then_inc(exped, 1)

            def round_weights(b):
                act.activation(w_parts[b][0][:].rearrange("p a k d -> p (a k d)"), w[b][:, 0:2 * KT * HD],
                               ACT.Copy).then_inc(rounded, 1)

            def pair(p, is_last):
                for s in range(2, STEPS + 2 * (not is_last)):
                    exps(p, s)
                    if s == 6 and not is_last:
                        act.wait_ge(w_sem[0], 16 * (p + 1))
                        round_weights(0)
                    if s == 14 and not is_last:
                        act.wait_ge(w_sem[1], 16 * (p + 1))
                        round_weights(1)
                    if s in GROUPS and not (is_last and s >= TILES):
                        j, b, what = GROUPS[s]
                        if what[0] != "q":
                            keep(b, what, NG * p + NF + j)

            act.activation(ht_parts[0][:], ht[:], ACT.Copy).then_inc(rounded, 1)
            act.wait_ge(core.early_in, 16)
            round_weights(1)
            for n, (b, what) in enumerate(FIRST):
                if what[0] != "q":
                    keep(b, what, n)
                if n == 5:
                    exps(0, 0)
                    exps(0, 1)
            with act.Fori(0, PAIRS - 1) as p:
                pair(p, False)
            pair(PAIRS - 1, True)
            for i in range(TILES):
                norm.keep(act, i, T)

        @block.gpsimd
        def _(pool):
            def weights_rest(b):
                pool.tensor_tensor(w_parts[b][1][:].rearrange("p a k d -> p (a k d)"), w[b][:, 0:2 * KT * HD],
                                   w_parts[b][0][:].rearrange("p a k d -> p (a k d)"),
                                   ALU.subtract).then_inc(rest_done, 1)

            pool.wait_ge(rounded, 2)
            weights_rest(1)
            with pool.Fori(0, PAIRS - 1) as p:
                for b in range(2):
                    pool.wait_ge(rounded, 2 * p + b + 3)
                    weights_rest(b)
            for i in range(TILES):
                norm.root(pool, i)

        @block.vector
        def _(dve):
            dve.sem_inc(turned_kept, CREDIT)
            dve.sem_inc(att_kept, 1)

            def keep_q(b, what, n):
                dve.wait_ge(projected, n + 1)
                if isinstance(n, int) and 0 < n < NF:
                    dve.wait_ge(kept, n)
                W = bank(n)
                c = int(what[1])
                dve.tensor_scalar(qt[b][:, c * BANK:c * BANK + BANK], W, w[b][:, BIAS_Q:BIAS_Q + 1], SCALE,
                                  ALU.add, ALU.mult).then_inc(kept, 1)

            def keep_att(p, s):
                dve.wait_ge(valued, STEPS * p + s + 1 + CREDIT)
                h, c = 2 * p + s // TILES, (s % TILES) // 4
                dve.tensor_scalar(att[:, bass.ds(h, 1), c * BANK:c * BANK + BANK].rearrange("p a t -> p (a t)"), V,
                                  bias_v[:, bass.ds(h, 1)], None, ALU.add).then_inc(att_kept, 1)

            def maxes(p, s):
                n = causal_blocks(s % TILES) * P
                dve.wait_ge(scored, STEPS * p + s + 1)
                dve.tensor_reduce(nmax[:, s % 2:s % 2 + 1], S[s % 2][:, 0:n], AX_X, ALU.max,
                                  negate=True).then_inc(maxed, 1)

            def scale_rows(p, s):
                n = causal_blocks(s % TILES) * P
                dve.wait_ge(exped, STEPS * p + s + 1 + CREDIT)
                dve.reciprocal(rinv[:, s % 2:s % 2 + 1], rsum[:, s % 2:s % 2 + 1]).then_inc(inverted, 1)
                dve.wait_ge(inverted, STEPS * p + s + 1)
                dve.tensor_scalar(probs[:, s % 2, 0:n], probs[:, s % 2, 0:n], rinv[:, s % 2:s % 2 + 1], None,
                                  ALU.mult).then_inc(normed, 1)

            def keep_turned(p, s):
                i = s % TILES
                for c in range(chunks[s]):
                    m = min(4, causal_blocks(i) - 4 * c)
                    dve.wait_ge(turned, PER_PAIR * p + before[s] + c + 1)
                    if c == 0:
                        dve.wait_ge(valued, STEPS * p + s - 2 + 1 + CREDIT)
                    dve.tensor_copy(probs_t[:, s % 2, 4 * c:4 * c + m, :],
                                    T[(before[s] + c) % 2][:, 0:m * P].rearrange("p (t d) -> p t d", t=m)
                                    ).then_inc(turned_kept, 1)

            def pair(p, is_last):
                for s in range(2, STEPS + 2):
                    if s < STEPS or not is_last:
                        maxes(p, s)
                    if s - 1 < STEPS or not is_last:
                        keep_turned(p, s - 1)
                    if s < STEPS or not is_last:
                        scale_rows(p, s)
                    if s in GROUPS and GROUPS[s][2][0] == "q" and not (is_last and s >= TILES):
                        keep_q(GROUPS[s][1], GROUPS[s][2], NG * p + NF + GROUPS[s][0])
                    if (s - 2) % 4 == 3:
                        keep_att(p, s - 2)

            dve.wait_ge(bias_loaded, 16)
            for n, (b, what) in enumerate(FIRST):
                if what[0] == "q":
                    keep_q(b, what, n)
            dve.wait_ge(rounded, 1)
            dve.tensor_tensor(ht_parts[1][:], ht[:], ht_parts[0][:], ALU.subtract).then_inc(rest_done, 1)
            maxes(0, 0)
            scale_rows(0, 0)
            maxes(0, 1)
            keep_turned(0, 0)
            scale_rows(0, 1)
            with dve.Fori(0, PAIRS - 1) as p:
                pair(p, False)
            pair(PAIRS - 1, True)
            add_gated(dve, core, 0, bo, wo_loaded, 32, gated, bo_gated, [S[i % 2][:, 0:D] for i in range(TILES)],
                      outed, added, norm)


def add_gated(dve, core, which, b, b_loaded, loaded, gated, gated_done, outs, outed, added, norm):
    x, gate = core.x, core.gate
    dve.wait_ge(b_loaded, loaded)
    dve.tensor_tensor(gated[:, 0, :], gate[:, which, :], b[:], ALU.mult).then_inc(gated_done, 1)
    dve.wait_ge(gated_done, 1)
    dve.tensor_tensor(x[:], x[:], gated[:, 0:1, :].to_broadcast([P, TILES, D]), ALU.add).then_inc(gated_done, 1)
    dve.wait_ge(gated_done, 2)
    for i in range(TILES):
        dve.wait_ge(outed, i + 1)
        dve.tensor_tensor(gated[:, i % 2, :], outs[i], gate[:, which, :], ALU.mult).then_inc(added, 1)
        dve.wait_ge(added, i + 1)
        dve.tensor_tensor(x[:, i, :], x[:, i, :], gated[:, i % 2, :], ALU.add).then_inc(gated_done, 1)
        if norm is not None:
            dve.wait_ge(gated_done, 2 + i + 1)
            norm.stats(dve, i)
            norm.scale(dve, i)


EXPERTS, TOP, GROUPS_OF, TOP_GROUPS, GROUP = 32, 4, 4, 2, 8
FFN = 128
CAP = 2 * (256 * TOP // EXPERTS)
SLOTS = EXPERTS * CAP
ROUTE_SCALE = 2.0
DROPPED = 65536.0
PAD = -3.0e38
RING = 4


def moe(core, A, norm):
    nc = core.nc
    x, xn, ht, ps = core.x, core.xn, core.ht, core.ps
    with ExitStack() as moe_ctx:
        slots_in = nc.dram_tensor("slots_in", (SLOTS, D), F32, kind="Internal").ap()
        slots_out = nc.dram_tensor("slots_out", (SLOTS, D), F32, kind="Internal").ap()
        idx = core.sb("idx", [P, TILES * TOP], U32, moe_ctx)
        wk = core.sb("wk", [P, TILES * TOP], F32, moe_ctx)
        shared = core.sb("shared", [P, TILES, D], F32, moe_ctx)
        picked = core.sb("picked", [P, TILES * TOP, D], F32, moe_ctx)
        wexp = [core.sb(f"wexp{r}", [P, 2 * 2 * KT * FFN + 2 * D], F32, moe_ctx) for r in range(RING)]
        loaded = [core.sem(f"e_loaded{r}", moe_ctx) for r in range(RING)]
        route(core, A, slots_in, idx, wk, shared, picked, wexp, loaded)
        experts(core, A, slots_in, slots_out, wexp, loaded)
        combine(core, slots_out, idx, wk, shared, picked, norm)


def route(core, A, slots_in, idx, wk, shared, picked, wexp, loaded):
    nc = core.nc
    x, xn, ht, ps = core.x, core.xn, core.ht, core.ps
    with ExitStack() as ctx:
        def buf(name, shape, dt=F32):
            return core.sb(name, shape, dt, ctx)

        gw, gbias, sw, sd = carve(core.arena, (KT, EXPERTS), (EXPERTS,), (2, KT, D), (KT, D))
        scores = buf("scores", [P, TILES, EXPERTS])
        sc = buf("scb_", [P, TILES, EXPERTS])
        gtop = buf("gtop", [P, TILES * GROUPS_OF, 8])
        gsum = buf("gsum", [P, TILES, 8])
        gmax = buf("gmax", [P, TILES, 8])
        gidx = buf("gidx", [P, TILES, 8], U32)
        gidf = buf("gidf", [P, TILES, TOP_GROUPS])
        gm = buf("gm", [P, TOP_GROUPS, TILES, GROUPS_OF])
        emax = buf("emax", [P, TILES, 8])
        eidx = buf("eidx", [P, TILES, 8], U32)
        eidf = buf("eidf", [P, TILES, TOP])
        hot = buf("hot", [P, TILES, TOP, EXPERTS])
        prod = buf("prod", [P, TILES, TOP, EXPERTS])
        chosen = buf("chosen", [P, TILES, EXPERTS], BF16)
        chosen_f = buf("chosen_f", [P, TILES, EXPERTS])
        s4 = buf("s4", [P, TILES, TOP])
        den = buf("den", [P, TILES])
        pos4 = buf("pos4", [P, TILES, TOP])
        late = buf("late", [P, TILES, TOP])
        early = buf("early", [P, TILES, TOP])
        slot = buf("slot", [P, TILES, TOP])
        iota_e = buf("iota_e", [P, EXPERTS])
        earlier = buf("earlier", [P, P], BF16)
        ones_bf = buf("ones_bf", [P, P], BF16)
        zero = buf("zero", [P, SLOTS * D // P // 4])
        act_s = buf("act_s", [P, 2, BANK])
        hid = buf("hid", [P, KT, TOKENS])
        const_done = core.sem("const_done", ctx)
        gated = core.sem("r_gated", ctx)
        sigmoid_done = core.sem("sigmoid_done", ctx)
        step = core.sem("route_step", ctx)
        chosen_done = core.sem("chosen_done", ctx)
        placed = core.sem("placed", ctx)
        idx_done = core.sem("idx_done", ctx)
        scattered = core.sem("scattered", ctx)
        upped = core.sem("upped", ctx)
        silued = core.sem("silued", ctx)
        hid_done = core.sem("hid_done", ctx)
        downed = core.sem("downed", ctx)
        shared_done = core.sem("shared_done", ctx)
        logits = ps[:, 0, 0:TILES * EXPERTS]
        where = ps[:, 1, 0:TILES * EXPERTS].rearrange("p (t e) -> p t e", t=TILES)
        mod = Modulation(core, 1, 6, 7)
        block = ctx.enter_context(nc.Block(no_gpsimd_drain=True))

        @block.sync
        def _(sp):
            core.load_early(sp, A, 1)
            for r in range(RING):
                sp.dma_start(wexp[r][:], A["l0_wexp"][r]).then_inc(loaded[r], 16)
            sp.wait_ge(const_done, 6)
            for q in range(4):
                sp.dma_start(slots_in.rearrange("(q p r) d -> q p (r d)", q=4, p=P)[q], zero[:]).then_inc(const_done, 16)
            sp.wait_ge(const_done, 6 + 64)

        @block.gpsimd
        def _(pool):
            pool.memset(zero[:], 0.0).then_inc(const_done, 1)
            pool.memset(earlier[:], 1.0).then_inc(const_done, 1)
            pool.memset(ones_bf[:], 1.0).then_inc(const_done, 1)
            pool.iota(iota_e[:], pattern=[[1, EXPERTS]], base=0, channel_multiplier=0,
                      allow_small_or_imprecise_dtypes=True).then_inc(const_done, 1)
            pool.memset(gsum[:], PAD).then_inc(const_done, 1)
            pool.wait_ge(const_done, 5)
            pool.affine_select(out=earlier[:], in_=earlier[:], compare_op=ALU.is_gt, fill=0.0, base=0,
                               pattern=[[1, P]], channel_multiplier=-1).then_inc(const_done, 1)
            pool.wait_ge(const_done, 6 + 64)
            pool.wait_ge(idx_done, 1)
            for i in range(TILES):
                for k in range(TOP):
                    j = i * TOP + k
                    pool.indirect_dma_start(out=slots_in, out_offset=bass.IndirectOffsetOnAxis(ap=idx[:, j:j + 1], axis=0),
                                            in_=xn[:, i, :], in_offset=None, bounds_check=SLOTS - 1,
                                            oob_is_err=False).then_inc(scattered, 16)
            pool.wait_ge(scattered, 16 * TILES * TOP)

        @block.tensor
        def _(pe):
            pe.wait_ge(core.arena_in, 16)
            for i in range(TILES):
                for k in range(KT):
                    last = pe.matmul(logits[:, i * EXPERTS:(i + 1) * EXPERTS], ht[:, k, i * P:i * P + P], gw[:, k, :],
                                     start=(k == 0), stop=(k == KT - 1))
            last.then_inc(gated, 1)
            mod.products(pe)
            def gate_up(n):
                f, c = n % KT, n // KT
                if n >= 2:
                    pe.wait_ge(hid_done, n - 1)
                for part in range(2):
                    for k in range(KT):
                        last = pe.matmul(ps[:, 2 + 2 * (n % 2) + part, :], sw[:, part, k, f * P:f * P + P],
                                         ht[:, k, c * BANK:c * BANK + BANK], start=(k == 0), stop=(k == KT - 1))
                last.then_inc(upped, 1)
            for n in range(2):
                gate_up(n)
            pe.wait_ge(chosen_done, 1)
            pe.wait_ge(const_done, 6)
            for i in range(TILES):
                for j in range(i + 1):
                    last = pe.matmul(where[:, i, :], (earlier if j == i else ones_bf)[:], chosen[:, j, :],
                                     start=(j == 0), stop=(j == i))
            last.then_inc(placed, 1)
            for n in range(2, KT * CHUNKS):
                gate_up(n)
            pe.wait_ge(hid_done, KT * CHUNKS)
            for i in range(TILES):
                if i >= 2:
                    pe.wait_ge(shared_done, i - 1)
                for f in range(KT):
                    last = pe.matmul(ps[:, 6 + i % 2, 0:D], hid[:, f, i * P:i * P + P], sd[:, f, :],
                                     start=(f == 0), stop=(f == KT - 1))
                last.then_inc(downed, 1)

        @block.scalar
        def _(act):
            act.wait_ge(gated, 1)
            act.activation(scores[:].rearrange("p t e -> p (t e)"), logits, ACT.Sigmoid).then_inc(sigmoid_done, 1)
            mod.condition(act)
            for n in range(KT * CHUNKS):
                act.wait_ge(upped, n + 1)
                if n >= 2:
                    act.wait_ge(hid_done, n - 1)
                act.activation(act_s[:, n % 2, :], ps[:, 2 + 2 * (n % 2), :], ACT.Silu).then_inc(silued, 1)
            for i in range(TILES):
                act.wait_ge(downed, i + 1)
                act.activation(shared[:, i, :], ps[:, 6 + i % 2, 0:D], ACT.Copy).then_inc(shared_done, 1)

        @block.vector
        def _(dve):
            done = [0]

            def after(ins):
                ins.then_inc(step, 1)
                done[0] += 1
                dve.wait_ge(step, done[0])

            def hidden(n):
                f, c = n % KT, n // KT
                dve.wait_ge(silued, n + 1)
                dve.tensor_tensor(hid[:, f, c * BANK:c * BANK + BANK], act_s[:, n % 2, :], ps[:, 3 + 2 * (n % 2), :],
                                  ALU.mult).then_inc(hid_done, 1)

            dve.wait_ge(core.arena_in, 16)
            dve.wait_ge(sigmoid_done, 1)
            after(dve.tensor_tensor(sc[:], scores[:], gbias[:].rearrange("p (a e) -> p a e", a=1).to_broadcast([P, TILES, EXPERTS]), ALU.add))
            mod.spread(dve)
            sc_g = sc[:].rearrange("p t (g e) -> p (t g) e", g=GROUPS_OF)
            for j in range(TILES * GROUPS_OF):
                last = dve.max(gtop[:, j, :], sc_g[:, j, :])
            after(last)
            dve.wait_ge(const_done, 6)
            gt = gtop[:].rearrange("p (t g) m -> p t g m", g=GROUPS_OF)
            after(dve.tensor_tensor(gsum[:, :, 0:GROUPS_OF], gt[:, :, :, 0], gt[:, :, :, 1], ALU.add))
            for i in range(TILES):
                last = dve.max(gmax[:, i, :], gsum[:, i, :])
            after(last)
            for i in range(TILES):
                last = dve.max_index(gidx[:, i, :], gmax[:, i, :], gsum[:, i, :])
            after(last)
            after(dve.tensor_copy(gidf[:], gidx[:, :, 0:TOP_GROUPS]))
            for m in range(TOP_GROUPS):
                last = dve.tensor_tensor(gm[:, m, :, :], gidf[:, :, m:m + 1].to_broadcast([P, TILES, GROUPS_OF]),
                                         iota_e[:, 0:GROUPS_OF].rearrange("p (a g) -> p a g", a=1).to_broadcast([P, TILES, GROUPS_OF]),
                                         ALU.is_equal)
            after(last)
            after(dve.tensor_tensor(gm[:, 0, :, :], gm[:, 0, :, :], gm[:, 1, :, :], ALU.add))
            g3 = gm[:, 0, :, :].rearrange("p t g -> p (t g)").rearrange("p (n a) -> p n a", a=1)
            after(dve.tensor_tensor(sc_g, sc_g, g3.to_broadcast([P, TILES * GROUPS_OF, GROUP]), ALU.mult))
            for i in range(TILES):
                last = dve.max(emax[:, i, :], sc[:, i, :])
            after(last)
            for i in range(TILES):
                last = dve.max_index(eidx[:, i, :], emax[:, i, :], sc[:, i, :])
            after(last)
            after(dve.tensor_copy(eidf[:], eidx[:, :, 0:TOP]))
            hot3 = hot[:].rearrange("p t k e -> p (t k) e")
            prod3 = prod[:].rearrange("p t k e -> p (t k) e")
            after(dve.tensor_tensor(hot3, eidf[:].rearrange("p t k -> p (t k)").rearrange("p (n a) -> p n a", a=1).to_broadcast([P, TILES * TOP, EXPERTS]),
                                    iota_e[:].rearrange("p (a e) -> p a e", a=1).to_broadcast([P, TILES * TOP, EXPERTS]), ALU.is_equal))
            after(dve.tensor_reduce(chosen_f[:], hot[:].rearrange("p t k e -> p t e k"), AX_X, ALU.add))
            dve.tensor_copy(chosen[:], chosen_f[:]).then_inc(chosen_done, 1)
            for i in range(TILES):
                last = dve.tensor_tensor(prod[:, i, :, :], hot[:, i, :, :], scores[:, i:i + 1, :].to_broadcast([P, TOP, EXPERTS]), ALU.mult)
            after(last)
            after(dve.tensor_reduce(s4[:].rearrange("p t k -> p (t k)"), prod3, AX_X, ALU.add))
            after(dve.tensor_reduce(den[:], s4[:], AX_X, ALU.add))
            after(dve.tensor_scalar(den[:], den[:], 1e-20, None, ALU.add))
            after(dve.reciprocal(den[:], den[:]))
            after(dve.tensor_scalar(den[:], den[:], ROUTE_SCALE, None, ALU.mult))
            after(dve.tensor_tensor(s4[:], s4[:], den[:].rearrange("p (t a) -> p t a", a=1).to_broadcast([P, TILES, TOP]), ALU.mult))
            for n in range(2):
                hidden(n)
            dve.wait_ge(placed, 1)
            for i in range(TILES):
                last = dve.tensor_tensor(prod[:, i, :, :], hot[:, i, :, :], where[:, i:i + 1, :].to_broadcast([P, TOP, EXPERTS]), ALU.mult)
            after(last)
            after(dve.tensor_reduce(pos4[:].rearrange("p t k -> p (t k)"), prod3, AX_X, ALU.add))
            after(dve.scalar_tensor_tensor(out=slot[:], in0=eidf[:], scalar=float(CAP), in1=pos4[:], op0=ALU.mult, op1=ALU.add))
            after(dve.tensor_scalar(late[:], pos4[:], float(CAP), DROPPED, ALU.is_ge, ALU.mult))
            dve.tensor_tensor(idx[:], slot[:].rearrange("p t k -> p (t k)"), late[:].rearrange("p t k -> p (t k)"), ALU.add).then_inc(idx_done, 1)
            after(dve.tensor_scalar(early[:], pos4[:], float(CAP), None, ALU.is_lt))
            dve.tensor_tensor(wk[:], s4[:].rearrange("p t k -> p (t k)"), early[:].rearrange("p t k -> p (t k)"), ALU.mult)
            mod.keep_cols(dve)
            mod.keep_rows(dve)
            for n in range(2, KT * CHUNKS):
                hidden(n)
            dve.memset(picked[:], 0.0)


def experts(core, A, slots_in, slots_out, wexp, loaded):
    nc = core.nc
    ps = core.ps
    PAIRS = EXPERTS // 2
    ROUNDS = PAIRS // RING
    with ExitStack() as ctx:
        rows = [core.sb(f"rows{r}", [P, D], F32, ctx) for r in range(RING)]
        w13, w2 = zip(*(carve(wexp[r], (4, KT, FFN), (2, D)) for r in range(RING)))
        bt = [core.sb(f"bt{r}", [P, KT, P], F32, ctx) for r in range(2)]
        sil = [core.sb(f"sil{r}", [P, P], F32, ctx) for r in range(2)]
        hid = [core.sb(f"ehid{r}", [P, P], F32, ctx) for r in range(2)]
        res = [core.sb(f"res{r}", [P, D], F32, ctx) for r in range(RING)]
        rows_loaded = [core.sem(f"rows_loaded{r}", ctx) for r in range(RING)]
        turned = core.sem("e_turned", ctx)
        bt_kept = core.sem("bt_kept", ctx)
        upped = core.sem("e_upped", ctx)
        silued = core.sem("e_silued", ctx)
        hid_done = core.sem("e_hid", ctx)
        downed = core.sem("e_downed", ctx)
        res_kept = core.sem("res_kept", ctx)
        stored = [core.sem(f"e_stored{r}", ctx) for r in range(RING)]
        in_rows = slots_in.rearrange("(q p) d -> q p d", p=P)
        out_rows = slots_out.rearrange("(q p) d -> q p d", p=P)
        T = [ps[:, b, 0:D].rearrange("p (k t) -> p k t", k=KT) for b in range(2)]
        U = [ps[:, 2 + b, 0:2 * P].rearrange("p (w t) -> p w t", w=2) for b in range(2)]
        O = [ps[:, 4 + b, 0:D] for b in range(2)]
        CREDIT = 2
        block = ctx.enter_context(nc.Block(no_gpsimd_drain=True))

        @block.sync
        def _(sp):
            with sp.Fori(0, ROUNDS - 1) as g:
                for r in range(RING):
                    q = bass.ds(g * RING + RING + r, 1)
                    sp.wait_ge(downed, RING * g + r + 1 + CREDIT)
                    sp.dma_start(wexp[r][:], A["l0_wexp"][q].rearrange("a p n -> (a p) n")).then_inc(loaded[r], 16)

        @block.tensor
        def _(pe):
            pe.sem_inc(downed, CREDIT)
            pe.sem_inc(upped, CREDIT)

            def turn(g, r):
                q = RING * g + r
                pe.wait_ge(rows_loaded[r], 16 * (g + 1))
                pe.wait_ge(bt_kept, q - 2 + 1 + CREDIT)
                for k in range(KT):
                    last = pe.transpose(T[r % 2][:, k, :], rows[r][:, k * P:k * P + P], core.ident[:])
                last.then_inc(turned, 1)

            def up(g, r):
                q = RING * g + r
                pe.wait_ge(loaded[r], 16 * (g + 1))
                pe.wait_ge(bt_kept, q + 1 + CREDIT)
                pe.wait_ge(hid_done, q - 2 + 1 + CREDIT)
                for w in range(2):
                    for e in range(2):
                        for k in range(KT):
                            last = pe.matmul(U[r % 2][:, w, e * CAP:(e + 1) * CAP], w13[r][:, 2 * e + w, k, :],
                                             bt[r % 2][:, k, e * CAP:(e + 1) * CAP], start=(k == 0), stop=(k == KT - 1))
                last.then_inc(upped, 1)

            def down(g, r):
                q = RING * g + r
                pe.wait_ge(hid_done, q + 1 + CREDIT)
                pe.wait_ge(res_kept, q - 2 + 1 + CREDIT)
                for e in range(2):
                    last = pe.matmul(O[r % 2][e * CAP:(e + 1) * CAP, :], hid[r % 2][:, e * CAP:(e + 1) * CAP],
                                     w2[r][:, e, :], start=True, stop=True)
                last.then_inc(downed, 1)

            def round_(g, is_last):
                for r in range(RING):
                    if r + 1 < RING:
                        turn(g, r + 1)
                    elif not is_last:
                        turn(g + 1, 0)
                    up(g, r)
                    if r > 0:
                        down(g, r - 1)
                down(g, RING - 1)

            turn(0, 0)
            with pe.Fori(0, ROUNDS - 1) as g:
                round_(g, False)
            round_(ROUNDS - 1, True)

        @block.scalar
        def _(act):
            act.sem_inc(bt_kept, CREDIT)

            def keep_turned(g, r):
                q = RING * g + r
                act.wait_ge(turned, q + 1)
                act.wait_ge(upped, q - 2 + 1 + CREDIT)
                for k in range(KT):
                    last = act.activation(bt[r % 2][:, k, :], T[r % 2][:, k, :], ACT.Identity,
                                          scale=core.modc[:, 2, k:k + 1], bias=core.modc[:, 3, k:k + 1])
                last.then_inc(bt_kept, 1)

            def silu(g, r):
                q = RING * g + r
                act.wait_ge(upped, q + 1 + CREDIT)
                act.wait_ge(hid_done, q - 2 + 1 + CREDIT)
                act.activation(sil[r % 2][:], U[r % 2][:, 0, :], ACT.Silu).then_inc(silued, 1)

            def round_(g, is_last):
                for r in range(RING):
                    if r + 1 < RING:
                        keep_turned(g, r + 1)
                    elif not is_last:
                        keep_turned(g + 1, 0)
                    silu(g, r)
                    if not is_last:
                        act.dma_start(rows[r][:], in_rows[bass.ds(RING * g + r + RING, 1)].rearrange("a p n -> (a p) n")
                                      ).then_inc(rows_loaded[r], 16)

            for r in range(RING):
                act.dma_start(rows[r][:], in_rows[r]).then_inc(rows_loaded[r], 16)
            keep_turned(0, 0)
            with act.Fori(0, ROUNDS - 1) as g:
                round_(g, False)
            round_(ROUNDS - 1, True)

        @block.vector
        def _(dve):
            dve.sem_inc(hid_done, CREDIT)
            dve.sem_inc(res_kept, CREDIT)

            def hidden(g, r):
                q = RING * g + r
                dve.wait_ge(silued, q + 1)
                dve.wait_ge(downed, q - 2 + 1 + CREDIT)
                dve.tensor_tensor(hid[r % 2][:], sil[r % 2][:], U[r % 2][:, 1, :], ALU.mult).then_inc(hid_done, 1)

            def keep(g, r, first):
                q = RING * g + r
                dve.wait_ge(downed, q + 1 + CREDIT)
                if not first:
                    dve.wait_ge(stored[r], 16 * g)
                dve.tensor_copy(res[r][:], O[r % 2]).then_inc(res_kept, 1)

            def round_(g, first):
                for r in range(RING):
                    hidden(g, r)
                    if r > 0:
                        keep(g, r - 1, first)
                keep(g, RING - 1, first)

            round_(0, True)
            with dve.Fori(1, ROUNDS) as g:
                round_(g, False)

        @block.gpsimd
        def _(pool):
            with pool.Fori(0, ROUNDS) as g:
                for r in range(RING):
                    q = g * RING + r
                    pool.wait_ge(res_kept, q + 1 + CREDIT)
                    pool.dma_start(out_rows[bass.ds(q, 1)].rearrange("a p n -> (a p) n"), res[r][:]).then_inc(stored[r], 16)
            for r in range(RING):
                pool.wait_ge(stored[r], 16 * ROUNDS)


def combine(core, slots_out, idx, wk, shared, picked, norm):
    nc = core.nc
    with ExitStack() as ctx:
        gathered = [core.sem(f"gathered{i}", ctx) for i in range(TILES // 2)]
        step = core.sem("c_step", ctx)
        banks = [core.ps[:, b, :] for b in range(2)]
        LAG = 4
        block = ctx.enter_context(nc.Block(no_gpsimd_drain=True))

        @block.gpsimd
        def _(pool):
            for i in range(TILES):
                if i >= LAG:
                    norm.root(pool, i - LAG)
                for k in range(TOP):
                    j = i * TOP + k
                    pool.indirect_dma_start(out=picked[:, j, :], out_offset=None, in_=slots_out,
                                            in_offset=bass.IndirectOffsetOnAxis(ap=idx[:, j:j + 1], axis=0),
                                            bounds_check=SLOTS - 1, oob_is_err=False).then_inc(gathered[i // 2], 16)
            for i in range(TILES - LAG, TILES):
                norm.root(pool, i)

        @block.tensor
        def _(pe):
            for i in range(TILES):
                norm.turn(pe, i, banks)

        @block.scalar
        def _(act):
            for i in range(TILES):
                norm.keep(act, i, banks)

        @block.vector
        def _(dve):
            n = 0
            for i in range(TILES):
                if i % 2 == 0:
                    dve.wait_ge(gathered[i // 2], 2 * 16 * TOP)
                for k in range(TOP):
                    j = i * TOP + k
                    dve.scalar_tensor_tensor(out=shared[:, i, :], in0=picked[:, j, :], scalar=wk[:, j:j + 1],
                                             in1=shared[:, i, :], op0=ALU.mult, op1=ALU.add).then_inc(step, 1)
                    n += 1
                    dve.wait_ge(step, n)
                dve.tensor_tensor(shared[:, i, :], shared[:, i, :], core.gate[:, 1, :], ALU.mult).then_inc(step, 1)
                n += 1
                dve.wait_ge(step, n)
                dve.tensor_tensor(core.x[:, i, :], core.x[:, i, :], shared[:, i, :], ALU.add).then_inc(step, 1)
                n += 1
                dve.wait_ge(step, n)
                norm.stats(dve, i)
                if i >= LAG:
                    norm.scale(dve, i - LAG)
            for i in range(TILES - LAG, TILES):
                norm.scale(dve, i)


def attention_l1(core, A, norm):
    nc = core.nc
    GROUPS, HD, MAPS = 4, 128, 2
    VD = 2 * HD
    STEPS = 2 * TILES
    SCALE = float(HD) ** -0.5
    LAMBDA_INIT = 0.8 - 0.6 * float(np.exp(-0.3 * 1))
    RMS_EPS = 1e-5
    x, ht, ps = core.x, core.ht, core.ps
    LAST = STEPS + 2
    chunks = [(causal_blocks(s % TILES) + 3) // 4 for s in range(LAST + 1)]
    PLAN = {3: [(None, "v", 1, 0)], 4: [(None, "v", 2, 0)], 5: [(1, "q", 0, 0)], 6: [(1, "q", 0, 1)],
            7: [(None, "v", 3, 0)], 8: [(1, "q", 1, 0)], 9: [(1, "q", 1, 1)],
            10: [(0, "q", 0, 0)], 11: [(0, "q", 0, 1)], 12: [(0, "q", 1, 0)], 13: [(0, "q", 1, 1)],
            15: [(None, "k", 0, 0), (None, "k", 0, 1)], 16: [(None, "k", 1, 0)], 17: [(None, "v", 0, 0)],
            18: [(None, "k", 1, 1)]}
    FIRST = [(None, "k", 0, 0), (0, "q", 0, 0), (None, "k", 0, 1), (0, "q", 0, 1), (0, "q", 1, 0), (0, "q", 1, 1),
             (None, "k", 1, 0), (None, "v", 0, 0), (None, "k", 1, 1)]
    NF = len(FIRST)
    number, NG = {}, 0
    for s in sorted(PLAN):
        for what in PLAN[s]:
            number[s, what] = NG
            NG += 1
    turn_index, NT = {("p", 0, 0): 2, ("p", 1, 0): 3}, 0
    for s in range(3, LAST + 1):
        for c in range(chunks[s - 1]):
            turn_index["p", s - 1, c] = 4 + NT
            NT += 1
        turn_index["o", s - 3, 0] = 4 + NT
        NT += 1
    for t in (-2, -1):
        turn_index["o", t, 0] = turn_index["o", t + STEPS, 0] - NT
    assert NT % 2 == 0

    with ExitStack() as ctx:
        KV_BIAS = (MAPS * KT * HD) + KT * VD
        wkv, wq0 = carve(core.early, (KV_BIAS + MAPS + VD,), (MAPS * KT * HD + MAPS,))
        wq = [wq0, core.sb("wq1", [P, MAPS * KT * HD + MAPS], F32, ctx)]
        h_parts = [core.sb(f"h_part{m}", [P, KT, TOKENS], F32R, ctx) for m in range(2)]
        w_parts = [[core.sb(f"w_part{b}{m}", [P, MAPS * KT * HD], F32R, ctx) for m in range(2)] for b in range(2)]
        q00, q01, q10 = carve(core.wmod[:].rearrange("p k n -> p (k n)"), *3 * [(TOKENS,)])
        q = [[q00, q01], [q10, core.sb("q11", [P, TOKENS], F32, ctx)[:]]]
        k = [core.sb(f"k{m}", [P, TOKENS], F32, ctx) for m in range(MAPS)]
        v = core.sb("v", [P, TILES, VD], F32, ctx)
        ex, mixed = carve(core.arena, (2, MAPS, TOKENS), (2, TOKENS))
        mixed_t = carve(core.xn[:].rearrange("p a d -> p (a d)"), (2, TILES, P))[0]
        nmax = core.sb("nmax", [P, 2, MAPS], F32, ctx)
        rsum = core.sb("rsum", [P, 2, MAPS], F32, ctx)
        rinv = core.sb("rinv", [P, 2, MAPS], F32, ctx)
        rneg = core.sb("rneg", [P, 2], F32, ctx)
        o = core.sb("o", [P, 2, VD], F32, ctx)
        osq = carve(core.sgn, (2, VD))[0]
        ssq = core.sb("ssq", [P, 2], F32, ctx)
        mean_sq = core.sb("mean_sq", [P, 2], F32, ctx)
        rms = core.sb("rms", [P, 2], F32, ctx)
        on = core.sb("on", [P, 2, VD], F32, ctx)
        att = core.sb("att", [P, 2 * GROUPS * KT, TOKENS], F32, ctx)
        wo = core.sb("wo", [P, 2 * GROUPS * KT, D], F32, ctx)
        bo = core.scb[:].rearrange("p k n -> p (k n)")
        lam_rows = osq.rearrange("p a b -> p (a b)").rearrange("p (a d) -> p a d", a=4)
        lam = core.sb("lam", [P, 8], F32, ctx)
        subln = core.sb("subln", [P, KT], F32, ctx)
        gated = on
        q_loaded = [core.sem(f"q_loaded{b}", ctx) for b in range(2)]
        kv_loaded = core.sem("kv_loaded", ctx)
        lam_loaded = core.sem("lam_loaded", ctx)
        wo_loaded = core.sem("wo_loaded", ctx)
        lam_step = core.sem("lam_step", ctx)
        rounded = core.sem("rounded", ctx)
        rest_done = core.sem("rest_done", ctx)
        wo_scaled = core.sem("wo_scaled", ctx)
        projected = core.sem("projected", ctx)
        kept = core.sem("kept", ctx)
        scored = core.sem("scored", ctx)
        maxed = core.sem("maxed", ctx)
        exped = core.sem("exped", ctx)
        mixed_done = core.sem("mixed_done", ctx)
        mix_step = core.sem("mix_step", ctx)
        turned = core.sem("turned", ctx)
        turned_kept = core.sem("turned_kept", ctx)
        valued = core.sem("valued", ctx)
        o_kept = core.sem("o_kept", ctx)
        squared = core.sem("squared", ctx)
        meaned = core.sem("meaned", ctx)
        rms_done = core.sem("rms_done", ctx)
        on_done = core.sem("on_done", ctx)
        outed = core.sem("outed", ctx)
        added = core.sem("added", ctx)
        bo_gated = core.sem("bo_gated", ctx)
        CREDIT = 2
        S = [ps[:, 0:2, :].rearrange("p a b -> p (a b)"), ps[:, 2:4, :].rearrange("p a b -> p (a b)")]
        T = [ps[:, 4, :], ps[:, 5, :]]
        O = ps[:, 6, 0:VD]
        W = ps[:, 7, :]

        def bank(n):
            return ps[:, 6, :] if isinstance(n, int) and n < NF and (NF - 1 - n) % 2 == 1 else W
        MICRO = STEPS * MAPS
        block = ctx.enter_context(nc.Block(no_gpsimd_drain=True))

        def order(g, s, what):
            return NG * g + NF + number[s, what]

        def turn_no(g, kind, t, c):
            missing = 0
            if isinstance(g, int) and g == GROUPS - 1 and kind == "o":
                missing = max(0, t - (STEPS - 3))
            return NT * g + turn_index[kind, t, c] - missing

        def turn_bank(g, kind, t, c):
            return T[turn_no(0 if not isinstance(g, int) else g, kind, t, c) % 2]

        def active(t, is_last):
            return t < STEPS or not is_last

        @block.sync
        def _(sp):
            def load(dst, name, g, sem):
                if isinstance(g, int):
                    sp.dma_start(dst[:], A[name][g]).then_inc(sem, 16)
                else:
                    sp.dma_start(dst[:], A[name][bass.ds(g, 1)].rearrange("a p n -> (a p) n")).then_inc(sem, 16)

            load(wq[1], "l1_wq", 1, q_loaded[1])
            sp.dma_start(osq.rearrange("p a b -> p (a b)"), A["l1_lambda"].to_broadcast([P, 4 * HD])).then_inc(lam_loaded, 16)
            sp.dma_start(subln[:], A["l1_subln"]).then_inc(lam_loaded, 16)
            sp.dma_start(wo[:], A["l1_wo"]).then_inc(wo_loaded, 16)
            sp.dma_start(bo[:], A["l1_bo"].to_broadcast([P, D])).then_inc(wo_loaded, 16)
            sp.wait_ge(kept, NF - 1)
            load(wq[0], "l1_wq", 2, q_loaded[0])
            with sp.Fori(0, GROUPS - 2) as g:
                sp.wait_ge(kept, order(g, 7, PLAN[7][0]) + 1)
                load(wkv, "l1_wkv", g + 1, kv_loaded)
                sp.wait_ge(kept, order(g, 9, PLAN[9][0]) + 1)
                load(wq[1], "l1_wq", 2 * g + 3, q_loaded[1])
                sp.wait_ge(kept, order(g, 13, PLAN[13][0]) + 1)
                load(wq[0], "l1_wq", 2 * g + 4, q_loaded[0])
            g = GROUPS - 2
            sp.wait_ge(kept, order(g, 7, PLAN[7][0]) + 1)
            load(wkv, "l1_wkv", g + 1, kv_loaded)
            sp.wait_ge(kept, order(g, 9, PLAN[9][0]) + 1)
            load(wq[1], "l1_wq", 2 * g + 3, q_loaded[1])
            sp.wait_ge(turned_kept, NT * GROUPS + 2 + CREDIT)
            core.load_arena(sp, A, 1)
            sp.dma_start(core.wmod[:], A["wmod2"]).then_inc(core.s_wmod, 16)

        @block.tensor
        def _(pe):
            def group(what, n):
                b, part, c, m = what
                if not isinstance(n, int) or n >= NF:
                    pe.wait_ge(kept, n)
                elif n >= 2:
                    pe.wait_ge(kept, n - 1)
                W = bank(n)
                if part == "v":
                    for j in range(2):
                        t = (2 * c + j) * P
                        for kk in range(KT):
                            at = (MAPS * KT * HD) + kk * VD
                            last = pe.matmul(W[:, j * VD:(j + 1) * VD], ht[:, kk, t:t + P], wkv[:, at:at + VD],
                                             start=(kk == 0), stop=(kk == KT - 1))
                else:
                    w = wkv if part == "k" else wq[b]
                    if not isinstance(n, int) or n >= NF:
                        parts = w_parts[0 if part == "k" or b == 1 else 1]
                        passes = [(mw, mh, kk) for mw, mh in ((0, 0), (0, 1), (1, 0)) for kk in range(KT)]
                        for step, (mw, mh, kk) in enumerate(passes):
                            at = (m * KT + kk) * HD
                            last = pe.matmul(W, parts[mw][:, at:at + HD], h_parts[mh][:, kk, c * BANK:c * BANK + BANK],
                                             start=(step == 0), stop=(step == len(passes) - 1))
                        last.then_inc(projected, 1)
                        return
                    for kk in range(KT):
                        at = (m * KT + kk) * HD
                        last = pe.matmul(W, w[:, at:at + HD], ht[:, kk, c * BANK:c * BANK + BANK],
                                         start=(kk == 0), stop=(kk == KT - 1))
                last.then_inc(projected, 1)

            def scores(g, s, m):
                b, i = (s // TILES) % 2, s % TILES
                pe.wait_ge(exped, MICRO * g + MAPS * (s - 1) + m + 1 + CREDIT)
                n = causal_blocks(i) * P
                for c in range(0, n, BANK):
                    e = min(n, c + BANK)
                    pe.matmul(S[m][:, c:e], q[b][m][:, i * P:i * P + P], k[m][:, c:e], start=True, stop=(e < n))
                pe.matmul(S[m][:, n - P:n], core.ident_bf[:], core.causal_bf[:], start=False,
                          stop=True).then_inc(scored, 1)

            def turn(g, t):
                pe.wait_ge(mixed_done, STEPS * g + t + 1 + CREDIT)
                for c in range(chunks[t]):
                    n = turn_no(g, "p", t, c)
                    to = turn_bank(g, "p", t, c)
                    pe.wait_ge(turned_kept, n - 2 + 1 + CREDIT)
                    for j in range(4 * c, min(4 * c + 4, causal_blocks(t % TILES))):
                        last = pe.transpose(to[:, (j % 4) * P:(j % 4) * P + P], mixed[:, t % 2, j * P:j * P + P],
                                            core.ident[:])
                    last.then_inc(turned, 1)

            def turn_out(g, t):
                n = turn_no(g, "o", t, 0)
                to = turn_bank(g, "o", t, 0)
                pe.wait_ge(on_done, STEPS * g + t + 1 + CREDIT)
                pe.wait_ge(turned_kept, n - 2 + 1 + CREDIT)
                for j in range(KT):
                    last = pe.transpose(to[:, j * P:j * P + P], on[:, t % 2, j * P:j * P + P], core.ident[:])
                last.then_inc(turned, 1)

            def values(g, t):
                pe.wait_ge(o_kept, STEPS * g + t + 1)
                n = causal_blocks(t % TILES)
                for j in range(n):
                    if j % 4 == 0:
                        pe.wait_ge(turned_kept, turn_no(g, "p", t, j // 4) + 1 + CREDIT)
                    last = pe.matmul(O, mixed_t[:, t % 2, j, :], v[:, j, :], start=(j == 0), stop=(j == n - 1))
                last.then_inc(valued, 1)

            def kv_group(g, is_last):
                for s in range(3, LAST + 1):
                    if s in (8, 12):
                        c = (s - 8) // 4
                        at = 6 if c == 0 else 9
                        pe.wait_ge(kept, order(g, at, PLAN[at][-1]) + 1)
                    if s == 4:
                        pe.wait_ge(kept, NG * g + NF)
                    if s == STEPS and not is_last:
                        pe.wait_ge(kept, order(g, 15, PLAN[15][1]) + 1)
                    if active(s, is_last):
                        for m in range(MAPS):
                            scores(g, s, m)
                    if active(s - 1, is_last):
                        turn(g, s - 1)
                    groups = [what for what in PLAN.get(s, []) if not (is_last and (what[0] == 0 or s >= 15))]
                    early = groups[0:0 if s == STEPS + 1 else 1]
                    for what in early:
                        if s == 5:
                            pe.wait_ge(rest_done, 3 * g + 2)
                        if s == 10:
                            pe.wait_ge(rest_done, 3 * g + 3)
                        if s == 15:
                            pe.wait_ge(rest_done, 3 * g + 4)
                        group(what, order(g, s, what))
                    if s - 2 in (2, 4, 6):
                        at = {2: 3, 4: 4, 6: 7}[s - 2]
                        pe.wait_ge(kept, order(g, at, PLAN[at][0]) + 1)
                    if s - 2 == STEPS and not is_last:
                        pe.wait_ge(kept, order(g, 17, PLAN[17][0]) + 1)
                    if active(s - 2, is_last):
                        values(g, s - 2)
                    for what in groups[len(early):]:
                        group(what, order(g, s, what))
                    turn_out(g, s - 3)

            pe.sem_inc(valued, CREDIT)
            pe.sem_inc(turned, 2)
            for n, what in enumerate(FIRST):
                if n == 0:
                    pe.wait_ge(core.early_in, 32)
                group(what, n)
                if n == 4:
                    pe.wait_ge(kept, 4)
                    for m in range(MAPS):
                        scores(0, 0, m)
            for s in (1, 2):
                for m in range(MAPS):
                    scores(0, s, m)
                turn(0, s - 1)
            pe.wait_ge(kept, NF - 1)
            values(0, 0)
            with pe.Fori(0, GROUPS - 1) as g:
                kv_group(g, False)
            kv_group(GROUPS - 1, True)
            pe.wait_ge(wo_scaled, 2 * GROUPS * KT)
            pe.wait_ge(turned_kept, NT * GROUPS + 2 + CREDIT)
            for i in range(TILES):
                if i >= 2:
                    pe.wait_ge(added, i - 1)
                for h in range(2 * GROUPS * KT):
                    last = pe.matmul(S[i % 2][:, 0:D], att[:, h, i * P:i * P + P], wo[:, h, :],
                                     start=(h == 0), stop=(h == 2 * GROUPS * KT - 1))
                last.then_inc(outed, 1)
                if i >= 1:
                    norm.turn(pe, i - 1, T)
            norm.turn(pe, TILES - 1, T)

        @block.scalar
        def _(act):
            act.sem_inc(exped, CREDIT)
            act.sem_inc(o_kept, 1)
            act.wait_ge(lam_step, 2)
            act.activation(lam[:, 2:4], lam[:, 0:2], ACT.Exp).then_inc(lam_step, 1)

            act.activation(h_parts[0][:], ht[:], ACT.Copy).then_inc(rounded, 1)

            def round_weights(b, w):
                act.activation(w_parts[b][0][:], w[:, 0:MAPS * KT * HD], ACT.Copy).then_inc(rounded, 1)

            def keep_k(what, n):
                b, part, c, m = what
                act.wait_ge(projected, n + 1)
                if isinstance(n, int) and 0 < n < NF:
                    act.wait_ge(kept, n)
                W = bank(n)
                act.activation(k[m][:, c * BANK:c * BANK + BANK], W, ACT.Identity,
                               bias=wkv[:, KV_BIAS + m:KV_BIAS + m + 1]).then_inc(kept, 1)

            def exps(g, s, m):
                n = causal_blocks(s % TILES) * P
                act.wait_ge(maxed, MICRO * g + MAPS * s + m + 1)
                act.wait_ge(mixed_done, STEPS * g + s - 2 + 1 + CREDIT)
                act.activation(ex[:, s % 2, m, 0:n], S[m][:, 0:n], ACT.Exp, bias=nmax[:, s % 2, m:m + 1],
                               accum_out=rsum[:, s % 2, m:m + 1]).then_inc(exped, 1)

            def keep_o(g, t):
                act.wait_ge(valued, STEPS * g + t + 1 + CREDIT)
                act.wait_ge(on_done, STEPS * g + t - 2 + 1 + CREDIT)
                act.activation(o[:, t % 2, :], O, ACT.Copy).then_inc(o_kept, 1)
                act.wait_ge(o_kept, STEPS * g + t + 1 + 1)
                act.activation(osq[:, t % 2, :], o[:, t % 2, :], ACT.Square, scale=float(VD) ** -0.5,
                               accum_out=ssq[:, t % 2:t % 2 + 1]).then_inc(squared, 1)

            def kv_group(g, is_last):
                for s in range(3, LAST + 1):
                    if active(s, is_last):
                        for m in range(MAPS):
                            exps(g, s, m)
                    ks = [what for what in PLAN.get(s, []) if what[1] == "k" and not (is_last and s >= 15)]
                    for what in ks[0:1]:
                        keep_k(what, order(g, s, what))
                    if active(s - 2, is_last):
                        keep_o(g, s - 2)
                    for what in ks[1:]:
                        keep_k(what, order(g, s, what))
                    if s == 3:
                        act.wait_ge(q_loaded[1], 16 * (g + 1))
                        round_weights(0, wq[1])
                    if s == 8 and not is_last:
                        act.wait_ge(q_loaded[0], 16 * (g + 1))
                        round_weights(1, wq[0])
                    if s == 13 and not is_last:
                        act.wait_ge(kv_loaded, 16 * (g + 1))
                        act.wait_ge(projected, order(g, 9, PLAN[9][0]) + 1)
                        round_weights(0, wkv)

            for n, what in enumerate(FIRST):
                if what[1] == "k":
                    keep_k(what, n)
            for s in range(3):
                for m in range(MAPS):
                    exps(0, s, m)
            keep_o(0, 0)
            with act.Fori(0, GROUPS - 1) as g:
                kv_group(g, False)
            kv_group(GROUPS - 1, True)
            for i in range(TILES):
                norm.keep(act, i, T)

        @block.gpsimd
        def _(pool):
            pool.wait_ge(lam_loaded, 32)
            pool.wait_ge(wo_loaded, 32)
            for h in range(2 * GROUPS * KT):
                pool.tensor_scalar(wo[:, h, :], wo[:, h, :], subln[:, h % KT:h % KT + 1], 1.0 - LAMBDA_INIT,
                                   ALU.mult, ALU.mult).then_inc(wo_scaled, 1)

            def weights_rest(b, w, n):
                pool.wait_ge(rounded, n)
                pool.tensor_tensor(w_parts[b][1][:], w[:, 0:MAPS * KT * HD], w_parts[b][0][:],
                                   ALU.subtract).then_inc(rest_done, 1)

            def kv_group(g, is_last):
                for t in range(STEPS):
                    if t == 2:
                        weights_rest(0, wq[1], 3 * g + 2)
                    if t == 7 and not is_last:
                        weights_rest(1, wq[0], 3 * g + 3)
                    if t == 12 and not is_last:
                        weights_rest(0, wkv, 3 * g + 4)
                    pool.wait_ge(squared, STEPS * g + t + 1)
                    pool.tensor_tensor(mean_sq[:, t % 2:t % 2 + 1], ssq[:, t % 2:t % 2 + 1], core.eps[:],
                                       ALU.add).then_inc(meaned, 1)
                    pool.wait_ge(meaned, STEPS * g + t + 1)
                    pool.tensor_tensor(rms[:, t % 2:t % 2 + 1], mean_sq[:, t % 2:t % 2 + 1], core.half_neg[:],
                                       ALU.pow).then_inc(rms_done, 1)

            with pool.Fori(0, GROUPS - 1) as g:
                kv_group(g, False)
            kv_group(GROUPS - 1, True)
            for i in range(TILES):
                norm.root(pool, i)

        @block.vector
        def _(dve):
            dve.sem_inc(turned_kept, CREDIT + 2)
            dve.sem_inc(mixed_done, CREDIT)
            dve.sem_inc(on_done, CREDIT)
            dve.wait_ge(lam_loaded, 32)
            for j in range(2):
                dve.tensor_tensor_reduce(out=lam_rows[:, 2 * j, :], in0=lam_rows[:, 2 * j, :], in1=lam_rows[:, 2 * j + 1, :],
                                         scale=1.0, scalar=0.0, op0=ALU.mult, op1=ALU.add,
                                         accum_out=lam[:, j:j + 1]).then_inc(lam_step, 1)
            dve.wait_ge(lam_step, 3)
            dve.tensor_tensor(lam[:, 4:5], lam[:, 3:4], lam[:, 2:3], ALU.subtract).then_inc(lam_step, 1)
            dve.wait_ge(lam_step, 4)
            dve.tensor_scalar(lam[:, 5:6], lam[:, 4:5], -LAMBDA_INIT, None, ALU.add).then_inc(lam_step, 1)
            dve.wait_ge(lam_step, 5)

            def keep(what, n):
                b, part, c, m = what
                dve.wait_ge(projected, n + 1)
                if isinstance(n, int) and 0 < n < NF:
                    dve.wait_ge(kept, n)
                W = bank(n)
                if part == "q":
                    dve.tensor_scalar(q[b][m][:, c * BANK:c * BANK + BANK], W,
                                      wq[b][:, MAPS * KT * HD + m:MAPS * KT * HD + m + 1], SCALE,
                                      ALU.add, ALU.mult).then_inc(kept, 1)
                else:
                    dve.tensor_tensor(v[:, 2 * c:2 * c + 2, :], W.rearrange("p (t d) -> p t d", t=2),
                                      wkv[:, KV_BIAS + MAPS:].rearrange("p (a d) -> p a d", a=1).to_broadcast([P, 2, VD]),
                                      ALU.add).then_inc(kept, 1)

            def maxes(g, s):
                n = causal_blocks(s % TILES) * P
                for m in range(MAPS):
                    dve.wait_ge(scored, MICRO * g + MAPS * s + m + 1)
                    dve.tensor_reduce(nmax[:, s % 2, m:m + 1], S[m][:, 0:n], AX_X, ALU.max,
                                      negate=True).then_inc(maxed, 1)

            def turned_by(g, kind, t):
                return turn_no(g, kind, t, chunks[t] - 1 if kind == "p" else 0) + 1

            def mix(g, s):
                n = causal_blocks(s % TILES) * P
                b = s % 2
                dve.wait_ge(exped, MICRO * g + MAPS * s + 2 + CREDIT)
                dve.reciprocal(rinv[:, b, :], rsum[:, b, :]).then_inc(mix_step, 1)
                dve.wait_ge(mix_step, 3 * (STEPS * g + s) + 1)
                dve.tensor_tensor(rneg[:, b:b + 1], rinv[:, b, 1:2], lam[:, 5:6], ALU.mult).then_inc(mix_step, 1)
                dve.wait_ge(mix_step, 3 * (STEPS * g + s) + 2)
                dve.tensor_scalar(ex[:, b, 1, 0:n], ex[:, b, 1, 0:n], rneg[:, b:b + 1], None,
                                  ALU.mult).then_inc(mix_step, 1)
                dve.wait_ge(mix_step, 3 * (STEPS * g + s) + 3)
                if s >= 2:
                    dve.wait_ge(turned, turned_by(g, "p", s - 2))
                dve.scalar_tensor_tensor(out=mixed[:, b, 0:n], in0=ex[:, b, 0, 0:n], scalar=rinv[:, b, 0:1],
                                         in1=ex[:, b, 1, 0:n], op0=ALU.mult, op1=ALU.add).then_inc(mixed_done, 1)

            def keep_turned(g, t):
                for c in range(chunks[t]):
                    m = min(4, causal_blocks(t % TILES) - 4 * c)
                    dve.wait_ge(turned, turn_no(g, "p", t, c) + 1)
                    if c == 0:
                        dve.wait_ge(valued, STEPS * g + t - 2 + 1 + CREDIT)
                    dve.tensor_copy(mixed_t[:, t % 2, 4 * c:4 * c + m, :],
                                    turn_bank(g, "p", t, c)[:, 0:m * P].rearrange("p (t d) -> p t d", t=m)
                                    ).then_inc(turned_kept, 1)

            def scale_rows(g, t):
                dve.wait_ge(rms_done, STEPS * g + t + 1)
                dve.wait_ge(turned, turned_by(g, "o", t - 2))
                dve.tensor_scalar(on[:, t % 2, :], o[:, t % 2, :], rms[:, t % 2:t % 2 + 1], None,
                                  ALU.mult).then_inc(on_done, 1)

            def keep_out(g, t):
                dve.wait_ge(turned, turn_no(g, "o", t, 0) + 1)
                i = t % TILES
                at = 2 * KT * g + KT * (t // TILES)
                dve.tensor_copy(att[:, bass.ds(at, KT), i * P:i * P + P],
                                turn_bank(g, "o", t, 0)[:, 0:VD].rearrange("p (e d) -> p e d", e=KT)
                                ).then_inc(turned_kept, 1)

            def kv_group(g, is_last):
                for s in range(3, LAST + 1):
                    if active(s, is_last):
                        maxes(g, s)
                    scale_rows(g, s - 3)
                    if active(s - 1, is_last):
                        keep_turned(g, s - 1)
                    if active(s, is_last):
                        mix(g, s)
                    for what in PLAN.get(s, []):
                        if what[1] != "k" and not (is_last and (what[0] == 0 or s >= 15)):
                            keep(what, order(g, s, what))
                    keep_out(g, s - 3)

            for n, what in enumerate(FIRST):
                if what[1] != "k":
                    keep(what, n)
            dve.wait_ge(rounded, 1)
            dve.tensor_tensor(h_parts[1][:], ht[:], h_parts[0][:], ALU.subtract).then_inc(rest_done, 1)
            for s in range(3):
                maxes(0, s)
                if s > 0:
                    keep_turned(0, s - 1)
                mix(0, s)
            with dve.Fori(0, GROUPS - 1) as g:
                kv_group(g, False)
            kv_group(GROUPS - 1, True)
            add_gated(dve, core, 0, bo, wo_loaded, 32, gated, bo_gated, [S[i % 2][:, 0:D] for i in range(TILES)],
                      outed, added, norm)


def swiglu(core, A, hidden, scaled, run, units_before, parts_before, norm):
    nc = core.nc
    x, ht, ps = core.x, core.ht, core.ps
    sizes = [min(P, hidden - f) for f in range(0, hidden, P)]
    NF = len(sizes)
    TILES_BEFORE = TILES * run
    FULL = hidden // P
    ITEMS = ["h0"] + list(range(FULL)) + ["h1"]
    rests_before = parts_before + 1
    UNITS = [(c, f) for c in range(CHUNKS) for f in range(NF)]
    with ExitStack() as ctx:
        wg, wu, wd, *scales_of = carve(core.arena, (KT, hidden), (KT, hidden), (NF, D), *scaled * [(2, NF), (D,)])
        if scaled:
            scales, down_s = scales_of
        gate_row = core.sb("gate_row", [P, D], F32, ctx)
        sil = core.sb("sil", [P, 2, BANK], F32, ctx)
        hid = core.sb("hid", [P, CHUNKS, NF, BANK], F32, ctx)
        gated = core.sb("gated", [P, 2, D], F32, ctx)
        h_parts = [core.sb(f"h_part{m}", [P, KT, TOKENS], F32R, ctx) for m in range(2)]
        w_parts = [core.sb(f"f_part{m}", [P, FULL, 2, KT, P], F32R, ctx) for m in range(2)]
        s = core.ffn_sems

        def pieces(at):
            item = ITEMS[at]
            if isinstance(item, str):
                c = slice(int(item[1]) * BANK, int(item[1]) * BANK + BANK)
                return [(ht[:, :, c], h_parts[0][:, :, c], h_parts[1][:, :, c])]
            return [(w[:, :, item * P:item * P + P], w_parts[0][:, item, part], w_parts[1][:, item, part])
                    for part, w in enumerate((wg, wu))]
        mod = Modulation(core, norm.layer, 6, 7)
        OUT = [ps[:, b, 0:D] for b in (4, 5)]
        turn_banks = [ps[:, b, :] for b in (6, 7)]
        block = ctx.enter_context(nc.Block(no_gpsimd_drain=True))

        @block.sync
        def _(sp):
            core.load_early(sp, A, norm.layer)
            mod.load_next(sp, A)

        @block.tensor
        def _(pe):
            def up(n):
                c, f = UNITS[n]
                m = sizes[f]
                if n >= 2:
                    pe.wait_ge(s["hid_done"], units_before + n - 1)
                if f < FULL:
                    pe.wait_ge(s["rest_done"], rests_before + (f + 2 if c == 0 else len(ITEMS)))
                    passes = [(mw, mh, k) for mw, mh in ((0, 0), (0, 1), (1, 0)) for k in range(KT)]
                    for part in range(2):
                        for at, (mw, mh, k) in enumerate(passes):
                            last = pe.matmul(ps[:, 2 * (n % 2) + part, :], w_parts[mw][:, f, part, k, :],
                                             h_parts[mh][:, k, c * BANK:c * BANK + BANK],
                                             start=(at == 0), stop=(at == len(passes) - 1))
                    last.then_inc(s["upped"], 1)
                    return
                for part, w in enumerate((wg, wu)):
                    for k in range(KT):
                        last = pe.matmul(ps[0:m, 2 * (n % 2) + part, :], w[:, k, f * P:f * P + m],
                                         ht[:, k, c * BANK:c * BANK + BANK], start=(k == 0), stop=(k == KT - 1))
                last.then_inc(s["upped"], 1)

            def down(c):
                pe.wait_ge(s["hid_done"], units_before + NF * (c + 1))
                for j in range(4):
                    i = 4 * c + j
                    if i >= 2:
                        pe.wait_ge(s["gated"], TILES_BEFORE + i - 1)
                    for f in range(NF):
                        m = sizes[f]
                        last = pe.matmul(OUT[i % 2], hid[0:m, c, f, j * P:j * P + P], wd[0:m, f, :],
                                         start=(f == 0), stop=(f == NF - 1))
                    last.then_inc(s["downed"], 1)
                    if c == 1:
                        for t in ((0, 1), (2, 3), (4,), (5, 6))[j]:
                            norm.turn(pe, t, turn_banks)

            mod.products(pe)
            pe.wait_ge(core.arena_in, 16 * norm.layer)
            for n in range(len(UNITS)):
                up(n)
                if n == NF + 1:
                    down(0)
            down(1)
            norm.turn(pe, TILES - 1, turn_banks)

        @block.scalar
        def _(act):
            def rounding(at):
                for whole, high, _ in pieces(at):
                    last = act.activation(high, whole, ACT.Copy)
                last.then_inc(s["rounded"], 1)

            mod.condition(act)
            act.wait_ge(core.arena_in, 16 * norm.layer)
            for at in range(3):
                rounding(at)
            for n, (c, f) in enumerate(UNITS):
                if n + 3 < len(ITEMS):
                    rounding(n + 3)
                m = sizes[f]
                act.wait_ge(s["upped"], units_before + n + 1)
                if n >= 2:
                    act.wait_ge(s["hid_done"], units_before + n - 1)
                act.activation(sil[0:m, n % 2, :], ps[0:m, 2 * (n % 2), :], ACT.Silu,
                               scale=scales[0:m, 0, f:f + 1] if scaled else 1.0).then_inc(s["silued"], 1)
            for i in range(TILES):
                norm.keep(act, i, turn_banks)

        @block.gpsimd
        def _(pool):
            for i in range(TILES):
                norm.root(pool, i)

        @block.vector
        def _(dve):
            row = core.gate[:, 1, :]
            mod.spread(dve)
            dve.wait_ge(core.arena_in, 16 * norm.layer)
            if scaled:
                dve.tensor_tensor(gate_row[:], row, down_s[:], ALU.mult).then_inc(s["rest_done"], 1)
                dve.wait_ge(s["rest_done"], 1)
                row = gate_row[:]

            def rest(at):
                dve.wait_ge(s["rounded"], parts_before + at + 1)
                for whole, high, low in pieces(at):
                    last = dve.tensor_tensor(low, whole, high, ALU.subtract)
                last.then_inc(s["rest_done"], 1)

            for at in range(3):
                rest(at)
            mod.keep_cols(dve)
            mod.keep_rows(dve)

            def hidden_unit(n):
                c, f = UNITS[n]
                m = sizes[f]
                dve.wait_ge(s["silued"], units_before + n + 1)
                if scaled:
                    dve.scalar_tensor_tensor(out=hid[0:m, c, f, :], in0=ps[0:m, 2 * (n % 2) + 1, :],
                                             scalar=scales[0:m, 1, f:f + 1], in1=sil[0:m, n % 2, :],
                                             op0=ALU.mult, op1=ALU.mult).then_inc(s["hid_done"], 1)
                else:
                    dve.tensor_tensor(hid[0:m, c, f, :], ps[0:m, 2 * (n % 2) + 1, :], sil[0:m, n % 2, :],
                                      ALU.mult).then_inc(s["hid_done"], 1)

            def add(c):
                for j in range(4):
                    i = 4 * c + j
                    dve.wait_ge(s["downed"], TILES_BEFORE + i + 1)
                    dve.tensor_tensor(gated[:, i % 2, :], OUT[i % 2], row, ALU.mult).then_inc(s["gated"], 1)
                    dve.wait_ge(s["gated"], TILES_BEFORE + i + 1)
                    dve.tensor_tensor(x[:, i, :], x[:, i, :], gated[:, i % 2, :], ALU.add).then_inc(s["added"], 1)
                    dve.wait_ge(s["added"], TILES_BEFORE + i + 1)
                    norm.stats(dve, i)
                    if c == 1:
                        norm.scale(dve, i)

            for n in range(len(UNITS)):
                if n + 3 < len(ITEMS):
                    rest(n + 3)
                hidden_unit(n)
                if n == NF + 1:
                    add(0)
            for i in range(4):
                norm.scale(dve, i)
            add(1)


def ffn_l1(core, A, norm):
    swiglu(core, A, 704, True, 0, 0, 0, norm)


def ffn_l2(core, A, norm):
    swiglu(core, A, 1024, False, 1, 2 * len(range(0, 704, P)), 2 + 704 // P, norm)


def attention_l2(core, A, norm):
    nc = core.nc
    HEADS, HD = 4, 64
    STEPS = 2 * HEADS
    ROUNDS = TILES // 2
    SCALE = 0.5
    x, ht, ps = core.x, core.ht, core.ps
    with ExitStack() as ctx:
        w, bias = carve(core.early, (3, KT, D), (3, KT))
        wo = core.sb("wo", [P, KT, D], F32, ctx)
        bo = core.sb("bo", [P, D], F32, ctx)
        qt = core.sb("qt", [P, KT, TOKENS], F32, ctx)
        kt = core.sb("kt", [P, KT, TOKENS], F32, ctx)
        v = core.sb("v", [P, TILES, D], F32, ctx)
        qc = core.sb("qc", [P, 2, KT, P], F32, ctx)
        probs = core.sb("probs", [P, 2, TOKENS], F32, ctx)
        probs_t = core.sb("probs_t", [P, 2, TILES, P], F32, ctx)
        nmax = core.sb("nmax", [P, 2], F32, ctx)
        rsum = core.sb("rsum", [P, 2], F32, ctx)
        rinv = core.sb("rinv", [P, 2], F32, ctx)
        att = core.sb("att", [P, 2, KT, P], F32, ctx)
        gated = core.sb("gated", [P, 2, D], F32, ctx)
        wo_loaded = core.sem("wo_loaded", ctx)
        projected = core.sem("projected", ctx)
        kept = core.sem("kept", ctx)
        q_copied = core.sem("q_copied", ctx)
        scored = core.sem("scored", ctx)
        maxed = core.sem("maxed", ctx)
        exped = core.sem("exped", ctx)
        inverted = core.sem("inverted", ctx)
        normed = core.sem("normed", ctx)
        turned = core.sem("turned", ctx)
        turned_kept = core.sem("turned_kept", ctx)
        valued = core.sem("valued", ctx)
        att_kept = core.sem("att_kept", ctx)
        outed = core.sem("outed", ctx)
        gated_done = core.sem("gated_done", ctx)
        bo_done = core.sem("bo_done", ctx)
        CREDIT = 2
        LAST = STEPS + 4

        def active(u, is_last):
            return u < STEPS or not is_last
        S = [ps[:, 0:2, :].rearrange("p a b -> p (a b)"), ps[:, 2:4, :].rearrange("p a b -> p (a b)")]
        T = [ps[:, 4, :], ps[:, 5, :]]
        V = ps[:, 6, 0:KT * P].rearrange("p (k q) -> p k q", k=KT)
        O = ps[:, 7, 0:D]
        GROUPS = [(part, m, c) for m in range(KT) for c in range(CHUNKS) for part in (0, 1)] + [(2, c, 0) for c in range(4)]
        block = ctx.enter_context(nc.Block(no_gpsimd_drain=True))

        @block.sync
        def _(sp):
            sp.dma_start(wo[:], A["l2_wo"]).then_inc(wo_loaded, 16)
            sp.dma_start(bo[:], A["l2_bo"].to_broadcast([P, D])).then_inc(wo_loaded, 16)
            core.load_arena(sp, A, 2)

        @block.tensor
        def _(pe):
            pe.sem_inc(valued, CREDIT)
            pe.sem_inc(outed, 1)
            pe.wait_ge(core.early_in, 48)
            for n, (part, m, c) in enumerate(GROUPS):
                if n >= 4:
                    pe.wait_ge(kept, n - 3)
                W = ps[:, 4 + n % 4, :]
                if part < 2:
                    for k in range(KT):
                        last = pe.matmul(W, w[:, part, k, m * P:m * P + P], ht[:, k, c * BANK:c * BANK + BANK],
                                         start=(k == 0), stop=(k == KT - 1))
                else:
                    for j in range(2):
                        t = (2 * m + j) * P
                        for k in range(KT):
                            last = pe.matmul(W[:, j * D:j * D + D], ht[:, k, t:t + P], w[:, part, k, :],
                                             start=(k == 0), stop=(k == KT - 1))
                last.then_inc(projected, 1)
            pe.wait_ge(kept, len(GROUPS))

            def scores(g, u):
                h, slot = u % HEADS, (u // HEADS) % 2
                if h == 0:
                    pe.wait_ge(q_copied, 2 * g + u // HEADS + 1)
                pe.wait_ge(exped, STEPS * g + u - 2 + 1 + CREDIT)
                r = HD * (h % 2)
                for c in range(CHUNKS):
                    last = pe.matmul(S[u % 2][:, c * BANK:c * BANK + BANK], qc[r:r + HD, slot, h // 2, :],
                                     kt[r:r + HD, h // 2, c * BANK:c * BANK + BANK], start=True, stop=True)
                last.then_inc(scored, 1)

            def turn(g, u):
                pe.wait_ge(normed, STEPS * g + u + 1)
                for c in range(2):
                    pe.wait_ge(turned_kept, 2 * (STEPS * g + u) + c - 2 + 1 + CREDIT)
                    for j in range(4):
                        last = pe.transpose(T[c][:, j * P:j * P + P], probs[:, u % 2, (4 * c + j) * P:(4 * c + j + 1) * P],
                                            core.ident[:])
                    last.then_inc(turned, 1)

            def values(g, u):
                h = u % HEADS
                if h == 0:
                    pe.wait_ge(att_kept, 2 * g + u // HEADS + 1)
                r = HD * (h % 2)
                for j in range(TILES):
                    if j % 4 == 0:
                        pe.wait_ge(turned_kept, 2 * (STEPS * g + u) + j // 4 + 1 + CREDIT)
                    last = pe.matmul(V[r:r + HD, h // 2, :], v[:, j, h * HD:h * HD + HD], probs_t[:, u % 2, j, :],
                                     start=(j == 0), stop=(j == TILES - 1))
                last.then_inc(valued, 1)

            def out(g, t):
                pe.wait_ge(att_kept, 2 * g + t + 1 + 1)
                pe.wait_ge(gated_done, 2 * g + t + 1)
                for k in range(KT):
                    last = pe.matmul(O, att[:, t, k, :], wo[:, k, :], start=(k == 0), stop=(k == KT - 1))
                last.then_inc(outed, 1)

            def round_(g, is_last):
                for u in range(HEADS, LAST):
                    if active(u, is_last):
                        scores(g, u)
                    if active(u - 1, is_last):
                        turn(g, u - 1)
                    if is_last and u == LAST - 2:
                        for i in range(5):
                            norm.turn(pe, i, T)
                    if u == 7 or u == 11:
                        out(g, u // 8)
                    if active(u - 2, is_last):
                        values(g, u - 2)

            for u in range(HEADS):
                scores(0, u)
                if u >= 1:
                    turn(0, u - 1)
                if u >= 2:
                    values(0, u - 2)
            pe.wait_ge(wo_loaded, 32)
            with pe.Fori(0, ROUNDS - 1) as g:
                round_(g, False)
            round_(ROUNDS - 1, True)
            for i in range(5, TILES):
                norm.turn(pe, i, T)

        @block.scalar
        def _(act):
            act.sem_inc(exped, CREDIT)
            act.sem_inc(att_kept, 1)
            act.wait_ge(core.early_in, 48)
            for n, (part, m, c) in enumerate(GROUPS):
                if part == 0:
                    continue
                act.wait_ge(projected, n + 1)
                act.wait_ge(kept, n)
                W = ps[:, 4 + n % 4, :]
                if part == 1:
                    act.activation(kt[:, m, c * BANK:c * BANK + BANK], W, ACT.Identity,
                                   bias=bias[:, 1, m:m + 1]).then_inc(kept, 1)
                else:
                    act.activation(v[:, 2 * m:2 * m + 2, :], W.rearrange("p (t d) -> p t d", t=2),
                                   ACT.Copy).then_inc(kept, 1)

            def exps(g, u):
                act.wait_ge(maxed, STEPS * g + u + 1)
                if u >= 2:
                    act.wait_ge(turned, 2 * (STEPS * g + u - 2) + 2)
                act.activation(probs[:, u % 2, :], S[u % 2], ACT.Exp, bias=nmax[:, u % 2:u % 2 + 1],
                               accum_out=rsum[:, u % 2:u % 2 + 1]).then_inc(exped, 1)

            def keep_att(g, t):
                act.wait_ge(valued, STEPS * g + HEADS * (t + 1) + CREDIT)
                act.wait_ge(outed, 2 * g + t - 1 + 1)
                for k in range(KT):
                    last = act.activation(att[:, t, k, :], V[:, k, :], ACT.Identity, bias=bias[:, 2, k:k + 1])
                last.then_inc(att_kept, 1)

            for u in range(HEADS):
                exps(0, u)

            def round_(g, is_last):
                for u in range(HEADS, LAST):
                    if active(u, is_last):
                        exps(g, u)
                    if u == 5 or u == 9:
                        keep_att(g, u // 8)

            with act.Fori(0, ROUNDS - 1) as g:
                round_(g, False)
            round_(ROUNDS - 1, True)
            for i in range(TILES):
                norm.keep(act, i, T)

        @block.gpsimd
        def _(pool):
            for i in range(TILES):
                norm.root(pool, i)

        @block.vector
        def _(dve):
            dve.sem_inc(turned_kept, CREDIT)
            dve.sem_inc(gated_done, 1)
            dve.wait_ge(core.early_in, 48)
            for n, (part, m, c) in enumerate(GROUPS):
                if part:
                    continue
                dve.wait_ge(projected, n + 1)
                if n > 0:
                    dve.wait_ge(kept, n)
                dve.tensor_scalar(qt[:, m, c * BANK:c * BANK + BANK], ps[:, 4 + n % 4, :], bias[:, 0, m:m + 1], SCALE,
                                  ALU.add, ALU.mult).then_inc(kept, 1)
            dve.wait_ge(wo_loaded, 32)
            dve.tensor_tensor(gated[:, 0, :], core.gate[:, 0, :], bo[:], ALU.mult).then_inc(bo_done, 1)
            dve.wait_ge(bo_done, 1)
            dve.tensor_tensor(x[:], x[:], gated[:, 0:1, :].to_broadcast([P, TILES, D]), ALU.add).then_inc(bo_done, 1)
            dve.wait_ge(bo_done, 2)
            dve.wait_ge(kept, len(GROUPS))

            def copy_q(g, t):
                tile = 2 * g + t
                at = slice(tile * P, tile * P + P) if isinstance(g, int) else bass.ds(tile * P, P)
                dve.tensor_copy(qc[:, t % 2, :, :], qt[:, :, at]).then_inc(q_copied, 1)

            def maxes(g, u):
                dve.wait_ge(scored, STEPS * g + u + 1)
                dve.tensor_reduce(nmax[:, u % 2:u % 2 + 1], S[u % 2], AX_X, ALU.max, negate=True).then_inc(maxed, 1)

            def scale_rows(g, u):
                dve.wait_ge(exped, STEPS * g + u + 1 + CREDIT)
                dve.reciprocal(rinv[:, u % 2:u % 2 + 1], rsum[:, u % 2:u % 2 + 1]).then_inc(inverted, 1)
                dve.wait_ge(inverted, STEPS * g + u + 1)
                dve.tensor_scalar(probs[:, u % 2, :], probs[:, u % 2, :], rinv[:, u % 2:u % 2 + 1], None,
                                  ALU.mult).then_inc(normed, 1)

            def keep_turned(g, u):
                for c in range(2):
                    dve.wait_ge(turned, 2 * (STEPS * g + u) + c + 1)
                    if c == 0:
                        dve.wait_ge(valued, STEPS * g + u - 2 + 1 + CREDIT)
                    dve.tensor_copy(probs_t[:, u % 2, 4 * c:4 * c + 4, :],
                                    T[c].rearrange("p (t d) -> p t d", t=4)).then_inc(turned_kept, 1)

            def add(g, t):
                dve.wait_ge(outed, 2 * g + t + 1 + 1)
                dve.tensor_tensor(gated[:, t, :], O, core.gate[:, 0, :], ALU.mult).then_inc(gated_done, 1)
                dve.wait_ge(gated_done, 2 * g + t + 1 + 1)
                tile = 2 * g + t
                at = slice(tile, tile + 1) if isinstance(g, int) else bass.ds(tile, 1)
                dve.tensor_tensor(x[:, at, :], x[:, at, :], gated[:, t:t + 1, :], ALU.add).then_inc(bo_done, 1)

            def step(g, u, is_last):
                if active(u, is_last):
                    maxes(g, u)
                if u >= 1 and active(u - 1, is_last):
                    keep_turned(g, u - 1)
                if active(u, is_last):
                    scale_rows(g, u)

            def round_(g, is_last):
                for u in range(HEADS, LAST):
                    if u == 6 and not is_last:
                        copy_q(g, 2)
                    if u == 10 and not is_last:
                        copy_q(g, 3)
                    step(g, u, is_last)
                    if u == 7:
                        add(g, 0)
                    if is_last:
                        if u == 10:
                            dve.wait_ge(bo_done, 2 + TILES - 1)
                        if u < 11:
                            norm.stats(dve, u - HEADS)
                            norm.scale(dve, u - HEADS)
                add(g, 1)

            copy_q(0, 0)
            copy_q(0, 1)
            for u in range(HEADS):
                step(0, u, False)
            with dve.Fori(0, ROUNDS - 1) as g:
                round_(g, False)
            round_(ROUNDS - 1, True)
            dve.wait_ge(bo_done, 2 + TILES)
            norm.stats(dve, TILES - 1)
            norm.scale(dve, TILES - 1)


ROUND = 1.5 * 2.0 ** 23
TURN = 6.283185
FRAME = 64


def recurrence_l3(core, A, norm):
    nc = core.nc
    x, ht, ps = core.x, core.ht, core.ps
    FRAMES = TOKENS // FRAME
    with ExitStack() as ctx:
        def buf(name, shape=(P, TOKENS), dt=F32):
            return core.sb("r_" + name, list(shape), dt, ctx)

        w_in, w_g, cols = carve(core.early, (KT, D), (2, KT, P), (6,))
        w_out = buf("w_out", (P, KT, D))
        b_out = buf("b_out", (P, D))
        xh = buf("xh", (P, KT, TOKENS))
        gx = buf("gx")
        ga = buf("ga")
        c = buf("c", (P, 16))
        r1 = buf("r1")
        r2 = buf("r2")
        g1 = buf("g1")
        g2 = buf("g2")
        yr = buf("yr")
        yi = buf("yi")
        p1 = buf("p1")
        p2 = buf("p2")
        keep = buf("keep")
        phi = buf("phi")
        ends = buf("ends", (P, FRAMES))
        ends_k = buf("ends_k", (P, FRAMES))
        ends_f = buf("ends_f", (P, FRAMES))
        base = buf("base", (P, FRAMES + 1))
        ones = buf("ones", (P, FRAMES))
        f1 = buf("f1")
        f2 = buf("f2")
        k1 = buf("k1")
        k2 = buf("k2")
        sin1 = buf("sin1")
        cos1 = buf("cos1")
        sin2 = buf("sin2")
        cos2 = buf("cos2")
        zr = buf("zr")
        zi = buf("zi")
        m1 = buf("m1")
        m2 = buf("m2")
        sr = buf("sr")
        si = buf("si")
        h = buf("h", (P, KT, TOKENS))
        gated = buf("gated", (P, 2, D))
        out_loaded = core.sem("r_out_loaded", ctx)
        projected = core.sem("r_projected", ctx)
        kept = core.sem("r_kept", ctx)
        gates = core.sem("r_gates", ctx)
        gated_act = core.sem("r_gated_act", ctx)
        step = core.sem("r_step", ctx)
        c_ready = core.sem("r_c_ready", ctx)
        a_exp = core.sem("r_a_exp", ctx)
        decayed = core.sem("r_decayed", ctx)
        angle = core.sem("r_angle", ctx)
        waved = core.sem("r_waved", ctx)
        squared = core.sem("r_squared", ctx)
        rooted = core.sem("r_rooted", ctx)
        half_done = core.sem("r_half", ctx)
        z_done = core.sem("r_z_done", ctx)
        from_dve = core.sem("r_from_dve", ctx)
        from_pool = core.sem("r_from_pool", ctx)
        ready = core.sem("r_ready", ctx)
        keep_done = core.sem("r_keep", ctx)
        outed = core.sem("r_outed", ctx)
        added = core.sem("r_added", ctx)
        bo_done = core.sem("r_bo", ctx)
        turn_banks = [ps[:, b, :] for b in (4, 5)]
        block = ctx.enter_context(nc.Block(no_gpsimd_drain=True))

        @block.sync
        def _(sp):
            sp.dma_start(w_out[:], A["l3_wout"]).then_inc(out_loaded, 16)
            sp.dma_start(b_out[:], A["l3_bout"].to_broadcast([P, D])).then_inc(out_loaded, 16)
            core.load_arena(sp, A, 3)

        @block.gpsimd
        def _(pool):
            pool.memset(keep[:], 1.0).then_inc(keep_done, 1)
            pool.wait_ge(keep_done, 1)
            pool.memset(keep[:].rearrange("p (f n) -> p f n", n=FRAME)[:, :, 0:1], 0.0).then_inc(keep_done, 1)
            pool.memset(ones[:], 1.0).then_inc(keep_done, 1)
            pool.memset(base[:], 0.0).then_inc(keep_done, 1)
            TT = pool.tensor_tensor
            pool.wait_ge(gated_act, 2)
            TT(xh[:, 0, :], xh[:, 0, :], gx[:], ALU.mult)
            TT(xh[:, 1, :], xh[:, 1, :], gx[:], ALU.mult).then_inc(from_pool, 1)
            pool.wait_ge(from_pool, 1)
            pool.wait_ge(rooted, 2)
            TT(g1[:], xh[:, 1, :], sr[:], ALU.mult).then_inc(from_pool, 1)
            pool.wait_ge(waved, 4)
            pool.wait_ge(from_dve, 1)
            TT(g2[:], yr[:], sin1[:], ALU.mult).then_inc(from_pool, 1)
            pool.wait_ge(from_dve, 2)
            TT(g1[:], f1[:], sin1[:], ALU.mult).then_inc(from_pool, 1)
            for i in range(TILES):
                norm.root(pool, i)

        @block.tensor
        def _(pe):
            pe.wait_ge(core.early_in, 64)
            for m in range(KT):
                for n in range(CHUNKS):
                    for k in range(KT):
                        last = pe.matmul(ps[:, 2 * m + n, :], w_in[:, k, m * P:m * P + P],
                                         ht[:, k, n * BANK:n * BANK + BANK], start=(k == 0), stop=(k == KT - 1))
                    last.then_inc(projected, 1)
            pe.wait_ge(kept, KT)
            for g in (1, 0):
                for n in range(CHUNKS):
                    for k in range(KT):
                        last = pe.matmul(ps[:, 4 + 2 * g + n, :], w_g[:, g, k, :], xh[:, k, n * BANK:n * BANK + BANK],
                                         start=(k == 0), stop=(k == KT - 1))
                last.then_inc(gates, 1)
            pe.wait_ge(out_loaded, 32)
            pe.wait_ge(ready, 2)
            for i in range(TILES):
                for k in range(KT):
                    last = pe.matmul(ps[:, i % 4, 0:D], h[:, k, i * P:i * P + P], w_out[:, k, :],
                                     start=(k == 0), stop=(k == KT - 1))
                last.then_inc(outed, 1)
                if 3 <= i < TILES - 1:
                    pe.wait_ge(added, i - 2)
                if i >= 1:
                    norm.turn(pe, i - 1, turn_banks)
            norm.turn(pe, TILES - 1, turn_banks)

        @block.scalar
        def _(act):
            for m in range(KT):
                act.wait_ge(projected, 2 * m + 2)
                act.activation(xh[:, m, :], ps[:, 2 * m:2 * m + 2, :].rearrange("p a b -> p (a b)"), ACT.Identity,
                               bias=cols[:, m:m + 1]).then_inc(kept, 1)
            act.wait_ge(gates, 1)
            act.activation(ga[:], ps[:, 6:8, :].rearrange("p a b -> p (a b)"), ACT.Sigmoid,
                           bias=cols[:, 3:4]).then_inc(gated_act, 1)
            act.wait_ge(gates, 2)
            act.activation(gx[:], ps[:, 4:6, :].rearrange("p a b -> p (a b)"), ACT.Sigmoid,
                           bias=cols[:, 2:3]).then_inc(gated_act, 1)
            act.wait_ge(c_ready, 1)
            act.activation(c[:, 2:3], c[:, 1:2], ACT.Exp, scale=-1.0).then_inc(a_exp, 1)
            act.wait_ge(c_ready, 2)
            act.wait_ge(c_ready, 3)
            act.activation(f1[:], ga[:], ACT.Copy, scale=c[:, 10:11]).then_inc(c_ready, 1)
            act.activation(r2[:], ga[:], ACT.Exp, scale=c[:, 8:9]).then_inc(decayed, 1)
            act.activation(r1[:], ga[:], ACT.Exp, scale=c[:, 9:10]).then_inc(decayed, 1)
            for n, (dst, src) in enumerate(((cos2, f2), (sin2, f1))):
                act.wait_ge(angle, n + 1)
                act.activation(dst[:], src[:], ACT.Sin, scale=TURN).then_inc(waved, 1)
            act.wait_ge(z_done, 1)
            act.activation(m1[:], zr[:], ACT.Square).then_inc(squared, 1)
            act.wait_ge(z_done, 2)
            act.activation(m2[:], zi[:], ACT.Square).then_inc(squared, 1)
            act.wait_ge(squared, 3)
            act.activation(m2[:], m1[:], ACT.Sqrt).then_inc(rooted, 1)
            act.wait_ge(half_done, 1)
            act.activation(sr[:], k1[:], ACT.Sqrt, scale=0.5).then_inc(rooted, 1)
            for n, (dst, src) in enumerate(((cos1, p2), (sin1, p1))):
                act.wait_ge(angle, n + 3)
                act.activation(dst[:], src[:], ACT.Sin, scale=TURN).then_inc(waved, 1)
            for i in range(TILES):
                norm.keep(act, i, turn_banks)

        @block.vector
        def _(dve):
            done = [0]

            def after(ins):
                ins.then_inc(step, 1)
                done[0] += 1
                dve.wait_ge(step, done[0])

            TT, TS, STT = dve.tensor_tensor, dve.tensor_scalar, dve.scalar_tensor_tensor
            dve.wait_ge(core.early_in, 64)
            a_re, a_im = cols[:, 4:5], cols[:, 5:6]
            after(TS(c[:, 0:1], a_re, -1.0, None, ALU.mult))
            dve.tensor_tensor(c[:, 1:2], c[:, 0:1], a_re, ALU.max).then_inc(c_ready, 1)
            after(TS(c[:, 3:4], a_re, 0.0, None, ALU.max))
            dve.wait_ge(a_exp, 1)
            after(TS(c[:, 4:5], c[:, 2:3], 2.0, None, ALU.add))
            after(dve.reciprocal(c[:, 4:5], c[:, 4:5]))
            after(TT(c[:, 5:6], c[:, 2:3], c[:, 4:5], ALU.mult))
            after(TT(c[:, 6:7], c[:, 5:6], c[:, 5:6], ALU.mult))
            after(TS(c[:, 7:8], c[:, 6:7], 1.0 / 17, 1.0 / 15, ALU.mult, ALU.add))
            for odd in (13, 11, 9, 7, 5, 3, 1):
                after(TT(c[:, 7:8], c[:, 7:8], c[:, 6:7], ALU.mult))
                after(TS(c[:, 7:8], c[:, 7:8], 1.0 / odd, None, ALU.add))
            after(TT(c[:, 7:8], c[:, 7:8], c[:, 5:6], ALU.mult))
            after(STT(out=c[:, 7:8], in0=c[:, 7:8], scalar=2.0, in1=c[:, 3:4], op0=ALU.mult, op1=ALU.add))
            after(TS(c[:, 8:9], c[:, 7:8], -16.0, None, ALU.mult))
            TS(c[:, 9:10], c[:, 7:8], -8.0, None, ALU.mult).then_inc(c_ready, 1)
            after(TS(c[:, 10:11], a_im, 1.0 / float(np.pi), None, ALU.mult))
            TS(c[:, 11:12], a_im, 0.5 / float(np.pi), None, ALU.mult).then_inc(c_ready, 1)
            dve.wait_ge(c_ready, 3)

            dve.wait_ge(gated_act, 1)
            after(TS(f2[:], ga[:], c[:, 10:11], 0.25, ALU.mult, ALU.add))
            after(TS(k2[:], f2[:], ROUND, -ROUND, ALU.add, ALU.add))
            TT(f2[:], f2[:], k2[:], ALU.subtract).then_inc(angle, 1)
            dve.wait_ge(c_ready, 4)
            after(TS(k1[:], f1[:], ROUND, -ROUND, ALU.add, ALU.add))
            TT(f1[:], f1[:], k1[:], ALU.subtract).then_inc(angle, 1)
            after(TS(m1[:], ga[:], c[:, 11:12], None, ALU.mult))
            dve.wait_ge(keep_done, 4)
            after(dve.tensor_tensor_scan(phi[:], keep[:], m1[:], 0.0, ALU.mult, ALU.add))
            ph3 = phi[:].rearrange("p (f n) -> p f n", n=FRAME)
            after(dve.tensor_copy(ends[:], ph3[:, :, FRAME - 1]))
            after(TS(ends_k[:], ends[:], ROUND, -ROUND, ALU.add, ALU.add))
            after(TT(ends_f[:], ends[:], ends_k[:], ALU.subtract))
            after(dve.tensor_tensor_scan(base[:, 1:FRAMES + 1], ones[:], ends_f[:], 0.0, ALU.mult, ALU.add))
            TT(ph3, ph3, base[:, 0:FRAMES].rearrange("p (f a) -> p f a", a=1).to_broadcast([P, FRAMES, FRAME]),
               ALU.add).then_inc(keep_done, 1)
            dve.wait_ge(waved, 1)
            dve.wait_ge(decayed, 1)
            after(TT(zr[:], r2[:], cos2[:], ALU.mult))
            TS(zr[:], zr[:], -1.0, 1.0, ALU.mult, ALU.add).then_inc(z_done, 1)
            dve.wait_ge(waved, 2)
            STT(out=zi[:], in0=r2[:], scalar=-1.0, in1=sin2[:], op0=ALU.mult, op1=ALU.mult).then_inc(z_done, 1)
            dve.wait_ge(keep_done, 5)
            after(TS(p2[:], phi[:], 0.25, None, ALU.add))
            after(TS(k2[:], p2[:], ROUND, -ROUND, ALU.add, ALU.add))
            TT(p2[:], p2[:], k2[:], ALU.subtract).then_inc(angle, 1)
            dve.wait_ge(squared, 2)
            after(TT(m1[:], m1[:], m2[:], ALU.add))
            TS(m1[:], m1[:], 1e-30, None, ALU.max).then_inc(squared, 1)
            dve.wait_ge(rooted, 1)
            TT(k1[:], m2[:], zr[:], ALU.add).then_inc(half_done, 1)
            dve.wait_ge(angle, 3)
            after(TS(k2[:], phi[:], ROUND, -ROUND, ALU.add, ALU.add))
            TT(p1[:], phi[:], k2[:], ALU.subtract).then_inc(angle, 1)
            dve.wait_ge(rooted, 2)
            after(dve.reciprocal(m1[:], sr[:]))
            after(STT(out=si[:], in0=zi[:], scalar=0.5, in1=m1[:], op0=ALU.mult, op1=ALU.mult))
            dve.wait_ge(from_pool, 1)
            after(TT(m1[:], xh[:, 0, :], sr[:], ALU.mult))
            after(TT(m2[:], xh[:, 1, :], si[:], ALU.mult))
            TT(yr[:], m1[:], m2[:], ALU.subtract).then_inc(from_dve, 1)
            dve.wait_ge(from_dve, 1)
            after(TT(m2[:], xh[:, 0, :], si[:], ALU.mult))
            dve.wait_ge(from_pool, 2)
            after(TT(yi[:], g1[:], m2[:], ALU.add))
            dve.wait_ge(waved, 4)
            after(TT(m1[:], yr[:], cos1[:], ALU.mult))
            after(TT(m2[:], yi[:], sin1[:], ALU.mult))
            after(TT(k1[:], m1[:], m2[:], ALU.add))
            dve.wait_ge(decayed, 2)
            dve.tensor_tensor_scan(f1[:], r1[:], k1[:], 0.0, ALU.mult, ALU.add).then_inc(from_dve, 1)
            after(TT(m1[:], yi[:], cos1[:], ALU.mult))
            dve.wait_ge(from_pool, 3)
            after(TT(k2[:], m1[:], g2[:], ALU.subtract))
            after(dve.tensor_tensor_scan(f2[:], r1[:], k2[:], 0.0, ALU.mult, ALU.add))
            dve.wait_ge(from_dve, 2)
            after(TT(m1[:], f1[:], cos1[:], ALU.mult))
            after(TT(m2[:], f2[:], sin1[:], ALU.mult))
            TT(h[:, 0, :], m1[:], m2[:], ALU.subtract).then_inc(ready, 1)
            dve.wait_ge(ready, 1)
            after(TT(m2[:], f2[:], cos1[:], ALU.mult))
            dve.wait_ge(from_pool, 4)
            TT(h[:, 1, :], g1[:], m2[:], ALU.add).then_inc(ready, 1)
            add_gated(dve, core, 0, b_out, out_loaded, 32, gated, bo_done, [ps[:, i % 4, 0:D] for i in range(TILES)],
                      outed, added, norm)


def lora_l3(core, A):
    nc = core.nc
    x, ht, ps = core.x, core.ht, core.ps
    E, R = 8, 16
    SCALING = 32.0 / R
    with ExitStack() as ctx:
        w_a, w_base, w_b, b_base = carve(core.arena, (KT, P + E), (KT, D), (D,), (D,))
        iota = core.sb("iota", [P, E], F32, ctx)
        logit = core.sb("logit", [P, TILES, E], F32, ctx)
        best = core.sb("best", [P, TILES, 8], F32, ctx)
        which = core.sb("which", [P, TILES, 8], U32, ctx)
        which_f = core.sb("which_f", [P, TILES], F32, ctx)
        hot = core.sb("hot", [P, TILES, E], F32, ctx)
        picked = core.sb("l_picked", [P, TILES, P], F32, ctx)
        inner = core.sb("inner", [P, TILES, P], F32, ctx)
        gated = core.sb("gated", [P, 2, D], F32, ctx)
        iota_done = core.sem("iota_done", ctx)
        routed = core.sem("routed", ctx)
        step = core.sem("l_step", ctx)
        picked_done = core.sem("picked_done", ctx)
        turned = core.sem("l_turned", ctx)
        inner_kept = core.sem("inner_kept", ctx)
        outed = core.sem("l_outed", ctx)
        added = core.sem("l_added", ctx)
        bo_done = core.sem("l_bo", ctx)
        IN = [ps[:, i // 3, (i % 3) * (P + E):(i % 3 + 1) * (P + E)] for i in range(TILES)]
        block = ctx.enter_context(nc.Block(no_gpsimd_drain=True))

        @block.gpsimd
        def _(pool):
            pool.iota(iota[:], pattern=[[1, E]], base=0, channel_multiplier=0,
                      allow_small_or_imprecise_dtypes=True).then_inc(iota_done, 1)

        @block.tensor
        def _(pe):
            pe.wait_ge(core.arena_in, 64)
            for i in range(TILES):
                for k in range(KT):
                    last = pe.matmul(IN[i], ht[:, k, i * P:i * P + P], w_a[:, k, :], start=(k == 0), stop=(k == KT - 1))
                if i % 3 == 2 or i == TILES - 1:
                    last.then_inc(routed, 1)
            for i in range(TILES):
                pe.wait_ge(picked_done, i + 1)
                if i >= 2:
                    pe.wait_ge(inner_kept, i - 1)
                pe.transpose(ps[:, 3 + i % 2, 0:P], picked[:, i, :], core.ident[:]).then_inc(turned, 1)
            for i in range(TILES):
                if i >= 2:
                    pe.wait_ge(added, i - 1)
                out = ps[:, 5 + i % 2, 0:D]
                for k in range(KT):
                    pe.matmul(out, ht[:, k, i * P:i * P + P], w_base[:, k, :], start=(k == 0), stop=False)
                pe.wait_ge(inner_kept, i + 1)
                pe.matmul(out, inner[:, i, :], w_b[:], start=False, stop=True).then_inc(outed, 1)

        @block.scalar
        def _(act):
            for i in range(TILES):
                act.wait_ge(turned, i + 1)
                act.activation(inner[:, i, :], ps[:, 3 + i % 2, 0:P], ACT.Copy).then_inc(inner_kept, 1)

        @block.vector
        def _(dve):
            done = [0]

            def after(ins):
                ins.then_inc(step, 1)
                done[0] += 1
                dve.wait_ge(step, done[0])

            for i in range(TILES):
                dve.wait_ge(routed, i // 3 + 1)
                last = dve.tensor_copy(logit[:, i, :], IN[i][:, P:P + E])
            after(last)
            for i in range(TILES):
                last = dve.max(best[:, i, :], logit[:, i, :])
            after(last)
            for i in range(TILES):
                last = dve.max_index(which[:, i, :], best[:, i, :], logit[:, i, :])
            after(last)
            after(dve.tensor_copy(which_f[:], which[:, :, 0]))
            dve.wait_ge(iota_done, 1)
            after(dve.tensor_tensor(hot[:], which_f[:].rearrange("p (t a) -> p t a", a=1).to_broadcast([P, TILES, E]),
                                    iota[:].rearrange("p (a e) -> p a e", a=1).to_broadcast([P, TILES, E]), ALU.is_equal))
            after(dve.tensor_scalar(hot[:], hot[:], SCALING, None, ALU.mult))
            for i in range(TILES):
                dve.tensor_tensor(picked[:, i, :].rearrange("p (e r) -> p e r", e=E),
                                  IN[i][:, 0:P].rearrange("p (e r) -> p e r", e=E),
                                  hot[:, i, :].rearrange("p (e a) -> p e a", a=1).to_broadcast([P, E, R]),
                                  ALU.mult).then_inc(picked_done, 1)
            add_gated(dve, core, 1, b_base, core.arena_in, 64, gated, bo_done, [ps[:, 5 + i % 2, 0:D] for i in range(TILES)],
                      outed, added, None)


def pack(inputs):
    a = {k: np.asarray(v) for k, v in inputs.items()}
    out = {}
    c = np.stack([a[f"L{i}_c"].reshape(KT, P) for i in range(LAYERS)])
    out["cond"] = c.transpose(2, 0, 1)
    for i in range(LAYERS):
        out[f"wmod{i}"] = rows_by_partition(a[f"L{i}_wmod"])
    out["x"] = a["L0_attn_query"].reshape(TILES, P, D).transpose(1, 0, 2)
    heads, hd = 16, 128
    w = np.stack([a[f"L0_attn_w_{n}"].reshape(KT, P, heads, hd) for n in "qkv"]).transpose(3, 2, 0, 1, 4)
    b = [a[f"L0_attn_b_{n}"].reshape(heads, hd, 1) for n in "qk"]
    out["l0_wqkv"] = np.concatenate([w.reshape(heads, P, -1), *b], axis=2)
    out["l0_bv"] = a["L0_attn_b_v"].reshape(heads, hd).T
    out["l0_wo"] = a["L0_attn_w_o"].reshape(heads, hd, D).transpose(1, 0, 2)
    out["l0_bo"] = a["L0_attn_b_o"].reshape(1, D)
    out["early0"] = beside(out["l0_wqkv"][0], out["l0_wqkv"][1])
    out["arena0"] = beside(rows_by_partition(a["L0_ffn_gate_w"].T), on_all(a["L0_ffn_gate_bias"]),
                           *(rows_by_partition(a[f"L0_ffn_shared_{n}"]) for n in ("gate", "up", "down")))
    w13 = np.stack([a["L0_ffn_w1"], a["L0_ffn_w3"]]).reshape(2, 16, 2, KT, P, 128).transpose(1, 4, 2, 0, 3, 5)
    w2 = a["L0_ffn_w2"].reshape(16, 2, 128, D).transpose(0, 2, 1, 3)
    out["l0_wexp"] = np.concatenate([w13.reshape(16, P, -1), w2.reshape(16, P, -1)], axis=2)
    groups, maps, hd = 4, 2, 128
    w, b = a["L1_attn_Wqkv_w"], a["L1_attn_Wqkv_b"]
    nq, nk = 16 * hd, 8 * hd
    wq = w[:nq].reshape(8, maps, hd, KT, P).transpose(0, 4, 1, 3, 2).reshape(8, P, -1)
    bq = b[:nq].reshape(8, maps, hd).transpose(0, 2, 1)
    out["l1_wq"] = np.concatenate([wq, bq], axis=2)
    wk = w[nq:nq + nk].reshape(groups, maps, hd, KT, P).transpose(0, 4, 1, 3, 2).reshape(groups, P, -1)
    bk = b[nq:nq + nk].reshape(groups, maps, hd).transpose(0, 2, 1)
    wv = w[nq + nk:].reshape(groups, 2 * hd, KT, P).transpose(0, 3, 2, 1).reshape(groups, P, -1)
    bv = np.broadcast_to(b[nq + nk:].reshape(groups, 1, 2 * hd), (groups, P, 2 * hd))
    out["l1_wkv"] = np.concatenate([wk, wv, bk, bv], axis=2)
    out["early1"] = beside(out["l1_wkv"][0], out["l1_wq"][0])
    out["l1_lambda"] = np.concatenate([a[f"L1_attn_lambda_{n}"] for n in ("q1", "k1", "q2", "k2")]).reshape(1, -1)
    out["l1_subln"] = a["L1_attn_subln_w"].reshape(KT, P).T
    out["l1_wo"] = rows_by_partition(a["L1_attn_out_w"].T)
    out["l1_bo"] = a["L1_attn_out_b"].reshape(1, D)
    inter = a["L1_ffn_gate_w"].shape[0]
    full = -(-inter // P) * P
    wd = np.pad(a["L1_ffn_down_w"].T, ((0, full - inter), (0, 0)))
    s = np.stack([np.pad(a[f"L1_ffn_{n}_s"], (0, full - inter)) for n in ("gate", "up")])
    out["arena1"] = beside(rows_by_partition(a["L1_ffn_gate_w"].T), rows_by_partition(a["L1_ffn_up_w"].T),
                           rows_by_partition(wd), s.reshape(2, -1, P).transpose(2, 0, 1), on_all(a["L1_ffn_down_s"]))
    out["early2"] = beside(*(rows_by_partition(a[f"L2_attn_W{n}"]) for n in "qkv"),
                           np.stack([a[f"L2_attn_b{n}"].reshape(KT, P) for n in "qkv"]).transpose(2, 0, 1))
    out["l2_wo"] = rows_by_partition(a["L2_attn_Wo"])
    out["l2_bo"] = a["L2_attn_bo"].reshape(1, D)
    out["arena2"] = beside(*(rows_by_partition(a[f"L2_ffn_w_{n}"].T) for n in ("gate", "up", "down")))
    wg = np.zeros((2, D, P), a["L3_attn_W_gx"].dtype)
    for g, n in enumerate(("x", "a")):
        blocks, rows, cols = a[f"L3_attn_W_g{n}"].shape
        for b in range(blocks):
            wg[g, b * rows:(b + 1) * rows, b * cols:(b + 1) * cols] = a[f"L3_attn_W_g{n}"][b]
    cols = np.stack([a["L3_attn_b_in"][:P], a["L3_attn_b_in"][P:], a["L3_attn_b_gx"].reshape(-1),
                     a["L3_attn_b_ga"].reshape(-1), a["L3_attn_a_real"], a["L3_attn_a_imag"]], axis=1)
    out["early3"] = beside(rows_by_partition(a["L3_attn_W_in"]), wg.reshape(2, KT, P, P).transpose(2, 0, 1, 3), cols)
    out["l3_wout"] = rows_by_partition(a["L3_attn_W_out"])
    out["l3_bout"] = a["L3_attn_b_out"].reshape(1, D)
    inner = np.concatenate([a["L3_ffn_A"].reshape(P, D), a["L3_ffn_router_W"]])
    out["arena3"] = beside(rows_by_partition(inner.T), rows_by_partition(a["L3_ffn_W_base"].T),
                           a["L3_ffn_Bw"].transpose(0, 2, 1).reshape(P, D), on_all(a["L3_ffn_b_base"]))
    return {k: np.ascontiguousarray(v) for k, v in out.items()}


def beside(*parts):
    return np.concatenate([p.reshape(P, -1) for p in parts], axis=1)


def on_all(row):
    return np.broadcast_to(row.reshape(1, -1), (P, row.size))


def rows_by_partition(w):
    return w.reshape(-1, P, w.shape[1]).transpose(1, 0, 2)


def adaln_stack(nc, A, out):
    attention = (attention_l0, attention_l1, attention_l2, recurrence_l3)
    ffn = (moe, ffn_l1, ffn_l2)
    with ExitStack() as ctx:
        core = Core(nc, ctx)
        start(core, A)
        for layer in range(LAYERS):
            core.use_layer(layer)
            attention[layer](core, A, Norm(core, 2 * layer + 1))
            if layer + 1 < LAYERS:
                ffn[layer](core, A, Norm(core, 2 * layer + 2))
            else:
                lora_l3(core, A)
        with nc.Block(no_gpsimd_drain=True) as block:
            @block.sync
            def _(sp):
                sp.dma_start(out.rearrange("a (t p) d -> p (a t) d", p=P), core.x[:]).then_inc(core.s_x, 16)
                sp.wait_ge(core.s_x, 48)


def kernel(**inputs):
    import concourse.bacc as bacc
    from concourse.bass_utils import run_bass_kernel_spmd

    nc = bacc.Bacc("TRN2", target_bir_lowering=False, num_devices=1)
    arrays = {f"in_{name}": array for name, array in pack(inputs).items()}
    A = {name[3:]: nc.dram_tensor(name, array.shape, mybir.dt.from_np(array.dtype), kind="ExternalInput").ap()
         for name, array in arrays.items()}
    out = nc.dram_tensor("out", (1, TOKENS, D), F32, kind="ExternalOutput").ap()
    adaln_stack(nc, A, out)
    r = run_bass_kernel_spmd(nc, [arrays], core_ids=[0])
    return r.results[0]["out"]
```
